# Optimizing a Trainium2 kernel written in Bass

```python
import numpy as np
import jax
import jax.numpy as jnp

def _softmax(x, axis=-1):
    return jax.nn.softmax(x, axis=axis)

def _gelu(x):
    return jax.nn.gelu(x, approximate=True)

def _silu(x):
    return jax.nn.silu(x)

def _sigmoid(x):
    return jax.nn.sigmoid(x)

def _layernorm(x, axis=-1, eps=1e-05):
    m = jnp.mean(x, axis=axis, keepdims=True)
    v = jnp.var(x, axis=axis, keepdims=True)
    return (x - m) / jnp.sqrt(v + eps)

def _scatter_add(tgt, idx, src, axis=0):
    return tgt.at[idx].add(src)

def _segment_sum(src, seg, n):
    return jax.ops.segment_sum(src, seg, n)
kernel_name = 'mk_decoder_preln_d4_seqx_r8_ebb16e'

def setup_inputs(seed: int=0):
    np.random.seed(seed)
    _w = jnp.asarray

    def _rec_inputs():
        import jax
        import jax.numpy as jnp
        _rk = jax.random.key(seed)
        x = 7.22e-05 + 1 * jax.random.normal(jax.random.fold_in(_rk, 1), (8, 256, 128), jnp.float32)
        _lenS = 256 - jax.random.randint(jax.random.fold_in(_rk, 7), (8,), 0, max(1, 256 // 4) + 1, jnp.int32)
        _lenS2 = 256 - jax.random.randint(jax.random.fold_in(_rk, 8), (8,), 0, max(1, 256 // 4) + 1, jnp.int32)
        _ctx_1024P = jax.random.normal(jax.random.fold_in(_rk, 11), (8, 16, 128), jnp.float32)
        _ctx_1024c = jax.random.dirichlet(jax.random.fold_in(_rk, 511), 0.3 * jnp.ones((16,), jnp.float32), (8, 256))
        _ctx_1024t = jnp.einsum('bsk,bkd->bsd', _ctx_1024c, _ctx_1024P)
        _ctx_1024t = _ctx_1024t * jax.lax.rsqrt(jnp.mean(jnp.square(_ctx_1024t)) + 1e-12) * 0.953939
        ctx_1024 = 4.13588e-05 + 0.999923 * (_ctx_1024t + 0.3 * jax.random.normal(jax.random.fold_in(_rk, 611), (8, 256, 128), jnp.float32))
        _validS = jnp.arange(256)[None, :] < _lenS[:, None]
        _validS2 = jnp.arange(256)[None, :] < _lenS2[:, None]
        _causal = jnp.tril(jnp.ones((256, 256), dtype=bool))
        mask_B_ik0 = jnp.where(jnp.ones((8,), dtype=bool), 69, 1564).astype(jnp.int32)
        mask_BxS2_bk0 = jnp.logical_not(jnp.broadcast_to(_validS2[:, :], (8, 256)))
        return (x, ctx_1024, mask_B_ik0, mask_BxS2_bk0)
    x, ctx_1024, mask_B_ik0, mask_BxS2_bk0 = _rec_inputs()

    def _L0_attn_setup():
        import math
        import jax, jax.numpy as jnp
        import numpy as np
        D = 128
        H = 16
        DH = D // H
        BETA_MIN, BETA_MAX = (0.1, 10.0)
        EPS_NORM = 1e-06

        def _layernorm(x, g, b, eps=1e-05):
            mu = jnp.mean(x, axis=-1, keepdims=True)
            var = jnp.mean((x - mu) ** 2, axis=-1, keepdims=True)
            return (x - mu) * jax.lax.rsqrt(var + eps) * g + b

        def _l2norm(x, eps=EPS_NORM):
            n = jnp.linalg.norm(x, axis=-1, keepdims=True)
            return x / jnp.maximum(n, eps)
        key = jax.random.key(seed)
        ks = jax.random.split(key, 10)
        B, T = (2, 256)
        gain_qk = 1.0 / math.sqrt(2.0)
        lim = math.sqrt(6.0 / (D + D))
        inp = {'query': jax.random.normal(ks[0], (B, T, D), dtype=jnp.float32), 'q_w': jax.random.uniform(ks[1], (D, D), jnp.float32, -lim * gain_qk, lim * gain_qk), 'k_w': jax.random.uniform(ks[2], (D, D), jnp.float32, -lim * gain_qk, lim * gain_qk), 'v_w': jax.random.uniform(ks[3], (D, D), jnp.float32, -lim, lim), 'o_w': jax.random.uniform(ks[4], (D, D), jnp.float32, -lim, lim), 'q_b': jnp.zeros((D,), jnp.float32), 'k_b': jnp.zeros((D,), jnp.float32), 'v_b': jnp.zeros((D,), jnp.float32), 'o_b': jnp.zeros((D,), jnp.float32), 'ln_q_g': jnp.ones((D,), jnp.float32), 'ln_q_b': jnp.zeros((D,), jnp.float32), 'ln_k_g': jnp.ones((D,), jnp.float32), 'ln_k_b': jnp.zeros((D,), jnp.float32), 'ln_v_g': jnp.ones((D,), jnp.float32), 'ln_v_b': jnp.zeros((D,), jnp.float32), 'beta_param': jnp.log(jnp.expm1(jax.random.uniform(ks[5], (H,), jnp.float32, 0.5, 1.5)))}
        return inp
    _L0_attn_all = _L0_attn_setup()
    _L0_attn_in = {k: v for k, v in _L0_attn_all.items() if k in ('q_w', 'k_w', 'v_w', 'o_w', 'q_b', 'k_b', 'v_b', 'o_b', 'ln_q_g', 'ln_q_b', 'ln_k_g', 'ln_k_b', 'ln_v_g', 'ln_v_b', 'beta_param')}
    del _L0_attn_all

    def _L0_xattn_setup():
        import jax, jax.numpy as jnp
        import numpy as np
        B, T, D, H = (4, 256, 128, 512)
        S = 32
        EPS = 1e-05

        def _layer_norm(x, gamma, beta):
            mu = jnp.mean(x, axis=-1, keepdims=True)
            var = jnp.mean(jnp.square(x - mu), axis=-1, keepdims=True)
            return (x - mu) * jax.lax.rsqrt(var + EPS) * gamma + beta

        def _aft_local(emb, wq, bq, wk, bk, wv, bv, wo, bo, pos_bias):
            q = emb @ wq + bq
            k = emb @ wk + bk
            v = emb @ wv + bv
            idx = jnp.arange(T)
            mask = (jnp.abs(idx[:, None] - idx[None, :]) < S).astype(pos_bias.dtype)
            w = pos_bias * mask
            max_k = jnp.max(k, axis=1, keepdims=True)
            max_w = jnp.max(w, axis=1, keepdims=True)
            ek = jnp.exp(k - max_k)
            ew = jnp.exp(w - max_w)
            num = jnp.einsum('tj,bjd->btd', ew, ek * v)
            den = jnp.einsum('tj,bjd->btd', ew, ek)
            y = jax.nn.sigmoid(q) * num / den
            return y @ wo + bo
        key = jax.random.key(seed)
        ks = jax.random.split(key, 16)
        sd = 0.02
        return {'x': jax.random.normal(ks[0], (B, T, D), jnp.float32), 'pos_encod': jax.random.normal(ks[1], (B, T, D), jnp.float32), 'wq': jax.random.normal(ks[2], (D, D), jnp.float32) * sd, 'bq': jnp.zeros((D,), jnp.float32), 'wk': jax.random.normal(ks[3], (D, D), jnp.float32) * sd, 'bk': jnp.zeros((D,), jnp.float32), 'wv': jax.random.normal(ks[4], (D, D), jnp.float32) * sd, 'bv': jnp.zeros((D,), jnp.float32), 'wo': jax.random.normal(ks[5], (D, D), jnp.float32) * sd, 'bo': jnp.zeros((D,), jnp.float32), 'pos_bias': jax.random.normal(ks[6], (T, T), jnp.float32) * sd, 'gamma': jnp.ones((D,), jnp.float32), 'beta': jnp.zeros((D,), jnp.float32), 'w1': jax.random.normal(ks[7], (D, H), jnp.float32) * sd, 'b1': jnp.zeros((H,), jnp.float32), 'w2': jax.random.normal(ks[8], (H, D), jnp.float32) * sd, 'b2': jnp.zeros((D,), jnp.float32)}
    _L0_xattn_all = _L0_xattn_setup()
    _L0_xattn_in = {k: v for k, v in _L0_xattn_all.items() if k in ('wq', 'bq', 'wk', 'bk', 'wv', 'bv', 'wo', 'bo', 'pos_bias', 'gamma', 'beta', 'w1', 'b1', 'w2', 'b2')}
    del _L0_xattn_all

    def _L0_ffn_setup():
        import jax, jax.numpy as jnp
        import numpy as np
        B, S, H = (4, 256, 128)
        E, K = (8, 2)
        I_R, I_S = (4 * H, 8 * H)
        CAP_FACTOR = 1.25
        SCALE = 1.0
        key = jax.random.key(seed)
        ks = jax.random.split(key, 9)
        std = 0.02
        return {'x': jax.random.normal(ks[0], (B, S, H), jnp.float32), 'router_w': std * jax.random.normal(ks[1], (E, H), jnp.float32), 'rg': std * jax.random.normal(ks[2], (E, H, I_R), jnp.float32), 'ru': std * jax.random.normal(ks[3], (E, H, I_R), jnp.float32), 'rd': std * jax.random.normal(ks[4], (E, I_R, H), jnp.float32), 'sg': std * jax.random.normal(ks[5], (H, I_S), jnp.float32), 'su': std * jax.random.normal(ks[6], (H, I_S), jnp.float32), 'sd': std * jax.random.normal(ks[7], (I_S, H), jnp.float32)}
    _L0_ffn_all = _L0_ffn_setup()
    _L0_ffn_in = {k: v for k, v in _L0_ffn_all.items() if k in ('router_w', 'rg', 'ru', 'rd', 'sg', 'su', 'sd')}
    del _L0_ffn_all

    def _L1_attn_setup():
        import jax, jax.numpy as jnp
        import numpy as np
        from jax import lax
        B, L, D = (2, 512, 128)
        H = 8
        DK = D // H
        DV = D // H
        CONV_K = 4
        CHUNK = 32
        EPS = 1e-05

        def _silu(x):
            return x * jax.nn.sigmoid(x)

        def _causal_depthwise_conv_silu(x, w):
            K = w.shape[1]
            l = x.shape[1]
            xp = jnp.pad(x, ((0, 0), (K - 1, 0), (0, 0)))
            y = sum((xp[:, i:i + l, :] * w[:, i] for i in range(K)))
            return _silu(y)

        def _l2norm(x):
            return x * lax.rsqrt(jnp.sum(x * x, axis=-1, keepdims=True) + 1e-12)

        def _delta_rule_chunkwise(q, k, v, beta, chunk=CHUNK):
            b, h, l, dk = q.shape
            dv = v.shape[-1]
            n = l // chunk
            q = _l2norm(q)
            k = _l2norm(k)
            v = v * beta[..., None]
            kb = k * beta[..., None]
            resh = lambda t: t.reshape(b, h, n, chunk, t.shape[-1])
            q, k, v, kb = map(resh, (q, k, v, kb))
            tri_strict = jnp.tril(jnp.ones((chunk, chunk), dtype=bool), -1)
            attn = jnp.where(tri_strict, -(kb @ jnp.swapaxes(k, -1, -2)), 0.0)
            col = jnp.arange(chunk)
            for i in range(1, chunk):
                row = attn[..., i, :]
                upd = jnp.einsum('bhnj,bhnjk->bhnk', row, attn)
                attn = attn.at[..., i, :].set(jnp.where(col < i, row + upd, row))
            attn = attn + jnp.eye(chunk, dtype=attn.dtype)
            u = attn @ v
            w = attn @ kb
            tri_incl = jnp.tril(jnp.ones((chunk, chunk), dtype=bool))
            qc, kc, uc, wc = (jnp.moveaxis(t, 2, 0) for t in (q, k, u, w))

            def step(S, inp):
                qi, ki, ui, wi = inp
                attn_i = jnp.where(tri_incl, qi @ jnp.swapaxes(ki, -1, -2), 0.0)
                ui = ui - wi @ S
                oi = qi @ S + attn_i @ ui
                S = S + jnp.swapaxes(ki, -1, -2) @ ui
                return (S, oi)
            S0 = jnp.zeros((b, h, dk, dv), dtype=q.dtype)
            S, o = lax.scan(step, S0, (qc, kc, uc, wc))
            o = jnp.moveaxis(o, 0, 2).reshape(b, h, l, dv)
            return (o, S)
        key = jax.random.key(seed)
        ks = jax.random.split(key, 10)
        s = 0.02
        return {'hidden_states': jax.random.normal(ks[0], (B, L, D), jnp.float32), 'q_w': jax.random.normal(ks[1], (D, D), jnp.float32) * s, 'k_w': jax.random.normal(ks[2], (D, D), jnp.float32) * s, 'v_w': jax.random.normal(ks[3], (D, D), jnp.float32) * s, 'conv_q_w': jax.random.normal(ks[4], (D, CONV_K), jnp.float32) * 0.3, 'conv_k_w': jax.random.normal(ks[5], (D, CONV_K), jnp.float32) * 0.3, 'conv_v_w': jax.random.normal(ks[6], (D, CONV_K), jnp.float32) * 0.3, 'b_w': jax.random.normal(ks[7], (D, H), jnp.float32) * s, 'mix_w': jax.random.normal(ks[8], (D, H), jnp.float32) * s, 'mix_b': jnp.full((H,), -1.0, jnp.float32), 'mix_bias': jnp.full((H,), -1.0, jnp.float32), 'o_norm_w': jnp.ones((DV,), jnp.float32), 'o_w': jax.random.normal(ks[9], (D, D), jnp.float32) * s}
    _L1_attn_all = _L1_attn_setup()
    _L1_attn_in = {k: v for k, v in _L1_attn_all.items() if k in ('q_w', 'k_w', 'v_w', 'conv_q_w', 'conv_k_w', 'conv_v_w', 'b_w', 'mix_w', 'mix_b', 'mix_bias', 'o_norm_w', 'o_w')}
    del _L1_attn_all

    def _L1_xattn_setup():
        import jax, jax.numpy as jnp
        import numpy as np
        import math
        N_HEADS = 16
        HEAD_DIM = 64
        D_MODEL = 128
        B, S = (2, 256)

        def _split_heads(x):
            b, s, _ = x.shape
            return x.reshape(b, s, N_HEADS, HEAD_DIM).transpose(0, 2, 1, 3)
        key = jax.random.key(seed)
        ks = jax.random.split(key, 12)
        Dh = N_HEADS * HEAD_DIM
        sc = 1.0 / math.sqrt(D_MODEL)
        return {'will_be_queries': jax.random.normal(ks[0], (B, S, D_MODEL), jnp.float32), 'will_be_keys': jax.random.normal(ks[1], (B, S, D_MODEL), jnp.float32), 'will_be_values': jax.random.normal(ks[2], (B, S, D_MODEL), jnp.float32), 'valid_len': jax.random.randint(ks[3], (B,), 1, S + 1, jnp.int32), 'w_q': jax.random.normal(ks[4], (Dh, D_MODEL), jnp.float32) * sc, 'b_q': jnp.zeros((Dh,), jnp.float32), 'w_k': jax.random.normal(ks[5], (Dh, D_MODEL), jnp.float32) * sc, 'b_k': jnp.zeros((Dh,), jnp.float32), 'w_v': jax.random.normal(ks[6], (Dh, D_MODEL), jnp.float32) * sc, 'b_v': jnp.zeros((Dh,), jnp.float32), 'w_o': jax.random.normal(ks[7], (D_MODEL, Dh), jnp.float32) * sc, 'b_o': jnp.zeros((D_MODEL,), jnp.float32)}
    _L1_xattn_all = _L1_xattn_setup()
    _L1_xattn_in = {k: v for k, v in _L1_xattn_all.items() if k in ('w_q', 'b_q', 'w_k', 'b_k', 'w_v', 'b_v', 'w_o', 'b_o')}
    del _L1_xattn_all

    def _L1_ffn_setup():
        import jax, jax.numpy as jnp
        import numpy as np
        B, S, D, H, O, E, K = (4, 256, 128, 256, 128, 8, 2)
        key = jax.random.key(seed)
        ks = jax.random.split(key, 8)
        x = jax.random.normal(ks[0], (B, S, D), dtype=jnp.float32)
        gate_w = jax.random.uniform(ks[1], (E, D), dtype=jnp.float32, minval=-1, maxval=1) * np.sqrt(6.0 / D)
        gate_b = jnp.zeros((E,), dtype=jnp.float32)
        w1 = jax.random.uniform(ks[2], (E, D, H), dtype=jnp.float32, minval=-1, maxval=1) * np.sqrt(6.0 / D)
        b1 = jnp.zeros((E, H), dtype=jnp.float32)
        w2 = jax.random.uniform(ks[3], (E, H, O), dtype=jnp.float32, minval=-1, maxval=1) * np.sqrt(6.0 / H)
        b2 = jnp.zeros((E, O), dtype=jnp.float32)
        return {'x': x, 'gate_w': gate_w, 'gate_b': gate_b, 'w1': w1, 'b1': b1, 'w2': w2, 'b2': b2}
    _L1_ffn_all = _L1_ffn_setup()
    _L1_ffn_in = {k: v for k, v in _L1_ffn_all.items() if k in ('gate_w', 'gate_b', 'w1', 'b1', 'w2', 'b2')}
    del _L1_ffn_all

    def _L2_attn_setup():
        import jax, jax.numpy as jnp
        import numpy as np
        N_EMBD = 128
        N_HEAD = 8
        HEAD_DIM = N_EMBD // N_HEAD
        EPS = 1e-06

        def _lrpe(xh, theta, n):
            idx = jnp.arange(n, dtype=xh.dtype).reshape(1, n, 1)
            th = theta * idx
            th = th[None]
            return jnp.concatenate([xh * jnp.cos(th), xh * jnp.sin(th)], axis=-1)

        def _srmsnorm(y):
            ms = jnp.mean(jnp.square(y), axis=-1, keepdims=True)
            return y * jax.lax.rsqrt(ms + EPS)
        key = jax.random.key(seed)
        ks = jax.random.split(key, 8)
        b, n = (2, 256)
        x = jax.random.normal(ks[0], (b, n, N_EMBD), dtype=jnp.float32)
        slope_rate = -jax.random.uniform(ks[1], (N_HEAD, 1, 1), dtype=jnp.float32)
        s = 0.02
        qkvu_w = jax.random.normal(ks[2], (4 * N_EMBD, N_EMBD), dtype=jnp.float32) * s
        qkvu_b = jnp.zeros((4 * N_EMBD,), dtype=jnp.float32)
        out_w = jax.random.normal(ks[3], (N_EMBD, N_EMBD), dtype=jnp.float32) * s
        out_b = jnp.zeros((N_EMBD,), dtype=jnp.float32)
        d = N_EMBD
        theta = (10000.0 ** (-2.0 / d * jnp.arange(d, dtype=jnp.float32))).reshape(N_HEAD, 1, HEAD_DIM)
        return {'x': x, 'slope_rate': slope_rate, 'qkvu_w': qkvu_w, 'qkvu_b': qkvu_b, 'out_w': out_w, 'out_b': out_b, 'theta': theta}
    _L2_attn_all = _L2_attn_setup()
    _L2_attn_in = {k: v for k, v in _L2_attn_all.items() if k in ('slope_rate', 'qkvu_w', 'qkvu_b', 'out_w', 'out_b', 'theta')}
    del _L2_attn_all

    def _L2_xattn_setup():
        import jax, jax.numpy as jnp
        import numpy as np
        NUM_HEADS, NUM_KV, HEAD_DIM, WIDTH = (4, 1, 32, 128)
        MASK_FILL = -2.3819763e+38

        def _apply_rope(x, positions, max_wavelength=10000.0):
            d = x.shape[-1]
            freq_exp = 2.0 / d * jnp.arange(d // 2, dtype=jnp.float32)
            timescale = max_wavelength ** freq_exp
            radians = positions[..., None].astype(jnp.float32) / timescale
            radians = radians[..., None, :]
            sin, cos = (jnp.sin(radians), jnp.cos(radians))
            x1, x2 = jnp.split(x, 2, axis=-1)
            out = jnp.concatenate([x1 * cos - x2 * sin, x2 * cos + x1 * sin], axis=-1)
            return out.astype(x.dtype)

        def _rmsnorm(x, scale):
            var = jnp.mean(jnp.square(x.astype(jnp.float32)), axis=-1, keepdims=True)
            normed = x * jax.lax.rsqrt(var + 1e-06)
            return (normed * (1 + scale)).astype(x.dtype)
        key = jax.random.key(seed)
        ks = jax.random.split(key, 7)
        B, T, S = (8, 64, 256)
        return {'x': jax.random.normal(ks[0], (B, T, WIDTH), jnp.float32), 'mem_seq': jax.random.normal(ks[1], (B, S, WIDTH), jnp.float32), 'mem_mask': jax.random.randint(ks[2], (B, S), 0, 2).astype(bool), 'rms_scale': jax.random.normal(ks[3], (WIDTH,), jnp.float32) * 0.02, 'q_w': jax.random.normal(ks[4], (NUM_HEADS, WIDTH, HEAD_DIM), jnp.float32) / np.sqrt(WIDTH), 'kv_w': jax.random.normal(ks[5], (2, NUM_KV, WIDTH, HEAD_DIM), jnp.float32) / np.sqrt(WIDTH), 'out_w': jax.random.normal(ks[6], (NUM_HEADS, HEAD_DIM, WIDTH), jnp.float32) / np.sqrt(NUM_HEADS * HEAD_DIM)}
    _L2_xattn_all = _L2_xattn_setup()
    _L2_xattn_in = {k: v for k, v in _L2_xattn_all.items() if k in ('rms_scale', 'q_w', 'kv_w', 'out_w')}
    del _L2_xattn_all

    def _L2_ffn_setup():
        import jax, jax.numpy as jnp
        import numpy as np
        QMAX = 127.0

        def _ste_round(v):
            return v + jax.lax.stop_gradient(jnp.round(v) - v)

        def _act_fake_quant(x, clip_factor):
            scale = jax.nn.sigmoid(clip_factor) * jnp.max(jnp.abs(x)) / QMAX
            return jnp.clip(_ste_round(x / scale), -QMAX - 1.0, QMAX) * scale

        def _weight_fake_quant(w):
            scale = jnp.max(jnp.abs(w), axis=1, keepdims=True) / QMAX
            return jnp.clip(_ste_round(w / scale), -QMAX - 1.0, QMAX) * scale
        key = jax.random.key(seed)
        k1, k2, k3, k4 = jax.random.split(key, 4)
        B, S, H, I = (8, 1024, 128, 352)
        return {'x': jax.random.normal(k1, (B, S, H), dtype=jnp.float32), 'clip_x': jnp.full((1,), 4.0, dtype=jnp.float32), 'clip_down': jnp.full((1,), 4.0, dtype=jnp.float32), 'w_gate': jax.random.normal(k2, (I, H), dtype=jnp.float32) * 0.02, 'w_up': jax.random.normal(k3, (I, H), dtype=jnp.float32) * 0.02, 'w_down': jax.random.normal(k4, (H, I), dtype=jnp.float32) * 0.02}
    _L2_ffn_all = _L2_ffn_setup()
    _L2_ffn_in = {k: v for k, v in _L2_ffn_all.items() if k in ('clip_x', 'clip_down', 'w_gate', 'w_up', 'w_down')}
    del _L2_ffn_all

    def _L3_attn_setup():
        import jax, jax.numpy as jnp
        import numpy as np
        B, S, E, H, K = (2, 256, 128, 16, 32)
        D = E // H
        key = jax.random.key(seed)
        ks = jax.random.split(key, 9)
        sc = 1.0 / np.sqrt(E)
        return {'x': jax.random.normal(ks[0], (B, S, E), dtype=jnp.float32), 'Wq': jax.random.normal(ks[1], (E, E), dtype=jnp.float32) * sc, 'bq': jnp.zeros((E,), dtype=jnp.float32), 'Wk': jax.random.normal(ks[2], (E, E), dtype=jnp.float32) * sc, 'bk': jnp.zeros((E,), dtype=jnp.float32), 'Wv': jax.random.normal(ks[3], (E, E), dtype=jnp.float32) * sc, 'bv': jnp.zeros((E,), dtype=jnp.float32), 'Wo': jax.random.normal(ks[4], (E, E), dtype=jnp.float32) * sc, 'bo': jnp.zeros((E,), dtype=jnp.float32)}
    _L3_attn_all = _L3_attn_setup()
    _L3_attn_in = {k: v for k, v in _L3_attn_all.items() if k in ('Wq', 'bq', 'Wk', 'bk', 'Wv', 'bv', 'Wo', 'bo')}
    del _L3_attn_all

    def _L3_xattn_setup():
        import jax, jax.numpy as jnp
        import numpy as np
        B, TQ, TK, D_MODEL, N_HEAD, STRIDE = (1, 128, 1024, 128, 16, 16)
        HEAD_DIM = D_MODEL // N_HEAD
        key = jax.random.key(seed)
        ks = jax.random.split(key, 11)
        s = 1.0 / np.sqrt(D_MODEL)
        return {'q': jax.random.normal(ks[0], (B, TQ, D_MODEL), jnp.float32), 'k': jax.random.normal(ks[1], (B, TK, D_MODEL), jnp.float32), 'v': jax.random.normal(ks[2], (B, TK, D_MODEL), jnp.float32), 'Wq': jax.random.normal(ks[3], (D_MODEL, D_MODEL), jnp.float32) * s, 'bq': jnp.zeros((D_MODEL,), jnp.float32), 'Wk': jax.random.normal(ks[4], (D_MODEL, D_MODEL), jnp.float32) * s, 'bk': jnp.zeros((D_MODEL,), jnp.float32), 'Wv': jax.random.normal(ks[5], (D_MODEL, D_MODEL), jnp.float32) * s, 'bv': jnp.zeros((D_MODEL,), jnp.float32), 'Wo': jax.random.normal(ks[6], (D_MODEL, D_MODEL), jnp.float32) * s, 'bo': jnp.zeros((D_MODEL,), jnp.float32)}
    _L3_xattn_all = _L3_xattn_setup()
    _L3_xattn_in = {k: v for k, v in _L3_xattn_all.items() if k in ('Wq', 'bq', 'Wk', 'bk', 'Wv', 'bv', 'Wo', 'bo')}
    del _L3_xattn_all

    def _L3_ffn_setup():
        import jax, jax.numpy as jnp
        import numpy as np
        D = 128
        H = 4
        HD = D // H
        E = 8
        FF = 512
        CAP_FACTOR = 1.0

        def _ln(x, g, b, eps=1e-05):
            mu = jnp.mean(x, -1, keepdims=True)
            v = jnp.mean((x - mu) ** 2, -1, keepdims=True)
            return (x - mu) * jax.lax.rsqrt(v + eps) * g + b

        def _mha(x, w, b, ow, ob):
            L, N, _ = x.shape
            qkv = x @ w.T + b
            q, k, v = jnp.split(qkv, 3, axis=-1)
            rh = lambda t: t.reshape(L, N, H, HD).transpose(1, 2, 0, 3)
            q, k, v = (rh(q), rh(k), rh(v))
            scores = jnp.einsum('nhld,nhmd->nhlm', q, k) / np.float32(np.sqrt(HD))
            attn = jax.nn.softmax(scores, axis=-1)
            o = jnp.einsum('nhlm,nhmd->nhld', attn, v).transpose(2, 0, 1, 3).reshape(L, N, D)
            return o @ ow.T + ob

        def _moe(x, wg, w1, b1, w2, b2):
            L, N, _ = x.shape
            S = L * N
            cap = int(CAP_FACTOR * S) // E
            xf = x.reshape(S, D)
            gates = jax.nn.softmax(xf @ wg, axis=-1)
            idx = jnp.argmax(gates, axis=-1)
            mask1 = jax.nn.one_hot(idx, E, dtype=x.dtype)
            loc = jnp.sum((jnp.cumsum(mask1, 0) - 1.0) * mask1, -1).astype(jnp.int32)
            keep = loc < cap
            gate_val = jnp.take_along_axis(gates, idx[:, None], -1)[:, 0]
            slot = jnp.where(keep, idx.astype(jnp.int32) * cap + loc, E * cap)
            disp = jnp.zeros((E * cap, D), x.dtype).at[slot].set(xf, mode='drop')
            disp = disp.reshape(E, cap, D)
            h = jnp.einsum('ecd,edf->ecf', disp, w1) + b1[:, None, :]
            y = (jnp.einsum('ecf,efd->ecd', h, w2) + b2[:, None, :]).reshape(E * cap, D)
            out = jnp.where(keep[:, None], gate_val[:, None] * y[jnp.minimum(slot, E * cap - 1)], 0.0)
            return out.reshape(L, N, D)
        key = jax.random.key(seed)
        ks = jax.random.split(key, 8)
        L, N = (128, 16)
        s = 0.02
        return {'x': jax.random.normal(ks[0], (L, N, D), jnp.float32), 'in_proj_w': jax.random.normal(ks[1], (3 * D, D), jnp.float32) * s, 'in_proj_b': jnp.zeros((3 * D,), jnp.float32), 'out_proj_w': jax.random.normal(ks[2], (D, D), jnp.float32) * s, 'out_proj_b': jnp.zeros((D,), jnp.float32), 'ln1_g': jnp.ones((D,), jnp.float32), 'ln1_b': jnp.zeros((D,), jnp.float32), 'ln2_g': jnp.ones((D,), jnp.float32), 'ln2_b': jnp.zeros((D,), jnp.float32), 'wg': jax.random.normal(ks[3], (D, E), jnp.float32) * s, 'w1': jax.random.normal(ks[4], (E, D, FF), jnp.float32) * s, 'b1': jnp.zeros((E, FF), jnp.float32), 'w2': jax.random.normal(ks[5], (E, FF, D), jnp.float32) * s, 'b2': jnp.zeros((E, D), jnp.float32)}
    _L3_ffn_all = _L3_ffn_setup()
    _L3_ffn_in = {k: v for k, v in _L3_ffn_all.items() if k in ('in_proj_w', 'in_proj_b', 'out_proj_w', 'out_proj_b', 'ln1_g', 'ln1_b', 'ln2_g', 'ln2_b', 'wg', 'w1', 'b1', 'w2', 'b2')}
    del _L3_ffn_all
    return {'x': x, 'ctx_1024': ctx_1024, 'mask_B_ik0': mask_B_ik0, 'mask_BxS2_bk0': mask_BxS2_bk0, 'L0_attn_q_w': _L0_attn_in['q_w'], 'L0_attn_k_w': _L0_attn_in['k_w'], 'L0_attn_v_w': _L0_attn_in['v_w'], 'L0_attn_o_w': _L0_attn_in['o_w'], 'L0_attn_q_b': _L0_attn_in['q_b'], 'L0_attn_k_b': _L0_attn_in['k_b'], 'L0_attn_v_b': _L0_attn_in['v_b'], 'L0_attn_o_b': _L0_attn_in['o_b'], 'L0_attn_ln_q_g': _L0_attn_in['ln_q_g'], 'L0_attn_ln_q_b': _L0_attn_in['ln_q_b'], 'L0_attn_ln_k_g': _L0_attn_in['ln_k_g'], 'L0_attn_ln_k_b': _L0_attn_in['ln_k_b'], 'L0_attn_ln_v_g': _L0_attn_in['ln_v_g'], 'L0_attn_ln_v_b': _L0_attn_in['ln_v_b'], 'L0_attn_beta_param': _L0_attn_in['beta_param'], 'L0_xattn_wq': _L0_xattn_in['wq'], 'L0_xattn_bq': _L0_xattn_in['bq'], 'L0_xattn_wk': _L0_xattn_in['wk'], 'L0_xattn_bk': _L0_xattn_in['bk'], 'L0_xattn_wv': _L0_xattn_in['wv'], 'L0_xattn_bv': _L0_xattn_in['bv'], 'L0_xattn_wo': _L0_xattn_in['wo'], 'L0_xattn_bo': _L0_xattn_in['bo'], 'L0_xattn_pos_bias': _L0_xattn_in['pos_bias'], 'L0_xattn_gamma': _L0_xattn_in['gamma'], 'L0_xattn_beta': _L0_xattn_in['beta'], 'L0_xattn_w1': _L0_xattn_in['w1'], 'L0_xattn_b1': _L0_xattn_in['b1'], 'L0_xattn_w2': _L0_xattn_in['w2'], 'L0_xattn_b2': _L0_xattn_in['b2'], 'L0_ffn_router_w': _L0_ffn_in['router_w'], 'L0_ffn_rg': _L0_ffn_in['rg'], 'L0_ffn_ru': _L0_ffn_in['ru'], 'L0_ffn_rd': _L0_ffn_in['rd'], 'L0_ffn_sg': _L0_ffn_in['sg'], 'L0_ffn_su': _L0_ffn_in['su'], 'L0_ffn_sd': _L0_ffn_in['sd'], 'L1_attn_q_w': _L1_attn_in['q_w'], 'L1_attn_k_w': _L1_attn_in['k_w'], 'L1_attn_v_w': _L1_attn_in['v_w'], 'L1_attn_conv_q_w': _L1_attn_in['conv_q_w'], 'L1_attn_conv_k_w': _L1_attn_in['conv_k_w'], 'L1_attn_conv_v_w': _L1_attn_in['conv_v_w'], 'L1_attn_b_w': _L1_attn_in['b_w'], 'L1_attn_mix_w': _L1_attn_in['mix_w'], 'L1_attn_mix_b': _L1_attn_in['mix_b'], 'L1_attn_mix_bias': _L1_attn_in['mix_bias'], 'L1_attn_o_norm_w': _L1_attn_in['o_norm_w'], 'L1_attn_o_w': _L1_attn_in['o_w'], 'L1_xattn_w_q': _L1_xattn_in['w_q'], 'L1_xattn_b_q': _L1_xattn_in['b_q'], 'L1_xattn_w_k': _L1_xattn_in['w_k'], 'L1_xattn_b_k': _L1_xattn_in['b_k'], 'L1_xattn_w_v': _L1_xattn_in['w_v'], 'L1_xattn_b_v': _L1_xattn_in['b_v'], 'L1_xattn_w_o': _L1_xattn_in['w_o'], 'L1_xattn_b_o': _L1_xattn_in['b_o'], 'L1_ffn_gate_w': _L1_ffn_in['gate_w'], 'L1_ffn_gate_b': _L1_ffn_in['gate_b'], 'L1_ffn_w1': _L1_ffn_in['w1'], 'L1_ffn_b1': _L1_ffn_in['b1'], 'L1_ffn_w2': _L1_ffn_in['w2'], 'L1_ffn_b2': _L1_ffn_in['b2'], 'L2_attn_slope_rate': _L2_attn_in['slope_rate'], 'L2_attn_qkvu_w': _L2_attn_in['qkvu_w'], 'L2_attn_qkvu_b': _L2_attn_in['qkvu_b'], 'L2_attn_out_w': _L2_attn_in['out_w'], 'L2_attn_out_b': _L2_attn_in['out_b'], 'L2_attn_theta': _L2_attn_in['theta'], 'L2_xattn_rms_scale': _L2_xattn_in['rms_scale'], 'L2_xattn_q_w': _L2_xattn_in['q_w'], 'L2_xattn_kv_w': _L2_xattn_in['kv_w'], 'L2_xattn_out_w': _L2_xattn_in['out_w'], 'L2_ffn_clip_x': _L2_ffn_in['clip_x'], 'L2_ffn_clip_down': _L2_ffn_in['clip_down'], 'L2_ffn_w_gate': _L2_ffn_in['w_gate'], 'L2_ffn_w_up': _L2_ffn_in['w_up'], 'L2_ffn_w_down': _L2_ffn_in['w_down'], 'L3_attn_Wq': _L3_attn_in['Wq'], 'L3_attn_bq': _L3_attn_in['bq'], 'L3_attn_Wk': _L3_attn_in['Wk'], 'L3_attn_bk': _L3_attn_in['bk'], 'L3_attn_Wv': _L3_attn_in['Wv'], 'L3_attn_bv': _L3_attn_in['bv'], 'L3_attn_Wo': _L3_attn_in['Wo'], 'L3_attn_bo': _L3_attn_in['bo'], 'L3_xattn_Wq': _L3_xattn_in['Wq'], 'L3_xattn_bq': _L3_xattn_in['bq'], 'L3_xattn_Wk': _L3_xattn_in['Wk'], 'L3_xattn_bk': _L3_xattn_in['bk'], 'L3_xattn_Wv': _L3_xattn_in['Wv'], 'L3_xattn_bv': _L3_xattn_in['bv'], 'L3_xattn_Wo': _L3_xattn_in['Wo'], 'L3_xattn_bo': _L3_xattn_in['bo'], 'L3_ffn_in_proj_w': _L3_ffn_in['in_proj_w'], 'L3_ffn_in_proj_b': _L3_ffn_in['in_proj_b'], 'L3_ffn_out_proj_w': _L3_ffn_in['out_proj_w'], 'L3_ffn_out_proj_b': _L3_ffn_in['out_proj_b'], 'L3_ffn_ln1_g': _L3_ffn_in['ln1_g'], 'L3_ffn_ln1_b': _L3_ffn_in['ln1_b'], 'L3_ffn_ln2_g': _L3_ffn_in['ln2_g'], 'L3_ffn_ln2_b': _L3_ffn_in['ln2_b'], 'L3_ffn_wg': _L3_ffn_in['wg'], 'L3_ffn_w1': _L3_ffn_in['w1'], 'L3_ffn_b1': _L3_ffn_in['b1'], 'L3_ffn_w2': _L3_ffn_in['w2'], 'L3_ffn_b2': _L3_ffn_in['b2']}

def reference(x, ctx_1024, mask_B_ik0, mask_BxS2_bk0, L0_attn_q_w, L0_attn_k_w, L0_attn_v_w, L0_attn_o_w, L0_attn_q_b, L0_attn_k_b, L0_attn_v_b, L0_attn_o_b, L0_attn_ln_q_g, L0_attn_ln_q_b, L0_attn_ln_k_g, L0_attn_ln_k_b, L0_attn_ln_v_g, L0_attn_ln_v_b, L0_attn_beta_param, L0_xattn_wq, L0_xattn_bq, L0_xattn_wk, L0_xattn_bk, L0_xattn_wv, L0_xattn_bv, L0_xattn_wo, L0_xattn_bo, L0_xattn_pos_bias, L0_xattn_gamma, L0_xattn_beta, L0_xattn_w1, L0_xattn_b1, L0_xattn_w2, L0_xattn_b2, L0_ffn_router_w, L0_ffn_rg, L0_ffn_ru, L0_ffn_rd, L0_ffn_sg, L0_ffn_su, L0_ffn_sd, L1_attn_q_w, L1_attn_k_w, L1_attn_v_w, L1_attn_conv_q_w, L1_attn_conv_k_w, L1_attn_conv_v_w, L1_attn_b_w, L1_attn_mix_w, L1_attn_mix_b, L1_attn_mix_bias, L1_attn_o_norm_w, L1_attn_o_w, L1_xattn_w_q, L1_xattn_b_q, L1_xattn_w_k, L1_xattn_b_k, L1_xattn_w_v, L1_xattn_b_v, L1_xattn_w_o, L1_xattn_b_o, L1_ffn_gate_w, L1_ffn_gate_b, L1_ffn_w1, L1_ffn_b1, L1_ffn_w2, L1_ffn_b2, L2_attn_slope_rate, L2_attn_qkvu_w, L2_attn_qkvu_b, L2_attn_out_w, L2_attn_out_b, L2_attn_theta, L2_xattn_rms_scale, L2_xattn_q_w, L2_xattn_kv_w, L2_xattn_out_w, L2_ffn_clip_x, L2_ffn_clip_down, L2_ffn_w_gate, L2_ffn_w_up, L2_ffn_w_down, L3_attn_Wq, L3_attn_bq, L3_attn_Wk, L3_attn_bk, L3_attn_Wv, L3_attn_bv, L3_attn_Wo, L3_attn_bo, L3_xattn_Wq, L3_xattn_bq, L3_xattn_Wk, L3_xattn_bk, L3_xattn_Wv, L3_xattn_bv, L3_xattn_Wo, L3_xattn_bo, L3_ffn_in_proj_w, L3_ffn_in_proj_b, L3_ffn_out_proj_w, L3_ffn_out_proj_b, L3_ffn_ln1_g, L3_ffn_ln1_b, L3_ffn_ln2_g, L3_ffn_ln2_b, L3_ffn_wg, L3_ffn_w1, L3_ffn_b1, L3_ffn_w2, L3_ffn_b2):
    import jax
    import jax.numpy as jnp

    def _L0_attn_ref(query, q_w, k_w, v_w, o_w, q_b, k_b, v_b, o_b, ln_q_g, ln_q_b, ln_k_g, ln_k_b, ln_v_g, ln_v_b, beta_param):
        import math
        import jax, jax.numpy as jnp
        import numpy as np
        D = 128
        H = 16
        DH = D // H
        BETA_MIN, BETA_MAX = (0.1, 10.0)
        EPS_NORM = 1e-06

        def _layernorm(x, g, b, eps=1e-05):
            mu = jnp.mean(x, axis=-1, keepdims=True)
            var = jnp.mean((x - mu) ** 2, axis=-1, keepdims=True)
            return (x - mu) * jax.lax.rsqrt(var + eps) * g + b

        def _l2norm(x, eps=EPS_NORM):
            n = jnp.linalg.norm(x, axis=-1, keepdims=True)
            return x / jnp.maximum(n, eps)
        B, T, _ = query.shape
        residual = query
        qn = _layernorm(query, ln_q_g, ln_q_b)
        kn = _layernorm(query, ln_k_g, ln_k_b)
        vn = _layernorm(query, ln_v_g, ln_v_b)
        q = qn @ q_w.T + q_b
        k = kn @ k_w.T + k_b
        v = vn @ v_w.T + v_b
        q = _l2norm(q)
        k = _l2norm(k)
        q = q.reshape(B, T, H, DH).transpose(0, 2, 1, 3)
        k = k.reshape(B, T, H, DH).transpose(0, 2, 1, 3)
        v = v.reshape(B, T, H, DH).transpose(0, 2, 1, 3)
        beta = jnp.clip(jax.nn.softplus(beta_param), BETA_MIN, BETA_MAX)
        scores = jnp.einsum('bhqd,bhkd->bhqk', q, k)
        scores = scores * (beta / math.sqrt(DH))[None, :, None, None]
        scores = jnp.clip(scores, -50.0, 50.0)
        scores = scores - jnp.max(scores, axis=-1, keepdims=True)
        attn = jax.nn.softmax(scores, axis=-1)
        attn = jnp.nan_to_num(attn)
        out = jnp.einsum('bhqk,bhkd->bhqd', attn, v)
        out = out.transpose(0, 2, 1, 3).reshape(B, T, D)
        out = out @ o_w.T + o_b
        return residual + out

    def _L0_xattn_ref(x, pos_encod, wq, bq, wk, bk, wv, bv, wo, bo, pos_bias, gamma, beta, w1, b1, w2, b2):
        import jax, jax.numpy as jnp
        import numpy as np
        B, T, D, H = (4, 256, 128, 512)
        S = 32
        EPS = 1e-05

        def _layer_norm(x, gamma, beta):
            mu = jnp.mean(x, axis=-1, keepdims=True)
            var = jnp.mean(jnp.square(x - mu), axis=-1, keepdims=True)
            return (x - mu) * jax.lax.rsqrt(var + EPS) * gamma + beta

        def _aft_local(emb, wq, bq, wk, bk, wv, bv, wo, bo, pos_bias):
            q = emb @ wq + bq
            k = emb @ wk + bk
            v = emb @ wv + bv
            idx = jnp.arange(T)
            mask = (jnp.abs(idx[:, None] - idx[None, :]) < S).astype(pos_bias.dtype)
            w = pos_bias * mask
            max_k = jnp.max(k, axis=1, keepdims=True)
            max_w = jnp.max(w, axis=1, keepdims=True)
            ek = jnp.exp(k - max_k)
            ew = jnp.exp(w - max_w)
            num = jnp.einsum('tj,bjd->btd', ew, ek * v)
            den = jnp.einsum('tj,bjd->btd', ew, ek)
            y = jax.nn.sigmoid(q) * num / den
            return y @ wo + bo
        emb = x + pos_encod
        attn = _aft_local(emb, wq, bq, wk, bk, wv, bv, wo, bo, pos_bias)
        a = _layer_norm(attn + emb, gamma, beta)
        ff = jax.nn.relu(a @ w1 + b1) @ w2 + b2
        return _layer_norm(ff + a, gamma, beta)

    def _L0_ffn_ref(x, router_w, rg, ru, rd, sg, su, sd):
        import jax, jax.numpy as jnp
        import numpy as np
        B, S, H = (4, 256, 128)
        E, K = (8, 2)
        I_R, I_S = (4 * H, 8 * H)
        CAP_FACTOR = 1.25
        SCALE = 1.0
        b, s, h = x.shape
        T = b * s
        capacity = max(int(CAP_FACTOR * T / E), 1)
        xf = x.reshape(T, h)
        eps = jnp.finfo(x.dtype).eps
        xn = xf * jax.lax.rsqrt(jnp.mean(xf * xf, axis=-1, keepdims=True) + eps)
        logits = xn @ router_w.T
        probs = jax.nn.softmax(logits, axis=-1)
        topk_p, topk_i = jax.lax.top_k(probs, K)
        rw = topk_p / jnp.sum(topk_p, axis=-1, keepdims=True)
        one_hot = jax.nn.one_hot(topk_i, E, dtype=x.dtype)
        mask = one_hot.sum(1)
        wdense = (one_hot * rw[..., None]).sum(1)
        sel = mask.T.astype(bool)
        order = jnp.argsort(~sel, axis=1, stable=True)
        dispatch = order[:, :capacity]
        count = sel.sum(axis=1)
        valid = (jnp.arange(capacity)[None, :] < count[:, None]).astype(x.dtype)
        xg = xf[dispatch]
        gate = jax.nn.silu(jnp.einsum('ech,ehi->eci', xg, rg))
        up = jnp.einsum('ech,ehi->eci', xg, ru)
        eout = jnp.einsum('eci,eih->ech', gate * up, rd)
        w = jnp.take_along_axis(wdense.T, dispatch, axis=1)
        contrib = eout * (w * valid)[..., None]
        routed = jnp.zeros_like(xf).at[dispatch.reshape(-1)].add(contrib.reshape(-1, h))
        shared = jax.nn.silu(x @ sg) * (x @ su) @ sd
        return shared + SCALE * routed.reshape(b, s, h)

    def _L1_attn_ref(hidden_states, q_w, k_w, v_w, conv_q_w, conv_k_w, conv_v_w, b_w, mix_w, mix_b, mix_bias, o_norm_w, o_w):
        import jax, jax.numpy as jnp
        import numpy as np
        from jax import lax
        B, L, D = (2, 512, 128)
        H = 8
        DK = D // H
        DV = D // H
        CONV_K = 4
        CHUNK = 32
        EPS = 1e-05

        def _silu(x):
            return x * jax.nn.sigmoid(x)

        def _causal_depthwise_conv_silu(x, w):
            K = w.shape[1]
            l = x.shape[1]
            xp = jnp.pad(x, ((0, 0), (K - 1, 0), (0, 0)))
            y = sum((xp[:, i:i + l, :] * w[:, i] for i in range(K)))
            return _silu(y)

        def _l2norm(x):
            return x * lax.rsqrt(jnp.sum(x * x, axis=-1, keepdims=True) + 1e-12)

        def _delta_rule_chunkwise(q, k, v, beta, chunk=CHUNK):
            b, h, l, dk = q.shape
            dv = v.shape[-1]
            n = l // chunk
            q = _l2norm(q)
            k = _l2norm(k)
            v = v * beta[..., None]
            kb = k * beta[..., None]
            resh = lambda t: t.reshape(b, h, n, chunk, t.shape[-1])
            q, k, v, kb = map(resh, (q, k, v, kb))
            tri_strict = jnp.tril(jnp.ones((chunk, chunk), dtype=bool), -1)
            attn = jnp.where(tri_strict, -(kb @ jnp.swapaxes(k, -1, -2)), 0.0)
            col = jnp.arange(chunk)
            for i in range(1, chunk):
                row = attn[..., i, :]
                upd = jnp.einsum('bhnj,bhnjk->bhnk', row, attn)
                attn = attn.at[..., i, :].set(jnp.where(col < i, row + upd, row))
            attn = attn + jnp.eye(chunk, dtype=attn.dtype)
            u = attn @ v
            w = attn @ kb
            tri_incl = jnp.tril(jnp.ones((chunk, chunk), dtype=bool))
            qc, kc, uc, wc = (jnp.moveaxis(t, 2, 0) for t in (q, k, u, w))

            def step(S, inp):
                qi, ki, ui, wi = inp
                attn_i = jnp.where(tri_incl, qi @ jnp.swapaxes(ki, -1, -2), 0.0)
                ui = ui - wi @ S
                oi = qi @ S + attn_i @ ui
                S = S + jnp.swapaxes(ki, -1, -2) @ ui
                return (S, oi)
            S0 = jnp.zeros((b, h, dk, dv), dtype=q.dtype)
            S, o = lax.scan(step, S0, (qc, kc, uc, wc))
            o = jnp.moveaxis(o, 0, 2).reshape(b, h, l, dv)
            return (o, S)
        b, l, _ = hidden_states.shape
        q = _causal_depthwise_conv_silu(hidden_states @ q_w, conv_q_w)
        k = _causal_depthwise_conv_silu(hidden_states @ k_w, conv_k_w)
        v = _causal_depthwise_conv_silu(hidden_states @ v_w, conv_v_w)
        v_token = v.reshape(b, l, H, DV)
        q = q.reshape(b, l, H, DK)
        k = k.reshape(b, l, H, DK)
        beta = jax.nn.sigmoid(hidden_states @ b_w)
        q_r = jnp.swapaxes(q, 1, 2)
        k_r = jnp.swapaxes(k, 1, 2)
        v_r = jnp.swapaxes(v_token, 1, 2)
        beta_r = jnp.swapaxes(beta, 1, 2)
        o, _S = _delta_rule_chunkwise(q_r, k_r, v_r, beta_r)
        o = jnp.swapaxes(o, 1, 2)
        g = jax.nn.sigmoid(hidden_states @ mix_w + mix_b + mix_bias)[..., None]
        o = g * o + (1.0 - g) * v_token
        o = o * lax.rsqrt(jnp.mean(o * o, axis=-1, keepdims=True) + EPS) * o_norm_w
        o = o.reshape(b, l, H * DV) @ o_w
        return o

    def _L1_xattn_ref(will_be_queries, will_be_keys, will_be_values, valid_len, w_q, b_q, w_k, b_k, w_v, b_v, w_o, b_o):
        import jax, jax.numpy as jnp
        import numpy as np
        import math
        N_HEADS = 16
        HEAD_DIM = 64
        D_MODEL = 128
        B, S = (2, 256)

        def _split_heads(x):
            b, s, _ = x.shape
            return x.reshape(b, s, N_HEADS, HEAD_DIM).transpose(0, 2, 1, 3)
        q = _split_heads(will_be_queries @ w_q.T + b_q)
        k = _split_heads(will_be_keys @ w_k.T + b_k)
        v = _split_heads(will_be_values @ w_v.T + b_v)
        scores = jnp.einsum('bhqd,bhkd->bhqk', q, k) / jnp.sqrt(jnp.asarray(HEAD_DIM, q.dtype))
        neg = jnp.finfo(scores.dtype).min
        q_idx = jnp.arange(scores.shape[2])[:, None]
        k_idx = jnp.arange(scores.shape[3])[None, :]
        causal = k_idx > q_idx
        vmask = k_idx[None] >= valid_len[:, None, None]
        mask = causal[None, None] | vmask[:, None]
        scores = jnp.where(mask, neg, scores)
        attn = jax.nn.softmax(scores, axis=-1)
        out = jnp.einsum('bhqk,bhkd->bhqd', attn, v)
        out = out.transpose(0, 2, 1, 3).reshape(out.shape[0], out.shape[2], N_HEADS * HEAD_DIM)
        return out @ w_o.T + b_o

    def _L1_ffn_ref(x, gate_w, gate_b, w1, b1, w2, b2):
        import jax, jax.numpy as jnp
        import numpy as np
        B, S, D, H, O, E, K = (4, 256, 128, 256, 128, 8, 2)
        logits = jnp.einsum('bsd,ed->bse', x, gate_w) + gate_b
        probs = jax.nn.softmax(logits, axis=-1)
        topk_vals, topk_idx = jax.lax.top_k(probs, K)
        h = jax.nn.relu(jnp.einsum('bsd,edh->bseh', x, w1) + b1)
        expert_out = jnp.einsum('bseh,eho->bseo', h, w2) + b2
        sel = jnp.take_along_axis(expert_out, topk_idx[..., None], axis=2)
        return jnp.sum(sel * topk_vals[..., None], axis=2)

    def _L2_attn_ref(x, slope_rate, qkvu_w, qkvu_b, out_w, out_b, theta):
        import jax, jax.numpy as jnp
        import numpy as np
        N_EMBD = 128
        N_HEAD = 8
        HEAD_DIM = N_EMBD // N_HEAD
        EPS = 1e-06

        def _lrpe(xh, theta, n):
            idx = jnp.arange(n, dtype=xh.dtype).reshape(1, n, 1)
            th = theta * idx
            th = th[None]
            return jnp.concatenate([xh * jnp.cos(th), xh * jnp.sin(th)], axis=-1)

        def _srmsnorm(y):
            ms = jnp.mean(jnp.square(y), axis=-1, keepdims=True)
            return y * jax.lax.rsqrt(ms + EPS)
        b, n, hd = x.shape
        h = N_HEAD
        qkvu = x @ qkvu_w.T + qkvu_b
        q, k, v, u = jnp.split(qkvu, 4, axis=-1)

        def to_heads(t):
            return t.reshape(b, n, h, hd // h).transpose(0, 2, 1, 3)
        q, k, v = (to_heads(q), to_heads(k), to_heads(v))
        q = jax.nn.silu(q)
        k = jax.nn.silu(k)
        q = _lrpe(q, theta, n)
        k = _lrpe(k, theta, n)
        tril = jnp.tril(jnp.ones((n, n), dtype=x.dtype))
        mask = jnp.exp(slope_rate * tril)
        energy = jnp.einsum('bhne,bhme->bhnm', q, k) * mask[None]
        out = jnp.einsum('bhnm,bhmd->bhnd', energy, v)
        out = out.transpose(0, 2, 1, 3).reshape(b, n, hd)
        out = _srmsnorm(out)
        out = u * out
        out = out @ out_w.T + out_b
        return out

    def _L2_xattn_ref(x, mem_seq, mem_mask, rms_scale, q_w, kv_w, out_w):
        import jax, jax.numpy as jnp
        import numpy as np
        NUM_HEADS, NUM_KV, HEAD_DIM, WIDTH = (4, 1, 32, 128)
        MASK_FILL = -2.3819763e+38

        def _apply_rope(x, positions, max_wavelength=10000.0):
            d = x.shape[-1]
            freq_exp = 2.0 / d * jnp.arange(d // 2, dtype=jnp.float32)
            timescale = max_wavelength ** freq_exp
            radians = positions[..., None].astype(jnp.float32) / timescale
            radians = radians[..., None, :]
            sin, cos = (jnp.sin(radians), jnp.cos(radians))
            x1, x2 = jnp.split(x, 2, axis=-1)
            out = jnp.concatenate([x1 * cos - x2 * sin, x2 * cos + x1 * sin], axis=-1)
            return out.astype(x.dtype)

        def _rmsnorm(x, scale):
            var = jnp.mean(jnp.square(x.astype(jnp.float32)), axis=-1, keepdims=True)
            normed = x * jax.lax.rsqrt(var + 1e-06)
            return (normed * (1 + scale)).astype(x.dtype)
        B, S, _ = mem_seq.shape
        T = x.shape[1]
        G = NUM_HEADS // NUM_KV
        xn = _rmsnorm(x, rms_scale)
        mn = _rmsnorm(mem_seq, rms_scale)
        q = jnp.einsum('BTD,NDH->BTNH', xn, q_w)
        kv = jnp.einsum('BSD,cKDH->cBSKH', mn, kv_w)
        k, v = (kv[0], kv[1])
        q_pos = jnp.broadcast_to(jnp.arange(S, T + S), (B, T))
        k_pos = jnp.broadcast_to(jnp.arange(S), (B, S))
        q = _apply_rope(q, q_pos) * HEAD_DIM ** (-0.5)
        k = _apply_rope(k, k_pos)
        q = q.reshape(B, T, NUM_KV, G, HEAD_DIM)
        logits = jnp.einsum('BTKGH,BSKH->BKGTS', q, k, preferred_element_type=jnp.float32)
        masked = jnp.where(mem_mask[:, None, None, None, :], logits, MASK_FILL)
        probs = jax.nn.softmax(masked, axis=-1).astype(x.dtype)
        enc = jnp.einsum('BKGTS,BSKH->BTKGH', probs, v).reshape(B, T, NUM_HEADS, HEAD_DIM)
        return jnp.einsum('BTNH,NHD->BTD', enc, out_w)

    def _L2_ffn_ref(x, clip_x, clip_down, w_gate, w_up, w_down):
        import jax, jax.numpy as jnp
        import numpy as np
        QMAX = 127.0

        def _ste_round(v):
            return v + jax.lax.stop_gradient(jnp.round(v) - v)

        def _act_fake_quant(x, clip_factor):
            scale = jax.nn.sigmoid(clip_factor) * jnp.max(jnp.abs(x)) / QMAX
            return jnp.clip(_ste_round(x / scale), -QMAX - 1.0, QMAX) * scale

        def _weight_fake_quant(w):
            scale = jnp.max(jnp.abs(w), axis=1, keepdims=True) / QMAX
            return jnp.clip(_ste_round(w / scale), -QMAX - 1.0, QMAX) * scale
        xq = _act_fake_quant(x, clip_x[0])
        gate = jnp.einsum('bsh,ih->bsi', xq, _weight_fake_quant(w_gate))
        up = jnp.einsum('bsh,ih->bsi', xq, _weight_fake_quant(w_up))
        h = _act_fake_quant(jax.nn.silu(gate) * up, clip_down[0])
        return jnp.einsum('bsi,hi->bsh', h, _weight_fake_quant(w_down))

    def _L3_attn_ref(x, Wq, bq, Wk, bk, Wv, bv, Wo, bo):
        import jax, jax.numpy as jnp
        import numpy as np
        B, S, E, H, K = (2, 256, 128, 16, 32)
        D = E // H
        b, s, e = x.shape
        scale = jnp.sqrt(jnp.asarray(D, x.dtype))
        q = (x @ Wq.T + bq).reshape(b, s, H, D).transpose(0, 2, 1, 3)
        k = (x @ Wk.T + bk).reshape(b, s, H, D).transpose(0, 2, 1, 3)
        v = (x @ Wv.T + bv).reshape(b, s, H, D).transpose(0, 2, 1, 3)
        scores = jnp.einsum('bhsd,bhtd->bhst', q, k) / scale
        kk = min(K, s)
        top_s, top_i = jax.lax.top_k(scores, kk)
        probs = jax.nn.softmax(top_s, axis=-1)
        gather = jax.vmap(jax.vmap(lambda vv, ii: vv[ii]))
        v_g = gather(v, top_i)
        out = jnp.einsum('bhsk,bhskd->bhsd', probs, v_g)
        out = out.transpose(0, 2, 1, 3).reshape(b, s, e)
        return out @ Wo.T + bo

    def _L3_xattn_ref(q, k, v, Wq, bq, Wk, bk, Wv, bv, Wo, bo):
        import jax, jax.numpy as jnp
        import numpy as np
        B, TQ, TK, D_MODEL, N_HEAD, STRIDE = (1, 128, 1024, 128, 16, 16)
        HEAD_DIM = D_MODEL // N_HEAD
        b, tq, _ = q.shape
        tk = k.shape[1]
        Q = (q @ Wq.T + bq).reshape(b, tq, N_HEAD, HEAD_DIM).transpose(0, 2, 1, 3)
        K = (k @ Wk.T + bk).reshape(b, tk, N_HEAD, HEAD_DIM).transpose(0, 2, 1, 3)
        V = (v @ Wv.T + bv).reshape(b, tk, N_HEAD, HEAD_DIM).transpose(0, 2, 1, 3)
        scores = jnp.einsum('bhqd,bhkd->bhqk', Q, K) / jnp.sqrt(jnp.float32(HEAD_DIM))
        kidx = jnp.arange(tk)
        hoff = jnp.arange(N_HEAD)
        hepos_mask = (kidx[None, :] - hoff[:, None]) % STRIDE != 0
        scores = jnp.where(hepos_mask[None, :, None, :], -jnp.inf, scores)
        attn = jax.nn.softmax(scores, axis=-1)
        attn = jnp.nan_to_num(attn, nan=0.0)
        out = jnp.einsum('bhqk,bhkd->bhqd', attn, V)
        out = out.transpose(0, 2, 1, 3).reshape(b, tq, D_MODEL)
        return out @ Wo.T + bo

    def _L3_ffn_ref(x, in_proj_w, in_proj_b, out_proj_w, out_proj_b, ln1_g, ln1_b, ln2_g, ln2_b, wg, w1, b1, w2, b2):
        import jax, jax.numpy as jnp
        import numpy as np
        D = 128
        H = 4
        HD = D // H
        E = 8
        FF = 512
        CAP_FACTOR = 1.0

        def _ln(x, g, b, eps=1e-05):
            mu = jnp.mean(x, -1, keepdims=True)
            v = jnp.mean((x - mu) ** 2, -1, keepdims=True)
            return (x - mu) * jax.lax.rsqrt(v + eps) * g + b

        def _mha(x, w, b, ow, ob):
            L, N, _ = x.shape
            qkv = x @ w.T + b
            q, k, v = jnp.split(qkv, 3, axis=-1)
            rh = lambda t: t.reshape(L, N, H, HD).transpose(1, 2, 0, 3)
            q, k, v = (rh(q), rh(k), rh(v))
            scores = jnp.einsum('nhld,nhmd->nhlm', q, k) / np.float32(np.sqrt(HD))
            attn = jax.nn.softmax(scores, axis=-1)
            o = jnp.einsum('nhlm,nhmd->nhld', attn, v).transpose(2, 0, 1, 3).reshape(L, N, D)
            return o @ ow.T + ob

        def _moe(x, wg, w1, b1, w2, b2):
            L, N, _ = x.shape
            S = L * N
            cap = int(CAP_FACTOR * S) // E
            xf = x.reshape(S, D)
            gates = jax.nn.softmax(xf @ wg, axis=-1)
            idx = jnp.argmax(gates, axis=-1)
            mask1 = jax.nn.one_hot(idx, E, dtype=x.dtype)
            loc = jnp.sum((jnp.cumsum(mask1, 0) - 1.0) * mask1, -1).astype(jnp.int32)
            keep = loc < cap
            gate_val = jnp.take_along_axis(gates, idx[:, None], -1)[:, 0]
            slot = jnp.where(keep, idx.astype(jnp.int32) * cap + loc, E * cap)
            disp = jnp.zeros((E * cap, D), x.dtype).at[slot].set(xf, mode='drop')
            disp = disp.reshape(E, cap, D)
            h = jnp.einsum('ecd,edf->ecf', disp, w1) + b1[:, None, :]
            y = (jnp.einsum('ecf,efd->ecd', h, w2) + b2[:, None, :]).reshape(E * cap, D)
            out = jnp.where(keep[:, None], gate_val[:, None] * y[jnp.minimum(slot, E * cap - 1)], 0.0)
            return out.reshape(L, N, D)
        y1 = _ln(x + _mha(x, in_proj_w, in_proj_b, out_proj_w, out_proj_b), ln1_g, ln1_b)
        y2 = _ln(y1 + _moe(y1, wg, w1, b1, w2, b2), ln2_g, ln2_b)
        return y2
    x = x + _L0_attn_ref(_layernorm(x, axis=-1), L0_attn_q_w, L0_attn_k_w, L0_attn_v_w, L0_attn_o_w, L0_attn_q_b, L0_attn_k_b, L0_attn_v_b, L0_attn_o_b, L0_attn_ln_q_g, L0_attn_ln_q_b, L0_attn_ln_k_g, L0_attn_ln_k_b, L0_attn_ln_v_g, L0_attn_ln_v_b, L0_attn_beta_param)
    x = x + _L0_xattn_ref(_layernorm(x, axis=-1), ctx_1024, L0_xattn_wq, L0_xattn_bq, L0_xattn_wk, L0_xattn_bk, L0_xattn_wv, L0_xattn_bv, L0_xattn_wo, L0_xattn_bo, L0_xattn_pos_bias, L0_xattn_gamma, L0_xattn_beta, L0_xattn_w1, L0_xattn_b1, L0_xattn_w2, L0_xattn_b2)
    x = x + _L0_ffn_ref(_layernorm(x, axis=-1), L0_ffn_router_w, L0_ffn_rg, L0_ffn_ru, L0_ffn_rd, L0_ffn_sg, L0_ffn_su, L0_ffn_sd)
    x = x + _L1_attn_ref(_layernorm(x, axis=-1), L1_attn_q_w, L1_attn_k_w, L1_attn_v_w, L1_attn_conv_q_w, L1_attn_conv_k_w, L1_attn_conv_v_w, L1_attn_b_w, L1_attn_mix_w, L1_attn_mix_b, L1_attn_mix_bias, L1_attn_o_norm_w, L1_attn_o_w)
    x = x + _L1_xattn_ref(_layernorm(x, axis=-1), ctx_1024, ctx_1024, mask_B_ik0, L1_xattn_w_q, L1_xattn_b_q, L1_xattn_w_k, L1_xattn_b_k, L1_xattn_w_v, L1_xattn_b_v, L1_xattn_w_o, L1_xattn_b_o)
    x = x + _L1_ffn_ref(_layernorm(x, axis=-1), L1_ffn_gate_w, L1_ffn_gate_b, L1_ffn_w1, L1_ffn_b1, L1_ffn_w2, L1_ffn_b2)
    x = x + _L2_attn_ref(_layernorm(x, axis=-1), L2_attn_slope_rate, L2_attn_qkvu_w, L2_attn_qkvu_b, L2_attn_out_w, L2_attn_out_b, L2_attn_theta)
    x = x + _L2_xattn_ref(_layernorm(x, axis=-1), ctx_1024, mask_BxS2_bk0, L2_xattn_rms_scale, L2_xattn_q_w, L2_xattn_kv_w, L2_xattn_out_w)
    x = x + _L2_ffn_ref(_layernorm(x, axis=-1), L2_ffn_clip_x, L2_ffn_clip_down, L2_ffn_w_gate, L2_ffn_w_up, L2_ffn_w_down)
    x = x + _L3_attn_ref(_layernorm(x, axis=-1), L3_attn_Wq, L3_attn_bq, L3_attn_Wk, L3_attn_bk, L3_attn_Wv, L3_attn_bv, L3_attn_Wo, L3_attn_bo)
    x = x + _L3_xattn_ref(_layernorm(x, axis=-1), ctx_1024, ctx_1024, L3_xattn_Wq, L3_xattn_bq, L3_xattn_Wk, L3_xattn_bk, L3_xattn_Wv, L3_xattn_bv, L3_xattn_Wo, L3_xattn_bo)
    x = x + _L3_ffn_ref(_layernorm(x, axis=-1), L3_ffn_in_proj_w, L3_ffn_in_proj_b, L3_ffn_out_proj_w, L3_ffn_out_proj_b, L3_ffn_ln1_g, L3_ffn_ln1_b, L3_ffn_ln2_g, L3_ffn_ln2_b, L3_ffn_wg, L3_ffn_w1, L3_ffn_b1, L3_ffn_w2, L3_ffn_b2)
    return x

_drawn_inputs = setup_inputs


def setup_inputs(seed=0):
    import zlib

    import numpy as np

    out = dict(_drawn_inputs(seed))
    spreads = {'L0_attn_q_b': (0.0, 0.8),
     'L0_attn_k_b': (0.0, 2.0),
     'L0_attn_v_b': (0.0, 0.1),
     'L0_attn_o_b': (0.0, 0.1),
     'L0_attn_ln_q_g': (1.0, 0.6),
     'L0_attn_ln_q_b': (0.0, 0.8),
     'L0_attn_ln_k_g': (1.0, 0.6),
     'L0_attn_ln_k_b': (0.0, 0.8),
     'L0_attn_ln_v_g': (1.0, 0.6),
     'L0_attn_ln_v_b': (0.0, 0.1),
     'L0_xattn_bq': (0.0, 0.8),
     'L0_xattn_bk': (0.0, 2.0),
     'L0_xattn_bv': (0.0, 0.8),
     'L0_xattn_bo': (0.0, 0.279),
     'L0_xattn_gamma': (1.0, 0.2),
     'L0_xattn_beta': (0.0, 0.1),
     'L0_xattn_b1': (0.0, 0.487),
     'L0_xattn_b2': (0.0, 0.1),
     'L1_attn_mix_b': (-1.0, 0.6),
     'L1_attn_mix_bias': (-1.0, 0.6),
     'L1_attn_o_norm_w': (1.0, 0.6),
     'L1_xattn_b_q': (0.0, 0.269),
     'L1_xattn_b_k': (0.0, 2.0),
     'L1_xattn_b_v': (0.0, 0.1),
     'L1_xattn_b_o': (0.0, 0.1),
     'L1_ffn_gate_b': (0.0, 0.319),
     'L1_ffn_b1': (0.0, 0.49),
     'L1_ffn_b2': (0.0, 0.484),
     'L2_attn_qkvu_b': (0.0, 0.524),
     'L2_attn_out_b': (0.0, 0.1),
     'L3_attn_bq': (0.0, 1.86),
     'L3_attn_bk': (0.0, 2.0),
     'L3_attn_bv': (0.0, 0.32),
     'L3_attn_bo': (0.0, 0.3),
     'L3_xattn_bq': (0.0, 0.8),
     'L3_xattn_bk': (0.0, 2.0),
     'L3_xattn_bv': (0.0, 0.332),
     'L3_xattn_bo': (0.0, 0.279),
     'L3_ffn_in_proj_b': (0.0, 0.8),
     'L3_ffn_out_proj_b': (0.0, 0.319),
     'L3_ffn_ln1_g': (1.0, 0.2),
     'L3_ffn_ln1_b': (0.0, 0.337),
     'L3_ffn_ln2_g': (1.0, 0.6),
     'L3_ffn_ln2_b': (0.0, 0.366),
     'L3_ffn_b1': (0.0, 0.8),
     'L3_ffn_b2': (0.0, 2.0)}
    factors = {'L0_attn_q_w': 8.0,
     'L0_attn_k_w': 8.0,
     'L0_attn_beta_param': 8.0,
     'L0_xattn_wq': 8.0,
     'L0_xattn_wk': 8.0,
     'L0_xattn_wv': 7.259,
     'L0_xattn_wo': 5.861,
     'L0_xattn_pos_bias': 8.0,
     'L0_ffn_router_w': 8.0,
     'L0_ffn_rg': 8.0,
     'L0_ffn_ru': 8.0,
     'L0_ffn_rd': 8.0,
     'L0_ffn_sg': 5.769,
     'L0_ffn_su': 6.829,
     'L0_ffn_sd': 6.003,
     'L1_attn_q_w': 5.621,
     'L1_attn_k_w': 5.304,
     'L1_attn_conv_q_w': 6.234,
     'L1_attn_conv_k_w': 6.117,
     'L1_attn_b_w': 8.0,
     'L1_attn_mix_w': 8.0,
     'L2_attn_slope_rate': 8.0,
     'L2_attn_qkvu_w': 3.495,
     'L2_attn_out_w': 3.562,
     'L2_attn_theta': 5.198,
     'L2_xattn_rms_scale': 8.0,
     'L2_ffn_w_gate': 8.0,
     'L2_ffn_w_up': 8.0,
     'L2_ffn_w_down': 8.0,
     'L3_ffn_in_proj_w': 8.0,
     'L3_ffn_out_proj_w': 7.997,
     'L3_ffn_wg': 8.0,
     'L3_ffn_w1': 8.0,
     'L3_ffn_w2': 8.0}
    for name, (base, spread) in spreads.items():
        noise = np.random.default_rng([zlib.crc32(name.encode()), seed]).standard_normal(out[name].shape)
        drawn = base * np.exp(spread * noise) if base else spread * noise
        out[name] = jnp.asarray(drawn.astype(out[name].dtype))
    for name, factor in factors.items():
        out[name] = (out[name] * factor).astype(out[name].dtype)
    return out
```

```python
import numpy as np

import concourse.bass as bass
from concourse import mybir

F32 = mybir.dt.float32
BF16 = mybir.dt.bfloat16
I32 = mybir.dt.int32
U8 = mybir.dt.uint8
ACT = mybir.ActivationFunctionType
ALU = mybir.AluOpType
AX = mybir.AxisListType

P = 128
B, S = 8, 256
N = B * S
CH = 512
NC = N // CH
NEG = -3.4028234663852886e38
REPLACED = -3.0e38


class Signal:

    def __init__(self, nc, name):
        self.sem = nc.alloc_semaphore(name)
        self.base = 0

    def at(self, n):
        return self.base + n

    def advance(self, n):
        self.base += n


class Chain:

    def __init__(self, eng, sem):
        self.eng, self.sem, self.n = eng, sem, 0

    def link(self, ins):
        self.n += 1
        ins.then_inc(self.sem, 1)
        self.eng.wait_ge(self.sem, self.n)

    def clear(self):
        if self.n:
            self.eng.wait_ge(self.sem, self.n)
            self.eng.sem_clear(self.sem)
            self.n = 0


class Core:

    SIGNALS = [
        "loaded", "stored", "mean_ready", "var_ready", "centred", "squared", "normed", "rooted",
        "product_ready", "product_taken", "product_taken_v", "staged", "proj_ready", "proj_taken_s", "proj_taken_v",
        "scores_ready", "scores_max", "probs_ready", "probs_picked", "probs_turned", "turned_copied",
        "mixed_ready", "mixed_taken", "out_turned", "out_copied", "out_product", "residual_added",
        "aux_pe", "aux_v", "aux_s", "aux_p", "aux_pe2", "aux_v2", "aux_s2", "aux_p2", "aux_pe3", "aux_v3", "aux_s3",
        "big_loaded",
    ]

    def __init__(self, nc, slots, packs):
        self.nc, self.slots, self.packs = nc, slots, packs
        self.sig = {n: Signal(nc, n) for n in self.SIGNALS}
        self.vector_chain = nc.alloc_semaphore("vector_chain")
        self.scalar_chain = nc.alloc_semaphore("scalar_chain")
        self.pool_chain = nc.alloc_semaphore("pool_chain")
        self.psum = nc.alloc_psum_tensor("psum", [P, 8, CH], F32)
        self.X = nc.alloc_sbuf_tensor("residual", [P, N], F32)
        self.CT = nc.alloc_sbuf_tensor("context", [P, N], F32)
        self.HN = nc.alloc_sbuf_tensor("normed_input", [P, N], F32)
        self.T = nc.alloc_sbuf_tensor("tiles", [P, 4, N], F32)
        self.small = nc.alloc_sbuf_tensor("small_weights", [P, packs["small"]], F32)
        self.big_words = max([packs[n] for n in packs if n != "small"], default=1)
        self.big = nc.alloc_sbuf_tensor("big_weights", [P, self.big_words], F32)
        self.work_words = 66 * 1024 // 4
        self.work = nc.alloc_sbuf_tensor("work", [P, self.work_words], F32)

    def __getattr__(self, name):
        return self.sig[name]

    def w(self, name):
        pack, off, shape = self.slots[name]
        t = self.small if pack == "small" else self.big
        n = int(np.prod(shape[1:]))
        return shaped(t[:, off:off + n], shape[1:])


def shaped(ap, dims):
    if len(dims) == 1:
        return ap
    if len(dims) == 2:
        return ap.rearrange("p (a b) -> p a b", b=dims[1])
    if len(dims) == 3:
        return ap.rearrange("p (a b c) -> p a b c", b=dims[1], c=dims[2])
    return ap.rearrange("p (a b c d) -> p a b c d", b=dims[1], c=dims[2], d=dims[3])


class Arena:

    def __init__(self, core):
        self.core, self.off = core, 0

    def take(self, *dims):
        n = int(np.prod(dims))
        a = self.core.work[:, self.off:self.off + n]
        self.off += n
        assert self.off <= self.core.work_words, (self.off, self.core.work_words)
        return shaped(a, dims)



def load_stage(c, big, dram, x_dram=None, ctx_dram=None):
    nc = c.nc
    with nc.Block() as block:
        @block.sync
        def _(sp):
            n = 0
            if x_dram is not None:
                sp.dma_start(c.X[:, :], x_dram).then_inc(c.loaded.sem, 16)
                sp.dma_start(c.small[:, :], dram["small"]).then_inc(c.loaded.sem, 16)
                sp.dma_start(c.CT[:, :], ctx_dram).then_inc(c.loaded.sem, 16)
                sp.dma_start(c.valid_i32[:, :], dram["valid"]).then_inc(c.loaded.sem, 16)
                sp.dma_start(c.attend[:, :], dram["attend"]).then_inc(c.loaded.sem, 16)
                n = 5
            if big:
                sp.dma_start(c.big[:, 0:c.packs[big]], dram[big]).then_inc(c.loaded.sem, 16)
                n += 1
            sp.wait_ge(c.loaded.sem, c.loaded.at(16 * n))
            c.loaded.advance(16 * n)


def norm_stage(c, src, dst, eps, centre=True, gain=None, shift=None):
    nc = c.nc
    a = Arena(c)
    cen, sq, std = a.take(N), a.take(N), a.take(N)
    avg = c.w("average")
    ch = [slice(i * CH, (i + 1) * CH) for i in range(NC)]
    with nc.Block() as block:
        @block.tensor
        def _(pe):
            if centre:
                for i in range(NC):
                    nc.tensor.matmul(c.psum[:, i, :], avg, src[:, ch[i]], start=True, stop=True) \
                        .then_inc(c.mean_ready.sem, 1)
            for i in range(NC):
                pe.wait_ge(c.squared.sem, c.squared.at(i + 1))
                nc.tensor.matmul(c.psum[:, 4 + i, :], avg, sq[:, ch[i]], start=True, stop=True) \
                    .then_inc(c.var_ready.sem, 1)

        @block.vector
        def _(dve):
            if centre:
                for i in range(NC):
                    dve.wait_ge(c.mean_ready.sem, c.mean_ready.at(i + 1))
                    nc.vector.tensor_tensor(cen[:, ch[i]], src[:, ch[i]], c.psum[:, i, :], ALU.subtract) \
                        .then_inc(c.centred.sem, 1)
            chain = Chain(dve, c.vector_chain)
            for i in range(NC):
                dve.wait_ge(c.rooted.sem, c.rooted.at(i + 1))
                chain.link(nc.vector.reciprocal(std[:, ch[i]], std[:, ch[i]]))
                nc.vector.tensor_tensor(dst[:, ch[i]], (cen if centre else src)[:, ch[i]], std[:, ch[i]], ALU.mult) \
                    .then_inc(c.normed.sem, 1)
            chain.clear()

        @block.scalar
        def _(act):
            for i in range(NC):
                if centre:
                    act.wait_ge(c.centred.sem, c.centred.at(i + 1))
                nc.scalar.activation(sq[:, ch[i]], (cen if centre else src)[:, ch[i]], ACT.Square) \
                    .then_inc(c.squared.sem, 1)
            for i in range(NC):
                act.wait_ge(c.var_ready.sem, c.var_ready.at(i + 1))
                nc.scalar.activation(std[:, ch[i]], c.psum[:, 4 + i, :], ACT.Sqrt, bias=c.w(eps)) \
                    .then_inc(c.rooted.sem, 1)
            if gain is not None:
                for i in range(NC):
                    act.wait_ge(c.normed.sem, c.normed.at(i + 1))
                    nc.scalar.activation(dst[:, ch[i]], dst[:, ch[i]], ACT.Identity, scale=gain,
                                         bias=0.0 if shift is None else shift)
    if centre:
        c.mean_ready.advance(NC)
        c.centred.advance(NC)
    c.squared.advance(NC)
    c.var_ready.advance(NC)
    c.normed.advance(NC)
    c.rooted.advance(NC)


def affine_stage(c, src, dsts, gains, shifts):
    nc = c.nc
    with nc.Block() as block:
        @block.scalar
        def _(act):
            for d, g, s in zip(dsts[0::2], gains[0::2], shifts[0::2]):
                nc.scalar.activation(d, src, ACT.Identity, scale=g, bias=s)

        @block.vector
        def _(dve):
            for d, g, s in zip(dsts[1::2], gains[1::2], shifts[1::2]):
                nc.vector.tensor_scalar(d, src, g, s, ALU.mult, ALU.add)


def project_stage(c, jobs):
    nc = c.nc
    steps = [(i, j) for i in range(NC) for j in range(len(jobs))]
    by_vector = [jobs[j][5] is not None for _, j in steps]
    taken = []
    ns = nv = 0
    for v in by_vector:
        nv, ns = nv + v, ns + (not v)
        taken.append((v, nv if v else ns))
    with nc.Block() as block:
        @block.tensor
        def _(pe):
            for n, (i, j) in enumerate(steps):
                srcs, ws = jobs[j][0:2]
                if n >= 8:
                    v, k = taken[n - 8]
                    sig = c.product_taken_v if v else c.product_taken
                    pe.wait_ge(sig.sem, sig.at(k))
                for k, (src, w) in enumerate(zip(srcs, ws)):
                    mm = nc.tensor.matmul(c.psum[:, n % 8, :], w, src[:, i * CH:(i + 1) * CH],
                                          start=(k == 0), stop=(k == len(srcs) - 1))
                mm.then_inc(c.product_ready.sem, 1)

        @block.scalar
        def _(act):
            for n, (i, j) in enumerate(steps):
                if by_vector[n]:
                    continue
                _, _, bias, func, out, _ = jobs[j]
                act.wait_ge(c.product_ready.sem, c.product_ready.at(n + 1))
                nc.scalar.activation(out[:, i * CH:(i + 1) * CH], c.psum[:, n % 8, :], func or ACT.Identity,
                                     bias=0.0 if bias is None else bias).then_inc(c.product_taken.sem, 1)

        @block.vector
        def _(dve):
            for n, (i, j) in enumerate(steps):
                if not by_vector[n]:
                    continue
                _, _, bias, func, out, res = jobs[j]
                dve.wait_ge(c.product_ready.sem, c.product_ready.at(n + 1))
                nc.vector.scalar_tensor_tensor(out[:, i * CH:(i + 1) * CH], c.psum[:, n % 8, :],
                                               0.0 if bias is None else bias, res[:, i * CH:(i + 1) * CH],
                                               ALU.add, ALU.add).then_inc(c.product_taken_v.sem, 1)
    c.product_ready.advance(len(steps))
    c.product_taken.advance(ns)
    c.product_taken_v.advance(nv)


def attention_stage(c, H, dh, q_src, k_src, v_src, wq, bq, wk, bk, wv, bv, wo, bo, scale=1.0,
                    head_scale=None, mask=None, prepare_mask=None, mask_words=0, shared_kv=False, top=0,
                    residual2=None, skip_max=False, room=None):
    nc = c.nc
    nt = len(wq)
    per_tile = H // nt
    pitch = P // per_tile
    nk = 1 if shared_kv else nt
    vw = dh if shared_kv else H * dh
    vparts = [(k, lo, min(lo + CH, vw)) for k in range(2) for lo in range(0, vw, CH)]
    no = H * dh // P
    U = 4
    NG = H // 2
    rows = 32 if dh < 32 else dh
    a = Arena(c)
    if room is None:
        qb, kb = a.take(nt, S), a.take(nk, S)
    else:
        qb, kb = room[:, 0, :].rearrange("p (t s) -> p t s", s=S), room[:, 1, :].rearrange("p (t s) -> p t s", s=S)
    vsb = a.take(S)
    vb = a.take(2, vw)
    probs = a.take(2, U, S)
    raw = a.take(2, U, S) if (mask or top) else None
    turned = a.take(2, U, 2, P)
    otok = a.take(2, H * dh)
    oT = a.take(no, S)
    rowmax = a.take(2, U)
    top8 = a.take(2, U, max(top // 8, 1), 8)
    nbias = a.take(2, U)
    sums = a.take(2, U)
    rsum = a.take(4, U)
    mb = a.take(mask_words) if mask_words else None
    gate = a.take(1)
    ident = c.w("identity")
    n_sc = nt + nk
    n_pr = n_sc + len(vparts)

    def unit(g, u):
        return 2 * g + u // 2, u % 2

    def scores(g):
        return c.psum[:, 2 * (g % 2):2 * (g % 2) + 2, :].rearrange("p a (q k) -> p (a q) k", k=S)

    turn = c.psum[:, 4:6, :].rearrange("p a (h t q) -> p (a h) t q", h=2, t=2)
    out_turn = c.psum[:, 4:6, 0:S]
    mixed = c.psum[:, 6, 0:U * dh].rearrange("p (u d) -> p u d", d=dh)

    with nc.Block() as block:
        @block.gpsimd
        def _(pool):
            with pool.Fori(0, B) as b:
                pool.wait_ge(c.proj_ready.sem, c.proj_ready.base + b * n_pr)
                nc.gpsimd.tensor_copy(vsb, v_src[:, bass.ds(b * S, S)]).then_inc(c.staged.sem, 1)

        @block.tensor
        def _(pe):
            with pe.Fori(0, B) as b:
                ps0 = c.proj_taken_s.base + b * n_sc
                pv0 = c.proj_taken_v.base + b * len(vparts)
                for i in range(n_sc):
                    if i >= 4:
                        pe.wait_ge(c.proj_taken_s.sem, ps0 + i - 3)
                    w, src = (wq[i], q_src) if i < nt else (wk[i - nt], k_src)
                    nc.tensor.matmul(c.psum[:, i % 4, 0:S], w, src[:, bass.ds(b * S, S)],
                                     start=True, stop=True).then_inc(c.proj_ready.sem, 1)
                pe.wait_ge(c.staged.sem, c.staged.base + b + 1)
                for j, (kt, lo, hi) in enumerate(vparts):
                    i = n_sc + j
                    if i >= 4:
                        if i - 4 < n_sc:
                            pe.wait_ge(c.proj_taken_s.sem, ps0 + i - 3)
                        else:
                            pe.wait_ge(c.proj_taken_v.sem, pv0 + i - 3 - n_sc)
                    nc.tensor.matmul(c.psum[:, i % 4, 0:hi - lo], vsb[:, kt * P:(kt + 1) * P], wv[:, lo:hi],
                                     start=True, stop=True).then_inc(c.proj_ready.sem, 1)
                pe.wait_ge(c.proj_taken_s.sem, ps0 + n_sc)
                pe.wait_ge(c.proj_taken_v.sem, pv0 + len(vparts))
                g0 = b * NG
                for g in range(NG + 2):
                    if g < NG:
                        if g >= 2:
                            pe.wait_ge(c.probs_ready.sem, c.probs_ready.base + g0 + g - 1)
                        for u in range(U):
                            h, qt = unit(g, u)
                            t, base = h // per_tile, (h % per_tile) * pitch
                            mm = nc.tensor.matmul(scores(g)[:, u, :],
                                                  qb[base:base + rows, t, qt * P:(qt + 1) * P],
                                                  kb[base:base + rows, 0 if shared_kv else t, :],
                                                  start=True, stop=True, tile_position=(base, 0))
                        mm.then_inc(c.scores_ready.sem, 1)
                    if 1 <= g <= NG:
                        ready = c.probs_picked if top else c.probs_ready
                        pe.wait_ge(ready.sem, ready.base + g0 + g)
                        if g >= 2:
                            pe.wait_ge(c.turned_copied.sem, c.turned_copied.base + g0 + g - 1)
                        for u in range(U):
                            for kt in range(2):
                                mm = nc.tensor.transpose(turn[:, u, kt, :],
                                                         probs[:, (g - 1) % 2, u, kt * P:(kt + 1) * P], ident)
                        mm.then_inc(c.probs_turned.sem, 1)
                    if g >= 2:
                        k = g - 2
                        pe.wait_ge(c.turned_copied.sem, c.turned_copied.base + g0 + k + 1)
                        if k >= 1:
                            pe.wait_ge(c.mixed_taken.sem, c.mixed_taken.base + g0 + k)
                        for u in range(U):
                            h, _ = unit(k, u)
                            lo = 0 if shared_kv else h * dh
                            for kt in range(2):
                                mm = nc.tensor.matmul(mixed[:, u, :], turned[:, k % 2, u, kt, :],
                                                      vb[:, kt, lo:lo + dh], start=(kt == 0), stop=(kt == 1))
                        mm.then_inc(c.mixed_ready.sem, 1)
                pe.wait_ge(c.mixed_taken.sem, c.mixed_taken.base + g0 + NG)
                for t in range(no):
                    if t >= 2:
                        pe.wait_ge(c.out_copied.sem, c.out_copied.base + b * no + t - 1)
                    for qt in range(2):
                        mm = nc.tensor.transpose(out_turn[:, t % 2, qt * P:(qt + 1) * P],
                                                 otok[:, qt, t * P:(t + 1) * P], ident)
                    mm.then_inc(c.out_turned.sem, 1)
                pe.wait_ge(c.residual_added.sem, c.residual_added.base + b)
                for t in range(no):
                    pe.wait_ge(c.out_copied.sem, c.out_copied.base + b * no + t + 1)
                    mm = nc.tensor.matmul(c.psum[:, 7, 0:S], wo[t], oT[:, t, :], start=(t == 0), stop=(t == no - 1))
                mm.then_inc(c.out_product.sem, 1)

        @block.scalar
        def _(act):
            with act.Fori(0, B) as b:
                for i in range(n_sc):
                    act.wait_ge(c.proj_ready.sem, c.proj_ready.base + b * n_pr + i + 1)
                    dst = qb[:, i, :] if i < nt else kb[:, i - nt, :]
                    bias = (bq if i < nt else bk)
                    bias = 0.0 if bias is None else bias[:, (i if i < nt else i - nt):(i if i < nt else i - nt) + 1]
                    nc.scalar.activation(dst, c.psum[:, i % 4, 0:S], ACT.Identity, bias=bias) \
                        .then_inc(c.proj_taken_s.sem, 1)
                for g in range(NG):
                    g0 = b * NG
                    if skip_max:
                        act.wait_ge(c.scores_ready.sem, c.scores_ready.base + g0 + g + 1)
                    else:
                        act.wait_ge(c.scores_max.sem, c.scores_max.base + g0 + g + 1)
                    if g >= 2:
                        act.wait_ge(c.turned_copied.sem, c.turned_copied.base + g0 + g - 1)
                    for u in range(U):
                        h, _ = unit(g, u)
                        src = raw[:, g % 2, u, :] if mask else scores(g)[:, u, :]
                        kw = {} if top else {"accum_out": sums[:, g % 2, u:u + 1]}
                        ins = nc.scalar.activation(
                            probs[:, g % 2, u, :], src, ACT.Exp,
                            bias=0.0 if skip_max else nbias[:, g % 2, u:u + 1],
                            scale=scale if head_scale is None else head_scale[:, h:h + 1], **kw)
                    ins.then_inc(c.probs_ready.sem, 1)
                for t in range(no):
                    act.wait_ge(c.out_turned.sem, c.out_turned.base + b * no + t + 1)
                    nc.scalar.copy(oT[:, t, :], out_turn[:, t % 2, :]).then_inc(c.out_copied.sem, 1)

        @block.vector
        def _(dve):
            chain = Chain(dve, c.vector_chain)
            with dve.Fori(0, B) as b:
                if prepare_mask is not None:
                    prepare_mask(nc, dve, chain, b, mb)
                for j, (kt, lo, hi) in enumerate(vparts):
                    i = n_sc + j
                    dve.wait_ge(c.proj_ready.sem, c.proj_ready.base + b * n_pr + i + 1)
                    if bv is None:
                        ins = nc.vector.tensor_copy(vb[:, kt, lo:hi], c.psum[:, i % 4, 0:hi - lo])
                    else:
                        ins = nc.vector.tensor_tensor(vb[:, kt, lo:hi], c.psum[:, i % 4, 0:hi - lo], bv[:, lo:hi],
                                                      ALU.add)
                    ins.then_inc(c.proj_taken_v.sem, 1)
                g0 = b * NG

                def maxima(g):
                    s = g % 2
                    dve.wait_ge(c.scores_ready.sem, c.scores_ready.base + g0 + g + 1)
                    if top or mask:
                        chain.link(nc.vector.tensor_copy(gate, ident[:, 0:1]))
                    if top:
                        for u in range(U):
                            work = raw[:, s, u, :]
                            src = scores(g)[:, u, :]
                            for r in range(top // 8):
                                chain.link(nc.vector.max(top8[:, s, u, r, :], src))
                                chain.link(nc.vector.match_replace(work, top8[:, s, u, r, :], src, REPLACED))
                                src = work
                        nc.vector.tensor_scalar(nbias[:, s, :], top8[:, s, :, 0, 0], -scale, None, ALU.mult) \
                            .then_inc(c.scores_max.sem, 1)
                        return
                    if mask:
                        for u in range(U):
                            ins = nc.vector.tensor_tensor_reduce(raw[:, s, u, :], scores(g)[:, u, :],
                                                                 mask(mb, *unit(g, u)), 1.0, NEG, ALU.add,
                                                                 ALU.max, rowmax[:, s, u:u + 1])
                            if u == U - 1:
                                chain.link(ins)
                    else:
                        chain.link(nc.vector.reduce_max(rowmax[:, s, :], scores(g), AX.X))
                    nc.vector.tensor_scalar(nbias[:, s, :], rowmax[:, s, :], -scale, None, ALU.mult) \
                        .then_inc(c.scores_max.sem, 1)

                def pick(g):
                    dve.wait_ge(c.probs_ready.sem, c.probs_ready.base + g0 + g + 1)
                    for u in range(U):
                        ins = nc.vector.scalar_tensor_tensor(probs[:, g % 2, u, :], raw[:, g % 2, u, :],
                                                             REPLACED, probs[:, g % 2, u, :], ALU.is_equal,
                                                             ALU.mult, accum_out=sums[:, g % 2, u:u + 1])
                    ins.then_inc(c.probs_picked.sem, 1)

                def copy_turned(g):
                    ready = c.probs_picked if top else c.probs_ready
                    dve.wait_ge(ready.sem, ready.base + g0 + g + 1)
                    chain.link(nc.vector.reciprocal(rsum[:, g % 4, :], sums[:, g % 2, :]))
                    dve.wait_ge(c.probs_turned.sem, c.probs_turned.base + g0 + g + 1)
                    if g >= 2:
                        dve.wait_ge(c.mixed_ready.sem, c.mixed_ready.base + g0 + g - 1)
                    nc.vector.tensor_copy(turned[:, g % 2], turn).then_inc(c.turned_copied.sem, 1)

                def normalise(g):
                    dve.wait_ge(c.mixed_ready.sem, c.mixed_ready.base + g0 + g + 1)
                    dst = otok[:, :, 2 * g * dh:2 * (g + 1) * dh].rearrange("p q (h d) -> p h q d", d=dh)
                    inv = rsum[:, g % 4, :].rearrange("p (h q) -> p h q", q=2).unsqueeze(3)
                    nc.vector.tensor_tensor(dst, mixed.rearrange("p (h q) d -> p h q d", q=2),
                                            inv.broadcast_to([P, 2, 2, dh]), ALU.mult) \
                        .then_inc(c.mixed_taken.sem, 1)

                for g in range(NG + 2):
                    if g < NG and not skip_max:
                        maxima(g)
                    if top and g < NG:
                        pick(g)
                    if 1 <= g <= NG:
                        copy_turned(g - 1)
                    if g >= 2:
                        normalise(g - 2)
                xs = c.X[:, bass.ds(b * S, S)]
                if residual2 is not None:
                    chain.link(nc.vector.tensor_tensor(xs, xs, residual2[:, bass.ds(b * S, S)], ALU.add))
                chain.clear()
                dve.wait_ge(c.out_product.sem, c.out_product.base + b + 1)
                nc.vector.scalar_tensor_tensor(xs, c.psum[:, 7, 0:S], 0.0 if bo is None else bo, xs,
                                               ALU.add, ALU.add).then_inc(c.residual_added.sem, 1)
    for s, n in ((c.staged, 1), (c.proj_ready, n_pr), (c.proj_taken_s, n_sc), (c.proj_taken_v, len(vparts)),
                 (c.scores_ready, NG), (c.scores_max, 0 if skip_max else NG), (c.probs_ready, NG),
                 (c.probs_picked, NG if top else 0), (c.probs_turned, NG), (c.turned_copied, NG),
                 (c.mixed_ready, NG), (c.mixed_taken, NG), (c.out_turned, no), (c.out_copied, no),
                 (c.out_product, 1), (c.residual_added, 1)):
        s.advance(B * n)



def l2_stage(c, tensors):
    nc = c.nc
    a = Arena(c)
    sq, norm = a.take(N), a.take(2, N)
    steps = [(t, i) for t in range(len(tensors)) for i in range(NC)]
    ones = c.w("ones")
    with nc.Block() as block:
        @block.scalar
        def _(act):
            for n, (t, i) in enumerate(steps):
                if n >= NC:
                    act.wait_ge(c.aux_pe.sem, c.aux_pe.at(n - NC + 1))
                nc.scalar.activation(sq[:, i * CH:(i + 1) * CH], tensors[t][:, i * CH:(i + 1) * CH], ACT.Square) \
                    .then_inc(c.aux_s.sem, 1)
            for n, (t, i) in enumerate(steps):
                act.wait_ge(c.aux_pe.sem, c.aux_pe.at(n + 1))
                nc.scalar.activation(norm[:, t, i * CH:(i + 1) * CH], c.psum[:, n, :], ACT.Sqrt) \
                    .then_inc(c.aux_s2.sem, 1)

        @block.tensor
        def _(pe):
            for n, (t, i) in enumerate(steps):
                pe.wait_ge(c.aux_s.sem, c.aux_s.at(n + 1))
                nc.tensor.matmul(c.psum[:, n, :], ones, sq[:, i * CH:(i + 1) * CH], start=True, stop=True) \
                    .then_inc(c.aux_pe.sem, 1)

        @block.vector
        def _(dve):
            chain = Chain(dve, c.vector_chain)
            for n, (t, i) in enumerate(steps):
                dve.wait_ge(c.aux_s2.sem, c.aux_s2.at(n + 1))
                ch = slice(i * CH, (i + 1) * CH)
                chain.link(nc.vector.tensor_scalar(norm[:, t, ch], norm[:, t, ch], 1e-6, None, ALU.max))
                chain.link(nc.vector.reciprocal(norm[:, t, ch], norm[:, t, ch]))
                nc.vector.tensor_tensor(tensors[t][:, ch], tensors[t][:, ch], norm[:, t, ch], ALU.mult)
            chain.clear()
    for s in (c.aux_s, c.aux_s2, c.aux_pe):
        s.advance(len(steps))


def layer0_attention(c):
    nc = c.nc
    load_stage(c, "L0", c.dram)
    n0, qn, kn, vn = c.HN, c.T[:, 0, :], c.T[:, 1, :], c.T[:, 2, :]
    norm_stage(c, c.X, c.HN, "eps5")
    n2 = c.T[:, 3, :]
    norm_stage(c, c.HN, n2, "eps5")
    affine_stage(c, n2, [qn, kn, vn], [c.w("L0a_gq"), c.w("L0a_gk"), c.w("L0a_gv")],
                 [c.w("L0a_hq"), c.w("L0a_hk"), c.w("L0a_hv")])
    project_stage(c, [([qn], [c.w("L0a_wq")], c.w("L0a_bq"), None, c.T[:, 3, :], None)])
    project_stage(c, [([kn], [c.w("L0a_wk")], c.w("L0a_bk"), None, qn, None)])
    l2_stage(c, [c.T[:, 3, :], qn])
    beta = c.w("L0a_beta")
    with nc.Block() as block:
        @block.scalar
        def _(act):
            chain = Chain(act, c.scalar_chain)
            chain.link(nc.scalar.activation(c.work[:, 0:16], beta, ACT.Abs))
            chain.link(nc.scalar.activation(c.work[:, 16:32], c.work[:, 0:16], ACT.Exp, scale=-1.0))
            nc.scalar.activation(c.work[:, 32:48], c.work[:, 16:32], ACT.Ln, bias=c.w("one")).then_inc(c.aux_s.sem, 1)
            act.wait_ge(c.aux_s.sem, c.aux_s.at(1))
            chain.clear()

        @block.vector
        def _(dve):
            chain = Chain(dve, c.vector_chain)
            chain.link(nc.vector.tensor_scalar(c.work[:, 64:80], beta, 0.0, None, ALU.max))
            dve.wait_ge(c.aux_s.sem, c.aux_s.at(1))
            chain.link(nc.vector.tensor_tensor(c.work[:, 80:96], c.work[:, 64:80], c.work[:, 32:48], ALU.add))
            chain.link(nc.vector.tensor_scalar(c.work[:, 96:112], c.work[:, 80:96], 0.1, 10.0, ALU.max, ALU.min))
            chain.link(nc.vector.tensor_scalar(beta, c.work[:, 96:112], float(1.0 / np.sqrt(8.0)), None, ALU.mult))
            chain.clear()
    c.aux_s.advance(1)
    pad = c.w("pad8")
    attention_stage(c, 16, 8, c.T[:, 3, :], qn, vn, [pad[:, t, :] for t in range(4)], None,
                    [pad[:, t, :] for t in range(4)], None, c.w("L0a_wv"), c.w("L0a_bv"), [c.w("L0a_wo")],
                    c.w("L0a_bo"), head_scale=beta, skip_max=True, residual2=c.HN)


def add_stage(c, dst, one, other):
    nc = c.nc
    lo, hi = slice(0, N * 5 // 8), slice(N * 5 // 8, N)
    with nc.Block() as block:
        @block.vector
        def _(dve):
            nc.vector.tensor_tensor(dst[:, lo], one[:, lo], other[:, lo], ALU.add)

        @block.gpsimd
        def _(pool):
            nc.gpsimd.tensor_tensor(dst[:, hi], one[:, hi], other[:, hi], ALU.add)


def layer0_cross(c):
    nc = c.nc
    norm_stage(c, c.X, c.HN, "eps5")
    emb = c.T[:, 3, :]
    add_stage(c, emb, c.HN, c.CT)
    sq, k, v = c.T[:, 0, :], c.T[:, 1, :], c.T[:, 2, :]
    project_stage(c, [([emb], [c.w("L0x_wq")], c.w("L0x_bq"), ACT.Sigmoid, sq, None),
                      ([emb], [c.w("L0x_wk")], c.w("L0x_bk"), None, k, None),
                      ([emb], [c.w("L0x_wv")], c.w("L0x_bv"), None, v, None)])
    a = Arena(c)
    w, ew, ewT = a.take(2, S), a.take(2, S), a.take(2, S)
    wmax, nwmax = a.take(2), a.take(2)
    kmax, nkmax = a.take(1), a.take(1)
    ek, ekv = a.take(S), a.take(S)
    ekT, ekvT = a.take(2, P), a.take(2, P)
    rden, ratio = a.take(S), a.take(S)
    ident = c.w("identity")
    with nc.Block() as block:
        @block.vector
        def _(dve):
            chain = Chain(dve, c.vector_chain)
            chain.link(nc.vector.tensor_tensor(w, c.w("L0x_pos"), c.w("L0x_band"), ALU.mult))
            chain.link(nc.vector.reduce_max(wmax, w, AX.X))
            nc.vector.tensor_scalar(nwmax, wmax, -1.0, None, ALU.mult).then_inc(c.aux_v.sem, 1)
            for t in range(2):
                dve.wait_ge(c.aux_pe.sem, c.aux_pe.at(2 * t + 2))
                ins = nc.vector.tensor_copy(ewT[:, t, :], c.psum[:, 4 + t, 0:S])
            chain.link(ins)
            chain.clear()
            with dve.Fori(0, B) as b:
                chain.link(nc.vector.reduce_max(kmax, k[:, bass.ds(b * S, S)], AX.X))
                nc.vector.tensor_scalar(nkmax, kmax, -1.0, None, ALU.mult).then_inc(c.aux_v2.sem, 1)
                dve.wait_ge(c.aux_pe2.sem, c.aux_pe2.base + b * 2 + 2)
                nc.vector.tensor_copy(ekvT, c.psum[:, 1, 0:S].rearrange("p (t d) -> p t d", t=2)) \
                    .then_inc(c.aux_v3.sem, 1)
                dve.wait_ge(c.aux_pe3.sem, c.aux_pe3.base + b * 2 + 2)
                chain.link(nc.vector.reciprocal(rden, c.psum[:, 2, 0:S]))
                chain.link(nc.vector.tensor_tensor(ratio, c.psum[:, 3, 0:S], rden, ALU.mult))
                q = sq[:, bass.ds(b * S, S)]
                chain.link(nc.vector.tensor_tensor(q, q, ratio, ALU.mult))
                chain.clear()

        @block.scalar
        def _(act):
            act.wait_ge(c.aux_v.sem, c.aux_v.at(1))
            for t in range(2):
                nc.scalar.activation(ew[:, t, :], w[:, t, :], ACT.Exp, bias=nwmax[:, t:t + 1]) \
                    .then_inc(c.aux_s.sem, 1)
            with act.Fori(0, B) as b:
                act.wait_ge(c.aux_v2.sem, c.aux_v2.base + b + 1)
                nc.scalar.activation(ek, k[:, bass.ds(b * S, S)], ACT.Exp, bias=nkmax).then_inc(c.aux_s2.sem, 1)
                act.wait_ge(c.aux_pe2.sem, c.aux_pe2.base + b * 2 + 1)
                nc.scalar.copy(ekT, c.psum[:, 0, 0:S].rearrange("p (t d) -> p t d", t=2)) \
                    .then_inc(c.aux_s3.sem, 1)

        @block.gpsimd
        def _(pool):
            with pool.Fori(0, B) as b:
                pool.wait_ge(c.aux_s2.sem, c.aux_s2.base + b + 1)
                nc.gpsimd.tensor_tensor(ekv, ek, v[:, bass.ds(b * S, S)], ALU.mult).then_inc(c.aux_p.sem, 1)

        @block.tensor
        def _(pe):
            pe.wait_ge(c.aux_s.sem, c.aux_s.at(2))
            for j in range(2):
                for t in range(2):
                    nc.tensor.transpose(c.psum[:, 4 + j, t * P:(t + 1) * P], ew[:, t, j * P:(j + 1) * P], ident) \
                        .then_inc(c.aux_pe.sem, 1)
            with pe.Fori(0, B) as b:
                for n, (src, sig) in enumerate(((ek, c.aux_s2), (ekv, c.aux_p))):
                    pe.wait_ge(sig.sem, sig.base + b + 1)
                    for t in range(2):
                        mm = nc.tensor.transpose(c.psum[:, n, t * P:(t + 1) * P], src[:, t * P:(t + 1) * P], ident)
                    mm.then_inc(c.aux_pe2.sem, 1)
                for n, (src, sig) in enumerate(((ekT, c.aux_s3), (ekvT, c.aux_v3))):
                    pe.wait_ge(sig.sem, sig.base + b + 1)
                    for t in range(2):
                        mm = nc.tensor.matmul(c.psum[:, 2 + n, 0:S], src[:, t, :], ewT[:, t, :],
                                              start=(t == 0), stop=(t == 1))
                    mm.then_inc(c.aux_pe3.sem, 1)
    for s, n in ((c.aux_v, 1), (c.aux_s, 2), (c.aux_pe, 4), (c.aux_v2, B), (c.aux_v3, B), (c.aux_s2, B),
                 (c.aux_s3, B), (c.aux_p, B), (c.aux_pe2, 2 * B), (c.aux_pe3, 2 * B)):
        s.advance(n)
    project_stage(c, [([sq], [c.w("L0x_wo")], c.w("L0x_bo"), None, k, emb)])
    norm_stage(c, k, c.HN, "eps5", gain=c.w("L0x_gamma"), shift=c.w("L0x_beta"))
    w1, b1, w2 = c.w("L0x_w1"), c.w("L0x_b1"), c.w("L0x_w2")
    hidden = [c.T[:, t, :] for t in range(4)]
    project_stage(c, [([c.HN], [w1[:, t * P:(t + 1) * P]], b1[:, t:t + 1], ACT.Relu, hidden[t], None)
                      for t in range(4)])
    project_stage(c, [(hidden, [w2[:, t, :] for t in range(4)], c.w("L0x_b2"), None, c.HN, c.HN)])
    norm_stage(c, c.HN, c.HN, "eps5", gain=c.w("L0x_gamma"), shift=c.w("L0x_beta"))
    add_stage(c, c.X, c.X, c.HN)



E = 8
NT = N // P


def route_stage(c, src, router, bias, w_t, a, mode, capacity=None):
    nc = c.nc
    ident = c.w("identity")
    logits, p, t1, t2, first, second, weight, chosen = [a.take(NT, E) for _ in range(8)]
    before = a.take(NT, E)
    m, r = a.take(NT), a.take(NT)
    falling = c.w("falling").unsqueeze(1).broadcast_to([P, NT, E])
    ps = c.psum[:, 0, 0:NT * E].rearrange("p (t e) -> p t e", e=E)

    def over(x):
        return x.unsqueeze(2).broadcast_to([P, NT, E])

    with nc.Block() as block:
        @block.tensor
        def _(pe):
            for t in range(NT):
                mm = nc.tensor.matmul(ps[:, t, :], src[:, t * P:(t + 1) * P], router, start=True, stop=True)
            mm.then_inc(c.aux_pe.sem, 1)
            if capacity is not None:
                pe.wait_ge(c.aux_v2.sem, c.aux_v2.at(1))
                flat = chosen.rearrange("p t e -> p (t e)")
                nc.tensor.matmul(c.psum[:, 1, 0:P], c.w("upper"), flat, start=True, stop=True)
                nc.tensor.matmul(c.psum[:, 2, 0:P], c.w("ones"), flat, start=True, stop=True) \
                    .then_inc(c.aux_pe2.sem, 1)
            pe.wait_ge(c.aux_v3.sem, c.aux_v3.at(1))
            for t in range(NT):
                mm = nc.tensor.transpose(c.psum[0:E, 4 + t // 4, (t % 4) * P:(t % 4 + 1) * P], weight[:, t, :], ident)
            mm.then_inc(c.aux_pe3.sem, 1)

        @block.gpsimd
        def _(pool):
            nc.gpsimd.memset(w_t, 0.0).then_inc(c.aux_p.sem, 1)

        @block.scalar
        def _(act):
            act.wait_ge(c.aux_v.sem, c.aux_v.at(1))
            nc.scalar.activation(p, t1, ACT.Exp).then_inc(c.aux_s.sem, 1)
            act.wait_ge(c.aux_p.sem, c.aux_p.at(1))
            act.wait_ge(c.aux_pe3.sem, c.aux_pe3.at(1))
            for i in range(NC):
                nc.scalar.copy(w_t[0:E, i * CH:(i + 1) * CH], c.psum[0:E, 4 + i, :])

        @block.vector
        def _(dve):
            ch = Chain(dve, c.vector_chain)
            v = nc.vector
            dve.wait_ge(c.aux_pe.sem, c.aux_pe.at(1))
            if bias is None:
                ch.link(v.tensor_copy(logits, ps))
            else:
                ch.link(v.tensor_tensor(logits, ps, bias.unsqueeze(1).broadcast_to([P, NT, E]), ALU.add))
            ch.link(v.reduce_max(m, logits, AX.X))
            v.tensor_tensor(t1, logits, over(m), ALU.subtract).then_inc(c.aux_v.sem, 1)
            dve.wait_ge(c.aux_s.sem, c.aux_s.at(1))
            ch.link(v.reduce_sum(m, p, AX.X))
            ch.link(v.reciprocal(r, m))
            ch.link(v.tensor_tensor(p, p, over(r), ALU.mult))

            def likeliest(q, one_hot):
                ch.link(v.reduce_max(m, q, AX.X))
                ch.link(v.tensor_tensor(t1, q, over(m), ALU.is_equal))
                ch.link(v.tensor_tensor(t1, t1, falling, ALU.mult))
                ch.link(v.reduce_max(m, t1, AX.X))
                ch.link(v.tensor_tensor(one_hot, t1, over(m), ALU.is_equal))

            likeliest(p, first)
            if mode == "single":
                ch.link(v.tensor_copy(chosen, first))
            else:
                ch.link(v.scalar_tensor_tensor(t2, first, -3.0, p, ALU.mult, ALU.add))
                likeliest(t2, second)
                ch.link(v.tensor_tensor(chosen, first, second, ALU.add))
            ch.link(v.tensor_tensor(weight, chosen, p, ALU.mult))
            if mode == "pair_normed":
                ch.link(v.reduce_sum(m, weight, AX.X))
                ch.link(v.reciprocal(r, m))
                ch.link(v.tensor_tensor(weight, weight, over(r), ALU.mult))
            if capacity is not None:
                v.memset(before[:, 0, :], 0.0).then_inc(c.aux_v2.sem, 1)
                dve.wait_ge(c.aux_pe2.sem, c.aux_pe2.at(1))
                totals = c.psum[:, 2, 0:P].rearrange("p (t e) -> p t e", e=E)
                ch.link(v.tensor_copy(t2, totals))
                for t in range(1, NT):
                    ch.link(v.tensor_tensor(before[:, t, :], before[:, t - 1, :], t2[:, t - 1, :], ALU.add))
                ch.link(v.tensor_tensor(t1, c.psum[:, 1, 0:P].rearrange("p (t e) -> p t e", e=E), before, ALU.add))
                ch.link(v.tensor_scalar(t1, t1, float(capacity), None, ALU.is_le))
                v.tensor_tensor(weight, weight, t1, ALU.mult).then_inc(c.aux_v3.sem, 1)
            else:
                v.memset(before[:, 0, :], 0.0).then_inc(c.aux_v3.sem, 1)
            dve.wait_ge(c.aux_v3.sem, c.aux_v3.at(1))
            ch.clear()
    for s in (c.aux_pe, c.aux_pe3, c.aux_v, c.aux_s, c.aux_v3, c.aux_p):
        s.advance(1)
    if capacity is not None:
        c.aux_pe2.advance(1)
        c.aux_v2.advance(1)


def expert_stage(c, src, experts, w_t, a, out_bias=None):
    nc = c.nc
    units = [(e, i) for e in range(len(experts)) for i in range(len(experts[e][1]))]
    gated = experts[0][2][0].shape[1] > 1
    NU, NE = len(units), len(experts)
    routed = [e for e in range(NE) if experts[e][0] is not None]
    NR = len(routed)
    last = [e for e in range(NE)]
    LAG = 2
    act_buf = a.take(2, CH) if gated else None
    hid = a.take(4, CH)
    wb = a.take(2, CH)
    part = a.take(2, CH)
    acc = a.take(CH)
    pick = c.w("pick")
    first_unit = {e: min(n for n, u in enumerate(units) if u[0] == e) for e in range(NE)}
    per_expert = NU // NE

    def gate_bank(n):
        return 2 * (n % 2) if gated else n % 4

    with nc.Block() as block:
        @block.tensor
        def _(pe):
            with pe.Fori(0, NC) as i:
                x = src[:, bass.ds(i * CH, CH)]
                u0, e0, r0 = i * NU, i * NE, i * NR
                for n in range(NU + LAG):
                    if n < NU:
                        e, t = units[n]
                        if t == 0 and experts[e][0] is not None:
                            r = routed.index(e)
                            pe.wait_ge(c.aux_s2.sem, c.aux_s2.base + r0 + r)
                            nc.tensor.matmul(c.psum[:, 6, :], pick[:, experts[e][0], :],
                                             w_t[:, bass.ds(i * CH, CH)], start=True, stop=True) \
                                .then_inc(c.aux_pe3.sem, 1)
                        depth = 2 if gated else 4
                        if n >= depth:
                            pe.wait_ge(c.aux_v.sem, c.aux_v.base + u0 + n - depth + 1)
                        nc.tensor.matmul(c.psum[:, gate_bank(n), :], experts[e][1][t], x, start=True, stop=True) \
                            .then_inc(c.aux_pe.sem, 1)
                        if gated:
                            nc.tensor.matmul(c.psum[:, gate_bank(n) + 1, :], experts[e][2][t], x,
                                             start=True, stop=True).then_inc(c.aux_pe.sem, 1)
                    if n >= LAG:
                        k = n - LAG
                        e, t = units[k]
                        if t == 0:
                            pe.wait_ge(c.aux_v2.sem, c.aux_v2.base + e0 + max(e - 1, 0))
                        pe.wait_ge(c.aux_v.sem, c.aux_v.base + u0 + k + 1)
                        mm = nc.tensor.matmul(c.psum[:, 4 + e % 2, :], experts[e][3][t], hid[:, k % 4, :],
                                              start=(t == 0), stop=(t == per_expert - 1))
                        mm.then_inc(c.aux_pe2.sem, 1)
                if out_bias is not None:
                    pe.wait_ge(c.residual_added.sem, c.residual_added.base + i)
                    nc.tensor.matmul(c.psum[:, 7, :], out_bias, w_t[:, bass.ds(i * CH, CH)],
                                     start=True, stop=True) \
                        .then_inc(c.product_ready.sem, 1)

        @block.scalar
        def _(act):
            with act.Fori(0, NC) as i:
                u0, r0 = i * NU, i * NR
                for n in range(NU):
                    e, t = units[n]
                    if t == 0 and experts[e][0] is not None:
                        r = routed.index(e)
                        act.wait_ge(c.aux_pe3.sem, c.aux_pe3.base + r0 + r + 1)
                        act.wait_ge(c.aux_v2.sem, c.aux_v2.base + i * NE + max(e - 1, 0))
                        nc.scalar.copy(wb[:, r % 2, :], c.psum[:, 6, :]).then_inc(c.aux_s2.sem, 1)
                    if gated:
                        act.wait_ge(c.aux_pe.sem, c.aux_pe.base + 2 * (u0 + n) + 1)
                        if n >= 2:
                            act.wait_ge(c.aux_v.sem, c.aux_v.base + u0 + n - 1)
                        nc.scalar.activation(act_buf[:, n % 2, :], c.psum[:, gate_bank(n), :], ACT.Silu) \
                            .then_inc(c.aux_s.sem, 1)

        @block.vector
        def _(dve):
            chain = Chain(dve, c.vector_chain)
            with dve.Fori(0, NC) as i:
                u0, e0, r0 = i * NU, i * NE, i * NR

                def take(e):
                    dve.wait_ge(c.aux_pe2.sem, c.aux_pe2.base + u0 + (e + 1) * per_expert)
                    if experts[e][0] is None:
                        src_ = c.psum[:, 4 + e % 2, :]
                    else:
                        r = routed.index(e)
                        dve.wait_ge(c.aux_s2.sem, c.aux_s2.base + r0 + r + 1)
                        src_ = part[:, e % 2, :]
                        chain.link(nc.vector.tensor_tensor(src_, c.psum[:, 4 + e % 2, :], wb[:, r % 2, :], ALU.mult))
                    if e == 0:
                        ins = nc.vector.tensor_copy(acc, src_)
                    else:
                        ins = nc.vector.tensor_tensor(acc, acc, src_, ALU.add)
                    ins.then_inc(c.aux_v2.sem, 1)
                    dve.wait_ge(c.aux_v2.sem, c.aux_v2.base + e0 + e + 1)

                for n in range(NU):
                    e, t = units[n]
                    if n >= 4:
                        dve.wait_ge(c.aux_pe2.sem, c.aux_pe2.base + u0 + n - 3)
                    if gated:
                        dve.wait_ge(c.aux_s.sem, c.aux_s.base + u0 + n + 1)
                        dve.wait_ge(c.aux_pe.sem, c.aux_pe.base + 2 * (u0 + n) + 2)
                        ins = nc.vector.tensor_tensor(hid[:, n % 4, :], act_buf[:, n % 2, :],
                                                      c.psum[:, gate_bank(n) + 1, :], ALU.mult)
                    else:
                        dve.wait_ge(c.aux_pe.sem, c.aux_pe.base + u0 + n + 1)
                        ins = nc.vector.tensor_scalar(hid[:, n % 4, :], c.psum[:, gate_bank(n), :],
                                                      experts[e][2][t], 0.0, ALU.add, ALU.max)
                    ins.then_inc(c.aux_v.sem, 1)
                    if t == per_expert - 1 and e >= 1:
                        take(e - 1)
                take(NE - 1)
                xs = c.X[:, bass.ds(i * CH, CH)]
                chain.link(nc.vector.tensor_tensor(xs, xs, acc, ALU.add))
                chain.clear()
                if out_bias is not None:
                    dve.wait_ge(c.product_ready.sem, c.product_ready.base + i + 1)
                    nc.vector.tensor_tensor(xs, xs, c.psum[:, 7, :], ALU.add).then_inc(c.residual_added.sem, 1)
    per = 2 if gated else 1
    for s, n in ((c.aux_pe, per * NU), (c.aux_pe2, NU), (c.aux_pe3, NR), (c.aux_s, NU if gated else 0),
                 (c.aux_s2, NR), (c.aux_v, NU), (c.aux_v2, NE)):
        s.advance(NC * n)
    if out_bias is not None:
        c.product_ready.advance(NC)
        c.residual_added.advance(NC)


def layer0_experts(c):
    load_stage(c, "L0f", c.dram)
    norm_stage(c, c.X, c.HN, "eps5")
    norm_stage(c, c.HN, c.T[:, 0, :], "epsf", centre=False)
    a = Arena(c)
    w_t = a.take(N)
    route_stage(c, c.T[:, 0, :], c.w("L0f_router"), None, w_t, a, "pair_normed", capacity=int(1.25 * N / E))
    rg, ru, rd = c.w("L0f_rg"), c.w("L0f_ru"), c.w("L0f_rd")
    sg, su, sd = c.w("L0f_sg"), c.w("L0f_su"), c.w("L0f_sd")
    experts = [(e, [rg[:, e, t * P:(t + 1) * P] for t in range(4)], [ru[:, e, t * P:(t + 1) * P] for t in range(4)],
                [rd[:, e, t, :] for t in range(4)]) for e in range(E)]
    experts += [(None, [sg[:, t * P:(t + 1) * P] for t in range(4 * h, 4 * h + 4)],
                 [su[:, t * P:(t + 1) * P] for t in range(4 * h, 4 * h + 4)],
                 [sd[:, t, :] for t in range(4 * h, 4 * h + 4)]) for h in range(2)]
    expert_stage(c, c.HN, experts, w_t, a)



def turn_stage(c, groups):
    nc = c.nc
    ident = c.w("identity")

    def bank(n, k):
        return c.psum[:, n % 8, 0:k * P].rearrange("p (k x) -> p k x", x=P)

    with nc.Block() as block:
        @block.tensor
        def _(pe):
            for n, (views, _) in enumerate(groups):
                if n >= 8:
                    sig = c.product_taken if n % 2 == 0 else c.product_taken_v
                    pe.wait_ge(sig.sem, sig.at((n - 8) // 2 + 1))
                for k, view in enumerate(views):
                    mm = nc.tensor.transpose(bank(n, len(views))[:, k, :], view, ident)
                mm.then_inc(c.product_ready.sem, 1)

        @block.scalar
        def _(act):
            for n in range(0, len(groups), 2):
                views, dst = groups[n]
                act.wait_ge(c.product_ready.sem, c.product_ready.at(n + 1))
                nc.scalar.copy(dst, bank(n, len(views))).then_inc(c.product_taken.sem, 1)

        @block.vector
        def _(dve):
            for n in range(1, len(groups), 2):
                views, dst = groups[n]
                dve.wait_ge(c.product_ready.sem, c.product_ready.at(n + 1))
                nc.vector.tensor_copy(dst, bank(n, len(views))).then_inc(c.product_taken_v.sem, 1)
    c.product_ready.advance(len(groups))
    c.product_taken.advance((len(groups) + 1) // 2)
    c.product_taken_v.advance(len(groups) // 2)


def conv_stage(c, tensors, taps):
    nc = c.nc
    a = Arena(c)
    acc = [a.take(N) for _ in tensors]
    with nc.Block() as block:
        @block.vector
        def _(dve):
            chain = Chain(dve, c.vector_chain)
            for x, w, y in zip(tensors, taps, acc):
                K = w.shape[1]
                xs = x.rearrange("p (b s) -> p b s", s=S)
                ys = y.rearrange("p (b s) -> p b s", s=S)
                chain.link(nc.vector.tensor_scalar(y, x, w[:, K - 1:K], None, ALU.mult))
                for back in range(1, K):
                    ins = nc.vector.scalar_tensor_tensor(ys[:, :, back:], xs[:, :, 0:S - back],
                                                         w[:, K - 1 - back:K - back], ys[:, :, back:],
                                                         ALU.mult, ALU.add)
                    if back < K - 1:
                        chain.link(ins)
                ins.then_inc(c.aux_v.sem, 1)
            dve.wait_ge(c.aux_v.sem, c.aux_v.at(len(tensors)))
            chain.clear()

        @block.scalar
        def _(act):
            for n, (x, y) in enumerate(zip(tensors, acc)):
                act.wait_ge(c.aux_v.sem, c.aux_v.at(n + 1))
                nc.scalar.activation(x, y, ACT.Silu)
    c.aux_v.advance(len(tensors))


def layer1_attention(c):
    nc = c.nc
    H, D = 8, 16
    load_stage(c, "L1", c.dram)
    norm_stage(c, c.X, c.HN, "eps5")
    q, k, v = c.T[:, 0, :], c.T[:, 1, :], c.T[:, 2, :]
    project_stage(c, [([c.HN], [c.w(f"L1a_w{s}")], None, None, t, None) for s, t in zip("qkv", (q, k, v))])
    conv_stage(c, [q, k, v], [c.w(f"L1a_conv_{s}") for s in "qkv"])

    a = Arena(c)
    mark0 = a.off
    qt, kt, vbt, _, vt = [a.take(2, B, P) for _ in range(5)]
    gates, gsum = a.take(NT, 2 * H), a.take(NT, H)
    lengths, inv = a.take(2, 2 * B * H), a.take(2, 2 * B * H)
    mark = a.off
    v_r, o_r, beta_r = a.take(S, 8), a.take(S, 8), a.take(S)
    end = a.off
    groups = []
    for src, dst in ((q, qt), (k, kt), (v, vt)):
        for th in range(2):
            for b0 in range(0, B, 4):
                groups.append(([src[:, b * S + th * P:b * S + (th + 1) * P] for b in range(b0, b0 + 4)],
                               dst[:, th, b0:b0 + 4, :]))
    turn_stage(c, groups)

    square = c.work[:, mark:mark + 2 * N].rearrange("p (n x) -> p n x", x=N)
    q2 = c.T[:, 0:2, :].rearrange("p t (g w d) -> p t g w d", w=2, d=D)
    k2 = c.T[:, 2:4, :].rearrange("p t (g w d) -> p t g w d", w=2, d=D)
    ps_g = c.psum[:, 0, 0:NT * 2 * H].rearrange("p (n e) -> p n e", e=2 * H)

    def heads(x):
        return x.rearrange("p t b (h d) -> p (t b h) d", d=D)

    with nc.Block() as block:
        @block.tensor
        def _(pe):
            for n in range(NT):
                mm = nc.tensor.matmul(ps_g[:, n, :], c.HN[:, n * P:(n + 1) * P], c.w("L1a_gates"),
                                      start=True, stop=True)
            mm.then_inc(c.aux_pe.sem, 1)

        @block.scalar
        def _(act):
            for n, x in enumerate((qt, kt)):
                nc.scalar.activation(square[:, n, :], x.rearrange("p t b f -> p (t b f)"), ACT.Square) \
                    .then_inc(c.aux_s.sem, 1)
            act.wait_ge(c.aux_v.sem, c.aux_v.at(2))
            nc.scalar.activation(lengths, lengths, ACT.Sqrt, bias=c.w("eps12")).then_inc(c.aux_s.sem, 1)
            act.wait_ge(c.aux_v2.sem, c.aux_v2.at(1))
            nc.scalar.activation(gates, gates, ACT.Sigmoid).then_inc(c.aux_s.sem, 1)

        @block.vector
        def _(dve):
            ch = Chain(dve, c.vector_chain)
            dve.wait_ge(c.aux_pe.sem, c.aux_pe.at(1))
            nc.vector.tensor_tensor(gates, ps_g, c.w("L1a_mix_b").unsqueeze(1).broadcast_to([P, NT, 2 * H]), ALU.add) \
                .then_inc(c.aux_v3.sem, 1)
            dve.wait_ge(c.aux_v3.sem, c.aux_v3.at(1))
            nc.vector.tensor_tensor(gates, gates, c.w("L1a_mix_bias").unsqueeze(1).broadcast_to([P, NT, 2 * H]),
                                    ALU.add).then_inc(c.aux_v2.sem, 1)
            for n in range(2):
                dve.wait_ge(c.aux_s.sem, c.aux_s.at(n + 1))
                nc.vector.reduce_sum(lengths[:, n, :], square[:, n, :].rearrange("p (g d) -> p g d", d=D), AX.X) \
                    .then_inc(c.aux_v.sem, 1)
            dve.wait_ge(c.aux_s.sem, c.aux_s.at(3))
            ch.link(nc.vector.reciprocal(inv, lengths))
            for n, (x, x2) in enumerate(((qt, q2), (kt, k2))):
                for th in range(2):
                    g = slice(th * B * H, (th + 1) * B * H)
                    for w in range(2):
                        nc.vector.tensor_tensor(x2[:, th, :, w, :], heads(x)[:, g, :],
                                                inv[:, n, g].unsqueeze(2).broadcast_to([P, B * H, D]), ALU.mult)
            dve.wait_ge(c.aux_s.sem, c.aux_s.at(4))
            beta = gates[:, :, 0:H].rearrange("p (b t) h -> p t b h", t=2)
            for th in range(2):
                nc.vector.tensor_tensor(vbt[:, th].rearrange("p b (h d) -> p b h d", d=D),
                                        vt[:, th].rearrange("p b (h d) -> p b h d", d=D),
                                        beta[:, th].unsqueeze(3).broadcast_to([P, B, H, D]), ALU.mult)
            ch.clear()
    for s, n in ((c.aux_pe, 1), (c.aux_s, 4), (c.aux_v, 2), (c.aux_v2, 1), (c.aux_v3, 1)):
        s.advance(n)

    q_r = c.work[:, mark0:mark0 + 2 * N].rearrange("p (t d) -> p t d", d=D)
    k_r = c.work[:, mark0 + 2 * N:mark0 + 4 * N].rearrange("p (t d) -> p t d", d=D)
    beta2 = c.HN[:, 0:2 * P].rearrange("p (t g w) -> p t g w", t=2, w=2)
    with nc.Block() as block:
        @block.vector
        def _(dve):
            for th in range(2):
                for w in range(2):
                    nc.vector.tensor_copy(beta2[:, th, :, w].rearrange("p (b h) -> p b h", h=H),
                                          gates[:, :, 0:H].rearrange("p (b t) h -> p t b h", t=2)[:, th])
    groups = []
    for th in range(2):
        for d0 in range(0, 8, 4):
            views = [vbt[:, th].rearrange("p b (g d) -> p (b g) d", d=8)[:, :, d] for d in range(d0, d0 + 4)]
            groups.append((views, v_r[:, th * P:(th + 1) * P, d0:d0 + 4].rearrange("p t d -> p d t")))
        groups.append(([beta2[:, th].rearrange("p g w -> p (g w)")],
                       beta_r[:, th * P:(th + 1) * P].unsqueeze(1)))
    turn_stage(c, groups)
    groups = []
    for th in range(2):
        for src, dst in ((q2, q_r), (k2, k_r)):
            for d0 in range(0, D, 4):
                views = [src[:, th].rearrange("p g w d -> p (g w) d")[:, :, d] for d in range(d0, d0 + 4)]
                groups.append((views, dst[:, th * P:(th + 1) * P, d0:d0 + 4].rearrange("p t d -> p d t")))
    turn_stage(c, groups)

    a.off = end
    GT = 16
    state = c.T[:, 0:2, :].rearrange("p r (t v d) -> p r t v d", v=8, d=D)
    qs = c.T[:, 2:4, :].rearrange("p r (t v d) -> p r t v d", v=8, d=D)
    k_b, v_b, nb_b = a.take(2 * GT, D), a.take(2 * GT, 8), a.take(2 * GT)
    sk, pred, u, outer = a.take(8, D), a.take(8), a.take(8), a.take(8, D)
    BT = 2 * GT
    NI = S // BT

    with nc.Block() as block:
        @block.scalar
        def _(act):
            with act.Fori(0, NI) as i:
                act.wait_ge(c.aux_v.sem, c.aux_v.base + i * 2)
                nc.scalar.copy(k_b, k_r[:, bass.ds(i * BT, BT), :])
                nc.scalar.copy(v_b, v_r[:, bass.ds(i * BT, BT), :])
                nc.scalar.activation(nb_b, beta_r[:, bass.ds(i * BT, BT)], ACT.Copy, scale=-1.0) \
                    .then_inc(c.aux_s.sem, 1)

        @block.gpsimd
        def _(pool):
            with pool.Fori(0, NI) as i:
                for r in range(2):
                    pool.wait_ge(c.aux_v.sem, c.aux_v.base + i * 2 + r + 1)
                    qv = q_r[:, bass.ds(i * BT + r * GT, GT), :].unsqueeze(2).broadcast_to([P, GT, 8, D])
                    nc.gpsimd.tensor_tensor(qs[:, r], state[:, r], qv, ALU.mult).then_inc(c.aux_p.sem, 1)

        @block.vector
        def _(dve):
            ch = Chain(dve, c.vector_chain)
            v = nc.vector
            ch.link(v.memset(state[:, 1, GT - 1], 0.0))
            ch.clear()
            with dve.Fori(0, NI) as i:
                dve.wait_ge(c.aux_s.sem, c.aux_s.base + i + 1)
                for s in range(BT):
                    r, t = s // GT, s % GT
                    old = state[:, r, t - 1] if t else state[:, 1 - r, GT - 1]
                    new = state[:, r, t]
                    key = k_b[:, s, :].unsqueeze(1).broadcast_to([P, 8, D])
                    ch.link(v.tensor_tensor(sk, old, key, ALU.mult))
                    ch.link(v.reduce_sum(pred, sk, AX.X))
                    ch.link(v.scalar_tensor_tensor(u, pred, nb_b[:, s:s + 1], v_b[:, s, :], ALU.mult, ALU.add))
                    ch.link(v.tensor_tensor(outer, u.unsqueeze(2).broadcast_to([P, 8, D]), key, ALU.mult))
                    if t == GT - 1:
                        v.tensor_tensor(new, old, outer, ALU.add).then_inc(c.aux_v.sem, 1)
                        dve.wait_ge(c.aux_v.sem, c.aux_v.base + i * 2 + r + 1)
                    else:
                        ch.link(v.tensor_tensor(new, old, outer, ALU.add))
                    if s == GT + 4 or s == BT - 1:
                        h = 0 if s < BT - 1 else 1
                        dve.wait_ge(c.aux_p.sem, c.aux_p.base + i * 2 + h + 1)
                        v.reduce_sum(o_r[:, bass.ds(i * BT + h * GT, GT), :], qs[:, h], AX.X) \
                            .then_inc(c.aux_v2.sem, 1)
                dve.wait_ge(c.aux_v2.sem, c.aux_v2.base + i * 2 + 2)
                ch.link(v.tensor_copy(pred, u))
                ch.clear()
    c.aux_s.advance(NI)
    for s in (c.aux_v, c.aux_v2, c.aux_p):
        s.advance(2 * NI)

    o_t = qt
    groups = []
    for th in range(2):
        for d0 in range(0, 8, 4):
            views = [o_r[:, th * P:(th + 1) * P, d] for d in range(d0, d0 + 4)]
            dst = o_t[:, th].rearrange("p b (g d) -> p d (b g)", d=8)[:, d0:d0 + 4, :]
            groups.append((views, dst))
    turn_stage(c, groups)

    def wide(x, th):
        return x[:, th].rearrange("p b (h d) -> p b h d", d=D)

    ms = lengths[:, 0, :]
    with nc.Block() as block:
        @block.vector
        def _(dve):
            ch = Chain(dve, c.vector_chain)
            v = nc.vector
            gate = gates[:, :, H:2 * H].rearrange("p (b t) h -> p t b h", t=2)
            flat = "p t b f -> p (t b f)"
            ch.link(v.tensor_tensor(o_t.rearrange(flat), o_t.rearrange(flat), vt.rearrange(flat), ALU.subtract))
            for th in range(2):
                ch.link(v.tensor_tensor(wide(o_t, th), wide(o_t, th), gate[:, th].unsqueeze(3)
                                        .broadcast_to([P, B, H, D]), ALU.mult))
            v.tensor_tensor(o_t.rearrange(flat), o_t.rearrange(flat), vt.rearrange(flat), ALU.add) \
                .then_inc(c.aux_v.sem, 1)
            dve.wait_ge(c.aux_s.sem, c.aux_s.at(1))
            v.reduce_sum(ms, kt.rearrange("p t b (h d) -> p (t b h) d", d=D), AX.X).then_inc(c.aux_v.sem, 1)
            dve.wait_ge(c.aux_s.sem, c.aux_s.at(2))
            ch.link(v.reciprocal(inv[:, 0, :], ms))
            ch.link(v.tensor_tensor(heads(o_t), heads(o_t), inv[:, 0, :].unsqueeze(2)
                                    .broadcast_to([P, 2 * B * H, D]), ALU.mult))
            ch.link(v.tensor_tensor(heads(o_t), heads(o_t), c.w("L1a_onorm").unsqueeze(1)
                                    .broadcast_to([P, 2 * B * H, D]), ALU.mult))
            ch.clear()

        @block.scalar
        def _(act):
            act.wait_ge(c.aux_v.sem, c.aux_v.at(1))
            nc.scalar.activation(kt.rearrange("p t b f -> p (t b f)"), o_t.rearrange("p t b f -> p (t b f)"),
                                 ACT.Square).then_inc(c.aux_s.sem, 1)
            act.wait_ge(c.aux_v.sem, c.aux_v.at(2))
            nc.scalar.activation(ms, ms, ACT.Sqrt, scale=1.0 / D, bias=c.w("eps5")).then_inc(c.aux_s.sem, 1)
    c.aux_v.advance(2)
    c.aux_s.advance(2)
    groups = []
    o_f = c.T[:, 0, :]
    for b in range(0, B, 2):
        groups.append(([o_t[:, th, bb, :] for bb in (b, b + 1) for th in range(2)],
                       o_f[:, b * S:(b + 2) * S].rearrange("p (k x) -> p k x", x=P)))
    turn_stage(c, groups)
    project_stage(c, [([o_f], [c.w("L1a_wo")], None, None, c.X, c.X)])


def layer1_cross(c):
    norm_stage(c, c.X, c.HN, "eps5")
    wq, wk, wo = c.w("L1x_wq"), c.w("L1x_wk"), c.w("L1x_wo")

    def prepare(nc, dve, chain, b, mb):
        far = mb[:, 2 * S:3 * S]
        chain.link(nc.vector.tensor_scalar(far, c.w("position"), c.valid[:, bass.ds(b, 1)], NEG, ALU.is_ge, ALU.mult))
        for qt in range(2):
            chain.link(nc.vector.tensor_tensor(mb[:, qt * S:(qt + 1) * S], c.w("causal")[:, qt, :], far, ALU.min))

    attention_stage(c, 16, 64, c.HN, c.CT, c.CT, [wq[:, t, :] for t in range(8)], c.w("L1x_bq"),
                    [wk[:, t, :] for t in range(8)], c.w("L1x_bk"), c.w("L1x_wv"), c.w("L1x_bv"),
                    [wo[:, t, :] for t in range(8)], c.w("L1x_bo"), scale=1.0 / 8.0,
                    mask=lambda mb, h, qt: mb[:, qt * S:(qt + 1) * S], prepare_mask=prepare, mask_words=3 * S,
                    room=c.T)


def layer1_experts(c):
    norm_stage(c, c.X, c.HN, "eps5")
    a = Arena(c)
    w_t = a.take(N)
    route_stage(c, c.HN, c.w("L1f_gate"), c.w("L1f_gate_b"), w_t, a, "pair")
    w1, b1, w2 = c.w("L1f_w1"), c.w("L1f_b1"), c.w("L1f_w2")
    experts = [(e, [w1[:, e, t * P:(t + 1) * P] for t in range(2)], [b1[:, e, t:t + 1] for t in range(2)],
                [w2[:, e, t, :] for t in range(2)]) for e in range(E)]
    expert_stage(c, c.HN, experts, w_t, a, out_bias=c.w("L1f_b2"))



def trig_stage(c, trig):
    nc = c.nc
    a = Arena(c)
    ang, turns, r, absr, sn, cs = [a.take(2, S) for _ in range(6)]
    theta = c.w("L2a_theta")
    flat = "p t s -> p (t s)"
    MAGIC = 1.5 * 2.0 ** 23
    two_pi = 2.0 * np.pi
    hi = 6.28125
    mid = float(np.float32(np.round((two_pi - hi) * 2.0 ** 20) / 2.0 ** 20))
    lo = float(two_pi - hi - mid)
    edge = 3.1415925
    with nc.Block() as block:
        @block.vector
        def _(dve):
            ch = Chain(dve, c.vector_chain)
            v = nc.vector
            for t in range(2):
                ch.link(v.tensor_scalar(ang[:, t], c.w("position"), theta[:, t:t + 1], None, ALU.mult))
            ch.link(v.tensor_scalar(turns, ang, float(1.0 / two_pi), MAGIC, ALU.mult, ALU.add))
            ch.link(v.tensor_scalar(turns, turns, MAGIC, None, ALU.subtract))
            ch.link(v.scalar_tensor_tensor(r, turns, -hi, ang, ALU.mult, ALU.add))
            ch.link(v.scalar_tensor_tensor(ang, turns, -mid, r, ALU.mult, ALU.add))
            ch.link(v.scalar_tensor_tensor(r, turns, -lo, ang, ALU.mult, ALU.add))
            v.tensor_scalar(r, r, edge, -edge, ALU.min, ALU.max).then_inc(c.aux_v.sem, 1)
            dve.wait_ge(c.aux_s.sem, c.aux_s.at(1))
            ch.link(v.tensor_scalar(turns, sn, c.w("L2a_sine_rows"), None, ALU.mult))
            ch.link(v.scalar_tensor_tensor(trig.rearrange(flat), cs.rearrange(flat), c.w("L2a_cosine_rows"),
                                           turns.rearrange(flat), ALU.mult, ALU.add))
            ch.clear()

        @block.scalar
        def _(act):
            ch = Chain(act, c.scalar_chain)
            act.wait_ge(c.aux_v.sem, c.aux_v.at(1))
            ch.link(nc.scalar.activation(absr, r, ACT.Abs))
            nc.scalar.activation(sn, r, ACT.Sin)
            nc.scalar.activation(cs, absr, ACT.Sin, scale=-1.0, bias=c.w("half_pi")).then_inc(c.aux_s.sem, 1)
            act.wait_ge(c.aux_s.sem, c.aux_s.at(1))
            ch.clear()
    c.aux_v.advance(1)
    c.aux_s.advance(1)


def layer2_attention(c):
    nc = c.nc
    H, D = 8, 16
    load_stage(c, "L2", c.dram)
    norm_stage(c, c.X, c.HN, "eps5")
    trig = c.T[:, 3, 0:2 * S].rearrange("p (t s) -> p t s", s=S)
    wide_a = Arena(c)
    wide_a.off = 6 * 2 * S
    k0, k1, u = wide_a.take(N), wide_a.take(N), wide_a.take(N)
    q0, q1 = c.T[:, 0, :], c.T[:, 1, :]
    trig_stage(c, trig)
    wq, wk = c.w("L2a_wq"), c.w("L2a_wk")
    bq, bk = c.w("L2a_bq"), c.w("L2a_bk")
    jobs = [([c.HN], [w[:, t, :]], bb[:, t:t + 1], ACT.Silu, dst, None)
            for w, bb, ds in ((wq, bq, (q0, q1)), (wk, bk, (k0, k1))) for t, dst in enumerate(ds)]
    jobs.append(([c.HN], [c.w("L2a_wu")], c.w("L2a_bu"), None, u, None))
    project_stage(c, jobs)

    a = Arena(c)
    a.off = 0
    vsb, vb, otok = a.take(S), a.take(2, P), a.take(2, P)
    es = a.take(8)
    assert a.off <= 6 * 2 * S
    a.off = wide_a.off
    decay = a.take(H, 2 * S)
    qk = c.T[:, 2, :].rearrange("p (t s) -> p t s", s=S)
    qb, kb = qk[:, 0:2, :], qk[:, 2:4, :]
    en = c.T[:, 3, 2 * S:2 * S + 1536].rearrange("p (r x) -> p r x", r=3)
    ident = c.w("identity")
    del es
    with nc.Block() as block:
        @block.gpsimd
        def _(pool):
            with pool.Fori(0, B) as b:
                pool.wait_ge(c.out_turned.sem, c.out_turned.base + b)
                nc.gpsimd.tensor_copy(vsb, c.HN[:, bass.ds(b * S, S)]).then_inc(c.staged.sem, 1)
                for t, q in enumerate((q0, q1)):
                    ins = nc.gpsimd.tensor_tensor(qb[:, t, :], q[:, bass.ds(b * S, S)], trig[:, t, :], ALU.mult)
                ins.then_inc(c.aux_p.sem, 1)

        @block.tensor
        def _(pe):
            with pe.Fori(0, B) as b:
                pe.wait_ge(c.staged.sem, c.staged.base + b + 1)
                for kt in range(2):
                    mm = nc.tensor.matmul(c.psum[:, 7, kt * P:(kt + 1) * P], vsb[:, kt * P:(kt + 1) * P],
                                          c.w("L2a_wv"), start=True, stop=True)
                mm.then_inc(c.proj_ready.sem, 1)
                pe.wait_ge(c.aux_p.sem, c.aux_p.base + b + 1)
                pe.wait_ge(c.aux_v.sem, c.aux_v.base + b + 1)
                pe.wait_ge(c.proj_taken_v.sem, c.proj_taken_v.base + b + 1)
                for h in range(H + 1):
                    if h < H:
                        if h >= 4:
                            pe.wait_ge(c.aux_v2.sem, c.aux_v2.base + b * H + h - 3)
                        t, base = h // 4, (h % 4) * 32
                        for mt in range(2):
                            mm = nc.tensor.matmul(c.psum[:, h % 4, mt * S:(mt + 1) * S],
                                                  kb[base:base + 32, t, mt * P:(mt + 1) * P],
                                                  qb[base:base + 32, t, :], start=True, stop=True,
                                                  tile_position=(base, 0))
                        mm.then_inc(c.scores_ready.sem, 1)
                    if h >= 1:
                        k = h - 1
                        pe.wait_ge(c.aux_v2.sem, c.aux_v2.base + b * H + k + 1)
                        for nt in range(2):
                            for mt in range(2):
                                mm = nc.tensor.matmul(c.psum[:, 6, nt * P + k * D:nt * P + (k + 1) * D],
                                                      en[:, k % 3, mt * S + nt * P:mt * S + (nt + 1) * P],
                                                      vb[:, mt, k * D:(k + 1) * D], start=(mt == 0), stop=(mt == 1))
                        mm.then_inc(c.mixed_ready.sem, 1)
                pe.wait_ge(c.mixed_taken.sem, c.mixed_taken.base + b + 1)
                for nt in range(2):
                    mm = nc.tensor.transpose(c.psum[:, 5, nt * P:(nt + 1) * P], otok[:, nt, :], ident)
                mm.then_inc(c.out_turned.sem, 1)

        @block.scalar
        def _(act):
            for h in range(H):
                ins = nc.scalar.activation(decay[:, h, :], c.w("L2a_lower").rearrange("p t s -> p (t s)"), ACT.Exp,
                                           scale=c.w("L2a_slope")[:, h:h + 1])
            ins.then_inc(c.aux_s.sem, 1)
            with act.Fori(0, B) as b:
                act.wait_ge(c.mixed_ready.sem, c.mixed_ready.base + (b + 1) * H)
                nc.scalar.copy(otok, c.psum[:, 6, 0:S].rearrange("p (t x) -> p t x", x=P)) \
                    .then_inc(c.mixed_taken.sem, 1)
                act.wait_ge(c.out_turned.sem, c.out_turned.base + b + 1)
                nc.scalar.copy(q0[:, bass.ds(b * S, S)], c.psum[:, 5, 0:S]).then_inc(c.out_copied.sem, 1)

        @block.vector
        def _(dve):
            dve.wait_ge(c.aux_s.sem, c.aux_s.at(1))
            with dve.Fori(0, B) as b:
                dve.wait_ge(c.out_turned.sem, c.out_turned.base + b)
                for t, k in enumerate((k0, k1)):
                    ins = nc.vector.tensor_tensor(kb[:, t, :], k[:, bass.ds(b * S, S)], trig[:, t, :], ALU.mult)
                ins.then_inc(c.aux_v.sem, 1)
                dve.wait_ge(c.proj_ready.sem, c.proj_ready.base + b + 1)
                nc.vector.tensor_tensor(vb, c.psum[:, 7, 0:S].rearrange("p (t x) -> p t x", x=P),
                                        c.w("L2a_bv").unsqueeze(1).broadcast_to([P, 2, P]), ALU.add) \
                    .then_inc(c.proj_taken_v.sem, 1)
                for h in range(H):
                    dve.wait_ge(c.scores_ready.sem, c.scores_ready.base + b * H + h + 1)
                    if h >= 3:
                        dve.wait_ge(c.mixed_ready.sem, c.mixed_ready.base + b * H + h - 2)
                    nc.vector.tensor_tensor(en[:, h % 3, :], c.psum[:, h % 4, :], decay[:, h, :], ALU.mult) \
                        .then_inc(c.aux_v2.sem, 1)
    for s, n in ((c.staged, 1), (c.aux_p, 1), (c.proj_ready, 1), (c.aux_v, 1), (c.proj_taken_v, 1), (c.aux_v2, H),
                 (c.scores_ready, H), (c.mixed_ready, H), (c.mixed_taken, 1), (c.out_turned, 1), (c.out_copied, 1)):
        s.advance(B * n)
    c.aux_s.advance(1)
    with nc.Block() as block:
        @block.vector
        def _(dve):
            nc.vector.tensor_copy(c.T[:, 1, :], u)
    norm_stage(c, q0, q0, "eps6", centre=False)
    with nc.Block() as block:
        @block.vector
        def _(dve):
            nc.vector.tensor_tensor(c.T[:, 0, :], c.T[:, 0, :], c.T[:, 1, :], ALU.mult)
    project_stage(c, [([q0], [c.w("L2a_wo")], c.w("L2a_bo"), None, c.X, c.X)])


def layer2_cross(c):
    nc = c.nc
    norm_stage(c, c.X, c.HN, "eps5")
    one_plus = c.w("L2x_scale")
    with nc.Block() as block:
        @block.vector
        def _(dve):
            nc.vector.tensor_scalar(one_plus, one_plus, 1.0, None, ALU.add)
    norm_stage(c, c.HN, c.HN, "eps6", centre=False, gain=one_plus)
    norm_stage(c, c.CT, c.T[:, 3, :], "eps6", centre=False, gain=one_plus)
    for src, name, dst in ((c.HN, "q", c.T[:, 0, :]), (c.T[:, 3, :], "k", c.T[:, 1, :])):
        swapped = c.T[:, 2, :]
        project_stage(c, [([src], [c.w(f"L2x_w{name}")], None, None, dst, None),
                          ([src], [c.w(f"L2x_w{name}_swapped")], None, None, swapped, None)])
        cos = c.w(f"L2x_cos_{name}").unsqueeze(1).broadcast_to([P, B, S])
        sin = c.w(f"L2x_sin_{name}").unsqueeze(1).broadcast_to([P, B, S])
        with nc.Block() as block:
            @block.vector
            def _(dve):
                d3, s3 = (x.rearrange("p (b s) -> p b s", s=S) for x in (dst, swapped))
                nc.vector.tensor_tensor(d3, d3, cos, ALU.mult).then_inc(c.aux_v.sem, 1)
                dve.wait_ge(c.aux_p.sem, c.aux_p.at(1))
                dve.wait_ge(c.aux_v.sem, c.aux_v.at(1))
                nc.vector.tensor_tensor(d3, d3, s3, ALU.add)

            @block.gpsimd
            def _(pool):
                s3 = swapped.rearrange("p (b s) -> p b s", s=S)
                nc.gpsimd.tensor_tensor(s3, s3, sin, ALU.mult).then_inc(c.aux_p.sem, 1)
        c.aux_v.advance(1)
        c.aux_p.advance(1)
    fill = 2.3819763e38
    madd = c.T[:, 2, :]
    with nc.Block() as block:
        @block.vector
        def _(dve):
            nc.vector.tensor_copy(madd, c.attend[:, :].bitcast(U8)).then_inc(c.aux_v.sem, 1)
            dve.wait_ge(c.aux_v.sem, c.aux_v.at(1))
            nc.vector.tensor_scalar(madd, madd, 1.0, fill, ALU.subtract, ALU.mult)
    c.aux_v.advance(1)

    def prepare(nc, dve, chain, b, mb):
        chain.link(nc.vector.tensor_copy(mb, madd[:, bass.ds(b * S, S)]))

    ident = c.w("identity")
    attention_stage(c, 4, 32, c.T[:, 0, :], c.T[:, 1, :], c.T[:, 3, :], [ident], None, [ident], None,
                    c.w("L2x_wv"), None, [c.w("L2x_wo")], None, scale=float(32 ** -0.5),
                    mask=lambda mb, h, qt: mb, prepare_mask=prepare, mask_words=S, shared_kv=True)


MAGIC = 1.5 * 2.0 ** 23


def layer2_mlp(c):
    nc = c.nc
    I = 352
    rows = [P, P, I - 2 * P]
    norm_stage(c, c.X, c.HN, "eps5")
    a = Arena(c)
    xq, hq = a.take(N // 2).bitcast(BF16), [a.take(N // 2).bitcast(BF16) for _ in range(3)]
    w_int = a.take(9, P)
    w_bf = a.take(9, P // 2).bitcast(BF16)
    w_t = a.take(9, P // 2).bitcast(BF16)
    ident = a.take(P // 2).bitcast(BF16)
    amax, ws, wr = a.take(8), a.take(9), a.take(9)
    xs, part = a.take(4), a.take(2, CH)
    peak = a.take(16)
    tmp = a.take(N)
    wg, wu, wd = c.w("L2f_gate"), c.w("L2f_up"), c.w("L2f_down")
    blocks = [(wg[0:rows[t], t, :], rows[t], 0 + t) for t in range(3)] + \
             [(wu[0:rows[t], t, :], rows[t], 3 + t) for t in range(3)]
    sigm = c.w("L2f_clips")

    with nc.Block() as block:
        @block.scalar
        def _(act):
            nc.scalar.activation(sigm, sigm, ACT.Sigmoid).then_inc(c.aux_s.sem, 1)
            nc.scalar.copy(ident, c.w("identity"))

        @block.gpsimd
        def _(pool):
            pool.wait_ge(c.aux_v.sem, c.aux_v.at(1))
            nc.gpsimd.partition_all_reduce(amax[:, 1:2], amax[:, 0:1], P, bass.bass_isa.ReduceOp.max) \
                .then_inc(c.aux_p.sem, 1)

        @block.vector
        def _(dve):
            ch = Chain(dve, c.vector_chain)
            v = nc.vector
            v.tensor_reduce(amax[:, 0:1], c.HN[:, :], AX.X, ALU.max, apply_absolute_value=True) \
                .then_inc(c.aux_v.sem, 1)
            ch.link(v.memset(ws, 127.0))
            for src, n, i in blocks:
                ch.link(v.tensor_reduce(ws[0:n, i:i + 1], src, AX.X, ALU.max, apply_absolute_value=True))
            ch.link(v.tensor_reduce(ws[:, 6:7], wd, AX.X, ALU.max, apply_absolute_value=True))
            ch.link(v.tensor_scalar(ws, ws, float(1.0 / 127.0), None, ALU.mult))
            ch.link(v.reciprocal(wr, ws))
            for src, n, i in blocks:
                ch.link(v.tensor_scalar(w_int[0:n, i, :], src, wr[0:n, i:i + 1], MAGIC, ALU.mult, ALU.add))
            for i in range(3):
                ch.link(v.tensor_scalar(w_int[:, 6 + i, 0:rows[i]], wd[:, i * P:i * P + rows[i]], wr[:, 6:7], MAGIC,
                                        ALU.mult, ALU.add))
            for lo, hi, r in ((0, 2, P), (2, 3, rows[2]), (3, 5, P), (5, 6, rows[2])):
                w = w_int[0:r, lo:hi, :]
                ch.link(v.tensor_scalar(w, w, MAGIC, 127.0, ALU.subtract, ALU.min))
                ch.link(v.tensor_scalar(w_bf[0:r, lo:hi, :], w, -128.0, None, ALU.max))
            for i in range(3):
                w = w_int[:, 6 + i, 0:rows[i]]
                ch.link(v.tensor_scalar(w, w, MAGIC, 127.0, ALU.subtract, ALU.min))
                ch.link(v.tensor_scalar(w_bf[:, 6 + i, 0:rows[i]], w, -128.0, None, ALU.max))
            dve.wait_ge(c.aux_p.sem, c.aux_p.at(1))
            dve.wait_ge(c.aux_s.sem, c.aux_s.at(1))
            ch.link(v.tensor_tensor(xs[:, 1:2], amax[:, 1:2], sigm[:, 0:1], ALU.mult))
            ch.link(v.tensor_scalar(xs[:, 0:1], xs[:, 1:2], float(1.0 / 127.0), None, ALU.mult))
            ch.link(v.reciprocal(xs[:, 1:2], xs[:, 0:1]))
            ch.link(v.tensor_scalar(tmp, c.HN[:, :], xs[:, 1:2], MAGIC, ALU.mult, ALU.add))
            ch.link(v.tensor_scalar(tmp, tmp, MAGIC, 127.0, ALU.subtract, ALU.min))
            ch.link(v.tensor_scalar(xq, tmp, -128.0, None, ALU.max))
            ch.link(v.tensor_scalar(ws[:, 0:6], ws[:, 0:6], xs[:, 0:1], None, ALU.mult))
            ch.clear()
    c.aux_v.advance(1)
    c.aux_p.advance(1)
    c.aux_s.advance(1)

    turned = c.psum[:, 0:4, :].rearrange("p a x -> p (a x)").bitcast(BF16)
    order = [(i, (rows[i % 3] if i < 6 else P), (P if i < 6 else rows[i - 6])) for i in range(9)]
    with nc.Block() as block:
        @block.tensor
        def _(pe):
            for i, r, m in order:
                mm = nc.tensor.transpose(turned[0:m, i * P:i * P + r], w_bf[0:r, i, 0:m], ident[0:r, 0:r])
            mm.then_inc(c.aux_pe.sem, 1)

        @block.vector
        def _(dve):
            dve.wait_ge(c.aux_pe.sem, c.aux_pe.at(1))
            for i, r, m in order:
                nc.vector.tensor_copy(w_t[0:m, i, 0:r], turned[0:m, i * P:i * P + r])
    c.aux_pe.advance(1)

    units = [(i, t) for i in range(NC) for t in range(3)]
    hidden = [c.T[:, t, :] for t in range(3)]
    with nc.Block() as block:
        @block.tensor
        def _(pe):
            for n, (i, t) in enumerate(units):
                if n >= 4:
                    pe.wait_ge(c.aux_v.sem, c.aux_v.at(n - 3))
                for g in range(2):
                    mm = nc.tensor.matmul(c.psum[0:rows[t], 2 * (n % 4) + g, :], w_t[:, 3 * g + t, 0:rows[t]],
                                          xq[:, i * CH:(i + 1) * CH], start=True, stop=True)
                mm.then_inc(c.aux_pe.sem, 1)

        @block.scalar
        def _(act):
            for n, (i, t) in enumerate(units):
                act.wait_ge(c.aux_pe.sem, c.aux_pe.at(n + 1))
                if n >= 2:
                    act.wait_ge(c.aux_v.sem, c.aux_v.at(n - 1))
                nc.scalar.activation(part[0:rows[t], n % 2, :], c.psum[0:rows[t], 2 * (n % 4), :], ACT.Silu,
                                     scale=ws[0:rows[t], t:t + 1]).then_inc(c.aux_s.sem, 1)

        @block.vector
        def _(dve):
            for n, (i, t) in enumerate(units):
                dve.wait_ge(c.aux_s.sem, c.aux_s.at(n + 1))
                nc.vector.scalar_tensor_tensor(hidden[t][0:rows[t], i * CH:(i + 1) * CH],
                                               c.psum[0:rows[t], 2 * (n % 4) + 1, :], ws[0:rows[t], 3 + t:4 + t],
                                               part[0:rows[t], n % 2, :], ALU.mult, ALU.mult) \
                    .then_inc(c.aux_v.sem, 1)
    for s in (c.aux_pe, c.aux_s, c.aux_v):
        s.advance(len(units))

    with nc.Block() as block:
        @block.vector
        def _(dve):
            ch = Chain(dve, c.vector_chain)
            v = nc.vector
            ch.link(v.memset(peak[:, 0:4], 0.0))
            for t in range(3):
                ch.link(v.tensor_reduce(peak[0:rows[t], t:t + 1], hidden[t][0:rows[t], :], AX.X, ALU.max,
                                        apply_absolute_value=True))
            v.reduce_max(amax[:, 2:3], peak[:, 0:3], AX.X).then_inc(c.aux_v.sem, 1)
            dve.wait_ge(c.aux_p.sem, c.aux_p.at(1))
            ch.link(v.tensor_tensor(xs[:, 2:3], amax[:, 3:4], sigm[:, 1:2], ALU.mult))
            ch.link(v.tensor_scalar(xs[:, 3:4], xs[:, 2:3], float(1.0 / 127.0), None, ALU.mult))
            ch.link(v.reciprocal(xs[:, 2:3], xs[:, 3:4]))
            ch.link(v.tensor_scalar(ws[:, 7:8], ws[:, 6:7], xs[:, 3:4], None, ALU.mult))
            for t in range(3):
                h = hidden[t][0:rows[t], :]
                ch.link(v.tensor_scalar(h, h, xs[0:rows[t], 2:3], MAGIC, ALU.mult, ALU.add))
                ch.link(v.tensor_scalar(h, h, MAGIC, 127.0, ALU.subtract, ALU.min))
                ch.link(v.tensor_scalar(hq[t][0:rows[t], :], h, -128.0, None, ALU.max))
            ch.clear()

        @block.gpsimd
        def _(pool):
            pool.wait_ge(c.aux_v.sem, c.aux_v.at(1))
            nc.gpsimd.partition_all_reduce(amax[:, 3:4], amax[:, 2:3], P, bass.bass_isa.ReduceOp.max) \
                .then_inc(c.aux_p.sem, 1)
    c.aux_v.advance(1)
    c.aux_p.advance(1)

    with nc.Block() as block:
        @block.tensor
        def _(pe):
            for i in range(NC):
                for t in range(3):
                    mm = nc.tensor.matmul(c.psum[:, i, :], w_t[0:rows[t], 6 + t, :],
                                          hq[t][0:rows[t], i * CH:(i + 1) * CH], start=(t == 0), stop=(t == 2))
                mm.then_inc(c.aux_pe.sem, 1)

        @block.vector
        def _(dve):
            for i in range(NC):
                dve.wait_ge(c.aux_pe.sem, c.aux_pe.at(i + 1))
                x = c.X[:, i * CH:(i + 1) * CH]
                nc.vector.scalar_tensor_tensor(x, c.psum[:, i, :], ws[:, 7:8], x, ALU.mult, ALU.add)
    c.aux_pe.advance(NC)



def layer3_attention(c):
    load_stage(c, "L3", c.dram)
    norm_stage(c, c.X, c.HN, "eps5")
    wq, wk = c.w("L3a_wq"), c.w("L3a_wk")
    attention_stage(c, 16, 8, c.HN, c.HN, c.HN, [wq[:, t, :] for t in range(4)], c.w("L3a_bq"),
                    [wk[:, t, :] for t in range(4)], c.w("L3a_bk"), c.w("L3a_wv"), c.w("L3a_bv"), [c.w("L3a_wo")],
                    c.w("L3a_bo"), scale=float(8 ** -0.5), top=32)


def layer3_cross(c):
    nc = c.nc
    H, D = 16, 8
    J = S // H
    norm_stage(c, c.X, c.HN, "eps5")
    q, k = c.T[:, 0, :], c.T[:, 1, :]
    project_stage(c, [([c.HN], [c.w("L3x_wq")], c.w("L3x_bq"), None, q, None),
                      ([c.CT], [c.w("L3x_wk")], c.w("L3x_bk"), None, k, None)])
    a = Arena(c)
    qb, kb, ctx_b = a.take(S), a.take(S), a.take(S)
    vb, probs, ex, turned = a.take(2, P), a.take(2, S), a.take(2, S), a.take(2, S)
    m, r = a.take(2, H), a.take(2, H)
    ident, kmask, vmask = c.w("identity"), c.w("L3x_kmask"), c.w("L3x_vmask")
    scale = float(D ** -0.5)

    def by_head(x):
        return x.rearrange("p (j h) -> p h j", h=H)

    def over(x):
        return x.unsqueeze(1).broadcast_to([P, J, H])

    with nc.Block() as block:
        @block.gpsimd
        def _(pool):
            with pool.Fori(0, B) as b:
                pool.wait_ge(c.mixed_ready.sem, c.mixed_ready.base + b)
                nc.gpsimd.tensor_copy(qb, q[:, bass.ds(b * S, S)])
                nc.gpsimd.tensor_tensor(kb, k[:, bass.ds(b * S, S)], kmask, ALU.mult)
                nc.gpsimd.tensor_copy(ctx_b, c.CT[:, bass.ds(b * S, S)]).then_inc(c.staged.sem, 1)

        @block.tensor
        def _(pe):
            with pe.Fori(0, B) as b:
                pe.wait_ge(c.staged.sem, c.staged.base + b + 1)
                for t in range(2):
                    nc.tensor.matmul(c.psum[:, t, 0:S], qb[:, t * P:(t + 1) * P], kb, start=True, stop=True) \
                        .then_inc(c.scores_ready.sem, 1)
                for t in range(2):
                    mm = nc.tensor.matmul(c.psum[:, 2, t * P:(t + 1) * P], ctx_b[:, t * P:(t + 1) * P],
                                          c.w("L3x_wv"), start=True, stop=True)
                mm.then_inc(c.proj_ready.sem, 1)
                for t in range(2):
                    pe.wait_ge(c.probs_picked.sem, c.probs_picked.base + 2 * b + t + 1)
                    for s in range(2):
                        mm = nc.tensor.transpose(c.psum[:, 3 + s, t * P:(t + 1) * P], probs[:, t, s * P:(s + 1) * P],
                                                 ident)
                mm.then_inc(c.probs_turned.sem, 1)
                pe.wait_ge(c.turned_copied.sem, c.turned_copied.base + 2 * b + 2)
                for s in range(2):
                    mm = nc.tensor.matmul(c.psum[:, 5, 0:S], vb[:, s, :], turned[:, s, :], start=(s == 0),
                                          stop=(s == 1))
                mm.then_inc(c.mixed_ready.sem, 1)

        @block.scalar
        def _(act):
            with act.Fori(0, B) as b:
                for t in range(2):
                    act.wait_ge(c.scores_max.sem, c.scores_max.base + 2 * b + t + 1)
                    nc.scalar.activation(ex[:, t, :], probs[:, t, :], ACT.Exp, scale=scale) \
                        .then_inc(c.probs_ready.sem, 1)
                act.wait_ge(c.probs_turned.sem, c.probs_turned.base + b + 1)
                for s in range(2):
                    nc.scalar.copy(turned[:, s, :], c.psum[:, 3 + s, 0:S]).then_inc(c.turned_copied.sem, 1)
                act.wait_ge(c.mixed_ready.sem, c.mixed_ready.base + b + 1)
                nc.scalar.copy(q[:, bass.ds(b * S, S)], c.psum[:, 5, 0:S]).then_inc(c.mixed_taken.sem, 1)

        @block.vector
        def _(dve):
            chain = Chain(dve, c.vector_chain)
            v = nc.vector
            with dve.Fori(0, B) as b:
                for t in range(2):
                    dve.wait_ge(c.scores_ready.sem, c.scores_ready.base + 2 * b + t + 1)
                    chain.link(v.reduce_max(m[:, t, :], by_head(c.psum[:, t, 0:S]), AX.X))
                    v.tensor_tensor(probs[:, t, :].rearrange("p (j h) -> p j h", h=H),
                                    c.psum[:, t, 0:S].rearrange("p (j h) -> p j h", h=H), over(m[:, t, :]),
                                    ALU.subtract).then_inc(c.scores_max.sem, 1)
                dve.wait_ge(c.proj_ready.sem, c.proj_ready.base + b + 1)
                chain.link(v.tensor_tensor(vb, c.psum[:, 2, 0:S].rearrange("p (t x) -> p t x", x=P),
                                           c.w("L3x_bv").unsqueeze(1).broadcast_to([P, 2, P]), ALU.add))
                chain.link(v.tensor_tensor(vb, vb, vmask.unsqueeze(1).broadcast_to([P, 2, P]), ALU.mult))
                for t in range(2):
                    dve.wait_ge(c.probs_ready.sem, c.probs_ready.base + 2 * b + t + 1)
                    chain.link(v.reduce_sum(r[:, t, :], by_head(ex[:, t, :]), AX.X))
                    chain.link(v.reciprocal(r[:, t, :], r[:, t, :]))
                    v.tensor_tensor(probs[:, t, :].rearrange("p (j h) -> p j h", h=H),
                                    ex[:, t, :].rearrange("p (j h) -> p j h", h=H), over(r[:, t, :]),
                                    ALU.mult).then_inc(c.probs_picked.sem, 1)
                chain.clear()
    for s, n in ((c.staged, 1), (c.scores_ready, 2), (c.scores_max, 2), (c.probs_ready, 2), (c.probs_picked, 2),
                 (c.proj_ready, 1), (c.probs_turned, 1), (c.turned_copied, 2), (c.mixed_ready, 1),
                 (c.mixed_taken, 1)):
        s.advance(B * n)
    project_stage(c, [([q], [c.w("L3x_wo")], c.w("L3x_bo"), None, c.X, c.X)])


def position_attention(c, q, k, v, out, scale):
    nc = c.nc
    a = Arena(c)
    prod, less, ex = a.take(N), a.take(N), a.take(N)
    m, total, mix = a.take(S), a.take(S), a.take(S)
    scores = c.psum[:, 0:4, :].rearrange("p a x -> p (a x)")
    half = N // 2

    def grid(x):
        return x.rearrange("p (m n) -> p m n", n=S)

    def last(x):
        return x.rearrange("p (m n) -> p n m", n=S)

    with nc.Block() as block:
        @block.gpsimd
        def _(pool):
            with pool.Fori(0, B) as l:
                pool.wait_ge(c.aux_pe.sem, c.aux_pe.base + l)
                nc.gpsimd.tensor_tensor(grid(prod)[:, 0:3], grid(k)[:, 0:3],
                                        q[:, bass.ds(l * S, S)].unsqueeze(1).broadcast_to([P, 3, S]), ALU.mult) \
                    .then_inc(c.aux_p.sem, 1)
                pool.wait_ge(c.aux_v2.sem, c.aux_v2.base + l + 1)
                nc.gpsimd.tensor_tensor(ex, ex, v, ALU.mult).then_inc(c.aux_p2.sem, 1)

        @block.tensor
        def _(pe):
            with pe.Fori(0, B) as l:
                pe.wait_ge(c.aux_p.sem, c.aux_p.base + l + 1)
                pe.wait_ge(c.aux_v.sem, c.aux_v.base + l + 1)
                for i in range(NC):
                    mm = nc.tensor.matmul(c.psum[:, i, :], c.w("L3f_heads"), prod[:, i * CH:(i + 1) * CH],
                                          start=True, stop=True)
                mm.then_inc(c.aux_pe.sem, 1)

        @block.scalar
        def _(act):
            with act.Fori(0, B) as l:
                act.wait_ge(c.aux_v3.sem, c.aux_v3.base + l + 1)
                nc.scalar.activation(ex, less, ACT.Exp, scale=scale).then_inc(c.aux_s.sem, 1)

        @block.vector
        def _(dve):
            chain = Chain(dve, c.vector_chain)
            with dve.Fori(0, B) as l:
                nc.vector.tensor_tensor(grid(prod)[:, 3:8], grid(k)[:, 3:8],
                                        q[:, bass.ds(l * S, S)].unsqueeze(1).broadcast_to([P, 5, S]), ALU.mult) \
                    .then_inc(c.aux_v.sem, 1)
                dve.wait_ge(c.aux_pe.sem, c.aux_pe.base + l + 1)
                chain.link(nc.vector.reduce_max(m, last(scores), AX.X))
                nc.vector.tensor_tensor(grid(less), grid(scores), m.unsqueeze(1).broadcast_to([P, B, S]),
                                        ALU.subtract).then_inc(c.aux_v3.sem, 1)
                dve.wait_ge(c.aux_s.sem, c.aux_s.base + l + 1)
                nc.vector.reduce_sum(total, last(ex), AX.X).then_inc(c.aux_v2.sem, 1)
                dve.wait_ge(c.aux_v2.sem, c.aux_v2.base + l + 1)
                chain.link(nc.vector.reciprocal(total, total))
                dve.wait_ge(c.aux_p2.sem, c.aux_p2.base + l + 1)
                chain.link(nc.vector.reduce_sum(mix, last(ex), AX.X))
                chain.link(nc.vector.tensor_tensor(out[:, bass.ds(l * S, S)], mix, total, ALU.mult))
                chain.clear()
    for s in (c.aux_pe, c.aux_p, c.aux_p2, c.aux_v, c.aux_v2, c.aux_v3, c.aux_s):
        s.advance(B)
    del half


def layer3_block(c):
    nc = c.nc
    norm_stage(c, c.X, c.HN, "eps5")
    q, k, v, o = (c.T[:, i, :] for i in range(4))
    w, bias = c.w("L3f_win"), c.w("L3f_bin")
    project_stage(c, [([c.HN], [w[:, i * P:(i + 1) * P]], bias[:, i:i + 1], None, dst, None)
                      for i, dst in enumerate((q, k, v))])
    position_attention(c, q, k, v, o, float(32 ** -0.5))
    project_stage(c, [([o], [c.w("L3f_wout")], c.w("L3f_bout"), None, c.HN, c.HN)])
    norm_stage(c, c.HN, c.HN, "eps5", gain=c.w("L3f_g1"), shift=c.w("L3f_h1"))

    a = Arena(c)
    w_t = a.take(N)
    both = a.take(E, P)
    b_col, b_row = a.take(P), a.take(P)
    w1, w2, b1, b2 = c.w("L3f_w1"), c.w("L3f_w2"), c.w("L3f_b1"), c.w("L3f_b2")
    with nc.Block() as block:
        @block.tensor
        def _(pe):
            for e in range(E):
                for f in range(4):
                    mm = nc.tensor.matmul(c.psum[:, e // 4, (e % 4) * P:(e % 4 + 1) * P], w1[:, e, f, :],
                                          w2[:, e, f, :], start=(f == 0), stop=(f == 3))
            mm.then_inc(c.aux_pe.sem, 1)
            for e in range(E):
                for f in range(4):
                    mm = nc.tensor.matmul(c.psum[:, 2, e:e + 1], w2[:, e, f, :], b1[:, e, f:f + 1],
                                          start=(f == 0), stop=(f == 3))
            mm.then_inc(c.aux_pe.sem, 1)
            pe.wait_ge(c.aux_v.sem, c.aux_v.at(2))
            nc.tensor.transpose(c.psum[:, 3, 0:P], b_col, c.w("identity")).then_inc(c.aux_pe.sem, 1)

        @block.scalar
        def _(act):
            act.wait_ge(c.aux_pe.sem, c.aux_pe.at(1))
            nc.scalar.copy(both, c.psum[:, 0:2, :].rearrange("p a (e x) -> p (a e) x", x=P))

        @block.vector
        def _(dve):
            nc.vector.memset(b_col, 0.0).then_inc(c.aux_v.sem, 1)
            dve.wait_ge(c.aux_v.sem, c.aux_v.at(1))
            dve.wait_ge(c.aux_pe.sem, c.aux_pe.at(2))
            nc.vector.tensor_tensor(b_col[:, 0:E], c.psum[:, 2, 0:E], b2, ALU.add).then_inc(c.aux_v.sem, 1)
            dve.wait_ge(c.aux_pe.sem, c.aux_pe.at(3))
            nc.vector.tensor_copy(b_row, c.psum[:, 3, 0:P])
    c.aux_pe.advance(3)
    c.aux_v.advance(2)
    route_stage(c, c.HN, c.w("L3f_wg"), None, w_t, a, "single", capacity=N // E)

    a2 = Arena(c)
    a2.off = a.off
    xe = a2.take(4, CH)
    pick = c.w("pick")
    units = [(i, e) for i in range(NC) for e in range(E)]
    with nc.Block() as block:
        @block.tensor
        def _(pe):
            def spread(n):
                i, e = units[n]
                if n >= 3:
                    pe.wait_ge(c.aux_v.sem, c.aux_v.at(n - 2))
                nc.tensor.matmul(c.psum[:, n % 3, :], pick[:, e, :], w_t[:, i * CH:(i + 1) * CH], start=True,
                                 stop=True).then_inc(c.aux_pe.sem, 1)

            spread(0)
            spread(1)
            for n, (i, e) in enumerate(units):
                if n + 2 < len(units):
                    spread(n + 2)
                pe.wait_ge(c.aux_v.sem, c.aux_v.at(n + 1))
                nc.tensor.matmul(c.psum[:, 4 + i, :], both[:, e, :], xe[:, n % 4, :], start=(e == 0), stop=False) \
                    .then_inc(c.aux_pe2.sem, 1)
                if e == E - 1:
                    nc.tensor.matmul(c.psum[:, 4 + i, :], b_row, w_t[:, i * CH:(i + 1) * CH], start=False,
                                     stop=True).then_inc(c.aux_pe3.sem, 1)

        @block.vector
        def _(dve):
            for n, (i, e) in enumerate(units):
                dve.wait_ge(c.aux_pe.sem, c.aux_pe.at(n + 1))
                if n >= 4:
                    dve.wait_ge(c.aux_pe2.sem, c.aux_pe2.at(n - 3))
                nc.vector.tensor_tensor(xe[:, n % 4, :], c.HN[:, i * CH:(i + 1) * CH], c.psum[:, n % 3, :],
                                        ALU.mult).then_inc(c.aux_v.sem, 1)
            dve.wait_ge(c.aux_v.sem, c.aux_v.at(len(units)))
            for i in range(NC):
                dve.wait_ge(c.aux_pe3.sem, c.aux_pe3.at(i + 1))
                x = c.HN[:, i * CH:(i + 1) * CH]
                nc.vector.tensor_tensor(x, x, c.psum[:, 4 + i, :], ALU.add)
    for s, n in ((c.aux_pe, len(units)), (c.aux_pe2, len(units)), (c.aux_pe3, NC), (c.aux_v, len(units))):
        s.advance(n)
    norm_stage(c, c.HN, c.HN, "eps5", gain=c.w("L3f_g2"), shift=c.w("L3f_h2"))
    add_stage(c, c.X, c.X, c.HN)



class Layout:

    def __init__(self):
        self.parts, self.slots, self.words = {}, {}, {}

    def add(self, pack, name, array):
        array = np.ascontiguousarray(array)
        if array.ndim == 1:
            array = array.reshape(array.shape[0], 1)
        assert array.shape[0] == P, (name, array.shape)
        off = self.words.get(pack, 0)
        flat = array.reshape(P, -1)
        self.parts.setdefault(pack, []).append(flat)
        self.slots[name] = (pack, off, array.shape)
        self.words[pack] = off + flat.shape[1]

    def packed(self):
        return {k: np.ascontiguousarray(np.concatenate(v, axis=1)) for k, v in self.parts.items()}


def columns(v):
    return v.reshape(-1, P).T


def everywhere(v):
    return np.broadcast_to(v.reshape(1, -1), (P, v.size))


def k_tiles(w):
    return w.reshape(-1, P, w.shape[1]).transpose(1, 0, 2)


def padded_heads(w_t):
    out = np.zeros((w_t.shape[0], 4, 4, 32), np.float32)
    out[:, :, :, 0:8] = w_t.reshape(w_t.shape[0], 4, 4, 8)
    return out.reshape(w_t.shape[0], 4, P)


def feature_major(x):
    return np.ascontiguousarray(x.reshape(N, P).T)


def top_rows(w):
    out = np.zeros((P, w.shape[1]), np.float32)
    out[0:w.shape[0]] = w
    return out


def row_tiles(w):
    n = -(-w.shape[0] // P)
    out = np.zeros((n * P, w.shape[1]), np.float32)
    out[0:w.shape[0]] = w
    return out.reshape(n, P, -1).transpose(1, 0, 2)


def lay_out(a):
    L = Layout()
    sm = "small"
    L.add(sm, "average", np.full((P, P), 1.0 / P, np.float32))
    L.add(sm, "ones", np.ones((P, P), np.float32))
    L.add(sm, "one", np.ones((P, 1), np.float32))
    for name, eps in (("eps5", 1e-5), ("eps6", 1e-6), ("eps12", 1e-12), ("epsf", float(np.finfo(np.float32).eps))):
        L.add(sm, name, np.full((P, 1), eps, np.float32))
    L.add(sm, "identity", np.eye(P, dtype=np.float32))
    L.add("L0", "pad8", padded_heads(np.eye(P, dtype=np.float32)))
    for s in "qkv":
        L.add("L0", f"L0a_g{s}", a[f"L0_attn_ln_{s}_g"])
        L.add("L0", f"L0a_h{s}", a[f"L0_attn_ln_{s}_b"])
        L.add("L0", f"L0a_w{s}", a[f"L0_attn_{s}_w"].T)
    L.add("L0", "L0a_bq", a["L0_attn_q_b"])
    L.add("L0", "L0a_bk", a["L0_attn_k_b"])
    L.add("L0", "L0a_bv", everywhere(a["L0_attn_v_b"]))
    L.add("L0", "L0a_beta", everywhere(a["L0_attn_beta_param"]))
    L.add("L0", "L0a_wo", a["L0_attn_o_w"].T)
    L.add("L0", "L0a_bo", a["L0_attn_o_b"])
    L.add("L0", "L0x_band", (np.abs(np.arange(S)[:, None] - np.arange(S)[None, :]) < 32).astype(np.float32)
          .reshape(2, P, S).transpose(1, 0, 2))
    L.add("L0", "L0x_pos", a["L0_xattn_pos_bias"].reshape(2, P, S).transpose(1, 0, 2))
    for s in "qkvo":
        L.add("L0", f"L0x_w{s}", a[f"L0_xattn_w{s}"])
        L.add("L0", f"L0x_b{s}", a[f"L0_xattn_b{s}"])
    L.add("L0", "L0x_gamma", a["L0_xattn_gamma"])
    L.add("L0", "L0x_beta", a["L0_xattn_beta"])
    L.add("L0", "L0x_w1", a["L0_xattn_w1"])
    L.add("L0", "L0x_b1", columns(a["L0_xattn_b1"]))
    L.add("L0", "L0x_w2", k_tiles(a["L0_xattn_w2"]))
    L.add("L0", "L0x_b2", a["L0_xattn_b2"])
    L.add(sm, "falling", everywhere(np.arange(E, 0, -1).astype(np.float32)))
    L.add(sm, "upper", np.triu(np.ones((P, P), np.float32)))
    pick = np.zeros((P, E, P), np.float32)
    pick[np.arange(E), np.arange(E), :] = 1.0
    L.add(sm, "pick", pick)
    L.add("L0f", "L0f_router", a["L0_ffn_router_w"].T)
    for s in ("rg", "ru"):
        L.add("L0f", f"L0f_{s}", a[f"L0_ffn_{s}"].transpose(1, 0, 2))
    L.add("L0f", "L0f_rd", a["L0_ffn_rd"].reshape(E, 4, P, P).transpose(2, 0, 1, 3))
    L.add("L0f", "L0f_sg", a["L0_ffn_sg"])
    L.add("L0f", "L0f_su", a["L0_ffn_su"])
    L.add("L0f", "L0f_sd", k_tiles(a["L0_ffn_sd"]))
    for s in "qkv":
        L.add("L1", f"L1a_w{s}", a[f"L1_attn_{s}_w"])
        L.add("L1", f"L1a_conv_{s}", a[f"L1_attn_conv_{s}_w"])
    L.add("L1", "L1a_gates", np.concatenate([a["L1_attn_b_w"], a["L1_attn_mix_w"]], axis=1))
    nothing = np.zeros(8, np.float32)
    L.add("L1", "L1a_mix_b", everywhere(np.concatenate([nothing, a["L1_attn_mix_b"]])))
    L.add("L1", "L1a_mix_bias", everywhere(np.concatenate([nothing, a["L1_attn_mix_bias"]])))
    L.add("L1", "L1a_onorm", everywhere(a["L1_attn_o_norm_w"]))
    L.add("L1", "L1a_wo", a["L1_attn_o_w"])
    L.add(sm, "position", everywhere(np.arange(S, dtype=np.float32)))
    after = np.arange(S)[None, :] > np.arange(S)[:, None]
    L.add("L1", "causal", np.where(after, np.float32(NEG), np.float32(0)).reshape(2, P, S).transpose(1, 0, 2))
    for s in "qk":
        L.add("L1", f"L1x_w{s}", a[f"L1_xattn_w_{s}"].T.reshape(P, 8, P))
        L.add("L1", f"L1x_b{s}", columns(a[f"L1_xattn_b_{s}"]))
    L.add("L1", "L1x_wv", a["L1_xattn_w_v"].T)
    L.add("L1", "L1x_bv", everywhere(a["L1_xattn_b_v"]))
    L.add("L1", "L1x_wo", k_tiles(a["L1_xattn_w_o"].T))
    L.add("L1", "L1x_bo", a["L1_xattn_b_o"])
    L.add("L1", "L1f_gate", a["L1_ffn_gate_w"].T)
    L.add("L1", "L1f_gate_b", everywhere(a["L1_ffn_gate_b"]))
    L.add("L1", "L1f_w1", a["L1_ffn_w1"].transpose(1, 0, 2))
    L.add("L1", "L1f_b1", a["L1_ffn_b1"].reshape(E, 2, P).transpose(2, 0, 1))
    L.add("L1", "L1f_w2", a["L1_ffn_w2"].reshape(E, 2, P, P).transpose(2, 0, 1, 3))
    L.add("L1", "L1f_b2", top_rows(a["L1_ffn_b2"]))
    twice = lambda w: np.repeat(w.reshape(8, 1, 16, -1), 2, axis=1).reshape(2, P, -1)
    w, bias = a["L2_attn_qkvu_w"].reshape(4, P, P), a["L2_attn_qkvu_b"].reshape(4, P)
    for n, s in enumerate("qk"):
        L.add("L2", f"L2a_w{s}", twice(w[n]).transpose(2, 0, 1))
        L.add("L2", f"L2a_b{s}", twice(bias[n])[:, :, 0].T)
    L.add("L2", "L2a_wv", w[2].T)
    L.add("L2", "L2a_bv", everywhere(bias[2]))
    L.add("L2", "L2a_wu", w[3].T)
    L.add("L2", "L2a_bu", bias[3])
    L.add("L2", "L2a_wo", a["L2_attn_out_w"].T)
    L.add("L2", "L2a_bo", a["L2_attn_out_b"])
    L.add("L2", "L2a_theta", twice(a["L2_attn_theta"].reshape(P))[:, :, 0].T)
    L.add("L2", "L2a_slope", everywhere(a["L2_attn_slope_rate"].reshape(8)))
    L.add("L2", "L2a_lower", (~after).astype(np.float32).T.reshape(2, P, S).transpose(1, 0, 2))
    cosine = (np.arange(P) % 32 < 16).astype(np.float32)
    L.add("L2", "L2a_cosine_rows", cosine)
    L.add("L2", "L2a_sine_rows", 1 - cosine)
    L.add("L2", "half_pi", np.full(P, np.pi / 2, np.float32))
    L.add("L2", "L2x_scale", a["L2_xattn_rms_scale"])
    wq = a["L2_xattn_q_w"].transpose(1, 0, 2)
    wk = np.broadcast_to(a["L2_xattn_kv_w"][0, 0][:, None, :], (P, 4, 32))
    for s, w in (("q", wq), ("k", wk)):
        L.add("L2", f"L2x_w{s}", w.reshape(P, P))
        L.add("L2", f"L2x_w{s}_swapped", np.concatenate([w[:, :, 16:], w[:, :, :16]], axis=2).reshape(P, P))
    timescale = 10000.0 ** (2.0 / 32 * np.arange(16, dtype=np.float64))
    for s, start in (("q", S), ("k", 0)):
        angle = (np.arange(S) + start)[None, :].astype(np.float32) / timescale.astype(np.float32)[:, None]
        cos, sin = np.cos(angle), np.sin(angle)
        L.add("L2", f"L2x_cos_{s}", np.tile(np.concatenate([cos, cos]), (4, 1)).astype(np.float32))
        L.add("L2", f"L2x_sin_{s}", np.tile(np.concatenate([-sin, sin]), (4, 1)).astype(np.float32))
    L.add("L2", "L2x_wv", a["L2_xattn_kv_w"][1, 0])
    L.add("L2", "L2x_wo", a["L2_xattn_out_w"].reshape(P, P))
    for s in ("gate", "up"):
        L.add("L2", f"L2f_{s}", row_tiles(a[f"L2_ffn_w_{s}"]))
    L.add("L2", "L2f_down", a["L2_ffn_w_down"])
    L.add("L2", "L2f_clips", everywhere(np.concatenate([a["L2_ffn_clip_x"], a["L2_ffn_clip_down"]])))
    for s in "qk":
        L.add("L3", f"L3a_w{s}", padded_heads(a[f"L3_attn_W{s}"].T))
        L.add("L3", f"L3a_b{s}", padded_heads(a[f"L3_attn_b{s}"][None, :])[0].T)
    for sub, name in (("a", "attn"), ("x", "xattn")):
        L.add("L3", f"L3{sub}_wv", a[f"L3_{name}_Wv"].T)
        L.add("L3", f"L3{sub}_bv", everywhere(a[f"L3_{name}_bv"]))
        L.add("L3", f"L3{sub}_wo", a[f"L3_{name}_Wo"].T)
        L.add("L3", f"L3{sub}_bo", a[f"L3_{name}_bo"])
    for s in "qk":
        L.add("L3", f"L3x_w{s}", a[f"L3_xattn_W{s}"].T)
        L.add("L3", f"L3x_b{s}", a[f"L3_xattn_b{s}"])
    L.add("L3", "L3x_kmask", (np.arange(S)[None, :] % 16 == np.arange(P)[:, None] // 8).astype(np.float32))
    L.add("L3", "L3x_vmask", (np.arange(P)[:, None] % 16 == np.arange(P)[None, :] // 8).astype(np.float32))
    L.add("L3", "L3f_win", a["L3_ffn_in_proj_w"].T)
    L.add("L3", "L3f_bin", columns(a["L3_ffn_in_proj_b"]))
    L.add("L3", "L3f_heads", (np.arange(P)[:, None] // 32 == np.arange(P)[None, :] // 32).astype(np.float32))
    L.add("L3", "L3f_wout", a["L3_ffn_out_proj_w"].T)
    L.add("L3", "L3f_bout", a["L3_ffn_out_proj_b"])
    for n in "12":
        L.add("L3", f"L3f_g{n}", a[f"L3_ffn_ln{n}_g"])
        L.add("L3", f"L3f_h{n}", a[f"L3_ffn_ln{n}_b"])
    L.add("L3", "L3f_wg", a["L3_ffn_wg"])
    L.add("L3", "L3f_w1", a["L3_ffn_w1"].reshape(E, P, 4, P).transpose(3, 0, 2, 1))
    L.add("L3", "L3f_w2", a["L3_ffn_w2"].reshape(E, 4, P, P).transpose(2, 0, 1, 3))
    L.add("L3", "L3f_b1", a["L3_ffn_b1"].reshape(E, 4, P).transpose(2, 0, 1))
    L.add("L3", "L3f_b2", a["L3_ffn_b2"].T)
    return L


def decoder(nc, slots, packs, dram, x, ctx, out, upto=12):
    c = Core(nc, slots, packs)
    c.dram = dram
    c.valid_i32 = nc.alloc_sbuf_tensor("valid_keys_i32", [P, B], I32)
    c.valid = nc.alloc_sbuf_tensor("valid_keys", [P, B], F32)
    c.attend = nc.alloc_sbuf_tensor("attended_keys", [P, N // 4], I32)
    load_stage(c, None, dram, x, ctx)
    with nc.Block() as block:
        @block.vector
        def _(dve):
            nc.vector.tensor_copy(c.valid[:, :], c.valid_i32[:, :])
    for sub in SUBLAYERS[:upto]:
        sub(c)
    with nc.Block() as block:
        @block.sync
        def _(sp):
            sp.dma_start(out, c.X[:, :]).then_inc(c.stored.sem, 16)
            sp.wait_ge(c.stored.sem, c.stored.at(16))


SUBLAYERS = [layer0_attention, layer0_cross, layer0_experts, layer1_attention, layer1_cross, layer1_experts, layer2_attention,
             layer2_cross, layer2_mlp, layer3_attention, layer3_cross, layer3_block]


def kernel(**inputs):
    from concourse import bacc
    from concourse.bass_utils import run_bass_kernel_spmd

    a = {k: np.asarray(v) for k, v in inputs.items()}
    L = lay_out(a)
    arrays = {f"{k}_dram": v for k, v in L.packed().items()}
    arrays["x_dram"] = feature_major(a["x"])
    arrays["ctx_dram"] = feature_major(a["ctx_1024"])
    arrays["valid_dram"] = np.ascontiguousarray(everywhere(a["mask_B_ik0"]))
    arrays["attend_dram"] = np.ascontiguousarray(
        everywhere(np.ascontiguousarray(a["mask_BxS2_bk0"]).view(np.int32)))
    nc = bacc.Bacc("TRN2", target_bir_lowering=False, num_devices=1)
    ap = {k: nc.dram_tensor(k, v.shape, mybir.dt.from_np(v.dtype), kind="ExternalInput").ap()
          for k, v in arrays.items()}
    out = nc.dram_tensor("out_dram", (P, N), F32, kind="ExternalOutput").ap()
    decoder(nc, L.slots, L.words, {k[:-5]: v for k, v in ap.items()}, ap["x_dram"], ap["ctx_dram"], out)
    r = run_bass_kernel_spmd(nc, [arrays], core_ids=[0])
    return r.results[0]["out_dram"].T.reshape(B, S, P)
```

```python
import numpy as np

import concourse.bass as bass
from concourse import mybir

F32 = mybir.dt.float32
BF16 = mybir.dt.bfloat16
I32 = mybir.dt.int32
U8 = mybir.dt.uint8
ACT = mybir.ActivationFunctionType
ALU = mybir.AluOpType
AX = mybir.AxisListType

P = 128
B, S = 8, 256
N = B * S
CH = 512
NC = N // CH
NEG = -3.4028234663852886e38
REPLACED = -3.0e38


class Signal:

    def __init__(self, nc, name):
        self.sem = nc.alloc_semaphore(name)
        self.base = 0

    def at(self, n):
        return self.base + n

    def advance(self, n):
        self.base += n


class Chain:

    def __init__(self, eng, sem):
        self.eng, self.sem, self.n = eng, sem, 0

    def link(self, ins):
        self.n += 1
        ins.then_inc(self.sem, 1)
        self.eng.wait_ge(self.sem, self.n)

    def step(self, ins):
        self.n += 1
        ins.then_inc(self.sem, 1)

    def all_but(self, last):
        if self.n > last:
            self.eng.wait_ge(self.sem, self.n - last)

    def clear(self):
        if self.n:
            self.eng.wait_ge(self.sem, self.n)
            self.eng.sem_clear(self.sem)
            self.n = 0


class Core:

    SIGNALS = [
        "loaded", "stored", "mean_ready", "var_ready", "centred", "squared", "normed", "rooted",
        "product_ready", "product_taken", "product_taken_v", "staged", "proj_ready", "proj_taken_s", "proj_taken_v",
        "scores_ready", "scores_max", "probs_ready", "probs_picked", "probs_turned", "turned_copied", "turned_copied_s", "qk_ready", "qk_taken", "v_ready", "v_taken", "out_added",
        "mixed_ready", "mixed_taken", "out_turned", "out_copied", "out_product", "residual_added",
        "aux_pe", "aux_v", "aux_s", "aux_p", "aux_pe2", "aux_v2", "aux_s2", "aux_p2", "aux_pe3", "aux_v3", "aux_s3",
        "big_loaded",
    ]

    def __init__(self, nc, slots, packs):
        self.nc, self.slots, self.packs = nc, slots, packs
        self.sig = {n: Signal(nc, n) for n in self.SIGNALS}
        self.vector_chain = nc.alloc_semaphore("vector_chain")
        self.scalar_chain = nc.alloc_semaphore("scalar_chain")
        self.pool_chain = nc.alloc_semaphore("pool_chain")
        self.psum = nc.alloc_psum_tensor("psum", [P, 8, CH], F32)
        self.X = nc.alloc_sbuf_tensor("residual", [P, N], F32)
        self.CT = nc.alloc_sbuf_tensor("context", [P, N], F32)
        self.HN = nc.alloc_sbuf_tensor("normed_input", [P, N], F32)
        self.T = nc.alloc_sbuf_tensor("tiles", [P, 4, N], F32)
        self.small = nc.alloc_sbuf_tensor("small_weights", [P, packs["small"]], F32)
        self.big_words = max([packs[n] for n in packs if n != "small"], default=1)
        self.big = nc.alloc_sbuf_tensor("big_weights", [P, self.big_words], F32)
        self.work_words = 66 * 1024 // 4
        self.work = nc.alloc_sbuf_tensor("work", [P, self.work_words], F32)

    def __getattr__(self, name):
        return self.sig[name]

    def w(self, name):
        pack, off, shape = self.slots[name]
        t = self.small if pack == "small" else self.big
        n = int(np.prod(shape[1:]))
        return shaped(t[:, off:off + n], shape[1:])


def shaped(ap, dims):
    if len(dims) == 1:
        return ap
    if len(dims) == 2:
        return ap.rearrange("p (a b) -> p a b", b=dims[1])
    if len(dims) == 3:
        return ap.rearrange("p (a b c) -> p a b c", b=dims[1], c=dims[2])
    return ap.rearrange("p (a b c d) -> p a b c d", b=dims[1], c=dims[2], d=dims[3])


class Arena:

    def __init__(self, core):
        self.core, self.off = core, 0

    def take(self, *dims):
        n = int(np.prod(dims))
        a = self.core.work[:, self.off:self.off + n]
        self.off += n
        assert self.off <= self.core.work_words, (self.off, self.core.work_words)
        return shaped(a, dims)



def load_stage(c, big, dram, x_dram=None, ctx_dram=None):
    nc = c.nc
    with nc.Block() as block:
        @block.sync
        def _(sp):
            n = 0
            if x_dram is not None:
                sp.dma_start(c.X[:, :], x_dram).then_inc(c.loaded.sem, 16)
                sp.dma_start(c.small[:, :], dram["small"]).then_inc(c.loaded.sem, 16)
                sp.dma_start(c.CT[:, :], ctx_dram).then_inc(c.loaded.sem, 16)
                sp.dma_start(c.valid_i32[:, :], dram["valid"]).then_inc(c.loaded.sem, 16)
                sp.dma_start(c.attend[:, :], dram["attend"]).then_inc(c.loaded.sem, 16)
                n = 5
            if big:
                sp.dma_start(c.big[:, 0:c.packs[big]], dram[big]).then_inc(c.loaded.sem, 16)
                n += 1
            sp.wait_ge(c.loaded.sem, c.loaded.at(16 * n))
            c.loaded.advance(16 * n)


def norm_stage(c, src, dst, eps, centre=True, gain=None, shift=None):
    nc = c.nc
    a = Arena(c)
    cen, sq, std = a.take(N), a.take(N), a.take(N)
    avg = c.w("average")
    ch = [slice(i * CH, (i + 1) * CH) for i in range(NC)]
    with nc.Block() as block:
        @block.tensor
        def _(pe):
            if centre:
                for i in range(NC):
                    nc.tensor.matmul(c.psum[:, i, :], avg, src[:, ch[i]], start=True, stop=True) \
                        .then_inc(c.mean_ready.sem, 1)
            for i in range(NC):
                pe.wait_ge(c.squared.sem, c.squared.at(i + 1))
                nc.tensor.matmul(c.psum[:, 4 + i, :], avg, sq[:, ch[i]], start=True, stop=True) \
                    .then_inc(c.var_ready.sem, 1)

        @block.vector
        def _(dve):
            if centre:
                for i in range(NC):
                    dve.wait_ge(c.mean_ready.sem, c.mean_ready.at(i + 1))
                    nc.vector.tensor_tensor(cen[:, ch[i]], src[:, ch[i]], c.psum[:, i, :], ALU.subtract) \
                        .then_inc(c.centred.sem, 1)
            chain = Chain(dve, c.vector_chain)
            for i in range(NC):
                dve.wait_ge(c.rooted.sem, c.rooted.at(i + 1))
                chain.link(nc.vector.reciprocal(std[:, ch[i]], std[:, ch[i]]))
                nc.vector.tensor_tensor(dst[:, ch[i]], (cen if centre else src)[:, ch[i]], std[:, ch[i]], ALU.mult) \
                    .then_inc(c.normed.sem, 1)
            chain.clear()

        @block.scalar
        def _(act):
            for i in range(NC):
                if centre:
                    act.wait_ge(c.centred.sem, c.centred.at(i + 1))
                nc.scalar.activation(sq[:, ch[i]], (cen if centre else src)[:, ch[i]], ACT.Square) \
                    .then_inc(c.squared.sem, 1)
            for i in range(NC):
                act.wait_ge(c.var_ready.sem, c.var_ready.at(i + 1))
                nc.scalar.activation(std[:, ch[i]], c.psum[:, 4 + i, :], ACT.Sqrt, bias=c.w(eps)) \
                    .then_inc(c.rooted.sem, 1)
            if gain is not None:
                for i in range(NC):
                    act.wait_ge(c.normed.sem, c.normed.at(i + 1))
                    nc.scalar.activation(dst[:, ch[i]], dst[:, ch[i]], ACT.Identity, scale=gain,
                                         bias=0.0 if shift is None else shift)
    if centre:
        c.mean_ready.advance(NC)
        c.centred.advance(NC)
    c.squared.advance(NC)
    c.var_ready.advance(NC)
    c.normed.advance(NC)
    c.rooted.advance(NC)


def affine_stage(c, src, dsts, gains, shifts):
    nc = c.nc
    with nc.Block() as block:
        @block.scalar
        def _(act):
            for d, g, s in zip(dsts[0::2], gains[0::2], shifts[0::2]):
                nc.scalar.activation(d, src, ACT.Identity, scale=g, bias=s)

        @block.vector
        def _(dve):
            for d, g, s in zip(dsts[1::2], gains[1::2], shifts[1::2]):
                nc.vector.tensor_scalar(d, src, g, s, ALU.mult, ALU.add)


def project_stage(c, jobs):
    nc = c.nc
    steps = [(i, j) for i in range(NC) for j in range(len(jobs))]
    by_vector = [jobs[j][5] is not None for _, j in steps]
    taken = []
    ns = nv = 0
    for v in by_vector:
        nv, ns = nv + v, ns + (not v)
        taken.append((v, nv if v else ns))
    with nc.Block() as block:
        @block.tensor
        def _(pe):
            for n, (i, j) in enumerate(steps):
                srcs, ws = jobs[j][0:2]
                if n >= 8:
                    v, k = taken[n - 8]
                    sig = c.product_taken_v if v else c.product_taken
                    pe.wait_ge(sig.sem, sig.at(k))
                for k, (src, w) in enumerate(zip(srcs, ws)):
                    mm = nc.tensor.matmul(c.psum[:, n % 8, :], w, src[:, i * CH:(i + 1) * CH],
                                          start=(k == 0), stop=(k == len(srcs) - 1))
                mm.then_inc(c.product_ready.sem, 1)

        @block.scalar
        def _(act):
            for n, (i, j) in enumerate(steps):
                if by_vector[n]:
                    continue
                _, _, bias, func, out, _ = jobs[j]
                act.wait_ge(c.product_ready.sem, c.product_ready.at(n + 1))
                nc.scalar.activation(out[:, i * CH:(i + 1) * CH], c.psum[:, n % 8, :], func or ACT.Identity,
                                     bias=0.0 if bias is None else bias).then_inc(c.product_taken.sem, 1)

        @block.vector
        def _(dve):
            for n, (i, j) in enumerate(steps):
                if not by_vector[n]:
                    continue
                _, _, bias, func, out, res = jobs[j]
                dve.wait_ge(c.product_ready.sem, c.product_ready.at(n + 1))
                nc.vector.scalar_tensor_tensor(out[:, i * CH:(i + 1) * CH], c.psum[:, n % 8, :],
                                               0.0 if bias is None else bias, res[:, i * CH:(i + 1) * CH],
                                               ALU.add, ALU.add).then_inc(c.product_taken_v.sem, 1)
    c.product_ready.advance(len(steps))
    c.product_taken.advance(ns)
    c.product_taken_v.advance(nv)


def attention_stage(c, H, dh, q_src, k_src, v_src, wq, bq, wk, bk, wv, bv, wo, bo, scale=1.0,
                    head_scale=None, mask=None, prepare_mask=None, mask_words=0, shared_kv=False, top=0,
                    residual2=None, skip_max=False):
    nc = c.nc
    nt = len(wq)
    per_tile = H // nt
    pitch = P // per_tile
    gpt = per_tile // 2
    NG = H // 2
    vg = P // (2 * dh)
    vw = dh if shared_kv else P
    U = 4
    rows = 32 if dh < 32 else dh
    TURN = 3
    MIX = 3 if skip_max else 4
    OUT = MIX + 1
    SQ = max(8 // NG, 2)
    W = SQ * NG
    NIT = B // SQ
    VR = {1: 8, 2: 4}.get(vg, 2)
    ve = 128 if skip_max else dh
    nvh = vw // dh
    a = Arena(c)
    qb, kb = a.take(2, S), a.take(2, S)
    vsb = a.take(2, S)
    vb = a.take(VR, 2, nvh * ve)
    probs = None if skip_max else a.take(2, U, S)
    raw = a.take(2, U, S) if (mask or top) else None
    rest = a.take(2, U, S) if top else None
    turned = a.take(2, 2, 2, S)
    otok = a.take(2, 2, P)
    oT = a.take(2, S)
    rowmax, nbias = a.take(2, U), a.take(2, U)
    top8 = a.take(2, U, max(top // 8, 1), 8)
    sums, rest_sums, kept_sums, rsum = a.take(4, U), a.take(4, U), a.take(4, U), a.take(4, U)
    mb = a.take(mask_words) if mask_words else None
    gate = a.take(1)
    ident = c.w("identity")

    def bank(i):
        return c.psum[:, i, :]

    def pair(g):
        return c.psum[:, 2 * (g % 2):2 * (g % 2) + 2, :]

    def scores(g):
        return pair(g).rearrange("p a (q k) -> p (a q) k", k=S)

    def turn(head):
        return bank(4 + head).rearrange("p (q t x) -> p q t x", q=2, t=2)

    mixed = c.psum[:, 6, 0:U * ve].rearrange("p (u d) -> p u d", d=ve)

    def starts_tile(g):
        return g % gpt == 0

    def starts_values(g):
        return g % (NG if shared_kv else vg) == 0

    def ends_output(g):
        return g % vg == vg - 1

    def values(g):
        return vb[:, (g // (NG if shared_kv else vg)) % VR]

    per = {"q": W // gpt, "v": W // (NG if shared_kv else vg), "o": W // vg, "g": W, "b": SQ}

    def after(sig, kind, it, n):
        return sig.base + it * per[kind] + n + 1

    def queries_taken(it, g):
        return c.qk_taken.base + it * 2 * per["q"] + 2 * tile_n(g) + 2

    def run(step_of):
        def steps(it, first, lo, hi):
            ok = lambda g: g < W and (g >= 0 or not first)
            for t in range(lo, hi):
                step_of(it, t, ok)
        return steps

    TAIL = OUT + 1
    tile_n = lambda g: g // gpt
    val_n = lambda g: g // (NG if shared_kv else vg)
    out_n = lambda g: g // vg
    seq_of = lambda it, g: it * SQ + g // NG

    def engine(eng, step, chain=None):
        run_steps = run(step)
        run_steps(0, True, 0, W)
        if chain is not None:
            chain.clear()
        with eng.Fori(1, NIT) as it:
            run_steps(it, False, 0, W)
            if chain is not None:
                chain.clear()
        run_steps(NIT - 1, False, W, W + TAIL)
        if chain is not None:
            chain.clear()

    with nc.Block() as block:
        @block.gpsimd
        def _(pool):
            def step(it, t, ok):
                if t < W and t % NG == 0:
                    if ok(t - 2 * NG):
                        pool.wait_ge(c.v_ready.sem, after(c.v_ready, "v", it, val_n(t - NG) - 1))
                    nc.gpsimd.tensor_copy(vsb[:, (t // NG) % 2], v_src[:, bass.ds(seq_of(it, t) * S, S)]) \
                        .then_inc(c.staged.sem, 1)
                g = t - 1
                if top and ok(g):
                    pool.wait_ge(c.probs_ready.sem, after(c.probs_ready, "g", it, g))
                    nc.gpsimd.tensor_tensor(probs[:, g % 2], probs[:, g % 2], rest[:, g % 2], ALU.subtract) \
                        .then_inc(c.probs_picked.sem, 1)

            if residual2 is not None:
                nc.gpsimd.tensor_tensor(c.X[:, :], c.X[:, :], residual2[:, :], ALU.add).then_inc(c.aux_p.sem, 1)
            if skip_max:
                nc.gpsimd.memset(vb, 1.0).then_inc(c.aux_p.sem, 1)
            engine(pool, step)

        @block.tensor
        def _(pe):
            def step(it, t, ok):
                g = t - 1
                if ok(g):
                    if starts_tile(g):
                        pe.wait_ge(c.qk_taken.sem, queries_taken(it, g))
                    if ok(g - 2):
                        pe.wait_ge(c.probs_ready.sem, after(c.probs_ready, "g", it, g - 2))
                    hs = g % NG * 2
                    for u in range(U):
                        h = hs + u // 2
                        base = (h % per_tile) * pitch
                        q = qb[base:base + rows, tile_n(g) % 2, :]
                        k = kb[base:base + rows, tile_n(g) % 2, :]
                        half = slice((u % 2) * P, (u % 2 + 1) * P)
                        lhs, rhs = (k[:, half], q) if skip_max else (q[:, half], k)
                        mm = nc.tensor.matmul(scores(g)[:, u, :], lhs, rhs, start=True, stop=True,
                                              tile_position=(base, 0))
                    mm.then_inc(c.scores_ready.sem, 1)
                g = t
                if g < W and starts_tile(g):
                    if ok(g - MIX - 1):
                        pe.wait_ge(c.mixed_taken.sem, after(c.mixed_taken, "g", it, g - MIX - 1))
                    if ok(g - 1) and ok(val_n(g - 1)):
                        pe.wait_ge(c.v_taken.sem, after(c.v_taken, "v", it, val_n(g - 1)))
                    i = g % NG // gpt
                    src = bass.ds(seq_of(it, g) * S, S)
                    nc.tensor.matmul(bank(6)[:, 0:S], wk[i], k_src[:, src], start=True, stop=True) \
                        .then_inc(c.qk_ready.sem, 1)
                    if ok(g - OUT - 1):
                        pe.wait_ge(c.out_added.sem, after(c.out_added, "o", it, (g - OUT) // vg - 1))
                    if ok(g - gpt):
                        pe.wait_ge(c.qk_taken.sem, queries_taken(it, g - gpt))
                    nc.tensor.matmul(bank(7)[:, 0:S], wq[i], q_src[:, src], start=True, stop=True) \
                        .then_inc(c.qk_ready.sem, 1)
                k3 = t - TURN
                turns = ok(k3) and not skip_max

                def turn_head(head):
                    for u in (2 * head, 2 * head + 1):
                        for kt in range(2):
                            mm = nc.tensor.transpose(turn(head)[:, kt, u % 2, :],
                                                     probs[:, k3 % 2, u, kt * P:(kt + 1) * P], ident)
                    mm.then_inc(c.probs_turned.sem, 1)

                if turns:
                    ready = c.probs_picked if top else c.probs_ready
                    pe.wait_ge(ready.sem, after(ready, "g", it, k3))
                    if ok(k3 - 1):
                        pe.wait_ge(c.turned_copied_s.sem, after(c.turned_copied_s, "g", it, k3 - 1))
                    turn_head(0)
                if g < W and starts_values(g):
                    pe.wait_ge(c.qk_taken.sem, queries_taken(it, g) - 1)
                    if t % NG == 0:
                        pe.wait_ge(c.staged.sem, after(c.staged, "b", it, t // NG))
                    lo = 0 if shared_kv else g % NG // vg * P
                    for kt in range(2):
                        mm = nc.tensor.matmul(bank(6)[:, kt * vw:(kt + 1) * vw],
                                              vsb[:, (t // NG) % 2, kt * P:(kt + 1) * P], wv[:, lo:lo + vw],
                                              start=True, stop=True)
                    mm.then_inc(c.v_ready.sem, 1)
                o = t - OUT
                out = ok(o) and ends_output(o)
                if out:
                    if g < W and starts_tile(g):
                        pe.wait_ge(c.qk_taken.sem, queries_taken(it, g))
                    elif ok(o - vg):
                        pe.wait_ge(c.out_added.sem, after(c.out_added, "o", it, out_n(o) - 1))
                    pe.wait_ge(c.mixed_taken.sem, after(c.mixed_taken, "g", it, o))
                    for qt in range(2):
                        mm = nc.tensor.transpose(bank(7)[:, qt * P:(qt + 1) * P], otok[:, out_n(o) % 2, qt, :], ident)
                    mm.then_inc(c.out_turned.sem, 1)
                if turns:
                    if ok(k3 - 1):
                        pe.wait_ge(c.turned_copied.sem, after(c.turned_copied, "g", it, k3 - 1))
                    turn_head(1)
                m = t - MIX
                if ok(m):
                    if skip_max:
                        pe.wait_ge(c.probs_ready.sem, after(c.probs_ready, "g", it, m))
                    else:
                        pe.wait_ge(c.turned_copied.sem, after(c.turned_copied, "g", it, m))
                        pe.wait_ge(c.turned_copied_s.sem, after(c.turned_copied_s, "g", it, m))
                    if g < W and starts_values(g):
                        pe.wait_ge(c.v_taken.sem, after(c.v_taken, "v", it, val_n(g)))
                    elif g < W and starts_tile(g):
                        pe.wait_ge(c.qk_taken.sem, queries_taken(it, g) - 1)
                    elif ok(m - 1):
                        pe.wait_ge(c.mixed_taken.sem, after(c.mixed_taken, "g", it, m - 1))
                    v = values(m)
                    for u in range(U):
                        lo = 0 if shared_kv else ((m % vg) * 2 + u // 2) * ve
                        for kt in range(2):
                            mm = nc.tensor.matmul(mixed[:, u, :], turned[:, m % 2, u // 2, kt, (u % 2) * P:(u % 2 + 1) * P],
                                                  v[:, kt, lo:lo + ve], start=(kt == 0), stop=(kt == 1))
                    mm.then_inc(c.mixed_ready.sem, 1)
                if out:
                    pe.wait_ge(c.out_copied.sem, after(c.out_copied, "o", it, out_n(o)))
                    nc.tensor.matmul(bank(7)[:, 0:S], wo[o % NG // vg], oT[:, out_n(o) % 2, :],
                                     start=True, stop=True).then_inc(c.out_product.sem, 1)

            engine(pe, step)

        @block.scalar
        def _(act):
            def step(it, t, ok):
                g = t
                if g < W and starts_tile(g):
                    i = g % NG // gpt
                    for n, (dst, b, src) in enumerate(((kb, bk, 6), (qb, bq, 7))):
                        act.wait_ge(c.qk_ready.sem, c.qk_ready.base + it * 2 * per["q"] + 2 * tile_n(g) + n + 1)
                        nc.scalar.activation(dst[:, tile_n(g) % 2, :], bank(src)[:, 0:S], ACT.Identity,
                                             bias=0.0 if b is None else b[:, i:i + 1]).then_inc(c.qk_taken.sem, 1)
                k = t - TURN
                if ok(k) and not skip_max:
                    act.wait_ge(c.probs_turned.sem, c.probs_turned.base + it * 2 * W + 2 * k + 1)
                    if ok(k - 2):
                        act.wait_ge(c.mixed_ready.sem, after(c.mixed_ready, "g", it, k - 2))
                    nc.scalar.copy(turned[:, k % 2, 0].rearrange("p t s -> p (t s)"), bank(4)) \
                        .then_inc(c.turned_copied_s.sem, 1)
                o = t - OUT
                if ok(o) and ends_output(o):
                    act.wait_ge(c.out_turned.sem, after(c.out_turned, "o", it, out_n(o)))
                    nc.scalar.copy(oT[:, out_n(o) % 2, :], bank(7)[:, 0:S]).then_inc(c.out_copied.sem, 1)
                if ok(k) and top:
                    act.wait_ge(c.probs_turned.sem, c.probs_turned.base + it * 2 * W + 2 * k + 2)
                    nc.scalar.copy(turned[:, k % 2, 1].rearrange("p t s -> p (t s)"), bank(5)) \
                        .then_inc(c.turned_copied.sem, 1)
                g = t - 1
                if ok(g) and skip_max:
                    act.wait_ge(c.scores_ready.sem, after(c.scores_ready, "g", it, g))
                    if ok(g - 2):
                        act.wait_ge(c.mixed_ready.sem, after(c.mixed_ready, "g", it, g - 2))
                    for head in range(2):
                        h = g % NG * 2 + head
                        ins = nc.scalar.activation(turned[:, g % 2, head].rearrange("p t s -> p (t s)"),
                                                   pair(g)[:, head, :], ACT.Exp, scale=head_scale[:, h:h + 1])
                    ins.then_inc(c.probs_ready.sem, 1)
                elif ok(g):
                    act.wait_ge(c.scores_max.sem, after(c.scores_max, "g", it, g))
                    if ok(g - 2):
                        act.wait_ge(c.probs_turned.sem, c.probs_turned.base + it * 2 * W + 2 * (g - 1))
                    for u in range(U):
                        src = raw[:, g % 2, u, :] if mask else scores(g)[:, u, :]
                        ins = nc.scalar.activation(probs[:, g % 2, u, :], src, ACT.Exp,
                                                   bias=nbias[:, g % 2, u:u + 1], scale=scale,
                                                   accum_out=sums[:, g % 4, u:u + 1])
                        if top:
                            ins = nc.scalar.activation(rest[:, g % 2, u, :], raw[:, g % 2, u, :], ACT.Exp,
                                                       bias=nbias[:, g % 2, u:u + 1], scale=scale,
                                                       accum_out=rest_sums[:, g % 4, u:u + 1])
                    ins.then_inc(c.probs_ready.sem, 1)

            engine(act, step)

        @block.vector
        def _(dve):
            chain = Chain(dve, c.vector_chain)

            def maxima(it, g):
                s = g % 2
                dve.wait_ge(c.scores_ready.sem, after(c.scores_ready, "g", it, g))
                if top or mask:
                    chain.link(nc.vector.tensor_copy(gate, ident[:, 0:1]))
                if top:
                    for r in range(top // 8):
                        src = scores(g) if r == 0 else raw[:, s]
                        for u in range(U):
                            chain.all_but(U - 1)
                            chain.step(nc.vector.max(top8[:, s, u, r, :], src[:, u, :]))
                        for u in range(U):
                            chain.all_but(U - 1)
                            chain.step(nc.vector.match_replace(raw[:, s, u, :], top8[:, s, u, r, :],
                                                               src[:, u, :], REPLACED))
                    chain.all_but(0)
                    nc.vector.tensor_scalar(nbias[:, s, :], top8[:, s, :, 0, 0], -scale, None, ALU.mult) \
                        .then_inc(c.scores_max.sem, 1)
                    return
                if mask:
                    for u in range(U):
                        ins = nc.vector.tensor_tensor_reduce(raw[:, s, u, :], scores(g)[:, u, :],
                                                             mask(mb, u % 2), 1.0, NEG, ALU.add,
                                                             ALU.max, rowmax[:, s, u:u + 1])
                    chain.link(ins)
                else:
                    chain.link(nc.vector.reduce_max(rowmax[:, s, :], scores(g), AX.X))
                nc.vector.tensor_scalar(nbias[:, s, :], rowmax[:, s, :], -scale, None, ALU.mult) \
                    .then_inc(c.scores_max.sem, 1)

            def step(it, t, ok):
                g = t - 1
                if ok(g):
                    if prepare_mask is not None and g % NG == 0:
                        prepare_mask(nc, dve, chain, seq_of(it, g), mb)
                    if not skip_max:
                        maxima(it, g)
                g = t
                if g < W and starts_values(g):
                    dve.wait_ge(c.v_ready.sem, after(c.v_ready, "v", it, val_n(g)))
                    dst = values(g).rearrange("p t (h e) -> p t h e", e=ve)[:, :, :, 0:dh]
                    src = bank(6)[:, 0:2 * vw].rearrange("p (t h e) -> p t h e", t=2, e=dh)
                    if bv is None:
                        ins = nc.vector.tensor_copy(dst, src)
                    else:
                        lo = g % NG // vg * P
                        b = bv[:, lo:lo + vw].rearrange("p (h e) -> p h e", e=dh).unsqueeze(1)
                        ins = nc.vector.tensor_tensor(dst, src, b.broadcast_to([P, 2, nvh, dh]), ALU.add)
                    ins.then_inc(c.v_taken.sem, 1)
                k = t - TURN
                if ok(k) and not skip_max:
                    dve.wait_ge(c.probs_ready.sem, after(c.probs_ready, "g", it, k))
                    total = sums[:, k % 4, :]
                    if top:
                        chain.link(nc.vector.tensor_tensor(kept_sums[:, k % 4, :], total, rest_sums[:, k % 4, :],
                                                           ALU.subtract))
                        total = kept_sums[:, k % 4, :]
                    chain.step(nc.vector.reciprocal(rsum[:, k % 4, :], total))
                    if not top:
                        dve.wait_ge(c.probs_turned.sem, c.probs_turned.base + it * 2 * W + 2 * k + 2)
                        if ok(k - 2):
                            dve.wait_ge(c.mixed_ready.sem, after(c.mixed_ready, "g", it, k - 2))
                        nc.vector.tensor_copy(turned[:, k % 2, 1].rearrange("p t s -> p (t s)"), bank(5)) \
                            .then_inc(c.turned_copied.sem, 1)
                m = t - MIX
                if ok(m):
                    dve.wait_ge(c.mixed_ready.sem, after(c.mixed_ready, "g", it, m))
                    if skip_max:
                        chain.link(nc.vector.reciprocal(rsum[:, m % 4, :].unsqueeze(2), mixed[:, :, dh:dh + 1]))
                    lo = m % vg * 2 * dh
                    dst = otok[:, out_n(m) % 2, :, lo:lo + 2 * dh].rearrange("p q (h d) -> p h q d", d=dh)
                    inv = rsum[:, m % 4, :].rearrange("p (h q) -> p h q", q=2).unsqueeze(3)
                    nc.vector.tensor_tensor(dst, mixed.rearrange("p (h q) d -> p h q d", q=2)[:, :, :, 0:dh],
                                            inv.broadcast_to([P, 2, 2, dh]), ALU.mult) \
                        .then_inc(c.mixed_taken.sem, 1)
                o = t - OUT
                if ok(o) and ends_output(o):
                    dve.wait_ge(c.out_product.sem, after(c.out_product, "o", it, out_n(o)))
                    xs = c.X[:, bass.ds(seq_of(it, o) * S, S)]
                    bias = 0.0 if bo is None or o % NG >= vg else bo
                    nc.vector.scalar_tensor_tensor(xs, bank(7)[:, 0:S], bias, xs, ALU.add, ALU.add) \
                        .then_inc(c.out_added.sem, 1)

            n_p = (residual2 is not None) + skip_max
            if n_p:
                dve.wait_ge(c.aux_p.sem, c.aux_p.at(n_p))
            engine(dve, step, chain)
    c.aux_p.advance((residual2 is not None) + skip_max)
    groups, outs = B * NG, B * NG // vg
    for s, n in ((c.staged, B), (c.qk_ready, 2 * groups // gpt), (c.qk_taken, 2 * groups // gpt),
                 (c.v_ready, B * per["v"] // SQ), (c.v_taken, B * per["v"] // SQ), (c.scores_ready, groups),
                 (c.scores_max, 0 if skip_max else groups), (c.probs_ready, groups),
                 (c.probs_picked, groups if top else 0), (c.probs_turned, 0 if skip_max else 2 * groups),
                 (c.turned_copied, 0 if skip_max else groups), (c.turned_copied_s, 0 if skip_max else groups),
                 (c.mixed_ready, groups), (c.mixed_taken, groups), (c.out_turned, outs), (c.out_copied, outs),
                 (c.out_product, outs), (c.out_added, outs)):
        s.advance(n)



def l2_stage(c, tensors):
    nc = c.nc
    a = Arena(c)
    sq, norm = a.take(N), a.take(2, N)
    steps = [(t, i) for t in range(len(tensors)) for i in range(NC)]
    ones = c.w("ones")
    with nc.Block() as block:
        @block.scalar
        def _(act):
            for n, (t, i) in enumerate(steps):
                if n >= NC:
                    act.wait_ge(c.aux_pe.sem, c.aux_pe.at(n - NC + 1))
                nc.scalar.activation(sq[:, i * CH:(i + 1) * CH], tensors[t][:, i * CH:(i + 1) * CH], ACT.Square) \
                    .then_inc(c.aux_s.sem, 1)
            for n, (t, i) in enumerate(steps):
                act.wait_ge(c.aux_pe.sem, c.aux_pe.at(n + 1))
                nc.scalar.activation(norm[:, t, i * CH:(i + 1) * CH], c.psum[:, n, :], ACT.Sqrt) \
                    .then_inc(c.aux_s2.sem, 1)

        @block.tensor
        def _(pe):
            for n, (t, i) in enumerate(steps):
                pe.wait_ge(c.aux_s.sem, c.aux_s.at(n + 1))
                nc.tensor.matmul(c.psum[:, n, :], ones, sq[:, i * CH:(i + 1) * CH], start=True, stop=True) \
                    .then_inc(c.aux_pe.sem, 1)

        @block.vector
        def _(dve):
            chain = Chain(dve, c.vector_chain)
            for n, (t, i) in enumerate(steps):
                dve.wait_ge(c.aux_s2.sem, c.aux_s2.at(n + 1))
                ch = slice(i * CH, (i + 1) * CH)
                chain.link(nc.vector.tensor_scalar(norm[:, t, ch], norm[:, t, ch], 1e-6, None, ALU.max))
                chain.link(nc.vector.reciprocal(norm[:, t, ch], norm[:, t, ch]))
                nc.vector.tensor_tensor(tensors[t][:, ch], tensors[t][:, ch], norm[:, t, ch], ALU.mult)
            chain.clear()
    for s in (c.aux_s, c.aux_s2, c.aux_pe):
        s.advance(len(steps))


def layer0_attention(c):
    nc = c.nc
    load_stage(c, "L0", c.dram)
    n0, qn, kn, vn = c.HN, c.T[:, 0, :], c.T[:, 1, :], c.T[:, 2, :]
    norm_stage(c, c.X, c.HN, "eps5")
    n2 = c.T[:, 3, :]
    norm_stage(c, c.HN, n2, "eps5")
    affine_stage(c, n2, [qn, kn, vn], [c.w("L0a_gq"), c.w("L0a_gk"), c.w("L0a_gv")],
                 [c.w("L0a_hq"), c.w("L0a_hk"), c.w("L0a_hv")])
    project_stage(c, [([qn], [c.w("L0a_wq")], c.w("L0a_bq"), None, c.T[:, 3, :], None)])
    project_stage(c, [([kn], [c.w("L0a_wk")], c.w("L0a_bk"), None, qn, None)])
    l2_stage(c, [c.T[:, 3, :], qn])
    beta = c.w("L0a_beta")
    with nc.Block() as block:
        @block.scalar
        def _(act):
            chain = Chain(act, c.scalar_chain)
            chain.link(nc.scalar.activation(c.work[:, 0:16], beta, ACT.Abs))
            chain.link(nc.scalar.activation(c.work[:, 16:32], c.work[:, 0:16], ACT.Exp, scale=-1.0))
            nc.scalar.activation(c.work[:, 32:48], c.work[:, 16:32], ACT.Ln, bias=c.w("one")).then_inc(c.aux_s.sem, 1)
            act.wait_ge(c.aux_s.sem, c.aux_s.at(1))
            chain.clear()

        @block.vector
        def _(dve):
            chain = Chain(dve, c.vector_chain)
            chain.link(nc.vector.tensor_scalar(c.work[:, 64:80], beta, 0.0, None, ALU.max))
            dve.wait_ge(c.aux_s.sem, c.aux_s.at(1))
            chain.link(nc.vector.tensor_tensor(c.work[:, 80:96], c.work[:, 64:80], c.work[:, 32:48], ALU.add))
            chain.link(nc.vector.tensor_scalar(c.work[:, 96:112], c.work[:, 80:96], 0.1, 10.0, ALU.max, ALU.min))
            chain.link(nc.vector.tensor_scalar(beta, c.work[:, 96:112], float(1.0 / np.sqrt(8.0)), None, ALU.mult))
            chain.clear()
    c.aux_s.advance(1)
    pad = c.w("pad8")
    attention_stage(c, 16, 8, c.T[:, 3, :], qn, vn, [pad[:, t, :] for t in range(4)], None,
                    [pad[:, t, :] for t in range(4)], None, c.w("L0a_wv"), c.w("L0a_bv"), [c.w("L0a_wo")],
                    c.w("L0a_bo"), head_scale=beta, skip_max=True, residual2=c.HN)


def add_stage(c, dst, one, other):
    nc = c.nc
    lo, hi = slice(0, N * 5 // 8), slice(N * 5 // 8, N)
    with nc.Block() as block:
        @block.vector
        def _(dve):
            nc.vector.tensor_tensor(dst[:, lo], one[:, lo], other[:, lo], ALU.add)

        @block.gpsimd
        def _(pool):
            nc.gpsimd.tensor_tensor(dst[:, hi], one[:, hi], other[:, hi], ALU.add)


def layer0_cross(c):
    nc = c.nc
    norm_stage(c, c.X, c.HN, "eps5")
    emb = c.T[:, 3, :]
    add_stage(c, emb, c.HN, c.CT)
    sq, k, v = c.T[:, 0, :], c.T[:, 1, :], c.T[:, 2, :]
    project_stage(c, [([emb], [c.w("L0x_wq")], c.w("L0x_bq"), ACT.Sigmoid, sq, None),
                      ([emb], [c.w("L0x_wk")], c.w("L0x_bk"), None, k, None),
                      ([emb], [c.w("L0x_wv")], c.w("L0x_bv"), None, v, None)])
    a = Arena(c)
    w, ew, ewT = a.take(2, S), a.take(2, S), a.take(2, S)
    wmax, nwmax = a.take(2), a.take(2)
    kmax, nkmax = a.take(1), a.take(1)
    ek, ekv = a.take(S), a.take(S)
    ekT, ekvT = a.take(2, P), a.take(2, P)
    rden, ratio = a.take(S), a.take(S)
    ident = c.w("identity")
    with nc.Block() as block:
        @block.vector
        def _(dve):
            chain = Chain(dve, c.vector_chain)
            chain.link(nc.vector.tensor_tensor(w, c.w("L0x_pos"), c.w("L0x_band"), ALU.mult))
            chain.link(nc.vector.reduce_max(wmax, w, AX.X))
            nc.vector.tensor_scalar(nwmax, wmax, -1.0, None, ALU.mult).then_inc(c.aux_v.sem, 1)
            for t in range(2):
                dve.wait_ge(c.aux_pe.sem, c.aux_pe.at(2 * t + 2))
                ins = nc.vector.tensor_copy(ewT[:, t, :], c.psum[:, 4 + t, 0:S])
            chain.link(ins)
            chain.clear()
            with dve.Fori(0, B) as b:
                chain.link(nc.vector.reduce_max(kmax, k[:, bass.ds(b * S, S)], AX.X))
                nc.vector.tensor_scalar(nkmax, kmax, -1.0, None, ALU.mult).then_inc(c.aux_v2.sem, 1)
                dve.wait_ge(c.aux_pe2.sem, c.aux_pe2.base + b * 2 + 2)
                nc.vector.tensor_copy(ekvT, c.psum[:, 1, 0:S].rearrange("p (t d) -> p t d", t=2)) \
                    .then_inc(c.aux_v3.sem, 1)
                dve.wait_ge(c.aux_pe3.sem, c.aux_pe3.base + b * 2 + 2)
                chain.link(nc.vector.reciprocal(rden, c.psum[:, 2, 0:S]))
                chain.link(nc.vector.tensor_tensor(ratio, c.psum[:, 3, 0:S], rden, ALU.mult))
                q = sq[:, bass.ds(b * S, S)]
                chain.link(nc.vector.tensor_tensor(q, q, ratio, ALU.mult))
                chain.clear()

        @block.scalar
        def _(act):
            act.wait_ge(c.aux_v.sem, c.aux_v.at(1))
            for t in range(2):
                nc.scalar.activation(ew[:, t, :], w[:, t, :], ACT.Exp, bias=nwmax[:, t:t + 1]) \
                    .then_inc(c.aux_s.sem, 1)
            with act.Fori(0, B) as b:
                act.wait_ge(c.aux_v2.sem, c.aux_v2.base + b + 1)
                nc.scalar.activation(ek, k[:, bass.ds(b * S, S)], ACT.Exp, bias=nkmax).then_inc(c.aux_s2.sem, 1)
                act.wait_ge(c.aux_pe2.sem, c.aux_pe2.base + b * 2 + 1)
                nc.scalar.copy(ekT, c.psum[:, 0, 0:S].rearrange("p (t d) -> p t d", t=2)) \
                    .then_inc(c.aux_s3.sem, 1)

        @block.gpsimd
        def _(pool):
            with pool.Fori(0, B) as b:
                pool.wait_ge(c.aux_s2.sem, c.aux_s2.base + b + 1)
                nc.gpsimd.tensor_tensor(ekv, ek, v[:, bass.ds(b * S, S)], ALU.mult).then_inc(c.aux_p.sem, 1)

        @block.tensor
        def _(pe):
            pe.wait_ge(c.aux_s.sem, c.aux_s.at(2))
            for j in range(2):
                for t in range(2):
                    nc.tensor.transpose(c.psum[:, 4 + j, t * P:(t + 1) * P], ew[:, t, j * P:(j + 1) * P], ident) \
                        .then_inc(c.aux_pe.sem, 1)
            with pe.Fori(0, B) as b:
                for n, (src, sig) in enumerate(((ek, c.aux_s2), (ekv, c.aux_p))):
                    pe.wait_ge(sig.sem, sig.base + b + 1)
                    for t in range(2):
                        mm = nc.tensor.transpose(c.psum[:, n, t * P:(t + 1) * P], src[:, t * P:(t + 1) * P], ident)
                    mm.then_inc(c.aux_pe2.sem, 1)
                for n, (src, sig) in enumerate(((ekT, c.aux_s3), (ekvT, c.aux_v3))):
                    pe.wait_ge(sig.sem, sig.base + b + 1)
                    for t in range(2):
                        mm = nc.tensor.matmul(c.psum[:, 2 + n, 0:S], src[:, t, :], ewT[:, t, :],
                                              start=(t == 0), stop=(t == 1))
                    mm.then_inc(c.aux_pe3.sem, 1)
    for s, n in ((c.aux_v, 1), (c.aux_s, 2), (c.aux_pe, 4), (c.aux_v2, B), (c.aux_v3, B), (c.aux_s2, B),
                 (c.aux_s3, B), (c.aux_p, B), (c.aux_pe2, 2 * B), (c.aux_pe3, 2 * B)):
        s.advance(n)
    project_stage(c, [([sq], [c.w("L0x_wo")], c.w("L0x_bo"), None, k, emb)])
    norm_stage(c, k, c.HN, "eps5", gain=c.w("L0x_gamma"), shift=c.w("L0x_beta"))
    w1, b1, w2 = c.w("L0x_w1"), c.w("L0x_b1"), c.w("L0x_w2")
    hidden = [c.T[:, t, :] for t in range(4)]
    project_stage(c, [([c.HN], [w1[:, t * P:(t + 1) * P]], b1[:, t:t + 1], ACT.Relu, hidden[t], None)
                      for t in range(4)])
    project_stage(c, [(hidden, [w2[:, t, :] for t in range(4)], c.w("L0x_b2"), None, c.HN, c.HN)])
    norm_stage(c, c.HN, c.HN, "eps5", gain=c.w("L0x_gamma"), shift=c.w("L0x_beta"))
    add_stage(c, c.X, c.X, c.HN)



E = 8
NT = N // P


def route_stage(c, src, router, bias, w_t, a, mode, capacity=None):
    nc = c.nc
    ident = c.w("identity")
    logits, p, t1, t2, first, second, weight, chosen = [a.take(NT, E) for _ in range(8)]
    before = a.take(NT, E)
    m, r = a.take(NT), a.take(NT)
    falling = c.w("falling").unsqueeze(1).broadcast_to([P, NT, E])
    ps = c.psum[:, 0, 0:NT * E].rearrange("p (t e) -> p t e", e=E)

    def over(x):
        return x.unsqueeze(2).broadcast_to([P, NT, E])

    with nc.Block() as block:
        @block.tensor
        def _(pe):
            for t in range(NT):
                mm = nc.tensor.matmul(ps[:, t, :], src[:, t * P:(t + 1) * P], router, start=True, stop=True)
            mm.then_inc(c.aux_pe.sem, 1)
            if capacity is not None:
                pe.wait_ge(c.aux_v2.sem, c.aux_v2.at(1))
                flat = chosen.rearrange("p t e -> p (t e)")
                nc.tensor.matmul(c.psum[:, 1, 0:P], c.w("upper"), flat, start=True, stop=True)
                nc.tensor.matmul(c.psum[:, 2, 0:P], c.w("ones"), flat, start=True, stop=True) \
                    .then_inc(c.aux_pe2.sem, 1)
            pe.wait_ge(c.aux_v3.sem, c.aux_v3.at(1))
            for t in range(NT):
                mm = nc.tensor.transpose(c.psum[0:E, 4 + t // 4, (t % 4) * P:(t % 4 + 1) * P], weight[:, t, :], ident)
            mm.then_inc(c.aux_pe3.sem, 1)

        @block.gpsimd
        def _(pool):
            nc.gpsimd.memset(w_t, 0.0).then_inc(c.aux_p.sem, 1)

        @block.scalar
        def _(act):
            act.wait_ge(c.aux_v.sem, c.aux_v.at(1))
            nc.scalar.activation(p, t1, ACT.Exp).then_inc(c.aux_s.sem, 1)
            act.wait_ge(c.aux_p.sem, c.aux_p.at(1))
            act.wait_ge(c.aux_pe3.sem, c.aux_pe3.at(1))
            for i in range(NC):
                nc.scalar.copy(w_t[0:E, i * CH:(i + 1) * CH], c.psum[0:E, 4 + i, :])

        @block.vector
        def _(dve):
            ch = Chain(dve, c.vector_chain)
            v = nc.vector
            dve.wait_ge(c.aux_pe.sem, c.aux_pe.at(1))
            if bias is None:
                ch.link(v.tensor_copy(logits, ps))
            else:
                ch.link(v.tensor_tensor(logits, ps, bias.unsqueeze(1).broadcast_to([P, NT, E]), ALU.add))
            ch.link(v.reduce_max(m, logits, AX.X))
            v.tensor_tensor(t1, logits, over(m), ALU.subtract).then_inc(c.aux_v.sem, 1)
            dve.wait_ge(c.aux_s.sem, c.aux_s.at(1))
            ch.link(v.reduce_sum(m, p, AX.X))
            ch.link(v.reciprocal(r, m))
            ch.link(v.tensor_tensor(p, p, over(r), ALU.mult))

            def likeliest(q, one_hot):
                ch.link(v.reduce_max(m, q, AX.X))
                ch.link(v.tensor_tensor(t1, q, over(m), ALU.is_equal))
                ch.link(v.tensor_tensor(t1, t1, falling, ALU.mult))
                ch.link(v.reduce_max(m, t1, AX.X))
                ch.link(v.tensor_tensor(one_hot, t1, over(m), ALU.is_equal))

            likeliest(p, first)
            if mode == "single":
                ch.link(v.tensor_copy(chosen, first))
            else:
                ch.link(v.scalar_tensor_tensor(t2, first, -3.0, p, ALU.mult, ALU.add))
                likeliest(t2, second)
                ch.link(v.tensor_tensor(chosen, first, second, ALU.add))
            ch.link(v.tensor_tensor(weight, chosen, p, ALU.mult))
            if mode == "pair_normed":
                ch.link(v.reduce_sum(m, weight, AX.X))
                ch.link(v.reciprocal(r, m))
                ch.link(v.tensor_tensor(weight, weight, over(r), ALU.mult))
            if capacity is not None:
                v.memset(before[:, 0, :], 0.0).then_inc(c.aux_v2.sem, 1)
                dve.wait_ge(c.aux_pe2.sem, c.aux_pe2.at(1))
                totals = c.psum[:, 2, 0:P].rearrange("p (t e) -> p t e", e=E)
                ch.link(v.tensor_copy(t2, totals))
                for t in range(1, NT):
                    ch.link(v.tensor_tensor(before[:, t, :], before[:, t - 1, :], t2[:, t - 1, :], ALU.add))
                ch.link(v.tensor_tensor(t1, c.psum[:, 1, 0:P].rearrange("p (t e) -> p t e", e=E), before, ALU.add))
                ch.link(v.tensor_scalar(t1, t1, float(capacity), None, ALU.is_le))
                v.tensor_tensor(weight, weight, t1, ALU.mult).then_inc(c.aux_v3.sem, 1)
            else:
                v.memset(before[:, 0, :], 0.0).then_inc(c.aux_v3.sem, 1)
            dve.wait_ge(c.aux_v3.sem, c.aux_v3.at(1))
            ch.clear()
    for s in (c.aux_pe, c.aux_pe3, c.aux_v, c.aux_s, c.aux_v3, c.aux_p):
        s.advance(1)
    if capacity is not None:
        c.aux_pe2.advance(1)
        c.aux_v2.advance(1)


def expert_stage(c, src, experts, w_t, a, out_bias=None):
    nc = c.nc
    units = [(e, i) for e in range(len(experts)) for i in range(len(experts[e][1]))]
    gated = experts[0][2][0].shape[1] > 1
    NU, NE = len(units), len(experts)
    routed = [e for e in range(NE) if experts[e][0] is not None]
    NR = len(routed)
    last = [e for e in range(NE)]
    LAG = 2
    act_buf = a.take(2, CH) if gated else None
    hid = a.take(4, CH)
    wb = a.take(2, CH)
    part = a.take(2, CH)
    acc = a.take(CH)
    pick = c.w("pick")
    first_unit = {e: min(n for n, u in enumerate(units) if u[0] == e) for e in range(NE)}
    per_expert = NU // NE

    def gate_bank(n):
        return 2 * (n % 2) if gated else n % 4

    with nc.Block() as block:
        @block.tensor
        def _(pe):
            with pe.Fori(0, NC) as i:
                x = src[:, bass.ds(i * CH, CH)]
                u0, e0, r0 = i * NU, i * NE, i * NR
                for n in range(NU + LAG):
                    if n < NU:
                        e, t = units[n]
                        if t == 0 and experts[e][0] is not None:
                            r = routed.index(e)
                            pe.wait_ge(c.aux_s2.sem, c.aux_s2.base + r0 + r)
                            nc.tensor.matmul(c.psum[:, 6, :], pick[:, experts[e][0], :],
                                             w_t[:, bass.ds(i * CH, CH)], start=True, stop=True) \
                                .then_inc(c.aux_pe3.sem, 1)
                        depth = 2 if gated else 4
                        if n >= depth:
                            pe.wait_ge(c.aux_v.sem, c.aux_v.base + u0 + n - depth + 1)
                        nc.tensor.matmul(c.psum[:, gate_bank(n), :], experts[e][1][t], x, start=True, stop=True) \
                            .then_inc(c.aux_pe.sem, 1)
                        if gated:
                            nc.tensor.matmul(c.psum[:, gate_bank(n) + 1, :], experts[e][2][t], x,
                                             start=True, stop=True).then_inc(c.aux_pe.sem, 1)
                    if n >= LAG:
                        k = n - LAG
                        e, t = units[k]
                        if t == 0:
                            pe.wait_ge(c.aux_v2.sem, c.aux_v2.base + e0 + max(e - 1, 0))
                        pe.wait_ge(c.aux_v.sem, c.aux_v.base + u0 + k + 1)
                        mm = nc.tensor.matmul(c.psum[:, 4 + e % 2, :], experts[e][3][t], hid[:, k % 4, :],
                                              start=(t == 0), stop=(t == per_expert - 1))
                        mm.then_inc(c.aux_pe2.sem, 1)
                if out_bias is not None:
                    pe.wait_ge(c.out_added.sem, c.out_added.base + i)
                    nc.tensor.matmul(c.psum[:, 7, :], out_bias, w_t[:, bass.ds(i * CH, CH)],
                                     start=True, stop=True) \
                        .then_inc(c.product_ready.sem, 1)

        @block.scalar
        def _(act):
            with act.Fori(0, NC) as i:
                u0, r0 = i * NU, i * NR
                for n in range(NU):
                    e, t = units[n]
                    if t == 0 and experts[e][0] is not None:
                        r = routed.index(e)
                        act.wait_ge(c.aux_pe3.sem, c.aux_pe3.base + r0 + r + 1)
                        act.wait_ge(c.aux_v2.sem, c.aux_v2.base + i * NE + max(e - 1, 0))
                        nc.scalar.copy(wb[:, r % 2, :], c.psum[:, 6, :]).then_inc(c.aux_s2.sem, 1)
                    if gated:
                        act.wait_ge(c.aux_pe.sem, c.aux_pe.base + 2 * (u0 + n) + 1)
                        if n >= 2:
                            act.wait_ge(c.aux_v.sem, c.aux_v.base + u0 + n - 1)
                        nc.scalar.activation(act_buf[:, n % 2, :], c.psum[:, gate_bank(n), :], ACT.Silu) \
                            .then_inc(c.aux_s.sem, 1)

        @block.vector
        def _(dve):
            chain = Chain(dve, c.vector_chain)
            with dve.Fori(0, NC) as i:
                u0, e0, r0 = i * NU, i * NE, i * NR

                def take(e):
                    dve.wait_ge(c.aux_pe2.sem, c.aux_pe2.base + u0 + (e + 1) * per_expert)
                    if experts[e][0] is None:
                        src_ = c.psum[:, 4 + e % 2, :]
                    else:
                        r = routed.index(e)
                        dve.wait_ge(c.aux_s2.sem, c.aux_s2.base + r0 + r + 1)
                        src_ = part[:, e % 2, :]
                        chain.link(nc.vector.tensor_tensor(src_, c.psum[:, 4 + e % 2, :], wb[:, r % 2, :], ALU.mult))
                    if e == 0:
                        ins = nc.vector.tensor_copy(acc, src_)
                    else:
                        ins = nc.vector.tensor_tensor(acc, acc, src_, ALU.add)
                    ins.then_inc(c.aux_v2.sem, 1)
                    dve.wait_ge(c.aux_v2.sem, c.aux_v2.base + e0 + e + 1)

                for n in range(NU):
                    e, t = units[n]
                    if n >= 4:
                        dve.wait_ge(c.aux_pe2.sem, c.aux_pe2.base + u0 + n - 3)
                    if gated:
                        dve.wait_ge(c.aux_s.sem, c.aux_s.base + u0 + n + 1)
                        dve.wait_ge(c.aux_pe.sem, c.aux_pe.base + 2 * (u0 + n) + 2)
                        ins = nc.vector.tensor_tensor(hid[:, n % 4, :], act_buf[:, n % 2, :],
                                                      c.psum[:, gate_bank(n) + 1, :], ALU.mult)
                    else:
                        dve.wait_ge(c.aux_pe.sem, c.aux_pe.base + u0 + n + 1)
                        ins = nc.vector.tensor_scalar(hid[:, n % 4, :], c.psum[:, gate_bank(n), :],
                                                      experts[e][2][t], 0.0, ALU.add, ALU.max)
                    ins.then_inc(c.aux_v.sem, 1)
                    if t == per_expert - 1 and e >= 1:
                        take(e - 1)
                take(NE - 1)
                xs = c.X[:, bass.ds(i * CH, CH)]
                chain.link(nc.vector.tensor_tensor(xs, xs, acc, ALU.add))
                chain.clear()
                if out_bias is not None:
                    dve.wait_ge(c.product_ready.sem, c.product_ready.base + i + 1)
                    nc.vector.tensor_tensor(xs, xs, c.psum[:, 7, :], ALU.add).then_inc(c.out_added.sem, 1)
    per = 2 if gated else 1
    for s, n in ((c.aux_pe, per * NU), (c.aux_pe2, NU), (c.aux_pe3, NR), (c.aux_s, NU if gated else 0),
                 (c.aux_s2, NR), (c.aux_v, NU), (c.aux_v2, NE)):
        s.advance(NC * n)
    if out_bias is not None:
        c.product_ready.advance(NC)
        c.out_added.advance(NC)


def layer0_experts(c):
    load_stage(c, "L0f", c.dram)
    norm_stage(c, c.X, c.HN, "eps5")
    norm_stage(c, c.HN, c.T[:, 0, :], "epsf", centre=False)
    a = Arena(c)
    w_t = a.take(N)
    route_stage(c, c.T[:, 0, :], c.w("L0f_router"), None, w_t, a, "pair_normed", capacity=int(1.25 * N / E))
    rg, ru, rd = c.w("L0f_rg"), c.w("L0f_ru"), c.w("L0f_rd")
    sg, su, sd = c.w("L0f_sg"), c.w("L0f_su"), c.w("L0f_sd")
    experts = [(e, [rg[:, e, t * P:(t + 1) * P] for t in range(4)], [ru[:, e, t * P:(t + 1) * P] for t in range(4)],
                [rd[:, e, t, :] for t in range(4)]) for e in range(E)]
    experts += [(None, [sg[:, t * P:(t + 1) * P] for t in range(4 * h, 4 * h + 4)],
                 [su[:, t * P:(t + 1) * P] for t in range(4 * h, 4 * h + 4)],
                 [sd[:, t, :] for t in range(4 * h, 4 * h + 4)]) for h in range(2)]
    expert_stage(c, c.HN, experts, w_t, a)



def turn_stage(c, groups):
    nc = c.nc
    ident = c.w("identity")

    def bank(n, k):
        return c.psum[:, n % 8, 0:k * P].rearrange("p (k x) -> p k x", x=P)

    with nc.Block() as block:
        @block.tensor
        def _(pe):
            for n, (views, _) in enumerate(groups):
                if n >= 8:
                    sig = c.product_taken if n % 2 == 0 else c.product_taken_v
                    pe.wait_ge(sig.sem, sig.at((n - 8) // 2 + 1))
                for k, view in enumerate(views):
                    mm = nc.tensor.transpose(bank(n, len(views))[:, k, :], view, ident)
                mm.then_inc(c.product_ready.sem, 1)

        @block.scalar
        def _(act):
            for n in range(0, len(groups), 2):
                views, dst = groups[n]
                act.wait_ge(c.product_ready.sem, c.product_ready.at(n + 1))
                nc.scalar.copy(dst, bank(n, len(views))).then_inc(c.product_taken.sem, 1)

        @block.vector
        def _(dve):
            for n in range(1, len(groups), 2):
                views, dst = groups[n]
                dve.wait_ge(c.product_ready.sem, c.product_ready.at(n + 1))
                nc.vector.tensor_copy(dst, bank(n, len(views))).then_inc(c.product_taken_v.sem, 1)
    c.product_ready.advance(len(groups))
    c.product_taken.advance((len(groups) + 1) // 2)
    c.product_taken_v.advance(len(groups) // 2)


def conv_stage(c, tensors, taps):
    nc = c.nc
    a = Arena(c)
    acc = [a.take(N) for _ in tensors]
    with nc.Block() as block:
        @block.vector
        def _(dve):
            chain = Chain(dve, c.vector_chain)
            for x, w, y in zip(tensors, taps, acc):
                K = w.shape[1]
                xs = x.rearrange("p (b s) -> p b s", s=S)
                ys = y.rearrange("p (b s) -> p b s", s=S)
                chain.link(nc.vector.tensor_scalar(y, x, w[:, K - 1:K], None, ALU.mult))
                for back in range(1, K):
                    ins = nc.vector.scalar_tensor_tensor(ys[:, :, back:], xs[:, :, 0:S - back],
                                                         w[:, K - 1 - back:K - back], ys[:, :, back:],
                                                         ALU.mult, ALU.add)
                    if back < K - 1:
                        chain.link(ins)
                ins.then_inc(c.aux_v.sem, 1)
            dve.wait_ge(c.aux_v.sem, c.aux_v.at(len(tensors)))
            chain.clear()

        @block.scalar
        def _(act):
            for n, (x, y) in enumerate(zip(tensors, acc)):
                act.wait_ge(c.aux_v.sem, c.aux_v.at(n + 1))
                nc.scalar.activation(x, y, ACT.Silu)
    c.aux_v.advance(len(tensors))


def layer1_attention(c):
    nc = c.nc
    H, D = 8, 16
    load_stage(c, "L1", c.dram)
    norm_stage(c, c.X, c.HN, "eps5")
    q, k, v = c.T[:, 0, :], c.T[:, 1, :], c.T[:, 2, :]
    project_stage(c, [([c.HN], [c.w(f"L1a_w{s}")], None, None, t, None) for s, t in zip("qkv", (q, k, v))])
    conv_stage(c, [q, k, v], [c.w(f"L1a_conv_{s}") for s in "qkv"])

    a = Arena(c)
    mark0 = a.off
    qt, kt, vbt, _, vt = [a.take(2, B, P) for _ in range(5)]
    gates, gsum = a.take(NT, 2 * H), a.take(NT, H)
    lengths, inv = a.take(2, 2 * B * H), a.take(2, 2 * B * H)
    mark = a.off
    GT = 16
    v_r, o_pad, beta_r = a.take(S, 8), a.take(S + GT, 8), a.take(S)
    o_r = o_pad[:, GT:, :]
    end = a.off
    groups = []
    for src, dst in ((q, qt), (k, kt), (v, vt)):
        for th in range(2):
            for b0 in range(0, B, 4):
                groups.append(([src[:, b * S + th * P:b * S + (th + 1) * P] for b in range(b0, b0 + 4)],
                               dst[:, th, b0:b0 + 4, :]))
    turn_stage(c, groups)

    square = c.work[:, mark:mark + 2 * N].rearrange("p (n x) -> p n x", x=N)
    q2 = c.T[:, 0:2, :].rearrange("p t (g w d) -> p t g w d", w=2, d=D)
    k2 = c.T[:, 2:4, :].rearrange("p t (g w d) -> p t g w d", w=2, d=D)
    ps_g = c.psum[:, 0, 0:NT * 2 * H].rearrange("p (n e) -> p n e", e=2 * H)

    def heads(x):
        return x.rearrange("p t b (h d) -> p (t b h) d", d=D)

    with nc.Block() as block:
        @block.tensor
        def _(pe):
            for n in range(NT):
                mm = nc.tensor.matmul(ps_g[:, n, :], c.HN[:, n * P:(n + 1) * P], c.w("L1a_gates"),
                                      start=True, stop=True)
            mm.then_inc(c.aux_pe.sem, 1)

        @block.scalar
        def _(act):
            for n, x in enumerate((qt, kt)):
                nc.scalar.activation(square[:, n, :], x.rearrange("p t b f -> p (t b f)"), ACT.Square) \
                    .then_inc(c.aux_s.sem, 1)
            act.wait_ge(c.aux_v.sem, c.aux_v.at(2))
            nc.scalar.activation(lengths, lengths, ACT.Sqrt, bias=c.w("eps12")).then_inc(c.aux_s.sem, 1)
            act.wait_ge(c.aux_v2.sem, c.aux_v2.at(1))
            nc.scalar.activation(gates, gates, ACT.Sigmoid).then_inc(c.aux_s.sem, 1)

        @block.vector
        def _(dve):
            ch = Chain(dve, c.vector_chain)
            dve.wait_ge(c.aux_pe.sem, c.aux_pe.at(1))
            nc.vector.tensor_tensor(gates, ps_g, c.w("L1a_mix_b").unsqueeze(1).broadcast_to([P, NT, 2 * H]), ALU.add) \
                .then_inc(c.aux_v3.sem, 1)
            dve.wait_ge(c.aux_v3.sem, c.aux_v3.at(1))
            nc.vector.tensor_tensor(gates, gates, c.w("L1a_mix_bias").unsqueeze(1).broadcast_to([P, NT, 2 * H]),
                                    ALU.add).then_inc(c.aux_v2.sem, 1)
            for n in range(2):
                dve.wait_ge(c.aux_s.sem, c.aux_s.at(n + 1))
                nc.vector.reduce_sum(lengths[:, n, :], square[:, n, :].rearrange("p (g d) -> p g d", d=D), AX.X) \
                    .then_inc(c.aux_v.sem, 1)
            dve.wait_ge(c.aux_s.sem, c.aux_s.at(3))
            ch.link(nc.vector.reciprocal(inv, lengths))
            for n, (x, x2) in enumerate(((qt, q2), (kt, k2))):
                for th in range(2):
                    g = slice(th * B * H, (th + 1) * B * H)
                    for w in range(2):
                        nc.vector.tensor_tensor(x2[:, th, :, w, :], heads(x)[:, g, :],
                                                inv[:, n, g].unsqueeze(2).broadcast_to([P, B * H, D]), ALU.mult)
            dve.wait_ge(c.aux_s.sem, c.aux_s.at(4))
            beta = gates[:, :, 0:H].rearrange("p (b t) h -> p t b h", t=2)
            for th in range(2):
                nc.vector.tensor_tensor(vbt[:, th].rearrange("p b (h d) -> p b h d", d=D),
                                        vt[:, th].rearrange("p b (h d) -> p b h d", d=D),
                                        beta[:, th].unsqueeze(3).broadcast_to([P, B, H, D]), ALU.mult)
            ch.clear()
    for s, n in ((c.aux_pe, 1), (c.aux_s, 4), (c.aux_v, 2), (c.aux_v2, 1), (c.aux_v3, 1)):
        s.advance(n)

    q_r = c.work[:, mark0:mark0 + 2 * N].rearrange("p (t d) -> p t d", d=D)
    k_r = c.work[:, mark0 + 2 * N:mark0 + 4 * N].rearrange("p (t d) -> p t d", d=D)
    beta2 = c.HN[:, 0:2 * P].rearrange("p (t g w) -> p t g w", t=2, w=2)
    with nc.Block() as block:
        @block.vector
        def _(dve):
            for th in range(2):
                for w in range(2):
                    nc.vector.tensor_copy(beta2[:, th, :, w].rearrange("p (b h) -> p b h", h=H),
                                          gates[:, :, 0:H].rearrange("p (b t) h -> p t b h", t=2)[:, th])
    groups = []
    for th in range(2):
        for d0 in range(0, 8, 4):
            views = [vbt[:, th].rearrange("p b (g d) -> p (b g) d", d=8)[:, :, d] for d in range(d0, d0 + 4)]
            groups.append((views, v_r[:, th * P:(th + 1) * P, d0:d0 + 4].rearrange("p t d -> p d t")))
        groups.append(([beta2[:, th].rearrange("p g w -> p (g w)")],
                       beta_r[:, th * P:(th + 1) * P].unsqueeze(1)))
    turn_stage(c, groups)
    groups = []
    for th in range(2):
        for src, dst in ((q2, q_r), (k2, k_r)):
            for d0 in range(0, D, 4):
                views = [src[:, th].rearrange("p g w d -> p (g w) d")[:, :, d] for d in range(d0, d0 + 4)]
                groups.append((views, dst[:, th * P:(th + 1) * P, d0:d0 + 4].rearrange("p t d -> p d t")))
    turn_stage(c, groups)

    a.off = end
    C = 4
    NCH = S // C
    tri = a.take(NCH, C * C)
    keys4 = k_r.rearrange("p (n i) d -> p n i d", i=C)
    two, one = a.take(NCH, 2), a.take(NCH, 1)
    flat = c.T[:, :, :].rearrange("p a x -> p (a x)")

    def pairs(back):
        base = sum(NCH * (C - x) * D for x in range(1, back))
        return flat[:, base:base + NCH * (C - back) * D].rearrange("p (n i d) -> p n i d", i=C - back, d=D)

    def entries(first, n=1):
        return tri[:, :, first:first + (n - 1) * (C + 1) + 1:C + 1]

    with nc.Block() as block:
        @block.gpsimd
        def _(pool):
            for back in range(1, C):
                nc.gpsimd.tensor_tensor(pairs(back), keys4[:, :, back:, :], keys4[:, :, 0:C - back, :], ALU.mult) \
                    .then_inc(c.aux_p.sem, 1)

        @block.vector
        def _(dve):
            ch = Chain(dve, c.vector_chain)
            v = nc.vector
            ch.step(v.tensor_scalar(beta_r, beta_r, -1.0, None, ALU.mult))
            ch.link(v.memset(tri, 0.0))
            for back in range(1, C):
                dve.wait_ge(c.aux_p.sem, c.aux_p.at(back))
                ch.step(v.reduce_sum(entries(back * C, C - back), pairs(back), AX.X))
            ch.all_but(0)
            rows = tri.rearrange("p n (i j) -> p n i j", j=C)
            ch.link(v.tensor_tensor(rows, rows, beta_r.rearrange("p (n i) -> p n i", i=C).unsqueeze(3)
                                    .broadcast_to([P, NCH, C, C]), ALU.mult))
            ch.step(v.tensor_tensor(two, entries(9, 2), entries(4, 2), ALU.mult))
            ch.link(v.tensor_tensor(one, entries(13), entries(4), ALU.mult))
            ch.step(v.tensor_tensor(entries(12), entries(12), one, ALU.add))
            ch.link(v.tensor_tensor(entries(8, 2), entries(8, 2), two, ALU.add))
            ch.link(v.tensor_tensor(one, entries(14), entries(8), ALU.mult))
            ch.link(v.tensor_tensor(entries(12), entries(12), one, ALU.add))
            v.memset(entries(0, C), 1.0)
            ch.clear()
    c.aux_p.advance(C - 1)

    CG = GT // C
    slots = c.T[:, 0:3, :].rearrange("p a x -> p (a x)")[:, 0:2 * CG * (C + 1) * 8 * D] \
        .rearrange("p (r c s x) -> p r c s x", r=2, c=CG, s=C + 1)
    qs = [c.T[:, 3, :].rearrange("p (t v d) -> p t v d", v=8, d=D), c.HN[:, :].rearrange("p (t v d) -> p t v d", v=8, d=D)]
    a.off = end + NCH * C * C
    pred, w, tw, u = a.take(C, 8), a.take(C, 8), a.take(C, 8, C), a.take(C, 8)
    sk = c.psum[:, 0, :].rearrange("p (i v d) -> p i v d", v=8, d=D)
    staged = c.T[:, 2, N - 4 * GT * D:].rearrange("p (n r t d) -> p n r t d", n=2, r=2, d=D)
    k_b, kb_b = staged[:, 0], staged[:, 1]
    NI = S // (2 * GT)

    rows = tri.rearrange("p n (i j) -> p (n i) j", j=C)

    def slot(r, cc, s):
        return slots[:, r, cc, s, :].rearrange("p (v d) -> p v d", d=D)

    with nc.Block() as block:
        @block.scalar
        def _(act):
            with act.Fori(0, NI) as i:
                for r in range(2):
                    g = i * 2 + r
                    act.wait_ge(c.aux_v.sem, c.aux_v.base + g - 1)
                    nc.scalar.copy(k_b[:, r], k_r[:, bass.ds(g * GT, GT), :]).then_inc(c.aux_s.sem, 1)

        @block.gpsimd
        def _(pool):
            ch = Chain(pool, c.pool_chain)

            nc.gpsimd.memset(qs[1], 0.0).then_inc(c.aux_p.sem, 1)
            with pool.Fori(0, NI) as i:
                for r in range(2):
                    g = i * 2 + r
                    pool.wait_ge(c.aux_v.sem, c.aux_v.base + g + 1)
                    for s in range(1, C + 1):
                        ch.link(nc.gpsimd.tensor_tensor(slots[:, r, :, s, :], slots[:, r, :, s, :],
                                                        slots[:, r, :, s - 1, :], ALU.add))
                    for cc in range(CG):
                        qv = q_r[:, bass.ds(g * GT + cc * C, C), :].unsqueeze(2).broadcast_to([P, C, 8, D])
                        ins = nc.gpsimd.tensor_tensor(qs[r][:, cc * C:(cc + 1) * C],
                                                      slots[:, r, cc, 1:C + 1, :].rearrange("p s (v d) -> p s v d", d=D),
                                                      qv, ALU.mult)
                    ins.then_inc(c.aux_p.sem, 1)
                ch.clear()

        @block.vector
        def _(dve):
            ch = Chain(dve, c.vector_chain)
            v = nc.vector
            ch.link(v.memset(slot(0, 0, 0), 0.0))
            ch.clear()
            with dve.Fori(0, NI) as i:
                for r in range(2):
                    g = i * 2 + r
                    dve.wait_ge(c.aux_s.sem, c.aux_s.base + g + 1)
                    ch.link(v.tensor_tensor(kb_b[:, r], k_b[:, r], beta_r[:, bass.ds(g * GT, GT)].unsqueeze(2)
                                            .broadcast_to([P, GT, D]), ALU.mult))
                    for cc in range(CG):
                        old = slot(r, cc, 0).unsqueeze(1).broadcast_to([P, C, 8, D])
                        tok = slice(cc * C, (cc + 1) * C)
                        ch.link(v.tensor_tensor(sk, old, kb_b[:, r, tok].unsqueeze(2).broadcast_to([P, C, 8, D]),
                                                ALU.mult))
                        ch.link(v.reduce_sum(pred, sk, AX.X))
                        ch.link(v.tensor_tensor(w, pred, v_r[:, bass.ds(g * GT + cc * C, C), :], ALU.add))
                        T4 = rows[:, bass.ds((g * CG + cc) * C, C), :].unsqueeze(2).broadcast_to([P, C, 8, C])
                        ch.link(v.tensor_tensor(tw, T4, w.rearrange("p j v -> p v j").unsqueeze(1)
                                                .broadcast_to([P, C, 8, C]), ALU.mult))
                        ch.link(v.reduce_sum(u, tw, AX.X))
                        ch.link(v.tensor_tensor(slots[:, r, cc, 1:C + 1, :].rearrange("p s (v d) -> p s v d", d=D),
                                                u.unsqueeze(3).broadcast_to([P, C, 8, D]),
                                                k_b[:, r, tok].unsqueeze(2).broadcast_to([P, C, 8, D]), ALU.mult))
                        nxt = slots[:, r, cc + 1, 0, :] if cc < CG - 1 else slots[:, 1 - r, 0, 0, :]
                        ins = v.reduce_sum(nxt, slots[:, r, cc].rearrange("p s x -> p x s"), AX.X)
                        if cc < CG - 1:
                            ch.link(ins)
                        else:
                            ins.then_inc(c.aux_v.sem, 1)
                            dve.wait_ge(c.aux_v.sem, c.aux_v.base + g + 1)
                        if cc == 0:
                            dve.wait_ge(c.aux_p.sem, c.aux_p.base + g + 1)
                            ch.step(v.reduce_sum(o_pad[:, bass.ds(g * GT, GT), :], qs[1 - r], AX.X))
                ch.link(v.tensor_copy(pred, u))
                ch.clear()
            dve.wait_ge(c.aux_p.sem, c.aux_p.base + 2 * NI + 1)
            v.reduce_sum(o_pad[:, S:S + GT, :], qs[1], AX.X)
    c.aux_s.advance(2 * NI)
    c.aux_v.advance(2 * NI)
    c.aux_p.advance(2 * NI + 1)

    o_t = qt
    groups = []
    for th in range(2):
        for d0 in range(0, 8, 4):
            views = [o_r[:, th * P:(th + 1) * P, d] for d in range(d0, d0 + 4)]
            dst = o_t[:, th].rearrange("p b (g d) -> p d (b g)", d=8)[:, d0:d0 + 4, :]
            groups.append((views, dst))
    turn_stage(c, groups)

    def wide(x, th):
        return x[:, th].rearrange("p b (h d) -> p b h d", d=D)

    ms = lengths[:, 0, :]
    with nc.Block() as block:
        @block.vector
        def _(dve):
            ch = Chain(dve, c.vector_chain)
            v = nc.vector
            gate = gates[:, :, H:2 * H].rearrange("p (b t) h -> p t b h", t=2)
            flat = "p t b f -> p (t b f)"
            ch.link(v.tensor_tensor(o_t.rearrange(flat), o_t.rearrange(flat), vt.rearrange(flat), ALU.subtract))
            for th in range(2):
                ch.link(v.tensor_tensor(wide(o_t, th), wide(o_t, th), gate[:, th].unsqueeze(3)
                                        .broadcast_to([P, B, H, D]), ALU.mult))
            v.tensor_tensor(o_t.rearrange(flat), o_t.rearrange(flat), vt.rearrange(flat), ALU.add) \
                .then_inc(c.aux_v.sem, 1)
            dve.wait_ge(c.aux_s.sem, c.aux_s.at(1))
            v.reduce_sum(ms, kt.rearrange("p t b (h d) -> p (t b h) d", d=D), AX.X).then_inc(c.aux_v.sem, 1)
            dve.wait_ge(c.aux_s.sem, c.aux_s.at(2))
            ch.link(v.reciprocal(inv[:, 0, :], ms))
            ch.link(v.tensor_tensor(heads(o_t), heads(o_t), inv[:, 0, :].unsqueeze(2)
                                    .broadcast_to([P, 2 * B * H, D]), ALU.mult))
            ch.link(v.tensor_tensor(heads(o_t), heads(o_t), c.w("L1a_onorm").unsqueeze(1)
                                    .broadcast_to([P, 2 * B * H, D]), ALU.mult))
            ch.clear()

        @block.scalar
        def _(act):
            act.wait_ge(c.aux_v.sem, c.aux_v.at(1))
            nc.scalar.activation(kt.rearrange("p t b f -> p (t b f)"), o_t.rearrange("p t b f -> p (t b f)"),
                                 ACT.Square).then_inc(c.aux_s.sem, 1)
            act.wait_ge(c.aux_v.sem, c.aux_v.at(2))
            nc.scalar.activation(ms, ms, ACT.Sqrt, scale=1.0 / D, bias=c.w("eps5")).then_inc(c.aux_s.sem, 1)
    c.aux_v.advance(2)
    c.aux_s.advance(2)
    groups = []
    o_f = c.T[:, 0, :]
    for b in range(0, B, 2):
        groups.append(([o_t[:, th, bb, :] for bb in (b, b + 1) for th in range(2)],
                       o_f[:, b * S:(b + 2) * S].rearrange("p (k x) -> p k x", x=P)))
    turn_stage(c, groups)
    project_stage(c, [([o_f], [c.w("L1a_wo")], None, None, c.X, c.X)])


def layer1_cross(c):
    norm_stage(c, c.X, c.HN, "eps5")
    wq, wk, wo = c.w("L1x_wq"), c.w("L1x_wk"), c.w("L1x_wo")

    def prepare(nc, dve, chain, b, mb):
        far = mb[:, 2 * S:3 * S]
        chain.link(nc.vector.tensor_scalar(far, c.w("position"), c.valid[:, bass.ds(b, 1)], NEG, ALU.is_ge, ALU.mult))
        for qt in range(2):
            chain.link(nc.vector.tensor_tensor(mb[:, qt * S:(qt + 1) * S], c.w("causal")[:, qt, :], far, ALU.min))

    attention_stage(c, 16, 64, c.HN, c.CT, c.CT, [wq[:, t, :] for t in range(8)], c.w("L1x_bq"),
                    [wk[:, t, :] for t in range(8)], c.w("L1x_bk"), c.w("L1x_wv"), c.w("L1x_bv"),
                    [wo[:, t, :] for t in range(8)], c.w("L1x_bo"), scale=1.0 / 8.0,
                    mask=lambda mb, qt: mb[:, qt * S:(qt + 1) * S], prepare_mask=prepare, mask_words=3 * S)


def layer1_experts(c):
    norm_stage(c, c.X, c.HN, "eps5")
    a = Arena(c)
    w_t = a.take(N)
    route_stage(c, c.HN, c.w("L1f_gate"), c.w("L1f_gate_b"), w_t, a, "pair")
    w1, b1, w2 = c.w("L1f_w1"), c.w("L1f_b1"), c.w("L1f_w2")
    experts = [(e, [w1[:, e, t * P:(t + 1) * P] for t in range(2)], [b1[:, e, t:t + 1] for t in range(2)],
                [w2[:, e, t, :] for t in range(2)]) for e in range(E)]
    expert_stage(c, c.HN, experts, w_t, a, out_bias=c.w("L1f_b2"))



def trig_stage(c, trig):
    nc = c.nc
    a = Arena(c)
    ang, turns, r, absr, sn, cs = [a.take(2, S) for _ in range(6)]
    theta = c.w("L2a_theta")
    flat = "p t s -> p (t s)"
    MAGIC = 1.5 * 2.0 ** 23
    two_pi = 2.0 * np.pi
    hi = 6.28125
    mid = float(np.float32(np.round((two_pi - hi) * 2.0 ** 20) / 2.0 ** 20))
    lo = float(two_pi - hi - mid)
    edge = 3.1415925
    with nc.Block() as block:
        @block.vector
        def _(dve):
            ch = Chain(dve, c.vector_chain)
            v = nc.vector
            for t in range(2):
                ch.link(v.tensor_scalar(ang[:, t], c.w("position"), theta[:, t:t + 1], None, ALU.mult))
            ch.link(v.tensor_scalar(turns, ang, float(1.0 / two_pi), MAGIC, ALU.mult, ALU.add))
            ch.link(v.tensor_scalar(turns, turns, MAGIC, None, ALU.subtract))
            ch.link(v.scalar_tensor_tensor(r, turns, -hi, ang, ALU.mult, ALU.add))
            ch.link(v.scalar_tensor_tensor(ang, turns, -mid, r, ALU.mult, ALU.add))
            ch.link(v.scalar_tensor_tensor(r, turns, -lo, ang, ALU.mult, ALU.add))
            v.tensor_scalar(r, r, edge, -edge, ALU.min, ALU.max).then_inc(c.aux_v.sem, 1)
            dve.wait_ge(c.aux_s.sem, c.aux_s.at(1))
            ch.link(v.tensor_scalar(turns, sn, c.w("L2a_sine_rows"), None, ALU.mult))
            ch.link(v.scalar_tensor_tensor(trig.rearrange(flat), cs.rearrange(flat), c.w("L2a_cosine_rows"),
                                           turns.rearrange(flat), ALU.mult, ALU.add))
            ch.clear()

        @block.scalar
        def _(act):
            ch = Chain(act, c.scalar_chain)
            act.wait_ge(c.aux_v.sem, c.aux_v.at(1))
            ch.link(nc.scalar.activation(absr, r, ACT.Abs))
            nc.scalar.activation(sn, r, ACT.Sin)
            nc.scalar.activation(cs, absr, ACT.Sin, scale=-1.0, bias=c.w("half_pi")).then_inc(c.aux_s.sem, 1)
            act.wait_ge(c.aux_s.sem, c.aux_s.at(1))
            ch.clear()
    c.aux_v.advance(1)
    c.aux_s.advance(1)


def layer2_attention(c):
    nc = c.nc
    H, D = 8, 16
    load_stage(c, "L2", c.dram)
    norm_stage(c, c.X, c.HN, "eps5")
    trig = c.T[:, 3, 0:2 * S].rearrange("p (t s) -> p t s", s=S)
    wide_a = Arena(c)
    wide_a.off = 6 * 2 * S
    k0, k1, u = wide_a.take(N), wide_a.take(N), wide_a.take(N)
    q0, q1 = c.T[:, 0, :], c.T[:, 1, :]
    trig_stage(c, trig)
    wq, wk = c.w("L2a_wq"), c.w("L2a_wk")
    bq, bk = c.w("L2a_bq"), c.w("L2a_bk")
    jobs = [([c.HN], [w[:, t, :]], bb[:, t:t + 1], ACT.Silu, dst, None)
            for w, bb, ds in ((wq, bq, (q0, q1)), (wk, bk, (k0, k1))) for t, dst in enumerate(ds)]
    jobs.append(([c.HN], [c.w("L2a_wu")], c.w("L2a_bu"), None, u, None))
    project_stage(c, jobs)

    a = Arena(c)
    vsb, vb = a.take(2, S), a.take(2, H, P)
    assert a.off <= 6 * 2 * S
    a.off = wide_a.off
    decay = a.take(H, 2 * S)
    qk = c.T[:, 2, :].rearrange("p (b t s) -> p b t s", t=4, s=S)
    qb, kb = qk[:, :, 0:2, :], qk[:, :, 2:4, :]
    en = a.take(4, 2 * S)
    LAG = 2
    with nc.Block() as block:
        @block.gpsimd
        def _(pool):
            nc.gpsimd.memset(vb, 0.0).then_inc(c.aux_v.sem, 1)
            with pool.Fori(0, B // 2) as i:
                for s in range(2):
                    pool.wait_ge(c.out_copied.sem, c.out_copied.base + i * 2 + s - 1)
                    src = bass.ds((i * 2 + s) * S, S)
                    nc.gpsimd.tensor_copy(vsb[:, s, :], c.HN[:, src]).then_inc(c.staged.sem, 1)
                    for t, (q, k) in enumerate(((q0, k0), (q1, k1))):
                        nc.gpsimd.tensor_tensor(qb[:, s, t, :], q[:, src], trig[:, t, :], ALU.mult)
                        ins = nc.gpsimd.tensor_tensor(kb[:, s, t, :], k[:, src], trig[:, t, :], ALU.mult)
                    ins.then_inc(c.aux_p.sem, 1)

        @block.tensor
        def _(pe):
            with pe.Fori(0, B // 2) as i:
                for s in range(2):
                    n0 = i * 2 + s
                    h0 = n0 * H
                    pe.wait_ge(c.staged.sem, c.staged.base + n0 + 1)
                    pe.wait_ge(c.proj_taken_v.sem, c.proj_taken_v.base + n0)
                    for kt in range(2):
                        mm = nc.tensor.matmul(c.psum[:, 7, kt * P:(kt + 1) * P], vsb[:, s, kt * P:(kt + 1) * P],
                                              c.w("L2a_wv"), start=True, stop=True)
                    mm.then_inc(c.proj_ready.sem, 1)
                    pe.wait_ge(c.aux_p.sem, c.aux_p.base + n0 + 1)
                    for h in range(H + LAG):
                        if h < H:
                            pe.wait_ge(c.aux_v2.sem, c.aux_v2.base + h0 + h - 3)
                            t, base = h // 4, (h % 4) * 32
                            for mt in range(2):
                                mm = nc.tensor.matmul(c.psum[:, h % 4, mt * S:(mt + 1) * S],
                                                      kb[base:base + 32, s, t, mt * P:(mt + 1) * P],
                                                      qb[base:base + 32, s, t, :], start=True, stop=True,
                                                      tile_position=(base, 0))
                            mm.then_inc(c.scores_ready.sem, 1)
                        if h >= LAG:
                            k = h - LAG
                            if k == 0:
                                pe.wait_ge(c.proj_taken_v.sem, c.proj_taken_v.base + n0 + 1)
                                pe.wait_ge(c.out_copied.sem, c.out_copied.base + n0 - 1)
                            pe.wait_ge(c.aux_v2.sem, c.aux_v2.base + h0 + k + 1)
                            for mt in range(2):
                                mm = nc.tensor.matmul(c.psum[:, 5 + s, 0:S], vb[:, mt, k, :],
                                                      en[:, k % 4, mt * S:(mt + 1) * S],
                                                      start=(k == 0 and mt == 0), stop=(k == H - 1 and mt == 1))
                            mm.then_inc(c.mixed_ready.sem, 1)

        @block.scalar
        def _(act):
            for h in range(H):
                ins = nc.scalar.activation(decay[:, h, :], c.w("L2a_lower").rearrange("p t s -> p (t s)"), ACT.Exp,
                                           scale=c.w("L2a_slope")[:, h:h + 1])
            ins.then_inc(c.aux_s.sem, 1)
            with act.Fori(0, B // 2) as i:
                for s in range(2):
                    n0 = i * 2 + s
                    act.wait_ge(c.mixed_ready.sem, c.mixed_ready.base + (n0 + 1) * H)
                    nc.scalar.copy(q0[:, bass.ds(n0 * S, S)], c.psum[:, 5 + s, 0:S]).then_inc(c.out_copied.sem, 1)

        @block.vector
        def _(dve):
            dve.wait_ge(c.aux_s.sem, c.aux_s.at(1))
            dve.wait_ge(c.aux_v.sem, c.aux_v.at(1))
            with dve.Fori(0, B // 2) as i:
                for s in range(2):
                    n0 = i * 2 + s
                    h0 = n0 * H
                    dve.wait_ge(c.proj_ready.sem, c.proj_ready.base + n0 + 1)
                    dve.wait_ge(c.mixed_ready.sem, c.mixed_ready.base + h0)
                    for kt in range(2):
                        dst = vb[:, kt].rearrange("p h x -> p (h x)")
                        dst = bass.AP(tensor=dst.tensor, offset=dst.offset, ap=[dst.ap[0], [P + D, H], [1, D]])
                        ins = nc.vector.tensor_tensor(dst, c.psum[:, 7, kt * P:(kt + 1) * P]
                                                      .rearrange("p (h d) -> p h d", d=D),
                                                      c.w("L2a_bv").rearrange("p (h d) -> p h d", d=D), ALU.add)
                    ins.then_inc(c.proj_taken_v.sem, 1)
                    for h in range(H):
                        dve.wait_ge(c.scores_ready.sem, c.scores_ready.base + h0 + h + 1)
                        dve.wait_ge(c.mixed_ready.sem, c.mixed_ready.base + h0 + h - 3)
                        nc.vector.tensor_tensor(en[:, h % 4, :], c.psum[:, h % 4, :], decay[:, h, :],
                                                ALU.mult).then_inc(c.aux_v2.sem, 1)
    for s, n in ((c.staged, 1), (c.aux_p, 1), (c.proj_ready, 1), (c.proj_taken_v, 1), (c.aux_v2, H),
                 (c.scores_ready, H), (c.mixed_ready, H), (c.out_copied, 1)):
        s.advance(B * n)
    c.aux_s.advance(1)
    c.aux_v.advance(1)
    with nc.Block() as block:
        @block.vector
        def _(dve):
            nc.vector.tensor_copy(c.T[:, 1, :], u)
    norm_stage(c, q0, q0, "eps6", centre=False)
    with nc.Block() as block:
        @block.vector
        def _(dve):
            nc.vector.tensor_tensor(c.T[:, 0, :], c.T[:, 0, :], c.T[:, 1, :], ALU.mult)
    project_stage(c, [([q0], [c.w("L2a_wo")], c.w("L2a_bo"), None, c.X, c.X)])


def layer2_cross(c):
    nc = c.nc
    norm_stage(c, c.X, c.HN, "eps5")
    one_plus = c.w("L2x_scale")
    with nc.Block() as block:
        @block.vector
        def _(dve):
            nc.vector.tensor_scalar(one_plus, one_plus, 1.0, None, ALU.add)
    norm_stage(c, c.HN, c.HN, "eps6", centre=False, gain=one_plus)
    norm_stage(c, c.CT, c.T[:, 3, :], "eps6", centre=False, gain=one_plus)
    for src, name, dst in ((c.HN, "q", c.T[:, 0, :]), (c.T[:, 3, :], "k", c.T[:, 1, :])):
        swapped = c.T[:, 2, :]
        project_stage(c, [([src], [c.w(f"L2x_w{name}")], None, None, dst, None),
                          ([src], [c.w(f"L2x_w{name}_swapped")], None, None, swapped, None)])
        cos = c.w(f"L2x_cos_{name}").unsqueeze(1).broadcast_to([P, B, S])
        sin = c.w(f"L2x_sin_{name}").unsqueeze(1).broadcast_to([P, B, S])
        with nc.Block() as block:
            @block.vector
            def _(dve):
                d3, s3 = (x.rearrange("p (b s) -> p b s", s=S) for x in (dst, swapped))
                nc.vector.tensor_tensor(d3, d3, cos, ALU.mult).then_inc(c.aux_v.sem, 1)
                dve.wait_ge(c.aux_p.sem, c.aux_p.at(1))
                dve.wait_ge(c.aux_v.sem, c.aux_v.at(1))
                nc.vector.tensor_tensor(d3, d3, s3, ALU.add)

            @block.gpsimd
            def _(pool):
                s3 = swapped.rearrange("p (b s) -> p b s", s=S)
                nc.gpsimd.tensor_tensor(s3, s3, sin, ALU.mult).then_inc(c.aux_p.sem, 1)
        c.aux_v.advance(1)
        c.aux_p.advance(1)
    fill = 2.3819763e38
    madd = c.T[:, 2, :]
    with nc.Block() as block:
        @block.vector
        def _(dve):
            nc.vector.tensor_copy(madd, c.attend[:, :].bitcast(U8)).then_inc(c.aux_v.sem, 1)
            dve.wait_ge(c.aux_v.sem, c.aux_v.at(1))
            nc.vector.tensor_scalar(madd, madd, 1.0, fill, ALU.subtract, ALU.mult)
    c.aux_v.advance(1)

    def prepare(nc, dve, chain, b, mb):
        chain.link(nc.vector.tensor_copy(mb, madd[:, bass.ds(b * S, S)]))

    ident = c.w("identity")
    attention_stage(c, 4, 32, c.T[:, 0, :], c.T[:, 1, :], c.T[:, 3, :], [ident], None, [ident], None,
                    c.w("L2x_wv"), None, [c.w("L2x_wo")], None, scale=float(32 ** -0.5),
                    mask=lambda mb, qt: mb, prepare_mask=prepare, mask_words=S, shared_kv=True)


MAGIC = 1.5 * 2.0 ** 23


def layer2_mlp(c):
    nc = c.nc
    I = 352
    rows = [P, P, I - 2 * P]
    norm_stage(c, c.X, c.HN, "eps5")
    a = Arena(c)
    xq, hq = a.take(N // 2).bitcast(BF16), [a.take(N // 2).bitcast(BF16) for _ in range(3)]
    w_int = a.take(9, P)
    w_bf = a.take(9, P // 2).bitcast(BF16)
    w_t = a.take(9, P // 2).bitcast(BF16)
    ident = a.take(P // 2).bitcast(BF16)
    amax, ws, wr = a.take(8), a.take(9), a.take(9)
    xs, part = a.take(4), a.take(2, CH)
    peak = a.take(16)
    tmp = a.take(N)
    wg, wu, wd = c.w("L2f_gate"), c.w("L2f_up"), c.w("L2f_down")
    blocks = [(wg[0:rows[t], t, :], rows[t], 0 + t) for t in range(3)] + \
             [(wu[0:rows[t], t, :], rows[t], 3 + t) for t in range(3)]
    sigm = c.w("L2f_clips")

    with nc.Block() as block:
        @block.scalar
        def _(act):
            nc.scalar.activation(sigm, sigm, ACT.Sigmoid).then_inc(c.aux_s.sem, 1)
            nc.scalar.copy(ident, c.w("identity"))

        @block.gpsimd
        def _(pool):
            pool.wait_ge(c.aux_v.sem, c.aux_v.at(1))
            nc.gpsimd.partition_all_reduce(amax[:, 1:2], amax[:, 0:1], P, bass.bass_isa.ReduceOp.max) \
                .then_inc(c.aux_p.sem, 1)

        @block.vector
        def _(dve):
            ch = Chain(dve, c.vector_chain)
            v = nc.vector
            v.tensor_reduce(amax[:, 0:1], c.HN[:, :], AX.X, ALU.max, apply_absolute_value=True) \
                .then_inc(c.aux_v.sem, 1)
            ch.link(v.memset(ws, 127.0))
            for src, n, i in blocks:
                ch.link(v.tensor_reduce(ws[0:n, i:i + 1], src, AX.X, ALU.max, apply_absolute_value=True))
            ch.link(v.tensor_reduce(ws[:, 6:7], wd, AX.X, ALU.max, apply_absolute_value=True))
            ch.link(v.tensor_scalar(ws, ws, float(1.0 / 127.0), None, ALU.mult))
            ch.link(v.reciprocal(wr, ws))
            for src, n, i in blocks:
                ch.link(v.tensor_scalar(w_int[0:n, i, :], src, wr[0:n, i:i + 1], MAGIC, ALU.mult, ALU.add))
            for i in range(3):
                ch.link(v.tensor_scalar(w_int[:, 6 + i, 0:rows[i]], wd[:, i * P:i * P + rows[i]], wr[:, 6:7], MAGIC,
                                        ALU.mult, ALU.add))
            for lo, hi, r in ((0, 2, P), (2, 3, rows[2]), (3, 5, P), (5, 6, rows[2])):
                w = w_int[0:r, lo:hi, :]
                ch.link(v.tensor_scalar(w, w, MAGIC, 127.0, ALU.subtract, ALU.min))
                ch.link(v.tensor_scalar(w_bf[0:r, lo:hi, :], w, -128.0, None, ALU.max))
            for i in range(3):
                w = w_int[:, 6 + i, 0:rows[i]]
                ch.link(v.tensor_scalar(w, w, MAGIC, 127.0, ALU.subtract, ALU.min))
                ch.link(v.tensor_scalar(w_bf[:, 6 + i, 0:rows[i]], w, -128.0, None, ALU.max))
            dve.wait_ge(c.aux_p.sem, c.aux_p.at(1))
            dve.wait_ge(c.aux_s.sem, c.aux_s.at(1))
            ch.link(v.tensor_tensor(xs[:, 1:2], amax[:, 1:2], sigm[:, 0:1], ALU.mult))
            ch.link(v.tensor_scalar(xs[:, 0:1], xs[:, 1:2], float(1.0 / 127.0), None, ALU.mult))
            ch.link(v.reciprocal(xs[:, 1:2], xs[:, 0:1]))
            ch.link(v.tensor_scalar(tmp, c.HN[:, :], xs[:, 1:2], MAGIC, ALU.mult, ALU.add))
            ch.link(v.tensor_scalar(tmp, tmp, MAGIC, 127.0, ALU.subtract, ALU.min))
            ch.link(v.tensor_scalar(xq, tmp, -128.0, None, ALU.max))
            ch.link(v.tensor_scalar(ws[:, 0:6], ws[:, 0:6], xs[:, 0:1], None, ALU.mult))
            ch.clear()
    c.aux_v.advance(1)
    c.aux_p.advance(1)
    c.aux_s.advance(1)

    turned = c.psum[:, 0:4, :].rearrange("p a x -> p (a x)").bitcast(BF16)
    order = [(i, (rows[i % 3] if i < 6 else P), (P if i < 6 else rows[i - 6])) for i in range(9)]
    with nc.Block() as block:
        @block.tensor
        def _(pe):
            for i, r, m in order:
                mm = nc.tensor.transpose(turned[0:m, i * P:i * P + r], w_bf[0:r, i, 0:m], ident[0:r, 0:r])
            mm.then_inc(c.aux_pe.sem, 1)

        @block.vector
        def _(dve):
            dve.wait_ge(c.aux_pe.sem, c.aux_pe.at(1))
            for i, r, m in order:
                nc.vector.tensor_copy(w_t[0:m, i, 0:r], turned[0:m, i * P:i * P + r])
    c.aux_pe.advance(1)

    units = [(i, t) for i in range(NC) for t in range(3)]
    hidden = [c.T[:, t, :] for t in range(3)]
    with nc.Block() as block:
        @block.tensor
        def _(pe):
            for n, (i, t) in enumerate(units):
                if n >= 4:
                    pe.wait_ge(c.aux_v.sem, c.aux_v.at(n - 3))
                for g in range(2):
                    mm = nc.tensor.matmul(c.psum[0:rows[t], 2 * (n % 4) + g, :], w_t[:, 3 * g + t, 0:rows[t]],
                                          xq[:, i * CH:(i + 1) * CH], start=True, stop=True)
                mm.then_inc(c.aux_pe.sem, 1)

        @block.scalar
        def _(act):
            for n, (i, t) in enumerate(units):
                act.wait_ge(c.aux_pe.sem, c.aux_pe.at(n + 1))
                if n >= 2:
                    act.wait_ge(c.aux_v.sem, c.aux_v.at(n - 1))
                nc.scalar.activation(part[0:rows[t], n % 2, :], c.psum[0:rows[t], 2 * (n % 4), :], ACT.Silu,
                                     scale=ws[0:rows[t], t:t + 1]).then_inc(c.aux_s.sem, 1)

        @block.vector
        def _(dve):
            for n, (i, t) in enumerate(units):
                dve.wait_ge(c.aux_s.sem, c.aux_s.at(n + 1))
                nc.vector.scalar_tensor_tensor(hidden[t][0:rows[t], i * CH:(i + 1) * CH],
                                               c.psum[0:rows[t], 2 * (n % 4) + 1, :], ws[0:rows[t], 3 + t:4 + t],
                                               part[0:rows[t], n % 2, :], ALU.mult, ALU.mult) \
                    .then_inc(c.aux_v.sem, 1)
    for s in (c.aux_pe, c.aux_s, c.aux_v):
        s.advance(len(units))

    with nc.Block() as block:
        @block.vector
        def _(dve):
            ch = Chain(dve, c.vector_chain)
            v = nc.vector
            ch.link(v.memset(peak[:, 0:4], 0.0))
            for t in range(3):
                ch.link(v.tensor_reduce(peak[0:rows[t], t:t + 1], hidden[t][0:rows[t], :], AX.X, ALU.max,
                                        apply_absolute_value=True))
            v.reduce_max(amax[:, 2:3], peak[:, 0:3], AX.X).then_inc(c.aux_v.sem, 1)
            dve.wait_ge(c.aux_p.sem, c.aux_p.at(1))
            ch.link(v.tensor_tensor(xs[:, 2:3], amax[:, 3:4], sigm[:, 1:2], ALU.mult))
            ch.link(v.tensor_scalar(xs[:, 3:4], xs[:, 2:3], float(1.0 / 127.0), None, ALU.mult))
            ch.link(v.reciprocal(xs[:, 2:3], xs[:, 3:4]))
            ch.link(v.tensor_scalar(ws[:, 7:8], ws[:, 6:7], xs[:, 3:4], None, ALU.mult))
            for t in range(3):
                h = hidden[t][0:rows[t], :]
                ch.link(v.tensor_scalar(h, h, xs[0:rows[t], 2:3], MAGIC, ALU.mult, ALU.add))
                ch.link(v.tensor_scalar(h, h, MAGIC, 127.0, ALU.subtract, ALU.min))
                ch.link(v.tensor_scalar(hq[t][0:rows[t], :], h, -128.0, None, ALU.max))
            ch.clear()

        @block.gpsimd
        def _(pool):
            pool.wait_ge(c.aux_v.sem, c.aux_v.at(1))
            nc.gpsimd.partition_all_reduce(amax[:, 3:4], amax[:, 2:3], P, bass.bass_isa.ReduceOp.max) \
                .then_inc(c.aux_p.sem, 1)
    c.aux_v.advance(1)
    c.aux_p.advance(1)

    with nc.Block() as block:
        @block.tensor
        def _(pe):
            for i in range(NC):
                for t in range(3):
                    mm = nc.tensor.matmul(c.psum[:, i, :], w_t[0:rows[t], 6 + t, :],
                                          hq[t][0:rows[t], i * CH:(i + 1) * CH], start=(t == 0), stop=(t == 2))
                mm.then_inc(c.aux_pe.sem, 1)

        @block.vector
        def _(dve):
            for i in range(NC):
                dve.wait_ge(c.aux_pe.sem, c.aux_pe.at(i + 1))
                x = c.X[:, i * CH:(i + 1) * CH]
                nc.vector.scalar_tensor_tensor(x, c.psum[:, i, :], ws[:, 7:8], x, ALU.mult, ALU.add)
    c.aux_pe.advance(NC)



def layer3_attention(c):
    load_stage(c, "L3", c.dram)
    norm_stage(c, c.X, c.HN, "eps5")
    wq, wk = c.w("L3a_wq"), c.w("L3a_wk")
    attention_stage(c, 16, 8, c.HN, c.HN, c.HN, [wq[:, t, :] for t in range(4)], c.w("L3a_bq"),
                    [wk[:, t, :] for t in range(4)], c.w("L3a_bk"), c.w("L3a_wv"), c.w("L3a_bv"), [c.w("L3a_wo")],
                    c.w("L3a_bo"), scale=float(8 ** -0.5), top=32)


def layer3_cross(c):
    nc = c.nc
    H, D = 16, 8
    J = S // H
    norm_stage(c, c.X, c.HN, "eps5")
    q, k = c.T[:, 0, :], c.T[:, 1, :]
    project_stage(c, [([c.HN], [c.w("L3x_wq")], c.w("L3x_bq"), None, q, None),
                      ([c.CT], [c.w("L3x_wk")], c.w("L3x_bk"), None, k, None)])
    a = Arena(c)
    qb, kb, ctx_b = a.take(S), a.take(S), a.take(S)
    vb, probs, ex, turned = a.take(2, P), a.take(2, S), a.take(2, S), a.take(2, S)
    m, r = a.take(2, H), a.take(2, H)
    ident, kmask, vmask = c.w("identity"), c.w("L3x_kmask"), c.w("L3x_vmask")
    scale = float(D ** -0.5)

    def by_head(x):
        return x.rearrange("p (j h) -> p h j", h=H)

    def over(x):
        return x.unsqueeze(1).broadcast_to([P, J, H])

    with nc.Block() as block:
        @block.gpsimd
        def _(pool):
            with pool.Fori(0, B) as b:
                pool.wait_ge(c.mixed_ready.sem, c.mixed_ready.base + b)
                nc.gpsimd.tensor_copy(qb, q[:, bass.ds(b * S, S)])
                nc.gpsimd.tensor_tensor(kb, k[:, bass.ds(b * S, S)], kmask, ALU.mult)
                nc.gpsimd.tensor_copy(ctx_b, c.CT[:, bass.ds(b * S, S)]).then_inc(c.staged.sem, 1)

        @block.tensor
        def _(pe):
            with pe.Fori(0, B) as b:
                pe.wait_ge(c.staged.sem, c.staged.base + b + 1)
                for t in range(2):
                    nc.tensor.matmul(c.psum[:, t, 0:S], qb[:, t * P:(t + 1) * P], kb, start=True, stop=True) \
                        .then_inc(c.scores_ready.sem, 1)
                for t in range(2):
                    mm = nc.tensor.matmul(c.psum[:, 2, t * P:(t + 1) * P], ctx_b[:, t * P:(t + 1) * P],
                                          c.w("L3x_wv"), start=True, stop=True)
                mm.then_inc(c.proj_ready.sem, 1)
                for t in range(2):
                    pe.wait_ge(c.probs_picked.sem, c.probs_picked.base + 2 * b + t + 1)
                    for s in range(2):
                        mm = nc.tensor.transpose(c.psum[:, 3 + s, t * P:(t + 1) * P], probs[:, t, s * P:(s + 1) * P],
                                                 ident)
                mm.then_inc(c.probs_turned.sem, 1)
                pe.wait_ge(c.turned_copied.sem, c.turned_copied.base + 2 * b + 2)
                for s in range(2):
                    mm = nc.tensor.matmul(c.psum[:, 5, 0:S], vb[:, s, :], turned[:, s, :], start=(s == 0),
                                          stop=(s == 1))
                mm.then_inc(c.mixed_ready.sem, 1)

        @block.scalar
        def _(act):
            with act.Fori(0, B) as b:
                for t in range(2):
                    act.wait_ge(c.scores_max.sem, c.scores_max.base + 2 * b + t + 1)
                    nc.scalar.activation(ex[:, t, :], probs[:, t, :], ACT.Exp, scale=scale) \
                        .then_inc(c.probs_ready.sem, 1)
                act.wait_ge(c.probs_turned.sem, c.probs_turned.base + b + 1)
                for s in range(2):
                    nc.scalar.copy(turned[:, s, :], c.psum[:, 3 + s, 0:S]).then_inc(c.turned_copied.sem, 1)
                act.wait_ge(c.mixed_ready.sem, c.mixed_ready.base + b + 1)
                nc.scalar.copy(q[:, bass.ds(b * S, S)], c.psum[:, 5, 0:S]).then_inc(c.mixed_taken.sem, 1)

        @block.vector
        def _(dve):
            chain = Chain(dve, c.vector_chain)
            v = nc.vector
            with dve.Fori(0, B) as b:
                for t in range(2):
                    dve.wait_ge(c.scores_ready.sem, c.scores_ready.base + 2 * b + t + 1)
                    chain.link(v.reduce_max(m[:, t, :], by_head(c.psum[:, t, 0:S]), AX.X))
                    v.tensor_tensor(probs[:, t, :].rearrange("p (j h) -> p j h", h=H),
                                    c.psum[:, t, 0:S].rearrange("p (j h) -> p j h", h=H), over(m[:, t, :]),
                                    ALU.subtract).then_inc(c.scores_max.sem, 1)
                dve.wait_ge(c.proj_ready.sem, c.proj_ready.base + b + 1)
                chain.link(v.tensor_tensor(vb, c.psum[:, 2, 0:S].rearrange("p (t x) -> p t x", x=P),
                                           c.w("L3x_bv").unsqueeze(1).broadcast_to([P, 2, P]), ALU.add))
                chain.link(v.tensor_tensor(vb, vb, vmask.unsqueeze(1).broadcast_to([P, 2, P]), ALU.mult))
                for t in range(2):
                    dve.wait_ge(c.probs_ready.sem, c.probs_ready.base + 2 * b + t + 1)
                    chain.link(v.reduce_sum(r[:, t, :], by_head(ex[:, t, :]), AX.X))
                    chain.link(v.reciprocal(r[:, t, :], r[:, t, :]))
                    v.tensor_tensor(probs[:, t, :].rearrange("p (j h) -> p j h", h=H),
                                    ex[:, t, :].rearrange("p (j h) -> p j h", h=H), over(r[:, t, :]),
                                    ALU.mult).then_inc(c.probs_picked.sem, 1)
                chain.clear()
    for s, n in ((c.staged, 1), (c.scores_ready, 2), (c.scores_max, 2), (c.probs_ready, 2), (c.probs_picked, 2),
                 (c.proj_ready, 1), (c.probs_turned, 1), (c.turned_copied, 2), (c.mixed_ready, 1),
                 (c.mixed_taken, 1)):
        s.advance(B * n)
    project_stage(c, [([q], [c.w("L3x_wo")], c.w("L3x_bo"), None, c.X, c.X)])


def position_attention(c, q, k, v, out, scale):
    nc = c.nc
    a = Arena(c)
    prod, less, ex = a.take(2, N), a.take(2, N), a.take(2, N)
    weighted = a.take(N)
    m, total, inv, mix = a.take(2, S), a.take(S), a.take(S), a.take(S)

    def scores(s):
        return c.psum[:, 4 * s:4 * s + 4, :].rearrange("p a x -> p (a x)")

    def grid(x):
        return x.rearrange("p (m n) -> p m n", n=S)

    def last(x):
        return x.rearrange("p (m n) -> p n m", n=S)

    def run(eng, step, chain=None):
        step(0, 0, True, False)
        if chain is not None:
            chain.clear()
        with eng.Fori(0, (B - 2) // 2) as i:
            step(i * 2 + 1, 1, True, True)
            step(i * 2 + 2, 0, True, True)
            if chain is not None:
                chain.clear()
        step(B - 1, 1, False, True)
        step(B, 0, False, True)
        if chain is not None:
            chain.clear()

    is_last = lambda l: isinstance(l, int) and l == B

    with nc.Block() as block:
        @block.gpsimd
        def _(pool):
            def product(l, s):
                nc.gpsimd.tensor_tensor(grid(prod[:, s]), grid(k),
                                        q[:, bass.ds(l * S, S)].unsqueeze(1).broadcast_to([P, B, S]), ALU.mult) \
                    .then_inc(c.aux_p.sem, 1)

            def step(l, s, more, before):
                if more:
                    if before:
                        pool.wait_ge(c.aux_pe.sem, c.aux_pe.base + l)
                    product(l + 1, 1 - s)
                if before:
                    pool.wait_ge(c.aux_s.sem, c.aux_s.base + l)
                    pool.wait_ge(c.aux_v2.sem, c.aux_v2.base + l)
                    nc.gpsimd.tensor_tensor(weighted, ex[:, 1 - s], v, ALU.mult).then_inc(c.aux_p2.sem, 1)

            product(0, 0)
            run(pool, step)

        @block.tensor
        def _(pe):
            def step(l, s, more, before):
                if is_last(l):
                    return
                pe.wait_ge(c.aux_p.sem, c.aux_p.base + l + 1)
                if before:
                    pe.wait_ge(c.aux_v3.sem, c.aux_v3.base + l)
                for i in range(NC):
                    mm = nc.tensor.matmul(c.psum[:, 4 * s + i, :], c.w("L3f_heads"), prod[:, s, i * CH:(i + 1) * CH],
                                          start=True, stop=True)
                mm.then_inc(c.aux_pe.sem, 1)

            run(pe, step)

        @block.scalar
        def _(act):
            def step(l, s, more, before):
                if is_last(l):
                    return
                act.wait_ge(c.aux_v3.sem, c.aux_v3.base + l + 2)
                nc.scalar.activation(ex[:, s], less[:, s], ACT.Exp, scale=scale).then_inc(c.aux_s.sem, 1)

            run(act, step)

        @block.vector
        def _(dve):
            chain = Chain(dve, c.vector_chain)
            nc.vector.memset(m[:, 0], 0.0).then_inc(c.aux_v3.sem, 1)
            nc.vector.memset(m[:, 1], 0.0).then_inc(c.aux_v2.sem, 1)
            dve.wait_ge(c.aux_v3.sem, c.aux_v3.base + 1)
            dve.wait_ge(c.aux_v2.sem, c.aux_v2.base + 1)

            def step(l, s, more, before):
                if not is_last(l):
                    dve.wait_ge(c.aux_pe.sem, c.aux_pe.base + l + 1)
                    chain.link(nc.vector.reduce_max(m[:, s], last(scores(s)), AX.X))
                    if before:
                        dve.wait_ge(c.aux_s.sem, c.aux_s.base + l)
                    nc.vector.tensor_tensor(grid(less[:, s]), grid(scores(s)),
                                            m[:, s].unsqueeze(1).broadcast_to([P, B, S]),
                                            ALU.subtract).then_inc(c.aux_v3.sem, 1)
                if before:
                    dve.wait_ge(c.aux_s.sem, c.aux_s.base + l)
                    chain.link(nc.vector.reduce_sum(total, last(ex[:, 1 - s]), AX.X))
                    chain.step(nc.vector.reciprocal(inv, total))
                    dve.wait_ge(c.aux_p2.sem, c.aux_p2.base + l)
                    nc.vector.reduce_sum(mix, last(weighted), AX.X).then_inc(c.aux_v2.sem, 1)
                    dve.wait_ge(c.aux_v2.sem, c.aux_v2.base + l + 1)
                    chain.all_but(0)
                    chain.link(nc.vector.tensor_tensor(out[:, bass.ds((l - 1) * S, S)], mix, inv, ALU.mult))

            run(dve, step, chain)
    for s in (c.aux_pe, c.aux_p, c.aux_p2, c.aux_s):
        s.advance(B)
    for s in (c.aux_v2, c.aux_v3):
        s.advance(B + 1)


def layer3_block(c):
    nc = c.nc
    norm_stage(c, c.X, c.HN, "eps5")
    q, k, v, o = (c.T[:, i, :] for i in range(4))
    w, bias = c.w("L3f_win"), c.w("L3f_bin")
    project_stage(c, [([c.HN], [w[:, i * P:(i + 1) * P]], bias[:, i:i + 1], None, dst, None)
                      for i, dst in enumerate((q, k, v))])
    position_attention(c, q, k, v, o, float(32 ** -0.5))
    project_stage(c, [([o], [c.w("L3f_wout")], c.w("L3f_bout"), None, c.HN, c.HN)])
    norm_stage(c, c.HN, c.HN, "eps5", gain=c.w("L3f_g1"), shift=c.w("L3f_h1"))

    a = Arena(c)
    w_t = a.take(N)
    both = a.take(E, P)
    b_col, b_row = a.take(P), a.take(P)
    w1, w2, b1, b2 = c.w("L3f_w1"), c.w("L3f_w2"), c.w("L3f_b1"), c.w("L3f_b2")
    with nc.Block() as block:
        @block.tensor
        def _(pe):
            for e in range(E):
                for f in range(4):
                    mm = nc.tensor.matmul(c.psum[:, e // 4, (e % 4) * P:(e % 4 + 1) * P], w1[:, e, f, :],
                                          w2[:, e, f, :], start=(f == 0), stop=(f == 3))
            mm.then_inc(c.aux_pe.sem, 1)
            for e in range(E):
                for f in range(4):
                    mm = nc.tensor.matmul(c.psum[:, 2, e:e + 1], w2[:, e, f, :], b1[:, e, f:f + 1],
                                          start=(f == 0), stop=(f == 3))
            mm.then_inc(c.aux_pe.sem, 1)
            pe.wait_ge(c.aux_v.sem, c.aux_v.at(2))
            nc.tensor.transpose(c.psum[:, 3, 0:P], b_col, c.w("identity")).then_inc(c.aux_pe.sem, 1)

        @block.scalar
        def _(act):
            act.wait_ge(c.aux_pe.sem, c.aux_pe.at(1))
            nc.scalar.copy(both, c.psum[:, 0:2, :].rearrange("p a (e x) -> p (a e) x", x=P))

        @block.vector
        def _(dve):
            nc.vector.memset(b_col, 0.0).then_inc(c.aux_v.sem, 1)
            dve.wait_ge(c.aux_v.sem, c.aux_v.at(1))
            dve.wait_ge(c.aux_pe.sem, c.aux_pe.at(2))
            nc.vector.tensor_tensor(b_col[:, 0:E], c.psum[:, 2, 0:E], b2, ALU.add).then_inc(c.aux_v.sem, 1)
            dve.wait_ge(c.aux_pe.sem, c.aux_pe.at(3))
            nc.vector.tensor_copy(b_row, c.psum[:, 3, 0:P])
    c.aux_pe.advance(3)
    c.aux_v.advance(2)
    route_stage(c, c.HN, c.w("L3f_wg"), None, w_t, a, "single", capacity=N // E)

    a2 = Arena(c)
    a2.off = a.off
    xe = a2.take(4, CH)
    pick = c.w("pick")
    units = [(i, e) for i in range(NC) for e in range(E)]
    with nc.Block() as block:
        @block.tensor
        def _(pe):
            def spread(n):
                i, e = units[n]
                if n >= 3:
                    pe.wait_ge(c.aux_v.sem, c.aux_v.at(n - 2))
                nc.tensor.matmul(c.psum[:, n % 3, :], pick[:, e, :], w_t[:, i * CH:(i + 1) * CH], start=True,
                                 stop=True).then_inc(c.aux_pe.sem, 1)

            spread(0)
            spread(1)
            for n, (i, e) in enumerate(units):
                if n + 2 < len(units):
                    spread(n + 2)
                pe.wait_ge(c.aux_v.sem, c.aux_v.at(n + 1))
                nc.tensor.matmul(c.psum[:, 4 + i, :], both[:, e, :], xe[:, n % 4, :], start=(e == 0), stop=False) \
                    .then_inc(c.aux_pe2.sem, 1)
                if e == E - 1:
                    nc.tensor.matmul(c.psum[:, 4 + i, :], b_row, w_t[:, i * CH:(i + 1) * CH], start=False,
                                     stop=True).then_inc(c.aux_pe3.sem, 1)

        @block.vector
        def _(dve):
            for n, (i, e) in enumerate(units):
                dve.wait_ge(c.aux_pe.sem, c.aux_pe.at(n + 1))
                if n >= 4:
                    dve.wait_ge(c.aux_pe2.sem, c.aux_pe2.at(n - 3))
                nc.vector.tensor_tensor(xe[:, n % 4, :], c.HN[:, i * CH:(i + 1) * CH], c.psum[:, n % 3, :],
                                        ALU.mult).then_inc(c.aux_v.sem, 1)
            dve.wait_ge(c.aux_v.sem, c.aux_v.at(len(units)))
            for i in range(NC):
                dve.wait_ge(c.aux_pe3.sem, c.aux_pe3.at(i + 1))
                x = c.HN[:, i * CH:(i + 1) * CH]
                nc.vector.tensor_tensor(x, x, c.psum[:, 4 + i, :], ALU.add)
    for s, n in ((c.aux_pe, len(units)), (c.aux_pe2, len(units)), (c.aux_pe3, NC), (c.aux_v, len(units))):
        s.advance(n)
    norm_stage(c, c.HN, c.HN, "eps5", gain=c.w("L3f_g2"), shift=c.w("L3f_h2"))
    add_stage(c, c.X, c.X, c.HN)



class Layout:

    def __init__(self):
        self.parts, self.slots, self.words = {}, {}, {}

    def add(self, pack, name, array):
        array = np.ascontiguousarray(array)
        if array.ndim == 1:
            array = array.reshape(array.shape[0], 1)
        assert array.shape[0] == P, (name, array.shape)
        off = self.words.get(pack, 0)
        flat = array.reshape(P, -1)
        self.parts.setdefault(pack, []).append(flat)
        self.slots[name] = (pack, off, array.shape)
        self.words[pack] = off + flat.shape[1]

    def packed(self):
        return {k: np.ascontiguousarray(np.concatenate(v, axis=1)) for k, v in self.parts.items()}


def columns(v):
    return v.reshape(-1, P).T


def everywhere(v):
    return np.broadcast_to(v.reshape(1, -1), (P, v.size))


def k_tiles(w):
    return w.reshape(-1, P, w.shape[1]).transpose(1, 0, 2)


def padded_heads(w_t):
    out = np.zeros((w_t.shape[0], 4, 4, 32), np.float32)
    out[:, :, :, 0:8] = w_t.reshape(w_t.shape[0], 4, 4, 8)
    return out.reshape(w_t.shape[0], 4, P)


def feature_major(x):
    return np.ascontiguousarray(x.reshape(N, P).T)


def top_rows(w):
    out = np.zeros((P, w.shape[1]), np.float32)
    out[0:w.shape[0]] = w
    return out


def row_tiles(w):
    n = -(-w.shape[0] // P)
    out = np.zeros((n * P, w.shape[1]), np.float32)
    out[0:w.shape[0]] = w
    return out.reshape(n, P, -1).transpose(1, 0, 2)


def lay_out(a):
    L = Layout()
    sm = "small"
    L.add(sm, "average", np.full((P, P), 1.0 / P, np.float32))
    L.add(sm, "ones", np.ones((P, P), np.float32))
    L.add(sm, "one", np.ones((P, 1), np.float32))
    for name, eps in (("eps5", 1e-5), ("eps6", 1e-6), ("eps12", 1e-12), ("epsf", float(np.finfo(np.float32).eps))):
        L.add(sm, name, np.full((P, 1), eps, np.float32))
    L.add(sm, "identity", np.eye(P, dtype=np.float32))
    L.add("L0", "pad8", padded_heads(np.eye(P, dtype=np.float32)))
    for s in "qkv":
        L.add("L0", f"L0a_g{s}", a[f"L0_attn_ln_{s}_g"])
        L.add("L0", f"L0a_h{s}", a[f"L0_attn_ln_{s}_b"])
        L.add("L0", f"L0a_w{s}", a[f"L0_attn_{s}_w"].T)
    L.add("L0", "L0a_bq", a["L0_attn_q_b"])
    L.add("L0", "L0a_bk", a["L0_attn_k_b"])
    L.add("L0", "L0a_bv", everywhere(a["L0_attn_v_b"]))
    L.add("L0", "L0a_beta", everywhere(a["L0_attn_beta_param"]))
    L.add("L0", "L0a_wo", a["L0_attn_o_w"].T)
    L.add("L0", "L0a_bo", a["L0_attn_o_b"])
    L.add("L0", "L0x_band", (np.abs(np.arange(S)[:, None] - np.arange(S)[None, :]) < 32).astype(np.float32)
          .reshape(2, P, S).transpose(1, 0, 2))
    L.add("L0", "L0x_pos", a["L0_xattn_pos_bias"].reshape(2, P, S).transpose(1, 0, 2))
    for s in "qkvo":
        L.add("L0", f"L0x_w{s}", a[f"L0_xattn_w{s}"])
        L.add("L0", f"L0x_b{s}", a[f"L0_xattn_b{s}"])
    L.add("L0", "L0x_gamma", a["L0_xattn_gamma"])
    L.add("L0", "L0x_beta", a["L0_xattn_beta"])
    L.add("L0", "L0x_w1", a["L0_xattn_w1"])
    L.add("L0", "L0x_b1", columns(a["L0_xattn_b1"]))
    L.add("L0", "L0x_w2", k_tiles(a["L0_xattn_w2"]))
    L.add("L0", "L0x_b2", a["L0_xattn_b2"])
    L.add(sm, "falling", everywhere(np.arange(E, 0, -1).astype(np.float32)))
    L.add(sm, "upper", np.triu(np.ones((P, P), np.float32)))
    pick = np.zeros((P, E, P), np.float32)
    pick[np.arange(E), np.arange(E), :] = 1.0
    L.add(sm, "pick", pick)
    L.add("L0f", "L0f_router", a["L0_ffn_router_w"].T)
    for s in ("rg", "ru"):
        L.add("L0f", f"L0f_{s}", a[f"L0_ffn_{s}"].transpose(1, 0, 2))
    L.add("L0f", "L0f_rd", a["L0_ffn_rd"].reshape(E, 4, P, P).transpose(2, 0, 1, 3))
    L.add("L0f", "L0f_sg", a["L0_ffn_sg"])
    L.add("L0f", "L0f_su", a["L0_ffn_su"])
    L.add("L0f", "L0f_sd", k_tiles(a["L0_ffn_sd"]))
    for s in "qkv":
        L.add("L1", f"L1a_w{s}", a[f"L1_attn_{s}_w"])
        L.add("L1", f"L1a_conv_{s}", a[f"L1_attn_conv_{s}_w"])
    L.add("L1", "L1a_gates", np.concatenate([a["L1_attn_b_w"], a["L1_attn_mix_w"]], axis=1))
    nothing = np.zeros(8, np.float32)
    L.add("L1", "L1a_mix_b", everywhere(np.concatenate([nothing, a["L1_attn_mix_b"]])))
    L.add("L1", "L1a_mix_bias", everywhere(np.concatenate([nothing, a["L1_attn_mix_bias"]])))
    L.add("L1", "L1a_onorm", everywhere(a["L1_attn_o_norm_w"]))
    L.add("L1", "L1a_wo", a["L1_attn_o_w"])
    L.add(sm, "position", everywhere(np.arange(S, dtype=np.float32)))
    after = np.arange(S)[None, :] > np.arange(S)[:, None]
    L.add("L1", "causal", np.where(after, np.float32(NEG), np.float32(0)).reshape(2, P, S).transpose(1, 0, 2))
    for s in "qk":
        L.add("L1", f"L1x_w{s}", a[f"L1_xattn_w_{s}"].T.reshape(P, 8, P))
        L.add("L1", f"L1x_b{s}", columns(a[f"L1_xattn_b_{s}"]))
    L.add("L1", "L1x_wv", a["L1_xattn_w_v"].T)
    L.add("L1", "L1x_bv", everywhere(a["L1_xattn_b_v"]))
    L.add("L1", "L1x_wo", k_tiles(a["L1_xattn_w_o"].T))
    L.add("L1", "L1x_bo", a["L1_xattn_b_o"])
    L.add("L1", "L1f_gate", a["L1_ffn_gate_w"].T)
    L.add("L1", "L1f_gate_b", everywhere(a["L1_ffn_gate_b"]))
    L.add("L1", "L1f_w1", a["L1_ffn_w1"].transpose(1, 0, 2))
    L.add("L1", "L1f_b1", a["L1_ffn_b1"].reshape(E, 2, P).transpose(2, 0, 1))
    L.add("L1", "L1f_w2", a["L1_ffn_w2"].reshape(E, 2, P, P).transpose(2, 0, 1, 3))
    L.add("L1", "L1f_b2", top_rows(a["L1_ffn_b2"]))
    twice = lambda w: np.repeat(w.reshape(8, 1, 16, -1), 2, axis=1).reshape(2, P, -1)
    w, bias = a["L2_attn_qkvu_w"].reshape(4, P, P), a["L2_attn_qkvu_b"].reshape(4, P)
    for n, s in enumerate("qk"):
        L.add("L2", f"L2a_w{s}", twice(w[n]).transpose(2, 0, 1))
        L.add("L2", f"L2a_b{s}", twice(bias[n])[:, :, 0].T)
    L.add("L2", "L2a_wv", w[2].T)
    L.add("L2", "L2a_bv", everywhere(bias[2]))
    L.add("L2", "L2a_wu", w[3].T)
    L.add("L2", "L2a_bu", bias[3])
    L.add("L2", "L2a_wo", a["L2_attn_out_w"].T)
    L.add("L2", "L2a_bo", a["L2_attn_out_b"])
    L.add("L2", "L2a_theta", twice(a["L2_attn_theta"].reshape(P))[:, :, 0].T)
    L.add("L2", "L2a_slope", everywhere(a["L2_attn_slope_rate"].reshape(8)))
    L.add("L2", "L2a_lower", (~after).astype(np.float32).T.reshape(2, P, S).transpose(1, 0, 2))
    cosine = (np.arange(P) % 32 < 16).astype(np.float32)
    L.add("L2", "L2a_cosine_rows", cosine)
    L.add("L2", "L2a_sine_rows", 1 - cosine)
    L.add("L2", "half_pi", np.full(P, np.pi / 2, np.float32))
    L.add("L2", "L2x_scale", a["L2_xattn_rms_scale"])
    wq = a["L2_xattn_q_w"].transpose(1, 0, 2)
    wk = np.broadcast_to(a["L2_xattn_kv_w"][0, 0][:, None, :], (P, 4, 32))
    for s, w in (("q", wq), ("k", wk)):
        L.add("L2", f"L2x_w{s}", w.reshape(P, P))
        L.add("L2", f"L2x_w{s}_swapped", np.concatenate([w[:, :, 16:], w[:, :, :16]], axis=2).reshape(P, P))
    timescale = 10000.0 ** (2.0 / 32 * np.arange(16, dtype=np.float64))
    for s, start in (("q", S), ("k", 0)):
        angle = (np.arange(S) + start)[None, :].astype(np.float32) / timescale.astype(np.float32)[:, None]
        cos, sin = np.cos(angle), np.sin(angle)
        L.add("L2", f"L2x_cos_{s}", np.tile(np.concatenate([cos, cos]), (4, 1)).astype(np.float32))
        L.add("L2", f"L2x_sin_{s}", np.tile(np.concatenate([-sin, sin]), (4, 1)).astype(np.float32))
    L.add("L2", "L2x_wv", a["L2_xattn_kv_w"][1, 0])
    L.add("L2", "L2x_wo", a["L2_xattn_out_w"].reshape(P, P))
    for s in ("gate", "up"):
        L.add("L2", f"L2f_{s}", row_tiles(a[f"L2_ffn_w_{s}"]))
    L.add("L2", "L2f_down", a["L2_ffn_w_down"])
    L.add("L2", "L2f_clips", everywhere(np.concatenate([a["L2_ffn_clip_x"], a["L2_ffn_clip_down"]])))
    for s in "qk":
        L.add("L3", f"L3a_w{s}", padded_heads(a[f"L3_attn_W{s}"].T))
        L.add("L3", f"L3a_b{s}", padded_heads(a[f"L3_attn_b{s}"][None, :])[0].T)
    for sub, name in (("a", "attn"), ("x", "xattn")):
        L.add("L3", f"L3{sub}_wv", a[f"L3_{name}_Wv"].T)
        L.add("L3", f"L3{sub}_bv", everywhere(a[f"L3_{name}_bv"]))
        L.add("L3", f"L3{sub}_wo", a[f"L3_{name}_Wo"].T)
        L.add("L3", f"L3{sub}_bo", a[f"L3_{name}_bo"])
    for s in "qk":
        L.add("L3", f"L3x_w{s}", a[f"L3_xattn_W{s}"].T)
        L.add("L3", f"L3x_b{s}", a[f"L3_xattn_b{s}"])
    L.add("L3", "L3x_kmask", (np.arange(S)[None, :] % 16 == np.arange(P)[:, None] // 8).astype(np.float32))
    L.add("L3", "L3x_vmask", (np.arange(P)[:, None] % 16 == np.arange(P)[None, :] // 8).astype(np.float32))
    L.add("L3", "L3f_win", a["L3_ffn_in_proj_w"].T)
    L.add("L3", "L3f_bin", columns(a["L3_ffn_in_proj_b"]))
    L.add("L3", "L3f_heads", (np.arange(P)[:, None] // 32 == np.arange(P)[None, :] // 32).astype(np.float32))
    L.add("L3", "L3f_wout", a["L3_ffn_out_proj_w"].T)
    L.add("L3", "L3f_bout", a["L3_ffn_out_proj_b"])
    for n in "12":
        L.add("L3", f"L3f_g{n}", a[f"L3_ffn_ln{n}_g"])
        L.add("L3", f"L3f_h{n}", a[f"L3_ffn_ln{n}_b"])
    L.add("L3", "L3f_wg", a["L3_ffn_wg"])
    L.add("L3", "L3f_w1", a["L3_ffn_w1"].reshape(E, P, 4, P).transpose(3, 0, 2, 1))
    L.add("L3", "L3f_w2", a["L3_ffn_w2"].reshape(E, 4, P, P).transpose(2, 0, 1, 3))
    L.add("L3", "L3f_b1", a["L3_ffn_b1"].reshape(E, 4, P).transpose(2, 0, 1))
    L.add("L3", "L3f_b2", a["L3_ffn_b2"].T)
    return L


def decoder(nc, slots, packs, dram, x, ctx, out, upto=12):
    c = Core(nc, slots, packs)
    c.dram = dram
    c.valid_i32 = nc.alloc_sbuf_tensor("valid_keys_i32", [P, B], I32)
    c.valid = nc.alloc_sbuf_tensor("valid_keys", [P, B], F32)
    c.attend = nc.alloc_sbuf_tensor("attended_keys", [P, N // 4], I32)
    load_stage(c, None, dram, x, ctx)
    with nc.Block() as block:
        @block.vector
        def _(dve):
            nc.vector.tensor_copy(c.valid[:, :], c.valid_i32[:, :])
    for sub in SUBLAYERS[:upto]:
        sub(c)
    with nc.Block() as block:
        @block.sync
        def _(sp):
            sp.dma_start(out, c.X[:, :]).then_inc(c.stored.sem, 16)
            sp.wait_ge(c.stored.sem, c.stored.at(16))


SUBLAYERS = [layer0_attention, layer0_cross, layer0_experts, layer1_attention, layer1_cross, layer1_experts, layer2_attention,
             layer2_cross, layer2_mlp, layer3_attention, layer3_cross, layer3_block]


def kernel(**inputs):
    from concourse import bacc
    from concourse.bass_utils import run_bass_kernel_spmd

    a = {k: np.asarray(v) for k, v in inputs.items()}
    L = lay_out(a)
    arrays = {f"{k}_dram": v for k, v in L.packed().items()}
    arrays["x_dram"] = feature_major(a["x"])
    arrays["ctx_dram"] = feature_major(a["ctx_1024"])
    arrays["valid_dram"] = np.ascontiguousarray(everywhere(a["mask_B_ik0"]))
    arrays["attend_dram"] = np.ascontiguousarray(
        everywhere(np.ascontiguousarray(a["mask_BxS2_bk0"]).view(np.int32)))
    nc = bacc.Bacc("TRN2", target_bir_lowering=False, num_devices=1)
    ap = {k: nc.dram_tensor(k, v.shape, mybir.dt.from_np(v.dtype), kind="ExternalInput").ap()
          for k, v in arrays.items()}
    out = nc.dram_tensor("out_dram", (P, N), F32, kind="ExternalOutput").ap()
    decoder(nc, L.slots, L.words, {k[:-5]: v for k, v in ap.items()}, ap["x_dram"], ap["ctx_dram"], out)
    r = run_bass_kernel_spmd(nc, [arrays], core_ids=[0])
    return r.results[0]["out_dram"].T.reshape(B, S, P)
```

```python
import numpy as np

import concourse.bass as bass
from concourse import mybir

F32 = mybir.dt.float32
BF16 = mybir.dt.bfloat16
I32 = mybir.dt.int32
U8 = mybir.dt.uint8
ACT = mybir.ActivationFunctionType
ALU = mybir.AluOpType
AX = mybir.AxisListType

P = 128
B, S = 8, 256
N = B * S
CH = 512
NC = N // CH
NEG = -3.4028234663852886e38
REPLACED = -3.0e38


class Signal:

    def __init__(self, nc, name):
        self.sem = nc.alloc_semaphore(name)
        self.base = 0

    def at(self, n):
        return self.base + n

    def advance(self, n):
        self.base += n


class Chain:

    def __init__(self, eng, sem):
        self.eng, self.sem, self.n = eng, sem, 0

    def link(self, ins):
        self.n += 1
        ins.then_inc(self.sem, 1)
        self.eng.wait_ge(self.sem, self.n)

    def step(self, ins):
        self.n += 1
        ins.then_inc(self.sem, 1)

    def all_but(self, last):
        if self.n > last:
            self.eng.wait_ge(self.sem, self.n - last)

    def clear(self):
        if self.n:
            self.eng.wait_ge(self.sem, self.n)
            self.eng.sem_clear(self.sem)
            self.n = 0


class Core:

    SIGNALS = [
        "loaded", "loaded_ahead", "stored", "var_ready", "centred", "squared", "normed", "rooted", "inverted", "spread", "copied",
        "product_ready", "product_taken", "product_taken_v", "staged", "proj_ready", "proj_taken_v",
        "scores_ready", "scores_max", "probs_ready", "probs_picked", "probs_turned", "turned_copied", "turned_copied_s", "qk_ready", "qk_taken", "v_ready", "v_taken", "out_added",
        "mixed_ready", "mixed_taken", "out_turned", "out_copied", "out_product",
        "aux_pe", "aux_v", "aux_s", "aux_p", "aux_pe2", "aux_v2", "aux_s2", "aux_p2", "aux_pe3", "aux_v3", "aux_s3",
        "big_loaded",
    ]

    def __init__(self, nc, slots, packs):
        self.nc, self.slots, self.packs = nc, slots, packs
        self.sig = {n: Signal(nc, n) for n in self.SIGNALS}
        self.vector_chain = nc.alloc_semaphore("vector_chain")
        self.scalar_chain = nc.alloc_semaphore("scalar_chain")
        self.pool_chain = nc.alloc_semaphore("pool_chain")
        self.psum = nc.alloc_psum_tensor("psum", [P, 8, CH], F32)
        self.X = nc.alloc_sbuf_tensor("residual", [P, N], F32)
        self.CT = nc.alloc_sbuf_tensor("context", [P, N], F32)
        self.HN = nc.alloc_sbuf_tensor("normed_input", [P, N], F32)
        self.T = nc.alloc_sbuf_tensor("tiles", [P, 4, N], F32)
        self.small = nc.alloc_sbuf_tensor("small_weights", [P, packs["small"]], F32)
        self.big_words = max([packs[n] for n in packs if n != "small"], default=1)
        self.big = nc.alloc_sbuf_tensor("big_weights", [P, self.big_words], F32)
        self.pack_base = {n: self.big_words - packs[n] if n == "L2" else 0 for n in packs}
        self.work_words = 66 * 1024 // 4
        self.work = nc.alloc_sbuf_tensor("work", [P, self.work_words], F32)

    def __getattr__(self, name):
        return self.sig[name]

    def w(self, name):
        pack, off, shape = self.slots[name]
        t = self.small if pack == "small" else self.big
        n = int(np.prod(shape[1:]))
        off += self.pack_base[pack] if pack != "small" else 0
        return shaped(t[:, off:off + n], shape[1:])


def shaped(ap, dims):
    if len(dims) == 1:
        return ap
    if len(dims) == 2:
        return ap.rearrange("p (a b) -> p a b", b=dims[1])
    if len(dims) == 3:
        return ap.rearrange("p (a b c) -> p a b c", b=dims[1], c=dims[2])
    return ap.rearrange("p (a b c d) -> p a b c d", b=dims[1], c=dims[2], d=dims[3])


class Arena:

    def __init__(self, core):
        self.core, self.off = core, 0

    def take(self, *dims):
        n = int(np.prod(dims))
        a = self.core.work[:, self.off:self.off + n]
        self.off += n
        assert self.off <= self.core.work_words, (self.off, self.core.work_words)
        return shaped(a, dims)



def start_loads(c, loads):
    nc = c.nc
    with nc.Block() as block:
        @block.sync
        def _(sp):
            for sig, dst, src in loads:
                sp.dma_start(dst, src).then_inc(sig.sem, 16)
    for sig, _, _ in loads:
        sig.advance(16)


def pack_load(c, sig, pack, lo=0, hi=None):
    words, at = c.packs[pack], c.pack_base[pack]
    hi = words if hi is None else min(hi, words)
    return sig, c.big[:, at + lo:at + hi], c.dram[pack][:, lo:hi]


def loads_done(c, sig):
    nc = c.nc
    with nc.Block() as block:
        @block.sync
        def _(sp):
            sp.wait_ge(sig.sem, sig.base)


def norm_stage(c, src, dst, eps, centre=True, gain=None, shift=None):
    nc = c.nc
    a = Arena(c)
    sq, std, inv = a.take(N), a.take(CH), a.take(CH)
    avg, G = c.w("average"), P // NC
    ch = [slice(i * CH, (i + 1) * CH) for i in range(NC)]
    group = [slice(i * G, (i + 1) * G) for i in range(NC)]
    spread = [5, 6, 7, 4]
    half = [slice(0, CH // 2), slice(CH // 2, CH)]
    with nc.Block() as block:
        @block.tensor
        def _(pe):
            if centre:
                for i in range(NC):
                    nc.tensor.matmul(c.psum[:, i, :], c.w("centre"), src[:, ch[i]], start=True, stop=True) \
                        .then_inc(c.centred.sem, 1)
            for i in range(NC):
                pe.wait_ge(c.squared.sem, c.squared.at(i + 1))
                mm = nc.tensor.matmul(c.psum[group[i], 4, :], avg[:, 0:G], sq[:, ch[i]], start=True, stop=True,
                                      tile_position=(0, i * G))
            mm.then_inc(c.var_ready.sem, 1)
            for n, h in enumerate(half):
                pe.wait_ge(c.inverted.sem, c.inverted.at(n + 1))
                for i in range(NC):
                    if n == 0 and i == NC - 1:
                        pe.wait_ge(c.rooted.sem, c.rooted.at(2))
                    mm = nc.tensor.matmul(c.psum[:, spread[i], h], avg[group[i], :], inv[group[i], h], start=True,
                                          stop=True, tile_position=(i * G, 0))
                    if n == 1:
                        mm.then_inc(c.spread.sem, 1)

        @block.vector
        def _(dve):
            for n, h in enumerate(half):
                dve.wait_ge(c.rooted.sem, c.rooted.at(n + 1))
                nc.vector.reciprocal(inv[:, h], std[:, h]).then_inc(c.inverted.sem, 1)
            for i in range(NC):
                if centre:
                    dve.wait_ge(c.copied.sem, c.copied.at(i + 1))
                dve.wait_ge(c.spread.sem, c.spread.at(i + 1))
                nc.vector.scalar_tensor_tensor(dst[:, ch[i]], (dst if centre else src)[:, ch[i]],
                                               float(P // G), c.psum[:, spread[i], :], ALU.mult, ALU.mult) \
                    .then_inc(c.normed.sem, 1)

        @block.scalar
        def _(act):
            for i in range(NC):
                if centre:
                    act.wait_ge(c.centred.sem, c.centred.at(i + 1))
                nc.scalar.activation(sq[:, ch[i]], c.psum[:, i, :] if centre else src[:, ch[i]], ACT.Square) \
                    .then_inc(c.squared.sem, 1)
            act.wait_ge(c.var_ready.sem, c.var_ready.at(1))
            for h in half:
                nc.scalar.activation(std[:, h], c.psum[:, 4, h], ACT.Sqrt, bias=c.w(eps)).then_inc(c.rooted.sem, 1)
            if centre:
                for i in range(NC):
                    nc.scalar.copy(dst[:, ch[i]], c.psum[:, i, :]).then_inc(c.copied.sem, 1)
            if gain is not None:
                for i in range(NC):
                    act.wait_ge(c.normed.sem, c.normed.at(i + 1))
                    nc.scalar.activation(dst[:, ch[i]], dst[:, ch[i]], ACT.Identity, scale=gain,
                                         bias=0.0 if shift is None else shift)
    if centre:
        c.centred.advance(NC)
        c.copied.advance(NC)
    for s, n in ((c.squared, NC), (c.var_ready, 1), (c.rooted, 2), (c.inverted, 2), (c.spread, NC), (c.normed, NC)):
        s.advance(n)


def affine_stage(c, src, dsts, gains, shifts):
    nc = c.nc
    with nc.Block() as block:
        @block.scalar
        def _(act):
            for d, g, s in zip(dsts[0::2], gains[0::2], shifts[0::2]):
                nc.scalar.activation(d, src, ACT.Identity, scale=g, bias=s)

        @block.vector
        def _(dve):
            for d, g, s in zip(dsts[1::2], gains[1::2], shifts[1::2]):
                nc.vector.tensor_scalar(d, src, g, s, ALU.mult, ALU.add)


def project_stage(c, jobs):
    nc = c.nc
    steps = [(i, j) for i in range(NC) for j in range(len(jobs))]
    by_vector = [jobs[j][5] is not None for _, j in steps]
    taken = []
    ns = nv = 0
    for v in by_vector:
        nv, ns = nv + v, ns + (not v)
        taken.append((v, nv if v else ns))
    with nc.Block() as block:
        @block.tensor
        def _(pe):
            for n, (i, j) in enumerate(steps):
                srcs, ws = jobs[j][0:2]
                if n >= 8:
                    v, k = taken[n - 8]
                    sig = c.product_taken_v if v else c.product_taken
                    pe.wait_ge(sig.sem, sig.at(k))
                for k, (src, w) in enumerate(zip(srcs, ws)):
                    mm = nc.tensor.matmul(c.psum[:, n % 8, :], w, src[:, i * CH:(i + 1) * CH],
                                          start=(k == 0), stop=(k == len(srcs) - 1))
                mm.then_inc(c.product_ready.sem, 1)

        @block.scalar
        def _(act):
            for n, (i, j) in enumerate(steps):
                if by_vector[n]:
                    continue
                _, _, bias, func, out, _ = jobs[j]
                act.wait_ge(c.product_ready.sem, c.product_ready.at(n + 1))
                nc.scalar.activation(out[:, i * CH:(i + 1) * CH], c.psum[:, n % 8, :], func or ACT.Identity,
                                     bias=0.0 if bias is None else bias).then_inc(c.product_taken.sem, 1)

        @block.vector
        def _(dve):
            for n, (i, j) in enumerate(steps):
                if not by_vector[n]:
                    continue
                _, _, bias, func, out, res = jobs[j]
                dve.wait_ge(c.product_ready.sem, c.product_ready.at(n + 1))
                nc.vector.scalar_tensor_tensor(out[:, i * CH:(i + 1) * CH], c.psum[:, n % 8, :],
                                               0.0 if bias is None else bias, res[:, i * CH:(i + 1) * CH],
                                               ALU.add, ALU.add).then_inc(c.product_taken_v.sem, 1)
    c.product_ready.advance(len(steps))
    c.product_taken.advance(ns)
    c.product_taken_v.advance(nv)


def attention_stage(c, H, dh, q_src, k_src, v_src, wq, bq, wk, bk, wv, bv, wo, bo, scale=1.0,
                    head_scale=None, mask=None, prepare_mask=None, mask_words=0, shared_kv=False, top=0,
                    residual2=None, skip_max=False):
    nc = c.nc
    nt = len(wq)
    per_tile = H // nt
    pitch = P // per_tile
    gpt = per_tile // 2
    NG = H // 2
    vg = P // (2 * dh)
    vw = dh if shared_kv else P
    U = 4
    rows = 32 if dh < 32 else dh
    TURN = 3
    MIX = 3 if skip_max else 4
    OUT = MIX + 1
    SQ = max(8 // NG, 2)
    W = SQ * NG
    NIT = B // SQ
    VR = {1: 8, 2: 4}.get(vg, 2)
    ve = P if skip_max else dh
    nvh = vw // dh
    a = Arena(c)
    qb, kb = a.take(2, S), a.take(2, S)
    vsb = a.take(2, S)
    vb = a.take(VR, 2, nvh * ve)
    probs = None if skip_max else a.take(2, U, S)
    raw = a.take(2, U, S) if (mask or top) else None
    rest = a.take(2, U, S) if top else None
    turned = a.take(2, 2, 2, S)
    otok = a.take(2, 2, P)
    oT = a.take(2, S)
    rowmax, nbias = a.take(2, U), a.take(2, U)
    top8 = a.take(2, U, max(top // 8, 1), 8)
    sums, rest_sums, kept_sums, rsum = a.take(4, U), a.take(4, U), a.take(4, U), a.take(4, U)
    mb = a.take(mask_words) if mask_words else None
    gate = a.take(1)
    ident = c.w("identity")

    def bank(i):
        return c.psum[:, i, :]

    def pair(g):
        return c.psum[:, 2 * (g % 2):2 * (g % 2) + 2, :]

    def scores(g):
        return pair(g).rearrange("p a (q k) -> p (a q) k", k=S)

    def turn(head):
        return bank(4 + head).rearrange("p (t q x) -> p t q x", t=2, q=2)

    mixed = c.psum[:, 6, 0:U * ve].rearrange("p (u d) -> p u d", d=ve)

    def starts_tile(g):
        return g % gpt == 0

    def starts_values(g):
        return g % (NG if shared_kv else vg) == 0

    def ends_output(g):
        return g % vg == vg - 1

    def values(g):
        return vb[:, (g // (NG if shared_kv else vg)) % VR]

    per = {"q": W // gpt, "v": W // (NG if shared_kv else vg), "o": W // vg, "g": W, "b": SQ}

    def after(sig, kind, it, n):
        return sig.base + it * per[kind] + n + 1

    def queries_taken(it, g):
        return c.qk_taken.base + it * 2 * per["q"] + 2 * tile_n(g) + 2

    TAIL = OUT + 1
    tile_n = lambda g: g // gpt
    val_n = lambda g: g // (NG if shared_kv else vg)
    out_n = lambda g: g // vg
    seq_of = lambda it, g: it * SQ + g // NG

    def engine(eng, step, chain=None):
        def steps(it, first, lo, hi):
            for t in range(lo, hi):
                step(it, t, lambda g: g < W and (g >= 0 or not first))
            if chain is not None:
                chain.clear()

        steps(0, True, 0, W)
        with eng.Fori(1, NIT) as it:
            steps(it, False, 0, W)
        steps(NIT - 1, False, W, W + TAIL)

    with nc.Block() as block:
        @block.gpsimd
        def _(pool):
            def step(it, t, ok):
                if t < W and t % NG == 0:
                    if ok(t - 2 * NG):
                        pool.wait_ge(c.v_ready.sem, after(c.v_ready, "v", it, val_n(t - NG) - 1))
                    nc.gpsimd.tensor_copy(vsb[:, (t // NG) % 2], v_src[:, bass.ds(seq_of(it, t) * S, S)]) \
                        .then_inc(c.staged.sem, 1)
                g = t - 1
                if top and ok(g):
                    pool.wait_ge(c.probs_ready.sem, after(c.probs_ready, "g", it, g))
                    nc.gpsimd.tensor_tensor(probs[:, g % 2], probs[:, g % 2], rest[:, g % 2], ALU.subtract) \
                        .then_inc(c.probs_picked.sem, 1)

            if residual2 is not None:
                nc.gpsimd.tensor_tensor(c.X[:, :], c.X[:, :], residual2[:, :], ALU.add).then_inc(c.aux_p.sem, 1)
            engine(pool, step)

        @block.tensor
        def _(pe):
            def step(it, t, ok):
                g = t - 1
                if ok(g):
                    if starts_tile(g):
                        pe.wait_ge(c.qk_taken.sem, queries_taken(it, g))
                    if ok(g - 2):
                        pe.wait_ge(c.probs_ready.sem, after(c.probs_ready, "g", it, g - 2))
                    hs = g % NG * 2
                    for u in range(U):
                        h = hs + u // 2
                        base = (h % per_tile) * pitch
                        q = qb[base:base + rows, tile_n(g) % 2, :]
                        k = kb[base:base + rows, tile_n(g) % 2, :]
                        half = slice((u % 2) * P, (u % 2 + 1) * P)
                        lhs, rhs = (k[:, half], q) if skip_max else (q[:, half], k)
                        mm = nc.tensor.matmul(scores(g)[:, u, :], lhs, rhs, start=True, stop=True,
                                              tile_position=(base, 0))
                    mm.then_inc(c.scores_ready.sem, 1)
                g = t
                if g < W and starts_tile(g):
                    if ok(g - MIX - 1):
                        pe.wait_ge(c.mixed_taken.sem, after(c.mixed_taken, "g", it, g - MIX - 1))
                    if ok(g - 1) and ok(val_n(g - 1)):
                        pe.wait_ge(c.v_taken.sem, after(c.v_taken, "v", it, val_n(g - 1)))
                    i = g % NG // gpt
                    src = bass.ds(seq_of(it, g) * S, S)
                    nc.tensor.matmul(bank(6)[:, 0:S], wk[i], k_src[:, src], start=True, stop=True) \
                        .then_inc(c.qk_ready.sem, 1)
                    if ok(g - OUT - 1):
                        pe.wait_ge(c.out_added.sem, after(c.out_added, "o", it, (g - OUT) // vg - 1))
                    if ok(g - gpt):
                        pe.wait_ge(c.qk_taken.sem, queries_taken(it, g - gpt))
                    nc.tensor.matmul(bank(7)[:, 0:S], wq[i], q_src[:, src], start=True, stop=True) \
                        .then_inc(c.qk_ready.sem, 1)
                k3 = t - TURN
                turns = ok(k3) and not skip_max

                def turn_head(head):
                    for u in (2 * head, 2 * head + 1):
                        for kt in range(2):
                            mm = nc.tensor.transpose(turn(head)[:, kt, u % 2, :],
                                                     probs[:, k3 % 2, u, kt * P:(kt + 1) * P], ident)
                    mm.then_inc(c.probs_turned.sem, 1)

                if turns:
                    ready = c.probs_picked if top else c.probs_ready
                    pe.wait_ge(ready.sem, after(ready, "g", it, k3))
                    if ok(k3 - 1):
                        pe.wait_ge(c.turned_copied_s.sem, after(c.turned_copied_s, "g", it, k3 - 1))
                    turn_head(0)
                if g < W and starts_values(g):
                    pe.wait_ge(c.qk_taken.sem, queries_taken(it, g) - 1)
                    if t % NG == 0:
                        pe.wait_ge(c.staged.sem, after(c.staged, "b", it, t // NG))
                    lo = 0 if shared_kv else g % NG // vg * P
                    for kt in range(2):
                        mm = nc.tensor.matmul(bank(6)[:, kt * vw:(kt + 1) * vw],
                                              vsb[:, (t // NG) % 2, kt * P:(kt + 1) * P], wv[:, lo:lo + vw],
                                              start=True, stop=True)
                    mm.then_inc(c.v_ready.sem, 1)
                o = t - OUT
                out = ok(o) and ends_output(o)
                if out:
                    if g < W and starts_tile(g):
                        pe.wait_ge(c.qk_taken.sem, queries_taken(it, g))
                    elif ok(o - vg):
                        pe.wait_ge(c.out_added.sem, after(c.out_added, "o", it, out_n(o) - 1))
                    pe.wait_ge(c.mixed_taken.sem, after(c.mixed_taken, "g", it, o))
                    for qt in range(2):
                        mm = nc.tensor.transpose(bank(7)[:, qt * P:(qt + 1) * P], otok[:, out_n(o) % 2, qt, :], ident)
                    mm.then_inc(c.out_turned.sem, 1)
                if turns:
                    if ok(k3 - 1):
                        pe.wait_ge(c.turned_copied.sem, after(c.turned_copied, "g", it, k3 - 1))
                    turn_head(1)
                m = t - MIX
                if ok(m):
                    if skip_max:
                        pe.wait_ge(c.probs_ready.sem, after(c.probs_ready, "g", it, m))
                    else:
                        pe.wait_ge(c.turned_copied.sem, after(c.turned_copied, "g", it, m))
                        pe.wait_ge(c.turned_copied_s.sem, after(c.turned_copied_s, "g", it, m))
                    if g < W and starts_values(g):
                        pe.wait_ge(c.v_taken.sem, after(c.v_taken, "v", it, val_n(g)))
                    elif g < W and starts_tile(g):
                        pe.wait_ge(c.qk_taken.sem, queries_taken(it, g) - 1)
                    elif ok(m - 1):
                        pe.wait_ge(c.mixed_taken.sem, after(c.mixed_taken, "g", it, m - 1))
                    v = values(m)
                    for u in range(U):
                        lo = 0 if shared_kv else ((m % vg) * 2 + u // 2) * ve
                        for kt in range(2):
                            mm = nc.tensor.matmul(mixed[:, u, :], turned[:, m % 2, u // 2, kt, (u % 2) * P:(u % 2 + 1) * P],
                                                  v[:, kt, lo:lo + ve], start=(kt == 0), stop=(kt == 1))
                    mm.then_inc(c.mixed_ready.sem, 1)
                if out:
                    pe.wait_ge(c.out_copied.sem, after(c.out_copied, "o", it, out_n(o)))
                    nc.tensor.matmul(bank(7)[:, 0:S], wo[o % NG // vg], oT[:, out_n(o) % 2, :],
                                     start=True, stop=True).then_inc(c.out_product.sem, 1)

            engine(pe, step)

        @block.scalar
        def _(act):
            def step(it, t, ok):
                g = t
                if g < W and starts_tile(g):
                    i = g % NG // gpt
                    for n, (dst, b, src) in enumerate(((kb, bk, 6), (qb, bq, 7))):
                        act.wait_ge(c.qk_ready.sem, c.qk_ready.base + it * 2 * per["q"] + 2 * tile_n(g) + n + 1)
                        nc.scalar.activation(dst[:, tile_n(g) % 2, :], bank(src)[:, 0:S], ACT.Identity,
                                             bias=0.0 if b is None else b[:, i:i + 1]).then_inc(c.qk_taken.sem, 1)
                k = t - TURN
                if ok(k) and not skip_max:
                    act.wait_ge(c.probs_turned.sem, c.probs_turned.base + it * 2 * W + 2 * k + 1)
                    if ok(k - 2):
                        act.wait_ge(c.mixed_ready.sem, after(c.mixed_ready, "g", it, k - 2))
                    nc.scalar.copy(turned[:, k % 2, 0].rearrange("p t s -> p (t s)"), bank(4)) \
                        .then_inc(c.turned_copied_s.sem, 1)
                o = t - OUT
                if ok(o) and ends_output(o):
                    act.wait_ge(c.out_turned.sem, after(c.out_turned, "o", it, out_n(o)))
                    nc.scalar.copy(oT[:, out_n(o) % 2, :], bank(7)[:, 0:S]).then_inc(c.out_copied.sem, 1)
                if ok(k) and top:
                    act.wait_ge(c.probs_turned.sem, c.probs_turned.base + it * 2 * W + 2 * k + 2)
                    nc.scalar.copy(turned[:, k % 2, 1].rearrange("p t s -> p (t s)"), bank(5)) \
                        .then_inc(c.turned_copied.sem, 1)
                g = t - 1
                if ok(g) and skip_max:
                    act.wait_ge(c.scores_ready.sem, after(c.scores_ready, "g", it, g))
                    if ok(g - 2):
                        act.wait_ge(c.mixed_ready.sem, after(c.mixed_ready, "g", it, g - 2))
                    for head in range(2):
                        h = g % NG * 2 + head
                        ins = nc.scalar.activation(turned[:, g % 2, head].rearrange("p t s -> p (t s)"),
                                                   pair(g)[:, head, :], ACT.Exp, scale=head_scale[:, h:h + 1])
                    ins.then_inc(c.probs_ready.sem, 1)
                elif ok(g):
                    act.wait_ge(c.scores_max.sem, after(c.scores_max, "g", it, g))
                    if ok(g - 2):
                        act.wait_ge(c.probs_turned.sem, c.probs_turned.base + it * 2 * W + 2 * (g - 1))
                    for u in range(U):
                        src = raw[:, g % 2, u, :] if mask else scores(g)[:, u, :]
                        ins = nc.scalar.activation(probs[:, g % 2, u, :], src, ACT.Exp,
                                                   bias=nbias[:, g % 2, u:u + 1], scale=scale,
                                                   accum_out=sums[:, g % 4, u:u + 1])
                        if top:
                            ins = nc.scalar.activation(rest[:, g % 2, u, :], raw[:, g % 2, u, :], ACT.Exp,
                                                       bias=nbias[:, g % 2, u:u + 1], scale=scale,
                                                       accum_out=rest_sums[:, g % 4, u:u + 1])
                    ins.then_inc(c.probs_ready.sem, 1)

            engine(act, step)

        @block.vector
        def _(dve):
            chain = Chain(dve, c.vector_chain)

            def maxima(it, g):
                s = g % 2
                dve.wait_ge(c.scores_ready.sem, after(c.scores_ready, "g", it, g))
                if top or mask:
                    chain.link(nc.vector.tensor_copy(gate, ident[:, 0:1]))
                if top:
                    for r in range(top // 8):
                        src = scores(g) if r == 0 else raw[:, s]
                        for u in range(U):
                            chain.all_but(U - 1)
                            chain.step(nc.vector.max(top8[:, s, u, r, :], src[:, u, :]))
                        for u in range(U):
                            chain.all_but(U - 1)
                            chain.step(nc.vector.match_replace(raw[:, s, u, :], top8[:, s, u, r, :],
                                                               src[:, u, :], REPLACED))
                    chain.all_but(0)
                    nc.vector.tensor_scalar(nbias[:, s, :], top8[:, s, :, 0, 0], -scale, None, ALU.mult) \
                        .then_inc(c.scores_max.sem, 1)
                    return
                if mask:
                    for u in range(U):
                        ins = nc.vector.tensor_tensor_reduce(raw[:, s, u, :], scores(g)[:, u, :],
                                                             mask(mb, u % 2), 1.0, NEG, ALU.add,
                                                             ALU.max, rowmax[:, s, u:u + 1])
                    chain.link(ins)
                else:
                    chain.link(nc.vector.reduce_max(rowmax[:, s, :], scores(g), AX.X))
                nc.vector.tensor_scalar(nbias[:, s, :], rowmax[:, s, :], -scale, None, ALU.mult) \
                    .then_inc(c.scores_max.sem, 1)

            def step(it, t, ok):
                g = t - 1
                if ok(g):
                    if prepare_mask is not None and g % NG == 0:
                        prepare_mask(nc, dve, chain, seq_of(it, g), mb)
                    if not skip_max:
                        maxima(it, g)
                g = t
                if g < W and starts_values(g):
                    dve.wait_ge(c.v_ready.sem, after(c.v_ready, "v", it, val_n(g)))
                    dst = values(g).rearrange("p t (h e) -> p t h e", e=ve)[:, :, :, 0:dh]
                    src = bank(6)[:, 0:2 * vw].rearrange("p (t h e) -> p t h e", t=2, e=dh)
                    if bv is None:
                        ins = nc.vector.tensor_copy(dst, src)
                    else:
                        lo = g % NG // vg * P
                        b = bv[:, lo:lo + vw].rearrange("p (h e) -> p h e", e=dh).unsqueeze(1)
                        ins = nc.vector.tensor_tensor(dst, src, b.broadcast_to([P, 2, nvh, dh]), ALU.add)
                    ins.then_inc(c.v_taken.sem, 1)
                k = t - TURN
                if ok(k) and not skip_max:
                    dve.wait_ge(c.probs_ready.sem, after(c.probs_ready, "g", it, k))
                    total = sums[:, k % 4, :]
                    if top:
                        chain.link(nc.vector.tensor_tensor(kept_sums[:, k % 4, :], total, rest_sums[:, k % 4, :],
                                                           ALU.subtract))
                        total = kept_sums[:, k % 4, :]
                    chain.step(nc.vector.reciprocal(rsum[:, k % 4, :], total))
                    if not top:
                        dve.wait_ge(c.probs_turned.sem, c.probs_turned.base + it * 2 * W + 2 * k + 2)
                        if ok(k - 2):
                            dve.wait_ge(c.mixed_ready.sem, after(c.mixed_ready, "g", it, k - 2))
                        nc.vector.tensor_copy(turned[:, k % 2, 1].rearrange("p t s -> p (t s)"), bank(5)) \
                            .then_inc(c.turned_copied.sem, 1)
                m = t - MIX
                if ok(m):
                    dve.wait_ge(c.mixed_ready.sem, after(c.mixed_ready, "g", it, m))
                    if skip_max:
                        chain.link(nc.vector.reciprocal(rsum[:, m % 4, :].unsqueeze(2), mixed[:, :, dh:dh + 1]))
                    lo = m % vg * 2 * dh
                    dst = otok[:, out_n(m) % 2, :, lo:lo + 2 * dh].rearrange("p q (h d) -> p h q d", d=dh)
                    inv = rsum[:, m % 4, :].rearrange("p (h q) -> p h q", q=2).unsqueeze(3)
                    nc.vector.tensor_tensor(dst, mixed.rearrange("p (h q) d -> p h q d", q=2)[:, :, :, 0:dh],
                                            inv.broadcast_to([P, 2, 2, dh]), ALU.mult) \
                        .then_inc(c.mixed_taken.sem, 1)
                o = t - OUT
                if ok(o) and ends_output(o):
                    dve.wait_ge(c.out_product.sem, after(c.out_product, "o", it, out_n(o)))
                    xs = c.X[:, bass.ds(seq_of(it, o) * S, S)]
                    bias = 0.0 if bo is None or o % NG >= vg else bo
                    nc.vector.scalar_tensor_tensor(xs, bank(7)[:, 0:S], bias, xs, ALU.add, ALU.add) \
                        .then_inc(c.out_added.sem, 1)

            if skip_max:
                chain.link(nc.vector.memset(vb, 1.0))
            if residual2 is not None:
                dve.wait_ge(c.aux_p.sem, c.aux_p.at(1))
            engine(dve, step, chain)
    c.aux_p.advance(int(residual2 is not None))
    groups, outs = B * NG, B * NG // vg
    for s, n in ((c.staged, B), (c.qk_ready, 2 * groups // gpt), (c.qk_taken, 2 * groups // gpt),
                 (c.v_ready, B * per["v"] // SQ), (c.v_taken, B * per["v"] // SQ), (c.scores_ready, groups),
                 (c.scores_max, 0 if skip_max else groups), (c.probs_ready, groups),
                 (c.probs_picked, groups if top else 0), (c.probs_turned, 0 if skip_max else 2 * groups),
                 (c.turned_copied, 0 if skip_max else groups), (c.turned_copied_s, 0 if skip_max else groups),
                 (c.mixed_ready, groups), (c.mixed_taken, groups), (c.out_turned, outs), (c.out_copied, outs),
                 (c.out_product, outs), (c.out_added, outs)):
        s.advance(n)



def l2_stage(c, tensors):
    nc = c.nc
    a = Arena(c)
    sq, norm, inv = a.take(len(tensors), N), a.take(len(tensors), CH), a.take(len(tensors), CH)
    steps = [(t, i) for t in range(len(tensors)) for i in range(NC)]
    G = P // NC
    ones, avg = c.w("ones"), c.w("average")
    ch = [slice(i * CH, (i + 1) * CH) for i in range(NC)]
    group = [slice(i * G, (i + 1) * G) for i in range(NC)]
    with nc.Block() as block:
        @block.scalar
        def _(act):
            for t, i in steps:
                nc.scalar.activation(sq[:, t, ch[i]], tensors[t][:, ch[i]], ACT.Square).then_inc(c.aux_s.sem, 1)
            for t in range(len(tensors)):
                act.wait_ge(c.aux_pe.sem, c.aux_pe.at(t + 1))
                nc.scalar.activation(norm[:, t, :], c.psum[:, t, :], ACT.Sqrt).then_inc(c.aux_s2.sem, 1)

        @block.tensor
        def _(pe):
            for n, (t, i) in enumerate(steps):
                pe.wait_ge(c.aux_s.sem, c.aux_s.at(n + 1))
                mm = nc.tensor.matmul(c.psum[group[i], t, :], ones[:, 0:G], sq[:, t, ch[i]], start=True, stop=True,
                                      tile_position=(0, i * G))
                if i == NC - 1:
                    mm.then_inc(c.aux_pe.sem, 1)
            for n, (t, i) in enumerate(steps):
                if i == 0:
                    pe.wait_ge(c.aux_v.sem, c.aux_v.at(t + 1))
                if n >= 4:
                    pe.wait_ge(c.aux_v2.sem, c.aux_v2.at(n - 3))
                nc.tensor.matmul(c.psum[:, 4 + n % 4, :], avg[group[i], :], inv[group[i], t, :], start=True,
                                 stop=True, tile_position=(i * G, 0)).then_inc(c.aux_pe2.sem, 1)

        @block.vector
        def _(dve):
            chain = Chain(dve, c.vector_chain)
            for t in range(len(tensors)):
                dve.wait_ge(c.aux_s2.sem, c.aux_s2.at(t + 1))
                chain.link(nc.vector.tensor_scalar(norm[:, t, :], norm[:, t, :], 1e-6, None, ALU.max))
                nc.vector.reciprocal(inv[:, t, :], norm[:, t, :]).then_inc(c.aux_v.sem, 1)
            for n, (t, i) in enumerate(steps):
                dve.wait_ge(c.aux_pe2.sem, c.aux_pe2.at(n + 1))
                nc.vector.scalar_tensor_tensor(tensors[t][:, ch[i]], tensors[t][:, ch[i]], float(P // G),
                                               c.psum[:, 4 + n % 4, :], ALU.mult, ALU.mult).then_inc(c.aux_v2.sem, 1)
            chain.clear()
    for s, n in ((c.aux_s, len(steps)), (c.aux_s2, len(tensors)), (c.aux_pe, len(tensors)), (c.aux_pe2, len(steps)),
                 (c.aux_v, len(tensors)), (c.aux_v2, len(steps))):
        s.advance(n)


def layer0_attention(c):
    nc = c.nc
    qn, kn, vn = c.T[:, 0, :], c.T[:, 1, :], c.T[:, 2, :]
    start_loads(c, [pack_load(c, c.big_loaded, "L0"), pack_load(c, c.loaded_ahead, "L0f", c.packs["L0"])])
    norm_stage(c, c.X, c.HN, "eps5")
    n2 = c.T[:, 3, :]
    norm_stage(c, c.HN, n2, "eps5")
    loads_done(c, c.big_loaded)
    affine_stage(c, n2, [qn, kn, vn], [c.w("L0a_gq"), c.w("L0a_gk"), c.w("L0a_gv")],
                 [c.w("L0a_hq"), c.w("L0a_hk"), c.w("L0a_hv")])
    project_stage(c, [([qn], [c.w("L0a_wq")], c.w("L0a_bq"), None, c.T[:, 3, :], None)])
    project_stage(c, [([kn], [c.w("L0a_wk")], c.w("L0a_bk"), None, qn, None)])
    l2_stage(c, [c.T[:, 3, :], qn])
    beta = c.w("L0a_beta")
    with nc.Block() as block:
        @block.scalar
        def _(act):
            chain = Chain(act, c.scalar_chain)
            chain.link(nc.scalar.activation(c.work[:, 0:16], beta, ACT.Abs))
            chain.link(nc.scalar.activation(c.work[:, 16:32], c.work[:, 0:16], ACT.Exp, scale=-1.0))
            nc.scalar.activation(c.work[:, 32:48], c.work[:, 16:32], ACT.Ln, bias=c.w("one")).then_inc(c.aux_s.sem, 1)
            act.wait_ge(c.aux_s.sem, c.aux_s.at(1))
            chain.clear()

        @block.vector
        def _(dve):
            chain = Chain(dve, c.vector_chain)
            chain.link(nc.vector.tensor_scalar(c.work[:, 64:80], beta, 0.0, None, ALU.max))
            dve.wait_ge(c.aux_s.sem, c.aux_s.at(1))
            chain.link(nc.vector.tensor_tensor(c.work[:, 80:96], c.work[:, 64:80], c.work[:, 32:48], ALU.add))
            chain.link(nc.vector.tensor_scalar(c.work[:, 96:112], c.work[:, 80:96], 0.1, 10.0, ALU.max, ALU.min))
            chain.link(nc.vector.tensor_scalar(beta, c.work[:, 96:112], float(1.0 / np.sqrt(8.0)), None, ALU.mult))
            chain.clear()
    c.aux_s.advance(1)
    pad = c.w("pad8")
    attention_stage(c, 16, 8, c.T[:, 3, :], qn, vn, [pad[:, t, :] for t in range(4)], None,
                    [pad[:, t, :] for t in range(4)], None, c.w("L0a_wv"), c.w("L0a_bv"), [c.w("L0a_wo")],
                    c.w("L0a_bo"), head_scale=beta, skip_max=True, residual2=c.HN)


def add_stage(c, dst, one, other):
    nc = c.nc
    lo, hi = slice(0, N * 5 // 8), slice(N * 5 // 8, N)
    with nc.Block() as block:
        @block.vector
        def _(dve):
            nc.vector.tensor_tensor(dst[:, lo], one[:, lo], other[:, lo], ALU.add)

        @block.gpsimd
        def _(pool):
            nc.gpsimd.tensor_tensor(dst[:, hi], one[:, hi], other[:, hi], ALU.add)


def sequence_pipeline(eng, step, depth, chain=None):
    def plain(l):
        step(l, l % 2, lambda j: 0 <= l - j < B)

    first = depth
    pairs = (B - first) // 2
    for l in range(first):
        plain(l)
    if chain is not None:
        chain.clear()
    with eng.Fori(0, pairs) as i:
        for n in range(2):
            step(i * 2 + (first + n), (first + n) % 2, lambda j: True)
        if chain is not None:
            chain.clear()
    for l in range(first + 2 * pairs, B + depth):
        plain(l)
    if chain is not None:
        chain.clear()


def layer0_cross(c):
    nc = c.nc
    norm_stage(c, c.X, c.HN, "eps5")
    emb = c.T[:, 3, :]
    add_stage(c, emb, c.HN, c.CT)
    sq, k, v = c.T[:, 0, :], c.T[:, 1, :], c.T[:, 2, :]
    project_stage(c, [([emb], [c.w("L0x_wq")], c.w("L0x_bq"), ACT.Sigmoid, sq, None),
                      ([emb], [c.w("L0x_wk")], c.w("L0x_bk"), None, k, None),
                      ([emb], [c.w("L0x_wv")], c.w("L0x_bv"), None, v, None)])
    a = Arena(c)
    w, ew, ewT = a.take(2, S), a.take(2, S), a.take(2, S)
    wmax, nwmax = a.take(2), a.take(2)
    kmax, nkmax = a.take(2, 1), a.take(2, 1)
    ek, ekv = a.take(2, S), a.take(2, S)
    ekT, ekvT = a.take(2, P), a.take(2, P)
    rden, ratio = a.take(S), a.take(S)
    ident = c.w("identity")

    def pair(s):
        return c.psum[:, 2:4, :] if s else c.psum[:, 6:8, :]

    with nc.Block() as block:
        @block.vector
        def _(dve):
            chain = Chain(dve, c.vector_chain)
            chain.link(nc.vector.tensor_tensor(w, c.w("L0x_pos"), c.w("L0x_band"), ALU.mult))
            chain.link(nc.vector.reduce_max(wmax, w, AX.X))
            nc.vector.tensor_scalar(nwmax, wmax, -1.0, None, ALU.mult).then_inc(c.aux_v.sem, 1)
            for t in range(2):
                dve.wait_ge(c.aux_pe.sem, c.aux_pe.at(2 * t + 2))
                ins = nc.vector.tensor_copy(ewT[:, t, :], c.psum[:, 4 + t, 0:S])
            chain.link(ins)
            chain.clear()

            def step(l, s, has):
                if has(0):
                    chain.link(nc.vector.reduce_max(kmax[:, s], k[:, bass.ds(l * S, S)], AX.X))
                    nc.vector.tensor_scalar(nkmax[:, s], kmax[:, s], -1.0, None, ALU.mult).then_inc(c.aux_v2.sem, 1)
                if has(1):
                    dve.wait_ge(c.aux_pe2.sem, c.aux_pe2.base + l * 2)
                    if has(2):
                        dve.wait_ge(c.aux_pe3.sem, c.aux_pe3.base + l * 2 - 2)
                    nc.vector.tensor_copy(ekvT, c.psum[:, 1, 0:S].rearrange("p (t d) -> p t d", t=2)) \
                        .then_inc(c.aux_v3.sem, 1)
                if has(2):
                    dve.wait_ge(c.aux_pe3.sem, c.aux_pe3.base + l * 2 - 2)
                    chain.link(nc.vector.reciprocal(rden, pair(1 - s)[:, 0, 0:S]))
                    nc.vector.tensor_tensor(ratio, pair(1 - s)[:, 1, 0:S], rden, ALU.mult).then_inc(c.aux_v.sem, 1)
                    dve.wait_ge(c.aux_v.sem, c.aux_v.base + l)
                    q = sq[:, bass.ds((l - 2) * S, S)]
                    chain.link(nc.vector.tensor_tensor(q, q, ratio, ALU.mult))

            sequence_pipeline(dve, step, 2, chain)

        @block.scalar
        def _(act):
            act.wait_ge(c.aux_v.sem, c.aux_v.at(1))
            for t in range(2):
                nc.scalar.activation(ew[:, t, :], w[:, t, :], ACT.Exp, bias=nwmax[:, t:t + 1]) \
                    .then_inc(c.aux_s.sem, 1)

            def step(l, s, has):
                if has(0):
                    act.wait_ge(c.aux_v2.sem, c.aux_v2.base + l + 1)
                    if has(2):
                        act.wait_ge(c.aux_pe2.sem, c.aux_pe2.base + l * 2 - 2)
                    nc.scalar.activation(ek[:, s], k[:, bass.ds(l * S, S)], ACT.Exp, bias=nkmax[:, s]) \
                        .then_inc(c.aux_s2.sem, 1)
                if has(1):
                    act.wait_ge(c.aux_pe2.sem, c.aux_pe2.base + l * 2 - 1)
                    if has(2):
                        act.wait_ge(c.aux_pe3.sem, c.aux_pe3.base + l * 2 - 2)
                    nc.scalar.copy(ekT, c.psum[:, 0, 0:S].rearrange("p (t d) -> p t d", t=2)) \
                        .then_inc(c.aux_s3.sem, 1)

            sequence_pipeline(act, step, 2)

        @block.gpsimd
        def _(pool):
            def step(l, s, has):
                if has(0):
                    pool.wait_ge(c.aux_s2.sem, c.aux_s2.base + l + 1)
                    nc.gpsimd.tensor_tensor(ekv[:, s], ek[:, s], v[:, bass.ds(l * S, S)], ALU.mult) \
                        .then_inc(c.aux_p.sem, 1)

            sequence_pipeline(pool, step, 2)

        @block.tensor
        def _(pe):
            pe.wait_ge(c.aux_s.sem, c.aux_s.at(2))
            for j in range(2):
                for t in range(2):
                    nc.tensor.transpose(c.psum[:, 4 + j, t * P:(t + 1) * P], ew[:, t, j * P:(j + 1) * P], ident) \
                        .then_inc(c.aux_pe.sem, 1)

            def step(l, s, has):
                if not has(1):
                    return
                for n, (src, sig, out) in enumerate(((ek, c.aux_s2, c.aux_s3), (ekv, c.aux_p, c.aux_v3))):
                    pe.wait_ge(sig.sem, sig.base + l)
                    if has(2):
                        pe.wait_ge(out.sem, out.base + l - 1)
                    for t in range(2):
                        mm = nc.tensor.transpose(c.psum[:, n, t * P:(t + 1) * P], src[:, 1 - s, t * P:(t + 1) * P],
                                                 ident)
                    mm.then_inc(c.aux_pe2.sem, 1)
                if has(3):
                    pe.wait_ge(c.aux_v.sem, c.aux_v.base + l - 1)
                for n, (src, sig) in enumerate(((ekT, c.aux_s3), (ekvT, c.aux_v3))):
                    pe.wait_ge(sig.sem, sig.base + l)
                    for t in range(2):
                        mm = nc.tensor.matmul(pair(s)[:, n, 0:S], src[:, t, :], ewT[:, t, :],
                                              start=(t == 0), stop=(t == 1))
                    mm.then_inc(c.aux_pe3.sem, 1)

            sequence_pipeline(pe, step, 2)
    c.aux_v.advance(B)
    for s, n in ((c.aux_v, 1), (c.aux_s, 2), (c.aux_pe, 4), (c.aux_v2, B), (c.aux_v3, B), (c.aux_s2, B),
                 (c.aux_s3, B), (c.aux_p, B), (c.aux_pe2, 2 * B), (c.aux_pe3, 2 * B)):
        s.advance(n)
    project_stage(c, [([sq], [c.w("L0x_wo")], c.w("L0x_bo"), None, k, emb)])
    norm_stage(c, k, c.HN, "eps5", gain=c.w("L0x_gamma"), shift=c.w("L0x_beta"))
    w1, b1, w2 = c.w("L0x_w1"), c.w("L0x_b1"), c.w("L0x_w2")
    hidden = [c.T[:, t, :] for t in range(4)]
    project_stage(c, [([c.HN], [w1[:, t * P:(t + 1) * P]], b1[:, t:t + 1], ACT.Relu, hidden[t], None)
                      for t in range(4)])
    project_stage(c, [(hidden, [w2[:, t, :] for t in range(4)], c.w("L0x_b2"), None, c.HN, c.HN)])
    norm_stage(c, c.HN, c.HN, "eps5", gain=c.w("L0x_gamma"), shift=c.w("L0x_beta"))
    add_stage(c, c.X, c.X, c.HN)



E = 8
NT = N // P


PARTS = 3


def parts_tile(a):
    words = a.take(N // 2)
    return words, words.bitcast(BF16)


def route_stage(c, src, router, bias, w_b, a, mode, capacity=None, w_t=None):
    nc = c.nc
    ident = c.w("identity")
    logits, p, t1, t2, first, second, weight, chosen = [a.take(NT, E) for _ in range(8)]
    before = a.take(NT, E)
    parts, rest = a.take(NT, PARTS * E), a.take(NT, E)
    rounded = a.take(NT * E // 2).bitcast(BF16).rearrange("p (t e) -> p t e", e=E)
    m, r = a.take(NT), a.take(NT)
    falling = c.w("falling").unsqueeze(1).broadcast_to([P, NT, E])
    ps = c.psum[:, 0, 0:NT * E].rearrange("p (t e) -> p t e", e=E)

    def over(x):
        return x.unsqueeze(2).broadcast_to([P, NT, E])

    with nc.Block() as block:
        @block.tensor
        def _(pe):
            for t in range(NT):
                mm = nc.tensor.matmul(ps[:, t, :], src[:, t * P:(t + 1) * P], router, start=True, stop=True)
            mm.then_inc(c.aux_pe.sem, 1)
            if capacity is not None:
                pe.wait_ge(c.aux_v2.sem, c.aux_v2.at(1))
                flat = chosen.rearrange("p t e -> p (t e)")
                nc.tensor.matmul(c.psum[:, 1, 0:P], c.w("upper"), flat, start=True, stop=True)
                nc.tensor.matmul(c.psum[:, 2, 0:P], c.w("ones"), flat, start=True, stop=True) \
                    .then_inc(c.aux_pe2.sem, 1)
            pe.wait_ge(c.aux_v3.sem, c.aux_v3.at(1))
            for t in range(NT):
                mm = nc.tensor.transpose(c.psum[0:PARTS * E, 4 + t // 4, (t % 4) * P:(t % 4 + 1) * P], parts[:, t, :],
                                         ident)
            mm.then_inc(c.aux_pe3.sem, 1)

        @block.gpsimd
        def _(pool):
            if w_t is not None:
                nc.gpsimd.memset(w_t, 0.0)
            nc.gpsimd.memset(w_b[0], 0.0).then_inc(c.aux_p.sem, 1)

        @block.scalar
        def _(act):
            act.wait_ge(c.aux_v.sem, c.aux_v.at(1))
            nc.scalar.activation(p, t1, ACT.Exp).then_inc(c.aux_s.sem, 1)
            act.wait_ge(c.aux_p.sem, c.aux_p.at(1))
            act.wait_ge(c.aux_pe3.sem, c.aux_pe3.at(1))
            for i in range(NC):
                nc.scalar.copy(w_b[1][0:PARTS * E, i * CH:(i + 1) * CH], c.psum[0:PARTS * E, 4 + i, :])
            if w_t is not None:
                for i in range(NC):
                    nc.scalar.copy(w_t[0:PARTS * E, i * CH:(i + 1) * CH], c.psum[0:PARTS * E, 4 + i, :])

        @block.vector
        def _(dve):
            ch = Chain(dve, c.vector_chain)
            v = nc.vector
            dve.wait_ge(c.aux_pe.sem, c.aux_pe.at(1))
            if bias is None:
                ch.link(v.tensor_copy(logits, ps))
            else:
                ch.link(v.tensor_tensor(logits, ps, bias.unsqueeze(1).broadcast_to([P, NT, E]), ALU.add))
            ch.link(v.reduce_max(m, logits, AX.X))
            v.tensor_tensor(t1, logits, over(m), ALU.subtract).then_inc(c.aux_v.sem, 1)
            dve.wait_ge(c.aux_s.sem, c.aux_s.at(1))
            ch.link(v.reduce_sum(m, p, AX.X))
            ch.link(v.reciprocal(r, m))
            ch.link(v.tensor_tensor(p, p, over(r), ALU.mult))

            def likeliest(q, one_hot):
                ch.link(v.reduce_max(m, q, AX.X))
                ch.link(v.tensor_tensor(t1, q, over(m), ALU.is_equal))
                ch.link(v.tensor_tensor(t1, t1, falling, ALU.mult))
                ch.link(v.reduce_max(m, t1, AX.X))
                ch.link(v.tensor_tensor(one_hot, t1, over(m), ALU.is_equal))

            likeliest(p, first)
            if mode == "single":
                ch.link(v.tensor_copy(chosen, first))
            else:
                ch.link(v.scalar_tensor_tensor(t2, first, -3.0, p, ALU.mult, ALU.add))
                likeliest(t2, second)
                ch.link(v.tensor_tensor(chosen, first, second, ALU.add))
            ch.link(v.tensor_tensor(weight, chosen, p, ALU.mult))
            if mode == "pair_normed":
                ch.link(v.reduce_sum(m, weight, AX.X))
                ch.link(v.reciprocal(r, m))
                ch.link(v.tensor_tensor(weight, weight, over(r), ALU.mult))
            if capacity is not None:
                v.memset(before[:, 0, :], 0.0).then_inc(c.aux_v2.sem, 1)
                dve.wait_ge(c.aux_pe2.sem, c.aux_pe2.at(1))
                totals = c.psum[:, 2, 0:P].rearrange("p (t e) -> p t e", e=E)
                ch.link(v.tensor_copy(t2, totals))
                for t in range(1, NT):
                    ch.link(v.tensor_tensor(before[:, t, :], before[:, t - 1, :], t2[:, t - 1, :], ALU.add))
                ch.link(v.tensor_tensor(t1, c.psum[:, 1, 0:P].rearrange("p (t e) -> p t e", e=E), before, ALU.add))
                ch.link(v.tensor_scalar(t1, t1, float(capacity), None, ALU.is_le))
                ch.link(v.tensor_tensor(weight, weight, t1, ALU.mult))
            left = weight
            for n in range(PARTS - 1):
                part = parts[:, :, n * E:(n + 1) * E]
                ch.link(v.tensor_copy(rounded, left))
                ch.link(v.tensor_copy(part, rounded))
                new = rest if n < PARTS - 2 else parts[:, :, (n + 1) * E:]
                ins = v.tensor_tensor(new, left, part, ALU.subtract)
                left = new
                if n < PARTS - 2:
                    ch.link(ins)
            ins.then_inc(c.aux_v3.sem, 1)
            dve.wait_ge(c.aux_v3.sem, c.aux_v3.at(1))
            ch.clear()
    for s in (c.aux_pe, c.aux_pe3, c.aux_v, c.aux_s, c.aux_v3, c.aux_p):
        s.advance(1)
    if capacity is not None:
        c.aux_pe2.advance(1)
        c.aux_v2.advance(1)


def picks(c):
    return c.w("pick").bitcast(BF16).rearrange("p (e x) -> p e x", x=P)


def expert_stage(c, src, experts, w_b, a, out_bias=None, w_t=None):
    nc = c.nc
    units = [(e, i) for e in range(len(experts)) for i in range(len(experts[e][1]))]
    gated = experts[0][2][0].shape[1] > 1
    NU, NE = len(units), len(experts)
    routed = [e for e in range(NE) if experts[e][0] is not None]
    NR = len(routed)
    LAG = 2
    act_buf = a.take(2, CH) if gated else None
    hid = a.take(4, CH)
    wb = a.take(2, CH)
    part = a.take(2, CH)
    acc = a.take(CH)
    pick = picks(c)
    per_expert = NU // NE

    def gate_bank(n):
        return 2 * (n % 2) if gated else n % 4

    with nc.Block() as block:
        @block.tensor
        def _(pe):
            with pe.Fori(0, NC) as i:
                x = src[:, bass.ds(i * CH, CH)]
                u0, e0, r0 = i * NU, i * NE, i * NR
                for n in range(NU + LAG):
                    if n < NU:
                        e, t = units[n]
                        if t == 0 and experts[e][0] is not None:
                            r = routed.index(e)
                            pe.wait_ge(c.aux_s2.sem, c.aux_s2.base + r0 + r)
                            nc.tensor.matmul(c.psum[:, 6, :], pick[:, experts[e][0], :],
                                             w_b[1][:, bass.ds(i * CH, CH)], start=True, stop=True) \
                                .then_inc(c.aux_pe3.sem, 1)
                        depth = 2 if gated else 4
                        if n >= depth:
                            pe.wait_ge(c.aux_v.sem, c.aux_v.base + u0 + n - depth + 1)
                        nc.tensor.matmul(c.psum[:, gate_bank(n), :], experts[e][1][t], x, start=True, stop=True) \
                            .then_inc(c.aux_pe.sem, 1)
                        if gated:
                            nc.tensor.matmul(c.psum[:, gate_bank(n) + 1, :], experts[e][2][t], x,
                                             start=True, stop=True).then_inc(c.aux_pe.sem, 1)
                    if n >= LAG:
                        k = n - LAG
                        e, t = units[k]
                        if t == 0:
                            pe.wait_ge(c.aux_v2.sem, c.aux_v2.base + e0 + max(e - 1, 0))
                        pe.wait_ge(c.aux_v.sem, c.aux_v.base + u0 + k + 1)
                        mm = nc.tensor.matmul(c.psum[:, 4 + e % 2, :], experts[e][3][t], hid[:, k % 4, :],
                                              start=(t == 0), stop=(t == per_expert - 1))
                        mm.then_inc(c.aux_pe2.sem, 1)
                if out_bias is not None:
                    pe.wait_ge(c.out_added.sem, c.out_added.base + i)
                    nc.tensor.matmul(c.psum[:, 7, :], out_bias, w_t[:, bass.ds(i * CH, CH)],
                                     start=True, stop=True) \
                        .then_inc(c.product_ready.sem, 1)

        @block.scalar
        def _(act):
            with act.Fori(0, NC) as i:
                u0, r0 = i * NU, i * NR
                for n in range(NU):
                    e, t = units[n]
                    if t == 0 and experts[e][0] is not None:
                        r = routed.index(e)
                        act.wait_ge(c.aux_pe3.sem, c.aux_pe3.base + r0 + r + 1)
                        act.wait_ge(c.aux_v2.sem, c.aux_v2.base + i * NE + max(e - 1, 0))
                        nc.scalar.copy(wb[:, r % 2, :], c.psum[:, 6, :]).then_inc(c.aux_s2.sem, 1)
                    if gated:
                        act.wait_ge(c.aux_pe.sem, c.aux_pe.base + 2 * (u0 + n) + 1)
                        if n >= 2:
                            act.wait_ge(c.aux_v.sem, c.aux_v.base + u0 + n - 1)
                        nc.scalar.activation(act_buf[:, n % 2, :], c.psum[:, gate_bank(n), :], ACT.Silu) \
                            .then_inc(c.aux_s.sem, 1)

        @block.vector
        def _(dve):
            chain = Chain(dve, c.vector_chain)
            with dve.Fori(0, NC) as i:
                u0, e0, r0 = i * NU, i * NE, i * NR

                def take(e):
                    dve.wait_ge(c.aux_pe2.sem, c.aux_pe2.base + u0 + (e + 1) * per_expert)
                    if experts[e][0] is None:
                        src_ = c.psum[:, 4 + e % 2, :]
                    else:
                        r = routed.index(e)
                        dve.wait_ge(c.aux_s2.sem, c.aux_s2.base + r0 + r + 1)
                        src_ = part[:, e % 2, :]
                        chain.link(nc.vector.tensor_tensor(src_, c.psum[:, 4 + e % 2, :], wb[:, r % 2, :], ALU.mult))
                    if e == 0:
                        ins = nc.vector.tensor_copy(acc, src_)
                    else:
                        ins = nc.vector.tensor_tensor(acc, acc, src_, ALU.add)
                    ins.then_inc(c.aux_v2.sem, 1)
                    dve.wait_ge(c.aux_v2.sem, c.aux_v2.base + e0 + e + 1)

                for n in range(NU):
                    e, t = units[n]
                    if n >= 4:
                        dve.wait_ge(c.aux_pe2.sem, c.aux_pe2.base + u0 + n - 3)
                    if gated:
                        dve.wait_ge(c.aux_s.sem, c.aux_s.base + u0 + n + 1)
                        dve.wait_ge(c.aux_pe.sem, c.aux_pe.base + 2 * (u0 + n) + 2)
                        ins = nc.vector.tensor_tensor(hid[:, n % 4, :], act_buf[:, n % 2, :],
                                                      c.psum[:, gate_bank(n) + 1, :], ALU.mult)
                    else:
                        dve.wait_ge(c.aux_pe.sem, c.aux_pe.base + u0 + n + 1)
                        ins = nc.vector.tensor_scalar(hid[:, n % 4, :], c.psum[:, gate_bank(n), :],
                                                      experts[e][2][t], 0.0, ALU.add, ALU.max)
                    ins.then_inc(c.aux_v.sem, 1)
                    if t == per_expert - 1 and e >= 1:
                        take(e - 1)
                take(NE - 1)
                xs = c.X[:, bass.ds(i * CH, CH)]
                chain.link(nc.vector.tensor_tensor(xs, xs, acc, ALU.add))
                chain.clear()
                if out_bias is not None:
                    dve.wait_ge(c.product_ready.sem, c.product_ready.base + i + 1)
                    nc.vector.tensor_tensor(xs, xs, c.psum[:, 7, :], ALU.add).then_inc(c.out_added.sem, 1)
    per = 2 if gated else 1
    for s, n in ((c.aux_pe, per * NU), (c.aux_pe2, NU), (c.aux_pe3, NR), (c.aux_s, NU if gated else 0),
                 (c.aux_s2, NR), (c.aux_v, NU), (c.aux_v2, NE)):
        s.advance(NC * n)
    if out_bias is not None:
        c.product_ready.advance(NC)
        c.out_added.advance(NC)


def layer0_experts(c):
    start_loads(c, [pack_load(c, c.big_loaded, "L0f", 0, c.packs["L0"])])
    norm_stage(c, c.X, c.HN, "eps5")
    norm_stage(c, c.HN, c.T[:, 0, :], "epsf", centre=False)
    a = Arena(c)
    w_b = parts_tile(a)
    loads_done(c, c.loaded_ahead)
    route_stage(c, c.T[:, 0, :], c.w("L0f_router"), None, w_b, a, "pair_normed", capacity=int(1.25 * N / E))
    rg, ru, rd = c.w("L0f_rg"), c.w("L0f_ru"), c.w("L0f_rd")
    sg, su, sd = c.w("L0f_sg"), c.w("L0f_su"), c.w("L0f_sd")
    experts = [(e, [rg[:, e, t * P:(t + 1) * P] for t in range(4)], [ru[:, e, t * P:(t + 1) * P] for t in range(4)],
                [rd[:, e, t, :] for t in range(4)]) for e in range(E)]
    experts += [(None, [sg[:, t * P:(t + 1) * P] for t in range(4 * h, 4 * h + 4)],
                 [su[:, t * P:(t + 1) * P] for t in range(4 * h, 4 * h + 4)],
                 [sd[:, t, :] for t in range(4 * h, 4 * h + 4)]) for h in range(2)]
    loads_done(c, c.big_loaded)
    expert_stage(c, c.HN, experts, w_b, a)



def turn_stage(c, groups):
    nc = c.nc
    ident = c.w("identity")

    def bank(n, k):
        return c.psum[:, n % 8, 0:k * P].rearrange("p (k x) -> p k x", x=P)

    with nc.Block() as block:
        @block.tensor
        def _(pe):
            for n, (views, _) in enumerate(groups):
                if n >= 8:
                    sig = c.product_taken if n % 2 == 0 else c.product_taken_v
                    pe.wait_ge(sig.sem, sig.at((n - 8) // 2 + 1))
                for k, view in enumerate(views):
                    mm = nc.tensor.transpose(bank(n, len(views))[:, k, :], view, ident)
                mm.then_inc(c.product_ready.sem, 1)

        @block.scalar
        def _(act):
            for n in range(0, len(groups), 2):
                views, dst = groups[n]
                act.wait_ge(c.product_ready.sem, c.product_ready.at(n + 1))
                nc.scalar.copy(dst, bank(n, len(views))).then_inc(c.product_taken.sem, 1)

        @block.vector
        def _(dve):
            for n in range(1, len(groups), 2):
                views, dst = groups[n]
                dve.wait_ge(c.product_ready.sem, c.product_ready.at(n + 1))
                nc.vector.tensor_copy(dst, bank(n, len(views))).then_inc(c.product_taken_v.sem, 1)
    c.product_ready.advance(len(groups))
    c.product_taken.advance((len(groups) + 1) // 2)
    c.product_taken_v.advance(len(groups) // 2)


def conv_stage(c, tensors, taps):
    nc = c.nc
    a = Arena(c)
    acc = [a.take(N) for _ in tensors]
    with nc.Block() as block:
        @block.vector
        def _(dve):
            chain = Chain(dve, c.vector_chain)
            for x, w, y in zip(tensors, taps, acc):
                K = w.shape[1]
                xs = x.rearrange("p (b s) -> p b s", s=S)
                ys = y.rearrange("p (b s) -> p b s", s=S)
                chain.link(nc.vector.tensor_scalar(y, x, w[:, K - 1:K], None, ALU.mult))
                for back in range(1, K):
                    ins = nc.vector.scalar_tensor_tensor(ys[:, :, back:], xs[:, :, 0:S - back],
                                                         w[:, K - 1 - back:K - back], ys[:, :, back:],
                                                         ALU.mult, ALU.add)
                    if back < K - 1:
                        chain.link(ins)
                ins.then_inc(c.aux_v.sem, 1)
            dve.wait_ge(c.aux_v.sem, c.aux_v.at(len(tensors)))
            chain.clear()

        @block.scalar
        def _(act):
            for n, (x, y) in enumerate(zip(tensors, acc)):
                act.wait_ge(c.aux_v.sem, c.aux_v.at(n + 1))
                nc.scalar.activation(x, y, ACT.Silu)
    c.aux_v.advance(len(tensors))


def layer1_attention(c):
    nc = c.nc
    H, D = 8, 16
    first = c.slots["causal"][1]
    start_loads(c, [pack_load(c, c.big_loaded, "L1", 0, first), pack_load(c, c.loaded_ahead, "L1", first),
                    pack_load(c, c.loaded_ahead, "L2")])
    norm_stage(c, c.X, c.HN, "eps5")
    loads_done(c, c.big_loaded)
    q, k, v = c.T[:, 0, :], c.T[:, 1, :], c.T[:, 2, :]
    project_stage(c, [([c.HN], [c.w(f"L1a_w{s}")], None, None, t, None) for s, t in zip("qkv", (q, k, v))])
    conv_stage(c, [q, k, v], [c.w(f"L1a_conv_{s}") for s in "qkv"])

    a = Arena(c)
    mark0 = a.off
    qt, kt, vbt, _, vt = [a.take(2, B, P) for _ in range(5)]
    gates = a.take(NT, 2 * H)
    lengths, inv = a.take(2, 2 * B * H), a.take(2, 2 * B * H)
    mark = a.off
    GT = 16
    v_r, o_pad, beta_r = a.take(S, 8), a.take(S + GT, 8), a.take(S)
    o_r = o_pad[:, GT:, :]
    end = a.off
    groups = []
    for src, dst in ((q, qt), (k, kt), (v, vt)):
        for th in range(2):
            for b0 in range(0, B, 4):
                groups.append(([src[:, b * S + th * P:b * S + (th + 1) * P] for b in range(b0, b0 + 4)],
                               dst[:, th, b0:b0 + 4, :]))
    turn_stage(c, groups)

    square = c.work[:, mark:mark + 2 * N].rearrange("p (n x) -> p n x", x=N)
    q2 = c.T[:, 0:2, :].rearrange("p t (g w d) -> p t g w d", w=2, d=D)
    k2 = c.T[:, 2:4, :].rearrange("p t (g w d) -> p t g w d", w=2, d=D)
    ps_g = c.psum[:, 0, 0:NT * 2 * H].rearrange("p (n e) -> p n e", e=2 * H)

    def heads(x):
        return x.rearrange("p t b (h d) -> p (t b h) d", d=D)

    with nc.Block() as block:
        @block.tensor
        def _(pe):
            for n in range(NT):
                mm = nc.tensor.matmul(ps_g[:, n, :], c.HN[:, n * P:(n + 1) * P], c.w("L1a_gates"),
                                      start=True, stop=True)
            mm.then_inc(c.aux_pe.sem, 1)

        @block.scalar
        def _(act):
            for n, x in enumerate((qt, kt)):
                nc.scalar.activation(square[:, n, :], x.rearrange("p t b f -> p (t b f)"), ACT.Square) \
                    .then_inc(c.aux_s.sem, 1)
            act.wait_ge(c.aux_v.sem, c.aux_v.at(2))
            nc.scalar.activation(lengths, lengths, ACT.Sqrt, bias=c.w("eps12")).then_inc(c.aux_s.sem, 1)
            act.wait_ge(c.aux_v2.sem, c.aux_v2.at(1))
            nc.scalar.activation(gates, gates, ACT.Sigmoid).then_inc(c.aux_s.sem, 1)

        @block.vector
        def _(dve):
            ch = Chain(dve, c.vector_chain)
            dve.wait_ge(c.aux_pe.sem, c.aux_pe.at(1))
            nc.vector.tensor_tensor(gates, ps_g, c.w("L1a_mix_b").unsqueeze(1).broadcast_to([P, NT, 2 * H]), ALU.add) \
                .then_inc(c.aux_v3.sem, 1)
            dve.wait_ge(c.aux_v3.sem, c.aux_v3.at(1))
            nc.vector.tensor_tensor(gates, gates, c.w("L1a_mix_bias").unsqueeze(1).broadcast_to([P, NT, 2 * H]),
                                    ALU.add).then_inc(c.aux_v2.sem, 1)
            for n in range(2):
                dve.wait_ge(c.aux_s.sem, c.aux_s.at(n + 1))
                nc.vector.reduce_sum(lengths[:, n, :], square[:, n, :].rearrange("p (g d) -> p g d", d=D), AX.X) \
                    .then_inc(c.aux_v.sem, 1)
            dve.wait_ge(c.aux_s.sem, c.aux_s.at(3))
            ch.link(nc.vector.reciprocal(inv, lengths))
            for n, (x, x2) in enumerate(((qt, q2), (kt, k2))):
                for th in range(2):
                    g = slice(th * B * H, (th + 1) * B * H)
                    for w in range(2):
                        nc.vector.tensor_tensor(x2[:, th, :, w, :], heads(x)[:, g, :],
                                                inv[:, n, g].unsqueeze(2).broadcast_to([P, B * H, D]), ALU.mult)
            dve.wait_ge(c.aux_s.sem, c.aux_s.at(4))
            beta = gates[:, :, 0:H].rearrange("p (b t) h -> p t b h", t=2)
            for th in range(2):
                nc.vector.tensor_tensor(vbt[:, th].rearrange("p b (h d) -> p b h d", d=D),
                                        vt[:, th].rearrange("p b (h d) -> p b h d", d=D),
                                        beta[:, th].unsqueeze(3).broadcast_to([P, B, H, D]), ALU.mult)
            ch.clear()
    for s, n in ((c.aux_pe, 1), (c.aux_s, 4), (c.aux_v, 2), (c.aux_v2, 1), (c.aux_v3, 1)):
        s.advance(n)

    q_r = c.work[:, mark0:mark0 + 2 * N].rearrange("p (t d) -> p t d", d=D)
    k_r = c.work[:, mark0 + 2 * N:mark0 + 4 * N].rearrange("p (t d) -> p t d", d=D)
    beta2 = c.HN[:, 0:2 * P].rearrange("p (t g w) -> p t g w", t=2, w=2)
    with nc.Block() as block:
        @block.vector
        def _(dve):
            for th in range(2):
                for w in range(2):
                    nc.vector.tensor_copy(beta2[:, th, :, w].rearrange("p (b h) -> p b h", h=H),
                                          gates[:, :, 0:H].rearrange("p (b t) h -> p t b h", t=2)[:, th])
    groups = []
    for th in range(2):
        for d0 in range(0, 8, 4):
            views = [vbt[:, th].rearrange("p b (g d) -> p (b g) d", d=8)[:, :, d] for d in range(d0, d0 + 4)]
            groups.append((views, v_r[:, th * P:(th + 1) * P, d0:d0 + 4].rearrange("p t d -> p d t")))
        groups.append(([beta2[:, th].rearrange("p g w -> p (g w)")],
                       beta_r[:, th * P:(th + 1) * P].unsqueeze(1)))
    turn_stage(c, groups)
    groups = []
    for th in range(2):
        for src, dst in ((q2, q_r), (k2, k_r)):
            for d0 in range(0, D, 4):
                views = [src[:, th].rearrange("p g w d -> p (g w) d")[:, :, d] for d in range(d0, d0 + 4)]
                groups.append((views, dst[:, th * P:(th + 1) * P, d0:d0 + 4].rearrange("p t d -> p d t")))
    turn_stage(c, groups)

    a.off = end
    C = 4
    NCH = S // C
    tri = a.take(NCH, C * C)
    keys4 = k_r.rearrange("p (n i) d -> p n i d", i=C)
    two, one = a.take(NCH, 2), a.take(NCH, 1)
    flat = c.T[:, :, :].rearrange("p a x -> p (a x)")

    def pairs(back):
        base = sum(NCH * (C - x) * D for x in range(1, back))
        return flat[:, base:base + NCH * (C - back) * D].rearrange("p (n i d) -> p n i d", i=C - back, d=D)

    def entries(first, n=1):
        return tri[:, :, first:first + (n - 1) * (C + 1) + 1:C + 1]

    with nc.Block() as block:
        @block.gpsimd
        def _(pool):
            for back in range(1, C):
                nc.gpsimd.tensor_tensor(pairs(back), keys4[:, :, back:, :], keys4[:, :, 0:C - back, :], ALU.mult) \
                    .then_inc(c.aux_p.sem, 1)

        @block.vector
        def _(dve):
            ch = Chain(dve, c.vector_chain)
            v = nc.vector
            ch.step(v.tensor_scalar(beta_r, beta_r, -1.0, None, ALU.mult))
            ch.link(v.memset(tri, 0.0))
            for back in range(1, C):
                dve.wait_ge(c.aux_p.sem, c.aux_p.at(back))
                ch.step(v.reduce_sum(entries(back * C, C - back), pairs(back), AX.X))
            ch.all_but(0)
            rows = tri.rearrange("p n (i j) -> p n i j", j=C)
            ch.link(v.tensor_tensor(rows, rows, beta_r.rearrange("p (n i) -> p n i", i=C).unsqueeze(3)
                                    .broadcast_to([P, NCH, C, C]), ALU.mult))
            ch.step(v.tensor_tensor(two, entries(9, 2), entries(4, 2), ALU.mult))
            ch.link(v.tensor_tensor(one, entries(13), entries(4), ALU.mult))
            ch.step(v.tensor_tensor(entries(12), entries(12), one, ALU.add))
            ch.link(v.tensor_tensor(entries(8, 2), entries(8, 2), two, ALU.add))
            ch.link(v.tensor_tensor(one, entries(14), entries(8), ALU.mult))
            ch.link(v.tensor_tensor(entries(12), entries(12), one, ALU.add))
            v.memset(entries(0, C), 1.0)
            ch.clear()
    c.aux_p.advance(C - 1)

    CG = GT // C
    slots = c.T[:, 0:3, :].rearrange("p a x -> p (a x)")[:, 0:2 * CG * (C + 1) * 8 * D] \
        .rearrange("p (r c s x) -> p r c s x", r=2, c=CG, s=C + 1)
    qs = [c.T[:, 3, :].rearrange("p (t v d) -> p t v d", v=8, d=D), c.HN[:, :].rearrange("p (t v d) -> p t v d", v=8, d=D)]
    a.off = end + NCH * C * C
    pred, w, tw, u = a.take(C, 8), a.take(C, 8), a.take(C, 8, C), a.take(C, 8)
    sk = c.psum[:, 0, :].rearrange("p (i v d) -> p i v d", v=8, d=D)
    staged = c.T[:, 2, N - 4 * GT * D:].rearrange("p (n r t d) -> p n r t d", n=2, r=2, d=D)
    k_b, kb_b = staged[:, 0], staged[:, 1]
    NI = S // (2 * GT)

    rows = tri.rearrange("p n (i j) -> p (n i) j", j=C)

    def slot(r, cc, s):
        return slots[:, r, cc, s, :].rearrange("p (v d) -> p v d", d=D)

    with nc.Block() as block:
        @block.scalar
        def _(act):
            with act.Fori(0, NI) as i:
                for r in range(2):
                    g = i * 2 + r
                    act.wait_ge(c.aux_v.sem, c.aux_v.base + g - 1)
                    nc.scalar.copy(k_b[:, r], k_r[:, bass.ds(g * GT, GT), :]).then_inc(c.aux_s.sem, 1)

        @block.gpsimd
        def _(pool):
            ch = Chain(pool, c.pool_chain)

            nc.gpsimd.memset(qs[1], 0.0).then_inc(c.aux_p.sem, 1)
            with pool.Fori(0, NI) as i:
                for r in range(2):
                    g = i * 2 + r
                    pool.wait_ge(c.aux_v.sem, c.aux_v.base + g + 1)
                    for s in range(1, C + 1):
                        ch.link(nc.gpsimd.tensor_tensor(slots[:, r, :, s, :], slots[:, r, :, s, :],
                                                        slots[:, r, :, s - 1, :], ALU.add))
                    for cc in range(CG):
                        qv = q_r[:, bass.ds(g * GT + cc * C, C), :].unsqueeze(2).broadcast_to([P, C, 8, D])
                        ins = nc.gpsimd.tensor_tensor(qs[r][:, cc * C:(cc + 1) * C],
                                                      slots[:, r, cc, 1:C + 1, :].rearrange("p s (v d) -> p s v d", d=D),
                                                      qv, ALU.mult)
                    ins.then_inc(c.aux_p.sem, 1)
                ch.clear()

        @block.vector
        def _(dve):
            ch = Chain(dve, c.vector_chain)
            v = nc.vector
            ch.link(v.memset(slot(0, 0, 0), 0.0))
            ch.clear()
            with dve.Fori(0, NI) as i:
                for r in range(2):
                    g = i * 2 + r
                    dve.wait_ge(c.aux_s.sem, c.aux_s.base + g + 1)
                    ch.link(v.tensor_tensor(kb_b[:, r], k_b[:, r], beta_r[:, bass.ds(g * GT, GT)].unsqueeze(2)
                                            .broadcast_to([P, GT, D]), ALU.mult))
                    for cc in range(CG):
                        old = slot(r, cc, 0).unsqueeze(1).broadcast_to([P, C, 8, D])
                        tok = slice(cc * C, (cc + 1) * C)
                        ch.link(v.tensor_tensor(sk, old, kb_b[:, r, tok].unsqueeze(2).broadcast_to([P, C, 8, D]),
                                                ALU.mult))
                        ch.link(v.reduce_sum(pred, sk, AX.X))
                        ch.link(v.tensor_tensor(w, pred, v_r[:, bass.ds(g * GT + cc * C, C), :], ALU.add))
                        T4 = rows[:, bass.ds((g * CG + cc) * C, C), :].unsqueeze(2).broadcast_to([P, C, 8, C])
                        ch.link(v.tensor_tensor(tw, T4, w.rearrange("p j v -> p v j").unsqueeze(1)
                                                .broadcast_to([P, C, 8, C]), ALU.mult))
                        ch.link(v.reduce_sum(u, tw, AX.X))
                        ch.link(v.tensor_tensor(slots[:, r, cc, 1:C + 1, :].rearrange("p s (v d) -> p s v d", d=D),
                                                u.unsqueeze(3).broadcast_to([P, C, 8, D]),
                                                k_b[:, r, tok].unsqueeze(2).broadcast_to([P, C, 8, D]), ALU.mult))
                        nxt = slots[:, r, cc + 1, 0, :] if cc < CG - 1 else slots[:, 1 - r, 0, 0, :]
                        ins = v.reduce_sum(nxt, slots[:, r, cc].rearrange("p s x -> p x s"), AX.X)
                        if cc < CG - 1:
                            ch.link(ins)
                        else:
                            ins.then_inc(c.aux_v.sem, 1)
                            dve.wait_ge(c.aux_v.sem, c.aux_v.base + g + 1)
                        if cc == CG - 2:
                            dve.wait_ge(c.aux_p.sem, c.aux_p.base + g + 1)
                            ch.step(v.reduce_sum(o_pad[:, bass.ds(g * GT, GT), :], qs[1 - r], AX.X))
                ch.link(v.tensor_copy(pred, u))
                ch.clear()
            dve.wait_ge(c.aux_p.sem, c.aux_p.base + 2 * NI + 1)
            v.reduce_sum(o_pad[:, S:S + GT, :], qs[1], AX.X)
    c.aux_s.advance(2 * NI)
    c.aux_v.advance(2 * NI)
    c.aux_p.advance(2 * NI + 1)

    o_t = qt
    groups = []
    for th in range(2):
        for d0 in range(0, 8, 4):
            views = [o_r[:, th * P:(th + 1) * P, d] for d in range(d0, d0 + 4)]
            dst = o_t[:, th].rearrange("p b (g d) -> p d (b g)", d=8)[:, d0:d0 + 4, :]
            groups.append((views, dst))
    turn_stage(c, groups)

    def wide(x, th):
        return x[:, th].rearrange("p b (h d) -> p b h d", d=D)

    ms = lengths[:, 0, :]
    with nc.Block() as block:
        @block.vector
        def _(dve):
            ch = Chain(dve, c.vector_chain)
            v = nc.vector
            gate = gates[:, :, H:2 * H].rearrange("p (b t) h -> p t b h", t=2)
            flat = "p t b f -> p (t b f)"
            ch.link(v.tensor_tensor(o_t.rearrange(flat), o_t.rearrange(flat), vt.rearrange(flat), ALU.subtract))
            for th in range(2):
                ch.link(v.tensor_tensor(wide(o_t, th), wide(o_t, th), gate[:, th].unsqueeze(3)
                                        .broadcast_to([P, B, H, D]), ALU.mult))
            v.tensor_tensor(o_t.rearrange(flat), o_t.rearrange(flat), vt.rearrange(flat), ALU.add) \
                .then_inc(c.aux_v.sem, 1)
            dve.wait_ge(c.aux_s.sem, c.aux_s.at(1))
            v.reduce_sum(ms, kt.rearrange("p t b (h d) -> p (t b h) d", d=D), AX.X).then_inc(c.aux_v.sem, 1)
            dve.wait_ge(c.aux_s.sem, c.aux_s.at(2))
            ch.link(v.reciprocal(inv[:, 0, :], ms))
            ch.link(v.tensor_tensor(heads(o_t), heads(o_t), inv[:, 0, :].unsqueeze(2)
                                    .broadcast_to([P, 2 * B * H, D]), ALU.mult))
            ch.link(v.tensor_tensor(heads(o_t), heads(o_t), c.w("L1a_onorm").unsqueeze(1)
                                    .broadcast_to([P, 2 * B * H, D]), ALU.mult))
            ch.clear()

        @block.scalar
        def _(act):
            act.wait_ge(c.aux_v.sem, c.aux_v.at(1))
            nc.scalar.activation(kt.rearrange("p t b f -> p (t b f)"), o_t.rearrange("p t b f -> p (t b f)"),
                                 ACT.Square).then_inc(c.aux_s.sem, 1)
            act.wait_ge(c.aux_v.sem, c.aux_v.at(2))
            nc.scalar.activation(ms, ms, ACT.Sqrt, scale=1.0 / D, bias=c.w("eps5")).then_inc(c.aux_s.sem, 1)
    c.aux_v.advance(2)
    c.aux_s.advance(2)
    groups = []
    o_f = c.T[:, 0, :]
    for b in range(0, B, 2):
        groups.append(([o_t[:, th, bb, :] for bb in (b, b + 1) for th in range(2)],
                       o_f[:, b * S:(b + 2) * S].rearrange("p (k x) -> p k x", x=P)))
    turn_stage(c, groups)
    project_stage(c, [([o_f], [c.w("L1a_wo")], None, None, c.X, c.X)])


def layer1_cross(c):
    nc = c.nc
    loads_done(c, c.loaded_ahead)
    with nc.Block() as block:
        @block.vector
        def _(dve):
            nc.vector.tensor_copy(c.valid[:, :], c.valid_i32[:, :])
    norm_stage(c, c.X, c.HN, "eps5")
    wq, wk, wo = c.w("L1x_wq"), c.w("L1x_wk"), c.w("L1x_wo")

    def prepare(nc, dve, chain, b, mb):
        far = mb[:, 2 * S:3 * S]
        chain.link(nc.vector.tensor_scalar(far, c.w("position"), c.valid[:, bass.ds(b, 1)], NEG, ALU.is_ge, ALU.mult))
        for qt in range(2):
            chain.link(nc.vector.tensor_tensor(mb[:, qt * S:(qt + 1) * S], c.w("causal")[:, qt, :], far, ALU.min))

    attention_stage(c, 16, 64, c.HN, c.CT, c.CT, [wq[:, t, :] for t in range(8)], c.w("L1x_bq"),
                    [wk[:, t, :] for t in range(8)], c.w("L1x_bk"), c.w("L1x_wv"), c.w("L1x_bv"),
                    [wo[:, t, :] for t in range(8)], c.w("L1x_bo"), scale=1.0 / 8.0,
                    mask=lambda mb, qt: mb[:, qt * S:(qt + 1) * S], prepare_mask=prepare, mask_words=3 * S)


def layer1_experts(c):
    norm_stage(c, c.X, c.HN, "eps5")
    a = Arena(c)
    w_t, w_b = a.take(N), parts_tile(a)
    route_stage(c, c.HN, c.w("L1f_gate"), c.w("L1f_gate_b"), w_b, a, "pair", w_t=w_t)
    w1, b1, w2 = c.w("L1f_w1"), c.w("L1f_b1"), c.w("L1f_w2")
    experts = [(e, [w1[:, e, t * P:(t + 1) * P] for t in range(2)], [b1[:, e, t:t + 1] for t in range(2)],
                [w2[:, e, t, :] for t in range(2)]) for e in range(E)]
    expert_stage(c, c.HN, experts, w_b, a, out_bias=c.w("L1f_b2"), w_t=w_t)



def trig_stage(c, trig):
    nc = c.nc
    a = Arena(c)
    ang, turns, r, absr, sn, cs = [a.take(2, S) for _ in range(6)]
    theta = c.w("L2a_theta")
    flat = "p t s -> p (t s)"
    MAGIC = 1.5 * 2.0 ** 23
    two_pi = 2.0 * np.pi
    hi = 6.28125
    mid = float(np.float32(np.round((two_pi - hi) * 2.0 ** 20) / 2.0 ** 20))
    lo = float(two_pi - hi - mid)
    edge = 3.1415925
    with nc.Block() as block:
        @block.vector
        def _(dve):
            ch = Chain(dve, c.vector_chain)
            v = nc.vector
            for t in range(2):
                ch.link(v.tensor_scalar(ang[:, t], c.w("position"), theta[:, t:t + 1], None, ALU.mult))
            ch.link(v.tensor_scalar(turns, ang, float(1.0 / two_pi), MAGIC, ALU.mult, ALU.add))
            ch.link(v.tensor_scalar(turns, turns, MAGIC, None, ALU.subtract))
            ch.link(v.scalar_tensor_tensor(r, turns, -hi, ang, ALU.mult, ALU.add))
            ch.link(v.scalar_tensor_tensor(ang, turns, -mid, r, ALU.mult, ALU.add))
            ch.link(v.scalar_tensor_tensor(r, turns, -lo, ang, ALU.mult, ALU.add))
            v.tensor_scalar(r, r, edge, -edge, ALU.min, ALU.max).then_inc(c.aux_v.sem, 1)
            dve.wait_ge(c.aux_s.sem, c.aux_s.at(1))
            ch.link(v.tensor_scalar(turns, sn, c.w("L2a_sine_rows"), None, ALU.mult))
            ch.link(v.scalar_tensor_tensor(trig.rearrange(flat), cs.rearrange(flat), c.w("L2a_cosine_rows"),
                                           turns.rearrange(flat), ALU.mult, ALU.add))
            ch.clear()

        @block.scalar
        def _(act):
            ch = Chain(act, c.scalar_chain)
            act.wait_ge(c.aux_v.sem, c.aux_v.at(1))
            ch.link(nc.scalar.activation(absr, r, ACT.Abs))
            nc.scalar.activation(sn, r, ACT.Sin)
            nc.scalar.activation(cs, absr, ACT.Sin, scale=-1.0, bias=c.w("half_pi")).then_inc(c.aux_s.sem, 1)
            act.wait_ge(c.aux_s.sem, c.aux_s.at(1))
            ch.clear()
    c.aux_v.advance(1)
    c.aux_s.advance(1)


def layer2_attention(c):
    nc = c.nc
    H, D = 8, 16
    start_loads(c, [pack_load(c, c.loaded_ahead, "L3", 0, c.pack_base["L2"])])
    norm_stage(c, c.X, c.HN, "eps5")
    trig = c.T[:, 3, 0:2 * S].rearrange("p (t s) -> p t s", s=S)
    wide_a = Arena(c)
    wide_a.off = 6 * 2 * S
    k0, k1, u = wide_a.take(N), wide_a.take(N), wide_a.take(N)
    q0, q1 = c.T[:, 0, :], c.T[:, 1, :]
    trig_stage(c, trig)
    wq, wk = c.w("L2a_wq"), c.w("L2a_wk")
    bq, bk = c.w("L2a_bq"), c.w("L2a_bk")
    jobs = [([c.HN], [w[:, t, :]], bb[:, t:t + 1], ACT.Silu, dst, None)
            for w, bb, ds in ((wq, bq, (q0, q1)), (wk, bk, (k0, k1))) for t, dst in enumerate(ds)]
    jobs.append(([c.HN], [c.w("L2a_wu")], c.w("L2a_bu"), None, u, None))
    project_stage(c, jobs)

    a = Arena(c)
    vsb, vb = a.take(2, S), a.take(2, H, P)
    assert a.off <= 6 * 2 * S
    a.off = wide_a.off
    decay = a.take(H, 2 * S)
    qk = c.T[:, 2, :].rearrange("p (b t s) -> p b t s", t=4, s=S)
    qb, kb = qk[:, :, 0:2, :], qk[:, :, 2:4, :]
    en = a.take(4, 2 * S)
    LAG = 2
    with nc.Block() as block:
        @block.gpsimd
        def _(pool):
            nc.gpsimd.memset(vb, 0.0).then_inc(c.aux_v.sem, 1)
            with pool.Fori(0, B // 2) as i:
                for s in range(2):
                    pool.wait_ge(c.out_copied.sem, c.out_copied.base + i * 2 + s - 1)
                    src = bass.ds((i * 2 + s) * S, S)
                    nc.gpsimd.tensor_copy(vsb[:, s, :], c.HN[:, src]).then_inc(c.staged.sem, 1)
                    for t, (q, k) in enumerate(((q0, k0), (q1, k1))):
                        nc.gpsimd.tensor_tensor(qb[:, s, t, :], q[:, src], trig[:, t, :], ALU.mult)
                        ins = nc.gpsimd.tensor_tensor(kb[:, s, t, :], k[:, src], trig[:, t, :], ALU.mult)
                    ins.then_inc(c.aux_p.sem, 1)

        @block.tensor
        def _(pe):
            with pe.Fori(0, B // 2) as i:
                for s in range(2):
                    n0 = i * 2 + s
                    h0 = n0 * H
                    pe.wait_ge(c.staged.sem, c.staged.base + n0 + 1)
                    pe.wait_ge(c.proj_taken_v.sem, c.proj_taken_v.base + n0)
                    for kt in range(2):
                        mm = nc.tensor.matmul(c.psum[:, 7, kt * P:(kt + 1) * P], vsb[:, s, kt * P:(kt + 1) * P],
                                              c.w("L2a_wv"), start=True, stop=True)
                    mm.then_inc(c.proj_ready.sem, 1)
                    pe.wait_ge(c.aux_p.sem, c.aux_p.base + n0 + 1)
                    for h in range(H + LAG):
                        if h < H:
                            pe.wait_ge(c.aux_v2.sem, c.aux_v2.base + h0 + h - 3)
                            t, base = h // 4, (h % 4) * 32
                            for mt in range(2):
                                mm = nc.tensor.matmul(c.psum[:, h % 4, mt * S:(mt + 1) * S],
                                                      kb[base:base + 32, s, t, mt * P:(mt + 1) * P],
                                                      qb[base:base + 32, s, t, :], start=True, stop=True,
                                                      tile_position=(base, 0))
                            mm.then_inc(c.scores_ready.sem, 1)
                        if h >= LAG:
                            k = h - LAG
                            if k == 0:
                                pe.wait_ge(c.proj_taken_v.sem, c.proj_taken_v.base + n0 + 1)
                                pe.wait_ge(c.out_copied.sem, c.out_copied.base + n0 - 1)
                            pe.wait_ge(c.aux_v2.sem, c.aux_v2.base + h0 + k + 1)
                            for mt in range(2):
                                mm = nc.tensor.matmul(c.psum[:, 5 + s, 0:S], vb[:, mt, k, :],
                                                      en[:, k % 4, mt * S:(mt + 1) * S],
                                                      start=(k == 0 and mt == 0), stop=(k == H - 1 and mt == 1))
                            mm.then_inc(c.mixed_ready.sem, 1)

        @block.scalar
        def _(act):
            for h in range(H):
                ins = nc.scalar.activation(decay[:, h, :], c.w("L2a_lower").rearrange("p t s -> p (t s)"), ACT.Exp,
                                           scale=c.w("L2a_slope")[:, h:h + 1])
            ins.then_inc(c.aux_s.sem, 1)
            with act.Fori(0, B // 2) as i:
                for s in range(2):
                    n0 = i * 2 + s
                    act.wait_ge(c.mixed_ready.sem, c.mixed_ready.base + (n0 + 1) * H)
                    nc.scalar.copy(q0[:, bass.ds(n0 * S, S)], c.psum[:, 5 + s, 0:S]).then_inc(c.out_copied.sem, 1)

        @block.vector
        def _(dve):
            dve.wait_ge(c.aux_s.sem, c.aux_s.at(1))
            dve.wait_ge(c.aux_v.sem, c.aux_v.at(1))
            with dve.Fori(0, B // 2) as i:
                for s in range(2):
                    n0 = i * 2 + s
                    h0 = n0 * H
                    dve.wait_ge(c.proj_ready.sem, c.proj_ready.base + n0 + 1)
                    dve.wait_ge(c.mixed_ready.sem, c.mixed_ready.base + h0)
                    for kt in range(2):
                        dst = vb[:, kt].rearrange("p h x -> p (h x)")
                        dst = bass.AP(tensor=dst.tensor, offset=dst.offset, ap=[dst.ap[0], [P + D, H], [1, D]])
                        ins = nc.vector.tensor_tensor(dst, c.psum[:, 7, kt * P:(kt + 1) * P]
                                                      .rearrange("p (h d) -> p h d", d=D),
                                                      c.w("L2a_bv").rearrange("p (h d) -> p h d", d=D), ALU.add)
                    ins.then_inc(c.proj_taken_v.sem, 1)
                    for h in range(H):
                        dve.wait_ge(c.scores_ready.sem, c.scores_ready.base + h0 + h + 1)
                        dve.wait_ge(c.mixed_ready.sem, c.mixed_ready.base + h0 + h - 3)
                        nc.vector.tensor_tensor(en[:, h % 4, :], c.psum[:, h % 4, :], decay[:, h, :],
                                                ALU.mult).then_inc(c.aux_v2.sem, 1)
    for s, n in ((c.staged, 1), (c.aux_p, 1), (c.proj_ready, 1), (c.proj_taken_v, 1), (c.aux_v2, H),
                 (c.scores_ready, H), (c.mixed_ready, H), (c.out_copied, 1)):
        s.advance(B * n)
    c.aux_s.advance(1)
    c.aux_v.advance(1)
    with nc.Block() as block:
        @block.vector
        def _(dve):
            nc.vector.tensor_copy(c.T[:, 1, :], u)
    norm_stage(c, q0, q0, "eps6", centre=False)
    with nc.Block() as block:
        @block.vector
        def _(dve):
            nc.vector.tensor_tensor(c.T[:, 0, :], c.T[:, 0, :], c.T[:, 1, :], ALU.mult)
    project_stage(c, [([q0], [c.w("L2a_wo")], c.w("L2a_bo"), None, c.X, c.X)])


def layer2_cross(c):
    nc = c.nc
    norm_stage(c, c.X, c.HN, "eps5")
    one_plus = c.w("L2x_scale")
    with nc.Block() as block:
        @block.vector
        def _(dve):
            nc.vector.tensor_scalar(one_plus, one_plus, 1.0, None, ALU.add)
    norm_stage(c, c.HN, c.HN, "eps6", centre=False, gain=one_plus)
    norm_stage(c, c.CT, c.T[:, 3, :], "eps6", centre=False, gain=one_plus)
    a = Arena(c)
    q, k = c.T[:, 0, :], c.T[:, 1, :]
    q_swapped, k_swapped = a.take(N), a.take(N)
    project_stage(c, [([src], [c.w(f"L2x_w{name}")], None, None, dst, None)
                      for src, name, dst in ((c.HN, "q", q), (c.HN, "q_swapped", q_swapped),
                                             (c.T[:, 3, :], "k", k), (c.T[:, 3, :], "k_swapped", k_swapped))])
    fill = 2.3819763e38
    madd = c.T[:, 2, :]

    def times(eng, x, factor):
        x = x.rearrange("p (b s) -> p b s", s=S)
        return eng.tensor_tensor(x, x, c.w(factor).unsqueeze(1).broadcast_to([P, B, S]), ALU.mult)

    with nc.Block() as block:
        @block.vector
        def _(dve):
            chain = Chain(dve, c.vector_chain)
            chain.step(times(nc.vector, k, "L2x_cos_k"))
            chain.step(times(nc.vector, k_swapped, "L2x_sin_k"))
            chain.step(times(nc.vector, q, "L2x_cos_q"))
            chain.step(nc.vector.tensor_copy(madd, c.attend[:, :].bitcast(U8)))
            chain.all_but(0)
            nc.vector.tensor_tensor(k, k, k_swapped, ALU.add)
            nc.vector.tensor_scalar(madd, madd, 1.0, fill, ALU.subtract, ALU.mult)
            chain.clear()
            dve.wait_ge(c.aux_p.sem, c.aux_p.at(1))
            nc.vector.tensor_tensor(q, q, q_swapped, ALU.add)

        @block.gpsimd
        def _(pool):
            times(nc.gpsimd, q_swapped, "L2x_sin_q").then_inc(c.aux_p.sem, 1)
    c.aux_p.advance(1)

    def prepare(nc, dve, chain, b, mb):
        chain.link(nc.vector.tensor_copy(mb, madd[:, bass.ds(b * S, S)]))

    ident = c.w("identity")
    attention_stage(c, 4, 32, q, k, c.T[:, 3, :], [ident], None, [ident], None,
                    c.w("L2x_wv"), None, [c.w("L2x_wo")], None, scale=float(32 ** -0.5),
                    mask=lambda mb, qt: mb, prepare_mask=prepare, mask_words=S, shared_kv=True)


MAGIC = 1.5 * 2.0 ** 23


def layer2_mlp(c):
    nc = c.nc
    I = 352
    rows = [P, P, I - 2 * P]
    norm_stage(c, c.X, c.HN, "eps5")
    a = Arena(c)
    xq, hq = a.take(N // 2).bitcast(BF16), [a.take(N // 2).bitcast(BF16) for _ in range(3)]
    w_int = a.take(9, P)
    w_bf = a.take(9, P // 2).bitcast(BF16)
    w_t = a.take(9, P // 2).bitcast(BF16)
    ident = a.take(P // 2).bitcast(BF16)
    amax, ws, wr = a.take(8), a.take(9), a.take(9)
    xs, part = a.take(4), a.take(2, CH)
    peak = a.take(16)
    tmp = a.take(N)
    wg, wu, wd = c.w("L2f_gate"), c.w("L2f_up"), c.w("L2f_down")
    blocks = [(wg[0:rows[t], t, :], rows[t], 0 + t) for t in range(3)] + \
             [(wu[0:rows[t], t, :], rows[t], 3 + t) for t in range(3)]
    sigm = c.w("L2f_clips")

    with nc.Block() as block:
        @block.scalar
        def _(act):
            nc.scalar.activation(sigm, sigm, ACT.Sigmoid).then_inc(c.aux_s.sem, 1)
            nc.scalar.copy(ident, c.w("identity"))

        @block.gpsimd
        def _(pool):
            pool.wait_ge(c.aux_v.sem, c.aux_v.at(1))
            nc.gpsimd.partition_all_reduce(amax[:, 1:2], amax[:, 0:1], P, bass.bass_isa.ReduceOp.max) \
                .then_inc(c.aux_p.sem, 1)

        @block.vector
        def _(dve):
            ch = Chain(dve, c.vector_chain)
            v = nc.vector
            v.tensor_reduce(amax[:, 0:1], c.HN[:, :], AX.X, ALU.max, apply_absolute_value=True) \
                .then_inc(c.aux_v.sem, 1)
            ch.link(v.memset(ws, 127.0))
            for src, n, i in blocks:
                ch.link(v.tensor_reduce(ws[0:n, i:i + 1], src, AX.X, ALU.max, apply_absolute_value=True))
            ch.link(v.tensor_reduce(ws[:, 6:7], wd, AX.X, ALU.max, apply_absolute_value=True))
            ch.link(v.tensor_scalar(ws, ws, float(1.0 / 127.0), None, ALU.mult))
            ch.link(v.reciprocal(wr, ws))
            for src, n, i in blocks:
                ch.link(v.tensor_scalar(w_int[0:n, i, :], src, wr[0:n, i:i + 1], MAGIC, ALU.mult, ALU.add))
            for i in range(3):
                ch.link(v.tensor_scalar(w_int[:, 6 + i, 0:rows[i]], wd[:, i * P:i * P + rows[i]], wr[:, 6:7], MAGIC,
                                        ALU.mult, ALU.add))
            for lo, hi, r in ((0, 2, P), (2, 3, rows[2]), (3, 5, P), (5, 6, rows[2])):
                w = w_int[0:r, lo:hi, :]
                ch.link(v.tensor_scalar(w, w, MAGIC, 127.0, ALU.subtract, ALU.min))
                ch.link(v.tensor_scalar(w_bf[0:r, lo:hi, :], w, -128.0, None, ALU.max))
            for i in range(3):
                w = w_int[:, 6 + i, 0:rows[i]]
                ch.link(v.tensor_scalar(w, w, MAGIC, 127.0, ALU.subtract, ALU.min))
                ch.link(v.tensor_scalar(w_bf[:, 6 + i, 0:rows[i]], w, -128.0, None, ALU.max))
            dve.wait_ge(c.aux_p.sem, c.aux_p.at(1))
            dve.wait_ge(c.aux_s.sem, c.aux_s.at(1))
            ch.link(v.tensor_tensor(xs[:, 1:2], amax[:, 1:2], sigm[:, 0:1], ALU.mult))
            ch.link(v.tensor_scalar(xs[:, 0:1], xs[:, 1:2], float(1.0 / 127.0), None, ALU.mult))
            ch.link(v.reciprocal(xs[:, 1:2], xs[:, 0:1]))
            ch.link(v.tensor_scalar(tmp, c.HN[:, :], xs[:, 1:2], MAGIC, ALU.mult, ALU.add))
            ch.link(v.tensor_scalar(tmp, tmp, MAGIC, 127.0, ALU.subtract, ALU.min))
            ch.link(v.tensor_scalar(xq, tmp, -128.0, None, ALU.max))
            ch.link(v.tensor_scalar(ws[:, 0:6], ws[:, 0:6], xs[:, 0:1], None, ALU.mult))
            ch.clear()
    c.aux_v.advance(1)
    c.aux_p.advance(1)
    c.aux_s.advance(1)

    turned = c.psum[:, 0:4, :].rearrange("p a x -> p (a x)").bitcast(BF16)
    order = [(i, (rows[i % 3] if i < 6 else P), (P if i < 6 else rows[i - 6])) for i in range(9)]
    with nc.Block() as block:
        @block.tensor
        def _(pe):
            for i, r, m in order:
                mm = nc.tensor.transpose(turned[0:m, i * P:i * P + r], w_bf[0:r, i, 0:m], ident[0:r, 0:r])
            mm.then_inc(c.aux_pe.sem, 1)

        @block.vector
        def _(dve):
            dve.wait_ge(c.aux_pe.sem, c.aux_pe.at(1))
            for i, r, m in order:
                nc.vector.tensor_copy(w_t[0:m, i, 0:r], turned[0:m, i * P:i * P + r])
    c.aux_pe.advance(1)

    units = [(i, t) for i in range(NC) for t in range(3)]
    hidden = [c.T[:, t, :] for t in range(3)]
    with nc.Block() as block:
        @block.tensor
        def _(pe):
            for n, (i, t) in enumerate(units):
                if n >= 4:
                    pe.wait_ge(c.aux_v.sem, c.aux_v.at(n - 3))
                for g in range(2):
                    mm = nc.tensor.matmul(c.psum[0:rows[t], 2 * (n % 4) + g, :], w_t[:, 3 * g + t, 0:rows[t]],
                                          xq[:, i * CH:(i + 1) * CH], start=True, stop=True)
                mm.then_inc(c.aux_pe.sem, 1)

        @block.scalar
        def _(act):
            for n, (i, t) in enumerate(units):
                act.wait_ge(c.aux_pe.sem, c.aux_pe.at(n + 1))
                if n >= 2:
                    act.wait_ge(c.aux_v.sem, c.aux_v.at(n - 1))
                nc.scalar.activation(part[0:rows[t], n % 2, :], c.psum[0:rows[t], 2 * (n % 4), :], ACT.Silu,
                                     scale=ws[0:rows[t], t:t + 1]).then_inc(c.aux_s.sem, 1)

        @block.vector
        def _(dve):
            for n, (i, t) in enumerate(units):
                dve.wait_ge(c.aux_s.sem, c.aux_s.at(n + 1))
                nc.vector.scalar_tensor_tensor(hidden[t][0:rows[t], i * CH:(i + 1) * CH],
                                               c.psum[0:rows[t], 2 * (n % 4) + 1, :], ws[0:rows[t], 3 + t:4 + t],
                                               part[0:rows[t], n % 2, :], ALU.mult, ALU.mult) \
                    .then_inc(c.aux_v.sem, 1)
    for s in (c.aux_pe, c.aux_s, c.aux_v):
        s.advance(len(units))

    with nc.Block() as block:
        @block.vector
        def _(dve):
            ch = Chain(dve, c.vector_chain)
            v = nc.vector
            ch.link(v.memset(peak[:, 0:4], 0.0))
            for t in range(3):
                ch.link(v.tensor_reduce(peak[0:rows[t], t:t + 1], hidden[t][0:rows[t], :], AX.X, ALU.max,
                                        apply_absolute_value=True))
            v.reduce_max(amax[:, 2:3], peak[:, 0:3], AX.X).then_inc(c.aux_v.sem, 1)
            dve.wait_ge(c.aux_p.sem, c.aux_p.at(1))
            ch.link(v.tensor_tensor(xs[:, 2:3], amax[:, 3:4], sigm[:, 1:2], ALU.mult))
            ch.link(v.tensor_scalar(xs[:, 3:4], xs[:, 2:3], float(1.0 / 127.0), None, ALU.mult))
            ch.link(v.reciprocal(xs[:, 2:3], xs[:, 3:4]))
            ch.link(v.tensor_scalar(ws[:, 7:8], ws[:, 6:7], xs[:, 3:4], None, ALU.mult))
            for t in range(3):
                h = hidden[t][0:rows[t], :]
                ch.link(v.tensor_scalar(h, h, xs[0:rows[t], 2:3], MAGIC, ALU.mult, ALU.add))
                ch.link(v.tensor_scalar(h, h, MAGIC, 127.0, ALU.subtract, ALU.min))
                ch.link(v.tensor_scalar(hq[t][0:rows[t], :], h, -128.0, None, ALU.max))
            ch.clear()

        @block.gpsimd
        def _(pool):
            pool.wait_ge(c.aux_v.sem, c.aux_v.at(1))
            nc.gpsimd.partition_all_reduce(amax[:, 3:4], amax[:, 2:3], P, bass.bass_isa.ReduceOp.max) \
                .then_inc(c.aux_p.sem, 1)
    c.aux_v.advance(1)
    c.aux_p.advance(1)

    with nc.Block() as block:
        @block.tensor
        def _(pe):
            for i in range(NC):
                for t in range(3):
                    mm = nc.tensor.matmul(c.psum[:, i, :], w_t[0:rows[t], 6 + t, :],
                                          hq[t][0:rows[t], i * CH:(i + 1) * CH], start=(t == 0), stop=(t == 2))
                mm.then_inc(c.aux_pe.sem, 1)

        @block.vector
        def _(dve):
            for i in range(NC):
                dve.wait_ge(c.aux_pe.sem, c.aux_pe.at(i + 1))
                x = c.X[:, i * CH:(i + 1) * CH]
                nc.vector.scalar_tensor_tensor(x, c.psum[:, i, :], ws[:, 7:8], x, ALU.mult, ALU.add)
    c.aux_pe.advance(NC)



def layer3_attention(c):
    start_loads(c, [pack_load(c, c.loaded_ahead, "L3", c.pack_base["L2"])])
    norm_stage(c, c.X, c.HN, "eps5")
    loads_done(c, c.loaded_ahead)
    wq, wk = c.w("L3a_wq"), c.w("L3a_wk")
    attention_stage(c, 16, 8, c.HN, c.HN, c.HN, [wq[:, t, :] for t in range(4)], c.w("L3a_bq"),
                    [wk[:, t, :] for t in range(4)], c.w("L3a_bk"), c.w("L3a_wv"), c.w("L3a_bv"), [c.w("L3a_wo")],
                    c.w("L3a_bo"), scale=float(8 ** -0.5), top=32)


def layer3_cross(c):
    nc = c.nc
    H, D = 16, 8
    J = S // H
    norm_stage(c, c.X, c.HN, "eps5")
    q, k = c.T[:, 0, :], c.T[:, 1, :]
    project_stage(c, [([c.HN], [c.w("L3x_wq")], c.w("L3x_bq"), None, q, None),
                      ([c.CT], [c.w("L3x_wk")], c.w("L3x_bk"), None, k, None)])
    a = Arena(c)
    qb, kb, ctx_b = a.take(2, S), a.take(2, S), a.take(2, S)
    vb, probs, ex, turned = a.take(2, 2, P), a.take(2, 2, S), a.take(2, 2, S), a.take(2, S)
    m, r, inv = a.take(2, H), a.take(2, H), a.take(2, H)
    ident, kmask, vmask = c.w("identity"), c.w("L3x_kmask"), c.w("L3x_vmask")
    scale = float(D ** -0.5)

    def by_head(x):
        return x.rearrange("p (j h) -> p h j", h=H)

    def over(x):
        return x.unsqueeze(1).broadcast_to([P, J, H])

    def bank(s, t):
        return c.psum[:, 6 * s + t, 0:S]

    with nc.Block() as block:
        @block.gpsimd
        def _(pool):
            def step(l, s, has):
                if has(2):
                    pool.wait_ge(c.proj_ready.sem, c.proj_ready.base + l - 1)
                if has(0):
                    nc.gpsimd.tensor_copy(qb[:, s], q[:, bass.ds(l * S, S)])
                    nc.gpsimd.tensor_tensor(kb[:, s], k[:, bass.ds(l * S, S)], kmask, ALU.mult)
                    nc.gpsimd.tensor_copy(ctx_b[:, s], c.CT[:, bass.ds(l * S, S)]).then_inc(c.staged.sem, 1)

            sequence_pipeline(pool, step, 2)

        @block.tensor
        def _(pe):
            def step(l, s, has):
                if has(0):
                    pe.wait_ge(c.staged.sem, c.staged.base + l + 1)
                    if has(2):
                        pe.wait_ge(c.scores_max.sem, c.scores_max.base + 2 * l - 2)
                    for t in range(2):
                        nc.tensor.matmul(bank(s, t), qb[:, s, t * P:(t + 1) * P], kb[:, s], start=True, stop=True) \
                            .then_inc(c.scores_ready.sem, 1)
                    if has(1):
                        pe.wait_ge(c.v_taken.sem, c.v_taken.base + l)
                    for t in range(2):
                        mm = nc.tensor.matmul(c.psum[:, 2, t * P:(t + 1) * P], ctx_b[:, s, t * P:(t + 1) * P],
                                              c.w("L3x_wv"), start=True, stop=True)
                    mm.then_inc(c.proj_ready.sem, 1)
                if has(1):
                    for t in range(2):
                        pe.wait_ge(c.probs_picked.sem, c.probs_picked.base + 2 * l - 1 + t)
                        for kt in range(2):
                            mm = nc.tensor.transpose(c.psum[:, 3 + kt, t * P:(t + 1) * P],
                                                     probs[:, 1 - s, t, kt * P:(kt + 1) * P], ident)
                    mm.then_inc(c.probs_turned.sem, 1)
                    pe.wait_ge(c.turned_copied.sem, c.turned_copied.base + 2 * l)
                    if has(2):
                        pe.wait_ge(c.mixed_taken.sem, c.mixed_taken.base + l - 1)
                    for kt in range(2):
                        mm = nc.tensor.matmul(c.psum[:, 5, 0:S], vb[:, 1 - s, kt, :], turned[:, kt, :],
                                              start=(kt == 0), stop=(kt == 1))
                    mm.then_inc(c.mixed_ready.sem, 1)

            sequence_pipeline(pe, step, 2)

        @block.scalar
        def _(act):
            def step(l, s, has):
                if has(0):
                    for t in range(2):
                        act.wait_ge(c.scores_max.sem, c.scores_max.base + 2 * l + t + 1)
                        nc.scalar.activation(ex[:, s, t, :], probs[:, s, t, :], ACT.Exp, scale=scale) \
                            .then_inc(c.probs_ready.sem, 1)
                if has(1):
                    act.wait_ge(c.probs_turned.sem, c.probs_turned.base + l)
                    if has(2):
                        act.wait_ge(c.mixed_ready.sem, c.mixed_ready.base + l - 1)
                    for kt in range(2):
                        nc.scalar.copy(turned[:, kt, :], c.psum[:, 3 + kt, 0:S]).then_inc(c.turned_copied.sem, 1)
                    act.wait_ge(c.mixed_ready.sem, c.mixed_ready.base + l)
                    nc.scalar.copy(q[:, bass.ds((l - 1) * S, S)], c.psum[:, 5, 0:S]).then_inc(c.mixed_taken.sem, 1)

            sequence_pipeline(act, step, 2)

        @block.vector
        def _(dve):
            chain = Chain(dve, c.vector_chain)
            v = nc.vector

            def step(l, s, has):
                if has(0):
                    if has(2):
                        dve.wait_ge(c.mixed_ready.sem, c.mixed_ready.base + l - 1)
                    for t in range(2):
                        dve.wait_ge(c.scores_ready.sem, c.scores_ready.base + 2 * l + t + 1)
                        chain.link(v.reduce_max(m[:, t, :], by_head(bank(s, t)), AX.X))
                        v.tensor_tensor(probs[:, s, t, :].rearrange("p (j h) -> p j h", h=H),
                                        bank(s, t).rearrange("p (j h) -> p j h", h=H), over(m[:, t, :]),
                                        ALU.subtract).then_inc(c.scores_max.sem, 1)
                    dve.wait_ge(c.proj_ready.sem, c.proj_ready.base + l + 1)
                    ins = v.tensor_tensor(vb[:, s], c.psum[:, 2, 0:S].rearrange("p (t x) -> p t x", x=P),
                                          c.w("L3x_bv").unsqueeze(1).broadcast_to([P, 2, P]), ALU.add)
                    ins.then_inc(c.v_taken.sem, 1)
                    dve.wait_ge(c.v_taken.sem, c.v_taken.base + l + 1)
                    chain.step(v.tensor_tensor(vb[:, s], vb[:, s], vmask.unsqueeze(1).broadcast_to([P, 2, P]),
                                               ALU.mult))
                if has(1):
                    for t in range(2):
                        dve.wait_ge(c.probs_ready.sem, c.probs_ready.base + 2 * l - 1 + t)
                        chain.link(v.reduce_sum(r[:, t, :], by_head(ex[:, 1 - s, t, :]), AX.X))
                        chain.link(v.reciprocal(inv[:, t, :], r[:, t, :]))
                        v.tensor_tensor(probs[:, 1 - s, t, :].rearrange("p (j h) -> p j h", h=H),
                                        ex[:, 1 - s, t, :].rearrange("p (j h) -> p j h", h=H), over(inv[:, t, :]),
                                        ALU.mult).then_inc(c.probs_picked.sem, 1)

            sequence_pipeline(dve, step, 2, chain)
    c.v_taken.advance(B)
    for s, n in ((c.staged, 1), (c.scores_ready, 2), (c.scores_max, 2), (c.probs_ready, 2), (c.probs_picked, 2),
                 (c.proj_ready, 1), (c.probs_turned, 1), (c.turned_copied, 2), (c.mixed_ready, 1),
                 (c.mixed_taken, 1)):
        s.advance(B * n)
    project_stage(c, [([q], [c.w("L3x_wo")], c.w("L3x_bo"), None, c.X, c.X)])


def position_attention(c, q, k, v, out, scale):
    nc = c.nc
    a = Arena(c)
    prod, less, ex = a.take(2, N), a.take(2, N), a.take(2, N)
    weighted = a.take(N)
    m, total, inv, mix = a.take(2, S), a.take(S), a.take(S), a.take(S)

    def scores(s):
        return c.psum[:, 4 * s:4 * s + 4, :].rearrange("p a x -> p (a x)")

    def grid(x):
        return x.rearrange("p (m n) -> p m n", n=S)

    def last(x):
        return x.rearrange("p (m n) -> p n m", n=S)

    def run(eng, step, chain=None):
        step(0, 0, True, False)
        if chain is not None:
            chain.clear()
        with eng.Fori(0, (B - 2) // 2) as i:
            step(i * 2 + 1, 1, True, True)
            step(i * 2 + 2, 0, True, True)
            if chain is not None:
                chain.clear()
        step(B - 1, 1, False, True)
        step(B, 0, False, True)
        if chain is not None:
            chain.clear()

    is_last = lambda l: isinstance(l, int) and l == B

    with nc.Block() as block:
        @block.gpsimd
        def _(pool):
            def product(l, s):
                nc.gpsimd.tensor_tensor(grid(prod[:, s]), grid(k),
                                        q[:, bass.ds(l * S, S)].unsqueeze(1).broadcast_to([P, B, S]), ALU.mult) \
                    .then_inc(c.aux_p.sem, 1)

            def step(l, s, more, before):
                if more:
                    if before:
                        pool.wait_ge(c.aux_pe.sem, c.aux_pe.base + l)
                    product(l + 1, 1 - s)
                if before:
                    pool.wait_ge(c.aux_s.sem, c.aux_s.base + l)
                    pool.wait_ge(c.aux_v2.sem, c.aux_v2.base + l)
                    nc.gpsimd.tensor_tensor(weighted, ex[:, 1 - s], v, ALU.mult).then_inc(c.aux_p2.sem, 1)

            product(0, 0)
            run(pool, step)

        @block.tensor
        def _(pe):
            def step(l, s, more, before):
                if is_last(l):
                    return
                pe.wait_ge(c.aux_p.sem, c.aux_p.base + l + 1)
                if before:
                    pe.wait_ge(c.aux_v3.sem, c.aux_v3.base + l)
                for i in range(NC):
                    mm = nc.tensor.matmul(c.psum[:, 4 * s + i, :], c.w("L3f_heads"), prod[:, s, i * CH:(i + 1) * CH],
                                          start=True, stop=True)
                mm.then_inc(c.aux_pe.sem, 1)

            run(pe, step)

        @block.scalar
        def _(act):
            def step(l, s, more, before):
                if is_last(l):
                    return
                act.wait_ge(c.aux_v3.sem, c.aux_v3.base + l + 2)
                nc.scalar.activation(ex[:, s], less[:, s], ACT.Exp, scale=scale).then_inc(c.aux_s.sem, 1)

            run(act, step)

        @block.vector
        def _(dve):
            chain = Chain(dve, c.vector_chain)
            nc.vector.memset(m[:, 0], 0.0).then_inc(c.aux_v3.sem, 1)
            nc.vector.memset(m[:, 1], 0.0).then_inc(c.aux_v2.sem, 1)
            dve.wait_ge(c.aux_v3.sem, c.aux_v3.base + 1)
            dve.wait_ge(c.aux_v2.sem, c.aux_v2.base + 1)

            def step(l, s, more, before):
                if not is_last(l):
                    dve.wait_ge(c.aux_pe.sem, c.aux_pe.base + l + 1)
                    chain.link(nc.vector.reduce_max(m[:, s], last(scores(s)), AX.X))
                    if before:
                        dve.wait_ge(c.aux_s.sem, c.aux_s.base + l)
                    nc.vector.tensor_tensor(grid(less[:, s]), grid(scores(s)),
                                            m[:, s].unsqueeze(1).broadcast_to([P, B, S]),
                                            ALU.subtract).then_inc(c.aux_v3.sem, 1)
                if before:
                    dve.wait_ge(c.aux_s.sem, c.aux_s.base + l)
                    chain.link(nc.vector.reduce_sum(total, last(ex[:, 1 - s]), AX.X))
                    chain.step(nc.vector.reciprocal(inv, total))
                    dve.wait_ge(c.aux_p2.sem, c.aux_p2.base + l)
                    nc.vector.reduce_sum(mix, last(weighted), AX.X).then_inc(c.aux_v2.sem, 1)
                    dve.wait_ge(c.aux_v2.sem, c.aux_v2.base + l + 1)
                    chain.all_but(0)
                    chain.link(nc.vector.tensor_tensor(out[:, bass.ds((l - 1) * S, S)], mix, inv, ALU.mult))

            run(dve, step, chain)
    for s in (c.aux_pe, c.aux_p, c.aux_p2, c.aux_s):
        s.advance(B)
    for s in (c.aux_v2, c.aux_v3):
        s.advance(B + 1)


def layer3_block(c):
    nc = c.nc
    norm_stage(c, c.X, c.HN, "eps5")
    q, k, v, o = (c.T[:, i, :] for i in range(4))
    w, bias = c.w("L3f_win"), c.w("L3f_bin")
    project_stage(c, [([c.HN], [w[:, i * P:(i + 1) * P]], bias[:, i:i + 1], None, dst, None)
                      for i, dst in enumerate((q, k, v))])
    position_attention(c, q, k, v, o, float(32 ** -0.5))
    project_stage(c, [([o], [c.w("L3f_wout")], c.w("L3f_bout"), None, c.HN, c.HN)])
    norm_stage(c, c.HN, c.HN, "eps5", gain=c.w("L3f_g1"), shift=c.w("L3f_h1"))

    a = Arena(c)
    w_t, w_b = a.take(N), parts_tile(a)
    both = a.take(E, P)
    b_col, b_row = a.take(P), a.take(P)
    w1, w2, b1, b2 = c.w("L3f_w1"), c.w("L3f_w2"), c.w("L3f_b1"), c.w("L3f_b2")
    with nc.Block() as block:
        @block.tensor
        def _(pe):
            for e in range(E):
                for f in range(4):
                    mm = nc.tensor.matmul(c.psum[:, e // 4, (e % 4) * P:(e % 4 + 1) * P], w1[:, e, f, :],
                                          w2[:, e, f, :], start=(f == 0), stop=(f == 3))
            mm.then_inc(c.aux_pe.sem, 1)
            for e in range(E):
                for f in range(4):
                    mm = nc.tensor.matmul(c.psum[:, 2, e:e + 1], w2[:, e, f, :], b1[:, e, f:f + 1],
                                          start=(f == 0), stop=(f == 3))
            mm.then_inc(c.aux_pe.sem, 1)
            pe.wait_ge(c.aux_v.sem, c.aux_v.at(2))
            nc.tensor.transpose(c.psum[:, 3, 0:P], b_col, c.w("identity")).then_inc(c.aux_pe.sem, 1)

        @block.scalar
        def _(act):
            act.wait_ge(c.aux_pe.sem, c.aux_pe.at(1))
            nc.scalar.copy(both, c.psum[:, 0:2, :].rearrange("p a (e x) -> p (a e) x", x=P))

        @block.vector
        def _(dve):
            nc.vector.memset(b_col, 0.0).then_inc(c.aux_v.sem, 1)
            dve.wait_ge(c.aux_v.sem, c.aux_v.at(1))
            dve.wait_ge(c.aux_pe.sem, c.aux_pe.at(2))
            for n in range(PARTS):
                ins = nc.vector.tensor_tensor(b_col[:, n * E:(n + 1) * E], c.psum[:, 2, 0:E], b2, ALU.add)
            ins.then_inc(c.aux_v.sem, 1)
            dve.wait_ge(c.aux_pe.sem, c.aux_pe.at(3))
            nc.vector.tensor_copy(b_row, c.psum[:, 3, 0:P])
    c.aux_pe.advance(3)
    c.aux_v.advance(2)
    route_stage(c, c.HN, c.w("L3f_wg"), None, w_b, a, "single", capacity=N // E, w_t=w_t)

    a2 = Arena(c)
    a2.off = a.off
    xe = a2.take(4, CH)
    pick = picks(c)
    units = [(i, e) for i in range(NC) for e in range(E)]
    with nc.Block() as block:
        @block.tensor
        def _(pe):
            def spread(n):
                i, e = units[n]
                if n >= 3:
                    pe.wait_ge(c.aux_v.sem, c.aux_v.at(n - 2))
                nc.tensor.matmul(c.psum[:, n % 3, :], pick[:, e, :], w_b[1][:, i * CH:(i + 1) * CH], start=True,
                                 stop=True).then_inc(c.aux_pe.sem, 1)

            spread(0)
            spread(1)
            for n, (i, e) in enumerate(units):
                if n + 2 < len(units):
                    spread(n + 2)
                pe.wait_ge(c.aux_v.sem, c.aux_v.at(n + 1))
                nc.tensor.matmul(c.psum[:, 4 + i, :], both[:, e, :], xe[:, n % 4, :], start=(e == 0), stop=False) \
                    .then_inc(c.aux_pe2.sem, 1)
                if e == E - 1:
                    nc.tensor.matmul(c.psum[:, 4 + i, :], b_row, w_t[:, i * CH:(i + 1) * CH], start=False,
                                     stop=True).then_inc(c.aux_pe3.sem, 1)

        @block.vector
        def _(dve):
            for n, (i, e) in enumerate(units):
                dve.wait_ge(c.aux_pe.sem, c.aux_pe.at(n + 1))
                if n >= 4:
                    dve.wait_ge(c.aux_pe2.sem, c.aux_pe2.at(n - 3))
                nc.vector.tensor_tensor(xe[:, n % 4, :], c.HN[:, i * CH:(i + 1) * CH], c.psum[:, n % 3, :],
                                        ALU.mult).then_inc(c.aux_v.sem, 1)
            dve.wait_ge(c.aux_v.sem, c.aux_v.at(len(units)))
            for i in range(NC):
                dve.wait_ge(c.aux_pe3.sem, c.aux_pe3.at(i + 1))
                x = c.HN[:, i * CH:(i + 1) * CH]
                nc.vector.tensor_tensor(x, x, c.psum[:, 4 + i, :], ALU.add)
    for s, n in ((c.aux_pe, len(units)), (c.aux_pe2, len(units)), (c.aux_pe3, NC), (c.aux_v, len(units))):
        s.advance(n)
    norm_stage(c, c.HN, c.HN, "eps5", gain=c.w("L3f_g2"), shift=c.w("L3f_h2"))
    add_stage(c, c.X, c.X, c.HN)



class Layout:

    def __init__(self):
        self.parts, self.slots, self.words = {}, {}, {}

    def add(self, pack, name, array):
        array = np.ascontiguousarray(array)
        if array.ndim == 1:
            array = array.reshape(array.shape[0], 1)
        assert array.shape[0] == P, (name, array.shape)
        off = self.words.get(pack, 0)
        flat = array.reshape(P, -1)
        self.parts.setdefault(pack, []).append(flat)
        self.slots[name] = (pack, off, array.shape)
        self.words[pack] = off + flat.shape[1]

    def packed(self):
        return {k: np.ascontiguousarray(np.concatenate(v, axis=1)) for k, v in self.parts.items()}


def columns(v):
    return v.reshape(-1, P).T


def everywhere(v):
    return np.broadcast_to(v.reshape(1, -1), (P, v.size))


def k_tiles(w):
    return w.reshape(-1, P, w.shape[1]).transpose(1, 0, 2)


def padded_heads(w_t):
    out = np.zeros((w_t.shape[0], 4, 4, 32), np.float32)
    out[:, :, :, 0:8] = w_t.reshape(w_t.shape[0], 4, 4, 8)
    return out.reshape(w_t.shape[0], 4, P)


def feature_major(x):
    return np.ascontiguousarray(x.reshape(N, P).T)


def top_rows(w):
    out = np.zeros((P, w.shape[1]), np.float32)
    out[0:w.shape[0]] = w
    return out


def row_tiles(w):
    n = -(-w.shape[0] // P)
    out = np.zeros((n * P, w.shape[1]), np.float32)
    out[0:w.shape[0]] = w
    return out.reshape(n, P, -1).transpose(1, 0, 2)


def lay_out(a):
    L = Layout()
    sm = "small"
    L.add(sm, "average", np.full((P, P), 1.0 / P, np.float32))
    L.add(sm, "centre", (np.eye(P) - 1.0 / P).astype(np.float32))
    L.add(sm, "ones", np.ones((P, P), np.float32))
    L.add(sm, "one", np.ones((P, 1), np.float32))
    for name, eps in (("eps5", 1e-5), ("eps6", 1e-6), ("eps12", 1e-12), ("epsf", float(np.finfo(np.float32).eps))):
        L.add(sm, name, np.full((P, 1), eps, np.float32))
    L.add(sm, "identity", np.eye(P, dtype=np.float32))
    L.add("L0", "pad8", padded_heads(np.eye(P, dtype=np.float32)))
    for s in "qkv":
        L.add("L0", f"L0a_g{s}", a[f"L0_attn_ln_{s}_g"])
        L.add("L0", f"L0a_h{s}", a[f"L0_attn_ln_{s}_b"])
        L.add("L0", f"L0a_w{s}", a[f"L0_attn_{s}_w"].T)
    L.add("L0", "L0a_bq", a["L0_attn_q_b"])
    L.add("L0", "L0a_bk", a["L0_attn_k_b"])
    L.add("L0", "L0a_bv", everywhere(a["L0_attn_v_b"]))
    L.add("L0", "L0a_beta", everywhere(a["L0_attn_beta_param"]))
    L.add("L0", "L0a_wo", a["L0_attn_o_w"].T)
    L.add("L0", "L0a_bo", a["L0_attn_o_b"])
    L.add("L0", "L0x_band", (np.abs(np.arange(S)[:, None] - np.arange(S)[None, :]) < 32).astype(np.float32)
          .reshape(2, P, S).transpose(1, 0, 2))
    L.add("L0", "L0x_pos", a["L0_xattn_pos_bias"].reshape(2, P, S).transpose(1, 0, 2))
    for s in "qkvo":
        L.add("L0", f"L0x_w{s}", a[f"L0_xattn_w{s}"])
        L.add("L0", f"L0x_b{s}", a[f"L0_xattn_b{s}"])
    L.add("L0", "L0x_gamma", a["L0_xattn_gamma"])
    L.add("L0", "L0x_beta", a["L0_xattn_beta"])
    L.add("L0", "L0x_w1", a["L0_xattn_w1"])
    L.add("L0", "L0x_b1", columns(a["L0_xattn_b1"]))
    L.add("L0", "L0x_w2", k_tiles(a["L0_xattn_w2"]))
    L.add("L0", "L0x_b2", a["L0_xattn_b2"])
    L.add(sm, "falling", everywhere(np.arange(E, 0, -1).astype(np.float32)))
    L.add(sm, "upper", np.triu(np.ones((P, P), np.float32)))
    pick = np.zeros((P, E, P), np.uint16)
    for n in range(PARTS):
        pick[n * E + np.arange(E), np.arange(E), :] = 0x3F80
    L.add(sm, "pick", pick.reshape(P, -1).view(np.float32))
    for s in ("rg", "ru"):
        L.add("L0f", f"L0f_{s}", a[f"L0_ffn_{s}"].transpose(1, 0, 2))
    L.add("L0f", "L0f_router", a["L0_ffn_router_w"].T)
    L.add("L0f", "L0f_rd", a["L0_ffn_rd"].reshape(E, 4, P, P).transpose(2, 0, 1, 3))
    L.add("L0f", "L0f_sg", a["L0_ffn_sg"])
    L.add("L0f", "L0f_su", a["L0_ffn_su"])
    L.add("L0f", "L0f_sd", k_tiles(a["L0_ffn_sd"]))
    for s in "qkv":
        L.add("L1", f"L1a_w{s}", a[f"L1_attn_{s}_w"])
        L.add("L1", f"L1a_conv_{s}", a[f"L1_attn_conv_{s}_w"])
    L.add("L1", "L1a_gates", np.concatenate([a["L1_attn_b_w"], a["L1_attn_mix_w"]], axis=1))
    nothing = np.zeros(8, np.float32)
    L.add("L1", "L1a_mix_b", everywhere(np.concatenate([nothing, a["L1_attn_mix_b"]])))
    L.add("L1", "L1a_mix_bias", everywhere(np.concatenate([nothing, a["L1_attn_mix_bias"]])))
    L.add("L1", "L1a_onorm", everywhere(a["L1_attn_o_norm_w"]))
    L.add("L1", "L1a_wo", a["L1_attn_o_w"])
    L.add(sm, "position", everywhere(np.arange(S, dtype=np.float32)))
    after = np.arange(S)[None, :] > np.arange(S)[:, None]
    L.add("L1", "causal", np.where(after, np.float32(NEG), np.float32(0)).reshape(2, P, S).transpose(1, 0, 2))
    for s in "qk":
        L.add("L1", f"L1x_w{s}", a[f"L1_xattn_w_{s}"].T.reshape(P, 8, P))
        L.add("L1", f"L1x_b{s}", columns(a[f"L1_xattn_b_{s}"]))
    L.add("L1", "L1x_wv", a["L1_xattn_w_v"].T)
    L.add("L1", "L1x_bv", everywhere(a["L1_xattn_b_v"]))
    L.add("L1", "L1x_wo", k_tiles(a["L1_xattn_w_o"].T))
    L.add("L1", "L1x_bo", a["L1_xattn_b_o"])
    L.add("L1", "L1f_gate", a["L1_ffn_gate_w"].T)
    L.add("L1", "L1f_gate_b", everywhere(a["L1_ffn_gate_b"]))
    L.add("L1", "L1f_w1", a["L1_ffn_w1"].transpose(1, 0, 2))
    L.add("L1", "L1f_b1", a["L1_ffn_b1"].reshape(E, 2, P).transpose(2, 0, 1))
    L.add("L1", "L1f_w2", a["L1_ffn_w2"].reshape(E, 2, P, P).transpose(2, 0, 1, 3))
    L.add("L1", "L1f_b2", top_rows(np.concatenate([a["L1_ffn_b2"]] * PARTS)))
    twice = lambda w: np.repeat(w.reshape(8, 1, 16, -1), 2, axis=1).reshape(2, P, -1)
    w, bias = a["L2_attn_qkvu_w"].reshape(4, P, P), a["L2_attn_qkvu_b"].reshape(4, P)
    for n, s in enumerate("qk"):
        L.add("L2", f"L2a_w{s}", twice(w[n]).transpose(2, 0, 1))
        L.add("L2", f"L2a_b{s}", twice(bias[n])[:, :, 0].T)
    L.add("L2", "L2a_wv", w[2].T)
    L.add("L2", "L2a_bv", everywhere(bias[2]))
    L.add("L2", "L2a_wu", w[3].T)
    L.add("L2", "L2a_bu", bias[3])
    L.add("L2", "L2a_wo", a["L2_attn_out_w"].T)
    L.add("L2", "L2a_bo", a["L2_attn_out_b"])
    L.add("L2", "L2a_theta", twice(a["L2_attn_theta"].reshape(P))[:, :, 0].T)
    L.add("L2", "L2a_slope", everywhere(a["L2_attn_slope_rate"].reshape(8)))
    L.add("L2", "L2a_lower", (~after).astype(np.float32).T.reshape(2, P, S).transpose(1, 0, 2))
    cosine = (np.arange(P) % 32 < 16).astype(np.float32)
    L.add("L2", "L2a_cosine_rows", cosine)
    L.add("L2", "L2a_sine_rows", 1 - cosine)
    L.add("L2", "half_pi", np.full(P, np.pi / 2, np.float32))
    L.add("L2", "L2x_scale", a["L2_xattn_rms_scale"])
    wq = a["L2_xattn_q_w"].transpose(1, 0, 2)
    wk = np.broadcast_to(a["L2_xattn_kv_w"][0, 0][:, None, :], (P, 4, 32))
    for s, w in (("q", wq), ("k", wk)):
        L.add("L2", f"L2x_w{s}", w.reshape(P, P))
        L.add("L2", f"L2x_w{s}_swapped", np.concatenate([w[:, :, 16:], w[:, :, :16]], axis=2).reshape(P, P))
    timescale = 10000.0 ** (2.0 / 32 * np.arange(16, dtype=np.float64))
    for s, start in (("q", S), ("k", 0)):
        angle = (np.arange(S) + start)[None, :].astype(np.float32) / timescale.astype(np.float32)[:, None]
        cos, sin = np.cos(angle), np.sin(angle)
        L.add("L2", f"L2x_cos_{s}", np.tile(np.concatenate([cos, cos]), (4, 1)).astype(np.float32))
        L.add("L2", f"L2x_sin_{s}", np.tile(np.concatenate([-sin, sin]), (4, 1)).astype(np.float32))
    L.add("L2", "L2x_wv", a["L2_xattn_kv_w"][1, 0])
    L.add("L2", "L2x_wo", a["L2_xattn_out_w"].reshape(P, P))
    for s in ("gate", "up"):
        L.add("L2", f"L2f_{s}", row_tiles(a[f"L2_ffn_w_{s}"]))
    L.add("L2", "L2f_down", a["L2_ffn_w_down"])
    L.add("L2", "L2f_clips", everywhere(np.concatenate([a["L2_ffn_clip_x"], a["L2_ffn_clip_down"]])))
    for s in "qk":
        L.add("L3", f"L3a_w{s}", padded_heads(a[f"L3_attn_W{s}"].T))
        L.add("L3", f"L3a_b{s}", padded_heads(a[f"L3_attn_b{s}"][None, :])[0].T)
    for sub, name in (("a", "attn"), ("x", "xattn")):
        L.add("L3", f"L3{sub}_wv", a[f"L3_{name}_Wv"].T)
        L.add("L3", f"L3{sub}_bv", everywhere(a[f"L3_{name}_bv"]))
        L.add("L3", f"L3{sub}_wo", a[f"L3_{name}_Wo"].T)
        L.add("L3", f"L3{sub}_bo", a[f"L3_{name}_bo"])
    for s in "qk":
        L.add("L3", f"L3x_w{s}", a[f"L3_xattn_W{s}"].T)
        L.add("L3", f"L3x_b{s}", a[f"L3_xattn_b{s}"])
    L.add("L3", "L3x_kmask", (np.arange(S)[None, :] % 16 == np.arange(P)[:, None] // 8).astype(np.float32))
    L.add("L3", "L3x_vmask", (np.arange(P)[:, None] % 16 == np.arange(P)[None, :] // 8).astype(np.float32))
    L.add("L3", "L3f_win", a["L3_ffn_in_proj_w"].T)
    L.add("L3", "L3f_bin", columns(a["L3_ffn_in_proj_b"]))
    L.add("L3", "L3f_heads", (np.arange(P)[:, None] // 32 == np.arange(P)[None, :] // 32).astype(np.float32))
    L.add("L3", "L3f_wout", a["L3_ffn_out_proj_w"].T)
    L.add("L3", "L3f_bout", a["L3_ffn_out_proj_b"])
    for n in "12":
        L.add("L3", f"L3f_g{n}", a[f"L3_ffn_ln{n}_g"])
        L.add("L3", f"L3f_h{n}", a[f"L3_ffn_ln{n}_b"])
    L.add("L3", "L3f_wg", a["L3_ffn_wg"])
    L.add("L3", "L3f_w1", a["L3_ffn_w1"].reshape(E, P, 4, P).transpose(3, 0, 2, 1))
    L.add("L3", "L3f_w2", a["L3_ffn_w2"].reshape(E, 4, P, P).transpose(2, 0, 1, 3))
    L.add("L3", "L3f_b1", a["L3_ffn_b1"].reshape(E, 4, P).transpose(2, 0, 1))
    L.add("L3", "L3f_b2", a["L3_ffn_b2"].T)
    return L


def decoder(nc, slots, packs, dram, x, ctx, out, upto=12):
    c = Core(nc, slots, packs)
    c.dram = dram
    c.valid_i32 = nc.alloc_sbuf_tensor("valid_keys_i32", [P, B], I32)
    c.valid = nc.alloc_sbuf_tensor("valid_keys", [P, B], F32)
    c.attend = nc.alloc_sbuf_tensor("attended_keys", [P, N // 4], I32)
    start_loads(c, [(c.loaded, c.X[:, :], x), (c.loaded, c.small[:, :], dram["small"]),
                    (c.big_loaded, c.CT[:, :], ctx), (c.big_loaded, c.valid_i32[:, :], dram["valid"]),
                    (c.big_loaded, c.attend[:, :], dram["attend"])])
    loads_done(c, c.loaded)
    for sub in SUBLAYERS[:upto]:
        sub(c)
    with nc.Block() as block:
        @block.sync
        def _(sp):
            sp.dma_start(out, c.X[:, :]).then_inc(c.stored.sem, 16)
            sp.wait_ge(c.stored.sem, c.stored.at(16))


SUBLAYERS = [layer0_attention, layer0_cross, layer0_experts, layer1_attention, layer1_cross, layer1_experts, layer2_attention,
             layer2_cross, layer2_mlp, layer3_attention, layer3_cross, layer3_block]


def kernel(**inputs):
    from concourse import bacc
    from concourse.bass_utils import run_bass_kernel_spmd

    a = {k: np.asarray(v) for k, v in inputs.items()}
    L = lay_out(a)
    arrays = {f"{k}_dram": v for k, v in L.packed().items()}
    arrays["x_dram"] = feature_major(a["x"])
    arrays["ctx_dram"] = feature_major(a["ctx_1024"])
    arrays["valid_dram"] = np.ascontiguousarray(everywhere(a["mask_B_ik0"]))
    arrays["attend_dram"] = np.ascontiguousarray(
        everywhere(np.ascontiguousarray(a["mask_BxS2_bk0"]).view(np.int32)))
    nc = bacc.Bacc("TRN2", target_bir_lowering=False, num_devices=1)
    ap = {k: nc.dram_tensor(k, v.shape, mybir.dt.from_np(v.dtype), kind="ExternalInput").ap()
          for k, v in arrays.items()}
    out = nc.dram_tensor("out_dram", (P, N), F32, kind="ExternalOutput").ap()
    decoder(nc, L.slots, L.words, {k[:-5]: v for k, v in ap.items()}, ap["x_dram"], ap["ctx_dram"], out)
    r = run_bass_kernel_spmd(nc, [arrays], core_ids=[0])
    return r.results[0]["out_dram"].T.reshape(B, S, P)
```
